# Optimizing a Trainium2 kernel written in Bass

```python
import numpy as np
import jax
import jax.numpy as jnp

def _softmax(x, axis=-1):
    return jax.nn.softmax(x, axis=axis)

def _gelu(x):
    return jax.nn.gelu(x, approximate=True)

def _silu(x):
    return jax.nn.silu(x)

def _sigmoid(x):
    return jax.nn.sigmoid(x)

def _layernorm(x, axis=-1, eps=1e-05):
    m = jnp.mean(x, axis=axis, keepdims=True)
    v = jnp.var(x, axis=axis, keepdims=True)
    return (x - m) / jnp.sqrt(v + eps)

def _scatter_add(tgt, idx, src, axis=0):
    return tgt.at[idx].add(src)

def _segment_sum(src, seg, n):
    return jax.ops.segment_sum(src, seg, n)
kernel_name = 'mk_macaron_d4_jaxref_r8_49c0b5'

def setup_inputs(seed: int=0):
    np.random.seed(seed)
    _w = jnp.asarray

    def _L0_attn_setup():
        import jax, jax.numpy as jnp
        import numpy as np
        EMBED = 128
        HEADS = 16
        HEAD_DIM = EMBED // HEADS
        MAP_DIM = HEAD_DIM
        B, S = (2, 512)
        key = jax.random.key(seed)
        ks = jax.random.split(key, 8)
        x = jax.random.normal(ks[0], (B, S, EMBED), jnp.float32)
        scale = 1.0 / np.sqrt(EMBED)
        Wq = jax.random.normal(ks[1], (EMBED, EMBED), jnp.float32) * scale
        Wk = jax.random.normal(ks[2], (EMBED, EMBED), jnp.float32) * scale
        Wv = jax.random.normal(ks[3], (EMBED, EMBED), jnp.float32) * scale
        bq = jax.random.normal(ks[4], (EMBED,), jnp.float32) * 0.01
        bk = jax.random.normal(ks[5], (EMBED,), jnp.float32) * 0.01
        bv = jax.random.normal(ks[6], (EMBED,), jnp.float32) * 0.01
        weights = jax.random.normal(ks[7], (HEADS, MAP_DIM, HEAD_DIM), jnp.float32)
        return {'x': x, 'Wq': Wq, 'bq': bq, 'Wk': Wk, 'bk': bk, 'Wv': Wv, 'bv': bv, 'weights': weights}
    _L0_attn_in = _L0_attn_setup()

    def _L0_ffn_setup():
        import jax, jax.numpy as jnp
        import numpy as np
        B, S, D, E = (4, 512, 128, 8)
        key = jax.random.key(seed)
        k1, k2, k3, k4, k5 = jax.random.split(key, 5)
        scale = 1.0 / np.sqrt(D)
        return {'x': jax.random.normal(k1, (B, S, D), dtype=jnp.float32), 'Wg': jax.random.normal(k2, (D, D), dtype=jnp.float32) * scale, 'bg': jnp.zeros((D,), dtype=jnp.float32), 'We': jax.random.normal(k3, (E, D, D), dtype=jnp.float32) * scale, 'be': jnp.zeros((E, D), dtype=jnp.float32)}
    _L0_ffn_in = _L0_ffn_setup()

    def _L1_attn_setup():
        import jax, jax.numpy as jnp
        from jax import lax
        import numpy as np
        D = 128
        H = 16
        DK = 64
        DV = 128
        KDIM = H * DK
        VDIM = H * DV
        CONV_K = 4
        B, T = (2, 512)
        EPS = 1e-05

        def _causal_conv_silu(x, w):
            C = x.shape[-1]
            Kw = w.shape[-1]
            xp = jnp.pad(x, ((0, 0), (Kw - 1, 0), (0, 0))).transpose(0, 2, 1)
            y = lax.conv_general_dilated(xp, w[:, None, :], window_strides=(1,), padding='VALID', feature_group_count=C, dimension_numbers=('NCH', 'OIH', 'NCH'))
            return jax.nn.silu(y.transpose(0, 2, 1))

        def _l2norm(x, eps=1e-06):
            return x * lax.rsqrt(jnp.sum(x * x, axis=-1, keepdims=True) + eps)

        def _gated_delta_rule(q, k, v, g, beta):
            scale = q.shape[-1] ** (-0.5)
            qs = jnp.moveaxis(q, 1, 0)
            ks_ = jnp.moveaxis(k, 1, 0)
            vs = jnp.moveaxis(v, 1, 0)
            gs = jnp.moveaxis(g, 1, 0)
            bs = jnp.moveaxis(beta, 1, 0)

            def step(S, inp):
                q_t, k_t, v_t, g_t, b_t = inp
                S = S * jnp.exp(g_t)[..., None, None]
                mem = jnp.einsum('bhk,bhkv->bhv', k_t, S)
                delta = (v_t - mem) * b_t[..., None]
                S = S + jnp.einsum('bhk,bhv->bhkv', k_t, delta)
                o_t = jnp.einsum('bhk,bhkv->bhv', q_t * scale, S)
                return (S, o_t)
            S0 = jnp.zeros((q.shape[0], q.shape[2], q.shape[3], v.shape[3]), q.dtype)
            _, o = lax.scan(step, S0, (qs, ks_, vs, gs, bs))
            return jnp.moveaxis(o, 0, 1)
        key = jax.random.key(seed)
        ks = jax.random.split(key, 14)

        def w(k, shape, s=0.02):
            return jax.random.normal(k, shape, jnp.float32) * s
        return {'x': jax.random.normal(ks[0], (B, T, D), jnp.float32), 'w_q': w(ks[1], (D, KDIM)), 'w_k': w(ks[2], (D, KDIM)), 'w_v': w(ks[3], (D, VDIM)), 'w_a': w(ks[4], (D, H)), 'w_b': w(ks[5], (D, H)), 'w_g': w(ks[6], (D, VDIM)), 'w_out': w(ks[7], (VDIM, D)), 'A_log': jnp.log(jax.random.uniform(ks[8], (H,), jnp.float32, 1.0, 16.0)), 'dt_bias': jax.random.uniform(ks[9], (H,), jnp.float32, -4.0, -1.0), 'conv_q': w(ks[10], (KDIM, CONV_K), 0.1), 'conv_k': w(ks[11], (KDIM, CONV_K), 0.1), 'conv_v': w(ks[12], (VDIM, CONV_K), 0.1), 'norm_w': jnp.ones((DV,), jnp.float32)}
    _L1_attn_in = _L1_attn_setup()

    def _L1_ffn_setup():
        import jax, jax.numpy as jnp
        import numpy as np
        NQ, NK, H, DH = (128, 64, 8, 64)
        key = jax.random.key(seed)
        ks = jax.random.split(key, 8)
        b, n, d, g = (4, 512, 128, 4)
        di = H * DH
        s = lambda fan: 1.0 / np.sqrt(fan)
        return {'x': jax.random.normal(ks[0], (b, n, d), jnp.float32), 'w_qr': jax.random.normal(ks[1], (g, d), jnp.float32) * s(d), 'w_kvr': jax.random.normal(ks[2], (g, d), jnp.float32) * s(d), 'w_q': jax.random.normal(ks[3], (g, di, d), jnp.float32) * s(d), 'w_kv': jax.random.normal(ks[4], (g, 2 * di, d), jnp.float32) * s(d), 'w_out': jax.random.normal(ks[5], (g, d, di), jnp.float32) * s(di), 'null_kv': jax.random.normal(ks[6], (2, g, H, 1, DH), jnp.float32), 'null_token': jax.random.normal(ks[7], (1, 1, d), jnp.float32)}
    _L1_ffn_in = _L1_ffn_setup()

    def _L2_attn_setup():
        import jax, jax.numpy as jnp
        import numpy as np
        N_HEADS = 16
        EPS = 1e-06
        key = jax.random.key(seed)
        ks = jax.random.split(key, 10)
        B, T, D = (2, 256, 128)
        x = jax.random.normal(ks[0], (B, T, D), dtype=jnp.float32)
        norm_w = jnp.ones((D,), dtype=jnp.float32)
        bound = float(np.sqrt(6.0 / (D + D)))

        def lin(k):
            return jax.random.uniform(k, (D, D), dtype=jnp.float32, minval=-bound, maxval=bound)
        Wq, Wk, Wv, Wo = (lin(ks[1]), lin(ks[2]), lin(ks[3]), lin(ks[4]))
        bq = jnp.zeros((D,), dtype=jnp.float32)
        bk = jnp.zeros((D,), dtype=jnp.float32)
        bv = jnp.zeros((D,), dtype=jnp.float32)
        bo = jnp.zeros((D,), dtype=jnp.float32)
        return {'x': x, 'norm_w': norm_w, 'Wq': Wq, 'bq': bq, 'Wk': Wk, 'bk': bk, 'Wv': Wv, 'bv': bv, 'Wo': Wo, 'bo': bo}
    _L2_attn_in = _L2_attn_setup()

    def _L2_ffn_setup():
        import jax, jax.numpy as jnp
        import numpy as np
        DIM = 128
        INTER = 128
        N_EXPERTS = 8
        TOPK = 2
        N_SHARED = 2
        key = jax.random.key(seed)
        ks = jax.random.split(key, 10)
        s = 0.02
        return {'x': jax.random.normal(ks[0], (4, 256, DIM), dtype=jnp.float32), 'gate_w': jax.random.normal(ks[1], (N_EXPERTS, DIM), dtype=jnp.float32) * s, 'gate_bias': jax.random.normal(ks[2], (N_EXPERTS,), dtype=jnp.float32) * s, 'w1': jax.random.normal(ks[3], (N_EXPERTS, INTER, DIM), dtype=jnp.float32) * s, 'w3': jax.random.normal(ks[4], (N_EXPERTS, INTER, DIM), dtype=jnp.float32) * s, 'w2': jax.random.normal(ks[5], (N_EXPERTS, DIM, INTER), dtype=jnp.float32) * s, 'sw1': jax.random.normal(ks[6], (N_SHARED * INTER, DIM), dtype=jnp.float32) * s, 'sw3': jax.random.normal(ks[7], (N_SHARED * INTER, DIM), dtype=jnp.float32) * s, 'sw2': jax.random.normal(ks[8], (DIM, N_SHARED * INTER), dtype=jnp.float32) * s}
    _L2_ffn_in = _L2_ffn_setup()

    def _L3_attn_setup():
        import jax, jax.numpy as jnp
        import numpy as np
        D = 128
        H = 16
        HD = D // H
        K = 4
        I = int(D * 2.7)
        B, T = (2, 256)
        EPS = 1e-06
        GATE_BIAS = 4.0

        def _rmsnorm(x, w):
            return x * jax.lax.rsqrt(jnp.mean(x * x, axis=-1, keepdims=True) + EPS) * w

        def _causal_depthwise_conv(x, conv_w, conv_b):
            xt = jnp.transpose(x, (0, 2, 1))
            y = jax.lax.conv_general_dilated(xt, conv_w[:, None, :], window_strides=(1,), padding=[(K - 1, 0)], feature_group_count=D, dimension_numbers=('NCH', 'OIH', 'NCH'))
            y = jnp.transpose(y, (0, 2, 1)) + conv_b
            return jax.nn.silu(y)

        def _l2norm(x):
            return x * jax.lax.rsqrt(jnp.sum(x * x, axis=-1, keepdims=True) + EPS)

        def _gated_delta_rule(xc, wq, wk, wv, wb, wa):
            b, t = (xc.shape[0], xc.shape[1])
            q = _l2norm((xc @ wq).reshape(b, t, H, HD))
            k = _l2norm((xc @ wk).reshape(b, t, H, HD))
            v = (xc @ wv).reshape(b, t, H, HD)
            beta = jax.nn.sigmoid(xc @ wb)
            alpha = jax.nn.sigmoid(xc @ wa + GATE_BIAS)
            qt = jnp.moveaxis(q, 1, 0)
            kt = jnp.moveaxis(k, 1, 0)
            vt = jnp.moveaxis(v, 1, 0)
            bt = jnp.moveaxis(beta, 1, 0)
            at = jnp.moveaxis(alpha, 1, 0)
            S0 = jnp.zeros((b, H, HD, HD), xc.dtype)

            def step(S, inp):
                q_, k_, v_, b_, a_ = inp
                S = a_[..., None, None] * S
                pred = jnp.einsum('bhkv,bhk->bhv', S, k_)
                S = S + k_[..., :, None] * (b_[..., None] * (v_ - pred))[..., None, :]
                o = jnp.einsum('bhkv,bhk->bhv', S, q_)
                return (S, o)
            _, o = jax.lax.scan(step, S0, (qt, kt, vt, bt, at))
            return jnp.moveaxis(o, 1, 0).reshape(b, t, D)
        key = jax.random.key(seed)
        ks = jax.random.split(key, 16)
        s = D ** (-0.5)
        return {'x': jax.random.normal(ks[0], (B, T, D), jnp.float32), 'norm1_w': jnp.ones((D,), jnp.float32), 'norm2_w': jnp.ones((D,), jnp.float32), 'conv_w': jax.random.normal(ks[1], (D, K), jnp.float32) * 0.2, 'conv_b': jnp.zeros((D,), jnp.float32), 'wq': jax.random.normal(ks[2], (D, D), jnp.float32) * s, 'wk': jax.random.normal(ks[3], (D, D), jnp.float32) * s, 'wv': jax.random.normal(ks[4], (D, D), jnp.float32) * s, 'wb': jax.random.normal(ks[5], (D, H), jnp.float32) * s, 'wa': jax.random.normal(ks[6], (D, H), jnp.float32) * s, 'wo': jax.random.normal(ks[7], (D, D), jnp.float32) * s, 'wg': jax.random.normal(ks[8], (D, I), jnp.float32) * s, 'wu': jax.random.normal(ks[9], (D, I), jnp.float32) * s, 'wd': jax.random.normal(ks[10], (I, D), jnp.float32) * I ** (-0.5)}
    _L3_attn_in = _L3_attn_setup()

    def _L3_ffn_setup():
        import jax, jax.numpy as jnp
        import numpy as np
        D_IN, D_HID = (128, 512)

        def _ternary(key, shape):
            return jax.random.randint(key, shape, -1, 2).astype(jnp.float32)

        def _tlin(x, w, s):
            return jnp.einsum('bsi,oi->bso', x, w) * s
        key = jax.random.key(seed)
        ks = jax.random.split(key, 12)
        inv = lambda fan: 1.0 / np.sqrt(fan).astype(np.float32)
        return {'x': jax.random.normal(ks[0], (4, 256, D_IN), dtype=jnp.float32), 'w1_w': _ternary(ks[1], (D_HID, D_IN)), 'w1_s': jax.random.uniform(ks[2], (D_HID,), dtype=jnp.float32) * inv(D_IN), 'w2_w': _ternary(ks[3], (D_HID, D_IN)), 'w2_s': jax.random.uniform(ks[4], (D_HID,), dtype=jnp.float32) * inv(D_IN), 'h1_w': _ternary(ks[5], (D_HID, D_HID)), 'h1_s': jax.random.uniform(ks[6], (D_HID,), dtype=jnp.float32) * inv(D_HID), 'h2_w': _ternary(ks[7], (D_HID, D_HID)), 'h2_s': jax.random.uniform(ks[8], (D_HID,), dtype=jnp.float32) * inv(D_HID), 'w3_w': _ternary(ks[9], (D_IN, D_HID)), 'w3_s': jax.random.uniform(ks[10], (D_IN,), dtype=jnp.float32) * inv(D_HID)}
    _L3_ffn_in = _L3_ffn_setup()
    _d = {'L0_attn_x': _L0_attn_in['x'], 'L0_attn_Wq': _L0_attn_in['Wq'], 'L0_attn_bq': _L0_attn_in['bq'], 'L0_attn_Wk': _L0_attn_in['Wk'], 'L0_attn_bk': _L0_attn_in['bk'], 'L0_attn_Wv': _L0_attn_in['Wv'], 'L0_attn_bv': _L0_attn_in['bv'], 'L0_attn_weights': _L0_attn_in['weights'], 'L0_ffn_Wg': _L0_ffn_in['Wg'], 'L0_ffn_bg': _L0_ffn_in['bg'], 'L0_ffn_We': _L0_ffn_in['We'], 'L0_ffn_be': _L0_ffn_in['be'], 'L1_attn_w_q': _L1_attn_in['w_q'], 'L1_attn_w_k': _L1_attn_in['w_k'], 'L1_attn_w_v': _L1_attn_in['w_v'], 'L1_attn_w_a': _L1_attn_in['w_a'], 'L1_attn_w_b': _L1_attn_in['w_b'], 'L1_attn_w_g': _L1_attn_in['w_g'], 'L1_attn_w_out': _L1_attn_in['w_out'], 'L1_attn_A_log': _L1_attn_in['A_log'], 'L1_attn_dt_bias': _L1_attn_in['dt_bias'], 'L1_attn_conv_q': _L1_attn_in['conv_q'], 'L1_attn_conv_k': _L1_attn_in['conv_k'], 'L1_attn_conv_v': _L1_attn_in['conv_v'], 'L1_attn_norm_w': _L1_attn_in['norm_w'], 'L1_ffn_w_qr': _L1_ffn_in['w_qr'], 'L1_ffn_w_kvr': _L1_ffn_in['w_kvr'], 'L1_ffn_w_q': _L1_ffn_in['w_q'], 'L1_ffn_w_kv': _L1_ffn_in['w_kv'], 'L1_ffn_w_out': _L1_ffn_in['w_out'], 'L1_ffn_null_kv': _L1_ffn_in['null_kv'], 'L1_ffn_null_token': _L1_ffn_in['null_token'], 'L2_attn_norm_w': _L2_attn_in['norm_w'], 'L2_attn_Wq': _L2_attn_in['Wq'], 'L2_attn_bq': _L2_attn_in['bq'], 'L2_attn_Wk': _L2_attn_in['Wk'], 'L2_attn_bk': _L2_attn_in['bk'], 'L2_attn_Wv': _L2_attn_in['Wv'], 'L2_attn_bv': _L2_attn_in['bv'], 'L2_attn_Wo': _L2_attn_in['Wo'], 'L2_attn_bo': _L2_attn_in['bo'], 'L2_ffn_gate_w': _L2_ffn_in['gate_w'], 'L2_ffn_gate_bias': _L2_ffn_in['gate_bias'], 'L2_ffn_w1': _L2_ffn_in['w1'], 'L2_ffn_w3': _L2_ffn_in['w3'], 'L2_ffn_w2': _L2_ffn_in['w2'], 'L2_ffn_sw1': _L2_ffn_in['sw1'], 'L2_ffn_sw3': _L2_ffn_in['sw3'], 'L2_ffn_sw2': _L2_ffn_in['sw2'], 'L3_attn_norm1_w': _L3_attn_in['norm1_w'], 'L3_attn_norm2_w': _L3_attn_in['norm2_w'], 'L3_attn_conv_w': _L3_attn_in['conv_w'], 'L3_attn_conv_b': _L3_attn_in['conv_b'], 'L3_attn_wq': _L3_attn_in['wq'], 'L3_attn_wk': _L3_attn_in['wk'], 'L3_attn_wv': _L3_attn_in['wv'], 'L3_attn_wb': _L3_attn_in['wb'], 'L3_attn_wa': _L3_attn_in['wa'], 'L3_attn_wo': _L3_attn_in['wo'], 'L3_attn_wg': _L3_attn_in['wg'], 'L3_attn_wu': _L3_attn_in['wu'], 'L3_attn_wd': _L3_attn_in['wd'], 'L3_ffn_w1_w': _L3_ffn_in['w1_w'], 'L3_ffn_w1_s': _L3_ffn_in['w1_s'], 'L3_ffn_w2_w': _L3_ffn_in['w2_w'], 'L3_ffn_w2_s': _L3_ffn_in['w2_s'], 'L3_ffn_h1_w': _L3_ffn_in['h1_w'], 'L3_ffn_h1_s': _L3_ffn_in['h1_s'], 'L3_ffn_h2_w': _L3_ffn_in['h2_w'], 'L3_ffn_h2_s': _L3_ffn_in['h2_s'], 'L3_ffn_w3_w': _L3_ffn_in['w3_w'], 'L3_ffn_w3_s': _L3_ffn_in['w3_s']}
    _x0 = _d['L0_attn_x']
    _d['L0_attn_x'] = jax.random.normal(jax.random.fold_in(jax.random.key(seed), 1), (16, 256, 128), dtype=_x0.dtype)
    del _x0
    return _d

def reference(L0_attn_x, L0_attn_Wq, L0_attn_bq, L0_attn_Wk, L0_attn_bk, L0_attn_Wv, L0_attn_bv, L0_attn_weights, L0_ffn_Wg, L0_ffn_bg, L0_ffn_We, L0_ffn_be, L1_attn_w_q, L1_attn_w_k, L1_attn_w_v, L1_attn_w_a, L1_attn_w_b, L1_attn_w_g, L1_attn_w_out, L1_attn_A_log, L1_attn_dt_bias, L1_attn_conv_q, L1_attn_conv_k, L1_attn_conv_v, L1_attn_norm_w, L1_ffn_w_qr, L1_ffn_w_kvr, L1_ffn_w_q, L1_ffn_w_kv, L1_ffn_w_out, L1_ffn_null_kv, L1_ffn_null_token, L2_attn_norm_w, L2_attn_Wq, L2_attn_bq, L2_attn_Wk, L2_attn_bk, L2_attn_Wv, L2_attn_bv, L2_attn_Wo, L2_attn_bo, L2_ffn_gate_w, L2_ffn_gate_bias, L2_ffn_w1, L2_ffn_w3, L2_ffn_w2, L2_ffn_sw1, L2_ffn_sw3, L2_ffn_sw2, L3_attn_norm1_w, L3_attn_norm2_w, L3_attn_conv_w, L3_attn_conv_b, L3_attn_wq, L3_attn_wk, L3_attn_wv, L3_attn_wb, L3_attn_wa, L3_attn_wo, L3_attn_wg, L3_attn_wu, L3_attn_wd, L3_ffn_w1_w, L3_ffn_w1_s, L3_ffn_w2_w, L3_ffn_w2_s, L3_ffn_h1_w, L3_ffn_h1_s, L3_ffn_h2_w, L3_ffn_h2_s, L3_ffn_w3_w, L3_ffn_w3_s):

    def _L0_attn_ref(x, Wq, bq, Wk, bk, Wv, bv, weights):
        import jax, jax.numpy as jnp
        import numpy as np
        EMBED = 128
        HEADS = 16
        HEAD_DIM = EMBED // HEADS
        MAP_DIM = HEAD_DIM
        B, S = (2, 512)
        Bx, Sx, E = x.shape
        H, M, D = weights.shape
        q = (x @ Wq.T + bq).reshape(Bx, Sx, H, D)
        k = (x @ Wk.T + bk).reshape(Bx, Sx, H, D)
        v = (x @ Wv.T + bv).reshape(Bx, Sx, H, D)
        q = q / jnp.linalg.norm(q)
        k = k / jnp.linalg.norm(k)

        def phi(t):
            sq_norm = jnp.sum(t * t)
            scale = jnp.exp(-sq_norm / 2) / jnp.sqrt(jnp.float32(M))
            return jnp.exp(jnp.einsum('hmd,bshd->bshm', weights, t)) * scale
        phi_q = phi(q)
        phi_k = phi(k)
        s = jnp.einsum('bshm,bshm->bsh', phi_q, phi_k)[..., None]
        out = s * v / s
        return out.reshape(Bx, Sx, E)

    def _L0_ffn_ref(x, Wg, bg, We, be):
        import jax, jax.numpy as jnp
        import numpy as np
        B, S, D, E = (4, 512, 128, 8)
        probs = jax.nn.softmax(x @ Wg + bg, axis=-1)
        idx = jnp.argmax(probs, axis=-1)
        p = jnp.take_along_axis(probs, idx[..., None], axis=-1)[..., 0]
        e_idx = idx % We.shape[0]
        h = jax.nn.relu(jnp.einsum('bsd,edf->besf', x, We) + be[None, :, None, :])
        onehot = jax.nn.one_hot(e_idx, We.shape[0], dtype=x.dtype)
        out = jnp.einsum('besf,bse->bsf', h, onehot) * p[..., None]
        return out

    def _L1_attn_ref(x, w_q, w_k, w_v, w_a, w_b, w_g, w_out, A_log, dt_bias, conv_q, conv_k, conv_v, norm_w):
        import jax, jax.numpy as jnp
        from jax import lax
        import numpy as np
        D = 128
        H = 16
        DK = 64
        DV = 128
        KDIM = H * DK
        VDIM = H * DV
        CONV_K = 4
        B, T = (2, 512)
        EPS = 1e-05

        def _causal_conv_silu(x, w):
            C = x.shape[-1]
            Kw = w.shape[-1]
            xp = jnp.pad(x, ((0, 0), (Kw - 1, 0), (0, 0))).transpose(0, 2, 1)
            y = lax.conv_general_dilated(xp, w[:, None, :], window_strides=(1,), padding='VALID', feature_group_count=C, dimension_numbers=('NCH', 'OIH', 'NCH'))
            return jax.nn.silu(y.transpose(0, 2, 1))

        def _l2norm(x, eps=1e-06):
            return x * lax.rsqrt(jnp.sum(x * x, axis=-1, keepdims=True) + eps)

        def _gated_delta_rule(q, k, v, g, beta):
            scale = q.shape[-1] ** (-0.5)
            qs = jnp.moveaxis(q, 1, 0)
            ks_ = jnp.moveaxis(k, 1, 0)
            vs = jnp.moveaxis(v, 1, 0)
            gs = jnp.moveaxis(g, 1, 0)
            bs = jnp.moveaxis(beta, 1, 0)

            def step(S, inp):
                q_t, k_t, v_t, g_t, b_t = inp
                S = S * jnp.exp(g_t)[..., None, None]
                mem = jnp.einsum('bhk,bhkv->bhv', k_t, S)
                delta = (v_t - mem) * b_t[..., None]
                S = S + jnp.einsum('bhk,bhv->bhkv', k_t, delta)
                o_t = jnp.einsum('bhk,bhkv->bhv', q_t * scale, S)
                return (S, o_t)
            S0 = jnp.zeros((q.shape[0], q.shape[2], q.shape[3], v.shape[3]), q.dtype)
            _, o = lax.scan(step, S0, (qs, ks_, vs, gs, bs))
            return jnp.moveaxis(o, 0, 1)
        Bx, Tx, _ = x.shape
        q = x @ w_q
        k = x @ w_k
        v = x @ w_v
        beta = jax.nn.sigmoid(x @ w_b) * 2.0
        g = -jnp.exp(A_log) * jax.nn.softplus(x @ w_a + dt_bias)
        q = _causal_conv_silu(q, conv_q)
        k = _causal_conv_silu(k, conv_k)
        v = _causal_conv_silu(v, conv_v)
        q = q.reshape(Bx, Tx, H, DK)
        k = k.reshape(Bx, Tx, H, DK)
        v = v.reshape(Bx, Tx, H, DV)
        q = _l2norm(q)
        k = _l2norm(k)
        o = _gated_delta_rule(q, k, v, g, beta)
        g_gate = (x @ w_g).reshape(Bx, Tx, H, DV)
        rms = o * lax.rsqrt(jnp.mean(o * o, axis=-1, keepdims=True) + EPS)
        y = rms * norm_w * jax.nn.silu(g_gate)
        return y.reshape(Bx, Tx, VDIM) @ w_out

    def _L1_ffn_ref(x, w_qr, w_kvr, w_q, w_kv, w_out, null_kv, null_token):
        import jax, jax.numpy as jnp
        import numpy as np
        NQ, NK, H, DH = (128, 64, 8, 64)
        b, n, d = x.shape
        g = w_qr.shape[0]
        bidx = jnp.arange(b)[:, None, None]
        q_logits = jnp.einsum('bnd,gd->bgn', x, w_qr)
        q_top, q_idx = jax.lax.top_k(q_logits, NQ)
        q_scores = jax.nn.sigmoid(q_top)[..., None]
        queries = x[bidx, q_idx]
        kv_logits = jnp.einsum('bnd,gd->bgn', x, w_kvr)
        kv_top, kv_idx = jax.lax.top_k(kv_logits, NK)
        kv_scores = jax.nn.sigmoid(kv_top)[:, :, None, :, None]
        key_values = x[bidx, kv_idx]
        q = jnp.einsum('bgnd,ged->bgne', queries, w_q)
        kv = jnp.einsum('bgnd,ged->bgne', key_values, w_kv)
        k, v = jnp.split(kv, 2, axis=-1)
        heads = lambda t: t.reshape(b, g, -1, H, DH).transpose(0, 1, 3, 2, 4)
        q, k, v = (heads(q), heads(k), heads(v))
        v = v * kv_scores
        nk = jnp.broadcast_to(null_kv[0][None], (b, g, H, 1, DH))
        nv = jnp.broadcast_to(null_kv[1][None], (b, g, H, 1, DH))
        k = jnp.concatenate([nk, k], axis=-2)
        v = jnp.concatenate([nv, v], axis=-2)
        attn = jax.nn.softmax(jnp.einsum('bghid,bghjd->bghij', q, k) * DH ** (-0.5), axis=-1)
        o = jnp.einsum('bghij,bghjd->bghid', attn, v)
        o = o.transpose(0, 1, 3, 2, 4).reshape(b, g, NQ, H * DH)
        o = jnp.einsum('bgne,gde->bgnd', o, w_out)
        o = o * q_scores
        flat_idx = q_idx.reshape(b, g * NQ)
        flat_o = o.reshape(b, g * NQ, d)
        b2 = jnp.arange(b)[:, None]
        summed = jnp.zeros_like(x).at[b2, flat_idx].add(flat_o)
        counts = jnp.zeros((b, n), x.dtype).at[b2, flat_idx].add(1.0)[..., None]
        meaned = summed / jnp.clip(counts, 1e-05)
        return jnp.where(counts > 0, meaned, null_token)

    def _L2_attn_ref(x, norm_w, Wq, bq, Wk, bk, Wv, bv, Wo, bo):
        import jax, jax.numpy as jnp
        import numpy as np
        N_HEADS = 16
        EPS = 1e-06
        B, T, D = x.shape
        H = N_HEADS
        hd = D // H
        xn = x * jax.lax.rsqrt(jnp.mean(x * x, axis=-1, keepdims=True) + EPS) * norm_w
        q = (xn @ Wq.T + bq).reshape(B, T, H, hd).transpose(0, 2, 1, 3)
        k = (xn @ Wk.T + bk).reshape(B, T, H, hd).transpose(0, 2, 1, 3)
        v = (xn @ Wv.T + bv).reshape(B, T, H, hd).transpose(0, 2, 1, 3)
        scale = 1.0 / jnp.sqrt(jnp.asarray(hd, dtype=x.dtype))
        scores = jnp.einsum('bhqd,bhkd->bhqk', q, k) * scale
        causal = jnp.triu(jnp.ones((T, T), dtype=bool), k=1)
        scores = jnp.where(causal, jnp.asarray(-jnp.inf, dtype=scores.dtype), scores)
        attn = jax.nn.softmax(scores, axis=-1)
        out = jnp.einsum('bhqk,bhkd->bhqd', attn, v)
        out = out.transpose(0, 2, 1, 3).reshape(B, T, D)
        out = out @ Wo.T + bo
        return xn + out

    def _L2_ffn_ref(x, gate_w, gate_bias, w1, w3, w2, sw1, sw3, sw2):
        import jax, jax.numpy as jnp
        import numpy as np
        DIM = 128
        INTER = 128
        N_EXPERTS = 8
        TOPK = 2
        N_SHARED = 2
        shape = x.shape
        xt = x.reshape(-1, shape[-1])
        scores = jax.nn.softmax((xt @ gate_w.T).astype(jnp.float32), axis=-1)
        _, idx = jax.lax.top_k(scores + gate_bias, TOPK)
        weights = jnp.take_along_axis(scores, idx, axis=1).astype(x.dtype)
        y = jnp.zeros_like(xt)
        for e in range(N_EXPERTS):
            gate_e = jnp.sum(jnp.where(idx == e, weights, 0.0), axis=1)
            h = jax.nn.silu(xt @ w1[e].T) * (xt @ w3[e].T)
            y = y + gate_e[:, None] * (h @ w2[e].T)
        z = jax.nn.silu(xt @ sw1.T) * (xt @ sw3.T) @ sw2.T
        return (y + z).reshape(shape)

    def _L3_attn_ref(x, norm1_w, norm2_w, conv_w, conv_b, wq, wk, wv, wb, wa, wo, wg, wu, wd):
        import jax, jax.numpy as jnp
        import numpy as np
        D = 128
        H = 16
        HD = D // H
        K = 4
        I = int(D * 2.7)
        B, T = (2, 256)
        EPS = 1e-06
        GATE_BIAS = 4.0

        def _rmsnorm(x, w):
            return x * jax.lax.rsqrt(jnp.mean(x * x, axis=-1, keepdims=True) + EPS) * w

        def _causal_depthwise_conv(x, conv_w, conv_b):
            xt = jnp.transpose(x, (0, 2, 1))
            y = jax.lax.conv_general_dilated(xt, conv_w[:, None, :], window_strides=(1,), padding=[(K - 1, 0)], feature_group_count=D, dimension_numbers=('NCH', 'OIH', 'NCH'))
            y = jnp.transpose(y, (0, 2, 1)) + conv_b
            return jax.nn.silu(y)

        def _l2norm(x):
            return x * jax.lax.rsqrt(jnp.sum(x * x, axis=-1, keepdims=True) + EPS)

        def _gated_delta_rule(xc, wq, wk, wv, wb, wa):
            b, t = (xc.shape[0], xc.shape[1])
            q = _l2norm((xc @ wq).reshape(b, t, H, HD))
            k = _l2norm((xc @ wk).reshape(b, t, H, HD))
            v = (xc @ wv).reshape(b, t, H, HD)
            beta = jax.nn.sigmoid(xc @ wb)
            alpha = jax.nn.sigmoid(xc @ wa + GATE_BIAS)
            qt = jnp.moveaxis(q, 1, 0)
            kt = jnp.moveaxis(k, 1, 0)
            vt = jnp.moveaxis(v, 1, 0)
            bt = jnp.moveaxis(beta, 1, 0)
            at = jnp.moveaxis(alpha, 1, 0)
            S0 = jnp.zeros((b, H, HD, HD), xc.dtype)

            def step(S, inp):
                q_, k_, v_, b_, a_ = inp
                S = a_[..., None, None] * S
                pred = jnp.einsum('bhkv,bhk->bhv', S, k_)
                S = S + k_[..., :, None] * (b_[..., None] * (v_ - pred))[..., None, :]
                o = jnp.einsum('bhkv,bhk->bhv', S, q_)
                return (S, o)
            _, o = jax.lax.scan(step, S0, (qt, kt, vt, bt, at))
            return jnp.moveaxis(o, 1, 0).reshape(b, t, D)
        residual = x
        xn = _rmsnorm(x, norm1_w)
        xc = _causal_depthwise_conv(xn, conv_w, conv_b)
        mixer_out = _gated_delta_rule(xc, wq, wk, wv, wb, wa) @ wo
        h = residual + mixer_out
        hn = _rmsnorm(h, norm2_w)
        ffn = jax.nn.silu(hn @ wg) * (hn @ wu) @ wd
        return h + ffn

    def _L3_ffn_ref(x, w1_w, w1_s, w2_w, w2_s, h1_w, h1_s, h2_w, h2_s, w3_w, w3_s):
        import jax, jax.numpy as jnp
        import numpy as np
        D_IN, D_HID = (128, 512)

        def _ternary(key, shape):
            return jax.random.randint(key, shape, -1, 2).astype(jnp.float32)

        def _tlin(x, w, s):
            return jnp.einsum('bsi,oi->bso', x, w) * s
        h = jax.nn.silu(_tlin(x, w1_w, w1_s)) * _tlin(x, w2_w, w2_s)
        h = jax.nn.gelu(_tlin(h, h1_w, h1_s), approximate=False)
        h = jax.nn.gelu(_tlin(h, h2_w, h2_s), approximate=False)
        return _tlin(h, w3_w, w3_s)
    x = L0_attn_x
    x = x + 0.5 * _L0_ffn_ref(_layernorm(x, axis=-1), L0_ffn_Wg, L0_ffn_bg, L0_ffn_We, L0_ffn_be)
    x = x + _L0_attn_ref(_layernorm(x, axis=-1), L0_attn_Wq, L0_attn_bq, L0_attn_Wk, L0_attn_bk, L0_attn_Wv, L0_attn_bv, L0_attn_weights)
    x = x + 0.5 * _L0_ffn_ref(_layernorm(x, axis=-1), L0_ffn_Wg, L0_ffn_bg, L0_ffn_We, L0_ffn_be)
    x = x + 0.5 * _L1_ffn_ref(_layernorm(x, axis=-1), L1_ffn_w_qr, L1_ffn_w_kvr, L1_ffn_w_q, L1_ffn_w_kv, L1_ffn_w_out, L1_ffn_null_kv, L1_ffn_null_token)
    x = x + _L1_attn_ref(_layernorm(x, axis=-1), L1_attn_w_q, L1_attn_w_k, L1_attn_w_v, L1_attn_w_a, L1_attn_w_b, L1_attn_w_g, L1_attn_w_out, L1_attn_A_log, L1_attn_dt_bias, L1_attn_conv_q, L1_attn_conv_k, L1_attn_conv_v, L1_attn_norm_w)
    x = x + 0.5 * _L1_ffn_ref(_layernorm(x, axis=-1), L1_ffn_w_qr, L1_ffn_w_kvr, L1_ffn_w_q, L1_ffn_w_kv, L1_ffn_w_out, L1_ffn_null_kv, L1_ffn_null_token)
    x = x + 0.5 * _L2_ffn_ref(_layernorm(x, axis=-1), L2_ffn_gate_w, L2_ffn_gate_bias, L2_ffn_w1, L2_ffn_w3, L2_ffn_w2, L2_ffn_sw1, L2_ffn_sw3, L2_ffn_sw2)
    x = x + _L2_attn_ref(_layernorm(x, axis=-1), L2_attn_norm_w, L2_attn_Wq, L2_attn_bq, L2_attn_Wk, L2_attn_bk, L2_attn_Wv, L2_attn_bv, L2_attn_Wo, L2_attn_bo)
    x = x + 0.5 * _L2_ffn_ref(_layernorm(x, axis=-1), L2_ffn_gate_w, L2_ffn_gate_bias, L2_ffn_w1, L2_ffn_w3, L2_ffn_w2, L2_ffn_sw1, L2_ffn_sw3, L2_ffn_sw2)
    x = x + 0.5 * _L3_ffn_ref(_layernorm(x, axis=-1), L3_ffn_w1_w, L3_ffn_w1_s, L3_ffn_w2_w, L3_ffn_w2_s, L3_ffn_h1_w, L3_ffn_h1_s, L3_ffn_h2_w, L3_ffn_h2_s, L3_ffn_w3_w, L3_ffn_w3_s)
    x = x + _L3_attn_ref(_layernorm(x, axis=-1), L3_attn_norm1_w, L3_attn_norm2_w, L3_attn_conv_w, L3_attn_conv_b, L3_attn_wq, L3_attn_wk, L3_attn_wv, L3_attn_wb, L3_attn_wa, L3_attn_wo, L3_attn_wg, L3_attn_wu, L3_attn_wd)
    x = x + 0.5 * _L3_ffn_ref(_layernorm(x, axis=-1), L3_ffn_w1_w, L3_ffn_w1_s, L3_ffn_w2_w, L3_ffn_w2_s, L3_ffn_h1_w, L3_ffn_h1_s, L3_ffn_h2_w, L3_ffn_h2_s, L3_ffn_w3_w, L3_ffn_w3_s)
    return x

_drawn_inputs = setup_inputs


def setup_inputs(seed=0):
    import zlib

    import numpy as np

    out = dict(_drawn_inputs(seed))
    spreads = {'L0_ffn_bg': (0.0, 0.1),
     'L0_ffn_be': (0.0, 0.1),
     'L1_attn_norm_w': (1.0, 0.2),
     'L2_attn_norm_w': (1.0, 0.2),
     'L2_attn_bq': (0.0, 0.1),
     'L2_attn_bk': (0.0, 0.1),
     'L2_attn_bv': (0.0, 0.1),
     'L2_attn_bo': (0.0, 0.1),
     'L3_attn_norm1_w': (1.0, 0.2),
     'L3_attn_norm2_w': (1.0, 0.2),
     'L3_attn_conv_b': (0.0, 0.1)}
    factors = {}
    for name, (base, spread) in spreads.items():
        noise = np.random.default_rng([zlib.crc32(name.encode()), seed]).standard_normal(out[name].shape)
        drawn = base * np.exp(spread * noise) if base else spread * noise
        out[name] = jnp.asarray(drawn.astype(out[name].dtype))
    for name, factor in factors.items():
        out[name] = (out[name] * factor).astype(out[name].dtype)
    return out
```

```python
from contextlib import ExitStack

import concourse.bass as bass
from concourse import mybir

F32 = mybir.dt.float32
ACT = mybir.ActivationFunctionType
ALU = mybir.AluOpType
AX = mybir.AxisListType

P = 128
D = 128
BATCH = 16
SEQ = 256
TOKENS = BATCH * SEQ
TILES = TOKENS // P
TPB = SEQ // P
LN_EPS = 1e-5
SEMAPHORES = 120
STEPS = tuple(range(12))

CONST_PARTS = [("ident", 128), ("ones", 128), ("iota", 128), ("rev_iota", 128), ("upto", 128),
               ("after", 128), ("blocks8", 128), ("heads8", 16), ("level1n", 128), ("level1tn", 128),
               ("level", 6 * 128), ("row_index", 1), ("is_query", 1), ("quarter", 4), ("minus_half", 512),
               ("eps_ln", 1), ("eps_l2", 1), ("causal", 128), ("before8", 64), ("alpha_bias", 1)]
CONST_AT = {}
_at = 0
for _name, _width in CONST_PARTS:
    CONST_AT[_name] = (_at, _width)
    _at += _width
CONST_COLS = _at


class Stage:
    pool = []
    taken = 0

    def __init__(self, nc, name):
        self.nc, self.name, self.ctx, self.first = nc, name, ExitStack(), Stage.taken

    def __enter__(self):
        return self

    def sb(self, name, shape):
        return self.ctx.enter_context(self.nc.sbuf_tensor(f"{self.name}_{name}", shape, F32))

    def ps(self, name, shape):
        return self.ctx.enter_context(self.nc.psum_tensor(f"{self.name}_{name}", shape, F32))

    def sem(self, name):
        Stage.taken += 1
        return Stage.pool[Stage.taken - 1]

    def sems(self, name, n):
        return [self.sem(f"{name}{i}") for i in range(n)]

    def __exit__(self, kind, value, trace):
        if kind is None and Stage.taken > self.first:
            used = [s.num for s in Stage.pool[self.first:Stage.taken]]
            self.nc.all_engine_barrier(sems_to_clear=range(used[0], used[-1] + 1))
            Stage.taken = self.first
        self.ctx.close()


class Globals:

    def __init__(self, nc, ctx, dram, out):
        self.dram, self.out = dram, out
        self.X = ctx.enter_context(nc.sbuf_tensor("X", [P, TILES, D], F32))
        self.const = ctx.enter_context(nc.sbuf_tensor("const", [P, CONST_COLS], F32))
        self.mean = ctx.enter_context(nc.sbuf_tensor("mean", [P, TILES], F32))
        self.rstd = ctx.enter_context(nc.sbuf_tensor("rstd", [P, TILES], F32))

    def c(self, name):
        at, width = CONST_AT[name]
        return self.const[:, at:at + width]

    def tile(self, t):
        return self.X[:, bass.ds(t, 1), :]


def load_stream(nc, g):
    with Stage(nc, "load") as st:
        s_in = st.sem("in")
        with nc.Block() as block:
            @block.sync
            def _(sp):
                sp.dma_start(g.X[:, :, :], g.dram["x"].rearrange("(t p) d -> p t d", p=P)).then_inc(s_in, 16)
                sp.dma_start(g.const[:, :], g.dram["consts"]).then_inc(s_in, 16)
                sp.wait_ge(s_in, 32)


def store_stream(nc, g):
    with Stage(nc, "store") as st:
        s_out = st.sem("out")
        with nc.Block() as block:
            @block.sync
            def _(sp):
                sp.dma_start(g.out.rearrange("(t p) d -> p t d", p=P), g.X[:, :, :]).then_inc(s_out, 16)
                sp.wait_ge(s_out, 16)


def row_statistics(nc, g, name, loads=()):
    with Stage(nc, name + "_stat") as st:
        parts = st.sb("parts", [P, TILES, 6])
        tmp = st.sb("tmp", [P, 3, TILES])
        s_load = st.sem("load")
        s_parts = st.sem("parts")
        s_step = st.sem("step")
        s_var = st.sem("var")
        s_std = st.sem("std")
        with nc.Block() as block:
            @block.sync
            def _(sp):
                for dst, src in loads:
                    sp.dma_start(dst, src).then_inc(s_load, 16)
                if loads:
                    sp.wait_ge(s_load, 16 * len(loads))

            @block.vector
            def _(dve):
                with dve.Fori(0, TILES) as t:
                    nc.vector.bn_stats(parts[:, bass.ds(t, 1), :], g.X[:, bass.ds(t, 1), :]).then_inc(s_parts, 1)
                dve.wait_ge(s_parts, TILES)
                nc.vector.tensor_tensor(g.mean[:, :], parts[:, :, 1], parts[:, :, 4], ALU.add).then_inc(s_step, 1)
                nc.vector.tensor_tensor(tmp[:, 0, :], parts[:, :, 1], parts[:, :, 4], ALU.subtract).then_inc(s_step, 1)
                nc.vector.tensor_tensor(tmp[:, 1, :], parts[:, :, 2], parts[:, :, 5], ALU.add).then_inc(s_step, 1)
                dve.wait_ge(s_step, 3)
                nc.vector.tensor_scalar(g.mean[:, :], g.mean[:, :], 0.5, None, ALU.mult).then_inc(s_step, 1)
                nc.vector.scalar_tensor_tensor(tmp[:, 2, :], tmp[:, 0, :], 0.25, tmp[:, 0, :],
                                               ALU.mult, ALU.mult).then_inc(s_step, 1)
                dve.wait_ge(s_step, 5)
                nc.vector.scalar_tensor_tensor(tmp[:, 0, :], tmp[:, 1, :], 1.0 / D, tmp[:, 2, :],
                                               ALU.mult, ALU.add).then_inc(s_var, 1)
                dve.wait_ge(s_std, 1)
                nc.vector.reciprocal(g.rstd[:, :], tmp[:, 1, :]).then_inc(s_step, 1)

            @block.scalar
            def _(act):
                act.wait_ge(s_var, 1)
                nc.scalar.activation(tmp[:, 1, :], tmp[:, 0, :], ACT.Sqrt, bias=g.c("eps_ln")).then_inc(s_std, 1)


L0_EXPERTS = 8
L0F_PARTS = [("wg", 128), ("we", L0_EXPERTS * 128), ("bg", 128), ("be", L0_EXPERTS * 128)]


def columns(parts):
    at, out = 0, {}
    for name, width in parts:
        out[name] = slice(at, at + width)
        at += width
    return out, at


def l0_ffn(nc, g, name):
    E = L0_EXPERTS
    cols, width = columns(L0F_PARTS)
    NS = 2
    with Stage(nc, name) as st:
        w = st.sb("w", [P, width])
        row_statistics(nc, g, name, [(w[:, :], g.dram["w_l0f"])])
        xn = [st.sb(f"xn{s}", [P, D]) for s in range(NS)]
        xT = [st.sb(f"xT{s}", [P, P]) for s in range(NS)]
        logits = [st.sb(f"logits{s}", [P, D]) for s in range(NS)]
        neg_max = [st.sb(f"neg_max{s}", [P, 1]) for s in range(NS)]
        key = [st.sb(f"key{s}", [P, D]) for s in range(NS)]
        first = [st.sb(f"first{s}", [P, 1]) for s in range(NS)]
        gate = [st.sb(f"gate{s}", [P, E]) for s in range(NS)]
        prob = [st.sb(f"prob{s}", [P, D]) for s in range(NS)]
        total = [st.sb(f"total{s}", [P, 2]) for s in range(NS)]
        acc = [st.sb(f"acc{s}", [P, D]) for s in range(NS)]
        small = [st.ps(f"small{s}", [P, 512]) for s in range(NS)]
        hidden = [st.ps(f"hidden{s}", [P, E * D]) for s in range(NS)]
        xn_ready = st.sems("xn_ready", NS)
        turned = st.sems("turned", NS)
        xT_ready = st.sems("xT_ready", NS)
        logits_ready = st.sems("logits_ready", NS)
        logits_saved = st.sems("logits_saved", NS)
        hidden_ready = st.sems("hidden_ready", NS)
        max_ready = st.sems("max_ready", NS)
        exp_done = st.sems("exp_done", NS)
        gate_step = st.sems("gate_step", NS)
        relu_done = st.sems("relu_done", NS)
        slot_free = st.sems("slot_free", NS)
        mix_step = st.sems("mix_step", NS)
        GATE_STEPS, MIX_STEPS = 5, E + 1

        with nc.Block() as block:
            @block.vector
            def _(dve):
                for s in range(NS):
                    dve.sem_inc(slot_free[s], 1)
                with dve.Fori(0, TILES // NS) as it:
                    for s in range(NS):
                        t = it * NS + s
                        dve.wait_ge(slot_free[s], it + 1)
                        nc.vector.tensor_scalar(xn[s][:, :], g.tile(t), g.mean[:, bass.ds(t, 1)],
                                                g.rstd[:, bass.ds(t, 1)], ALU.subtract, ALU.mult).then_inc(xn_ready[s], 1)
                    for s in range(NS):
                        dve.wait_ge(logits_saved[s], it + 1)
                        nc.vector.tensor_reduce(neg_max[s][:, :], logits[s][:, :], AX.X, ALU.max,
                                                negate=True).then_inc(max_ready[s], 1)
                        nc.vector.tensor_reduce(total[s][:, 1:2], logits[s][:, :], AX.X,
                                                ALU.max).then_inc(gate_step[s], 1)
                    for s in range(NS):
                        dve.wait_ge(gate_step[s], it * GATE_STEPS + 1)
                        nc.vector.scalar_tensor_tensor(key[s][:, :], logits[s][:, :], total[s][:, 1:2],
                                                       g.c("rev_iota"), ALU.is_equal, ALU.mult).then_inc(gate_step[s], 1)
                    for s in range(NS):
                        dve.wait_ge(gate_step[s], it * GATE_STEPS + 2)
                        nc.vector.tensor_reduce(first[s][:, :], key[s][:, :], AX.X, ALU.max).then_inc(gate_step[s], 1)
                    for s in range(NS):
                        dve.wait_ge(gate_step[s], it * GATE_STEPS + 3)
                        nc.vector.tensor_scalar(key[s][:, :], g.c("rev_iota"), first[s][:, :], None,
                                                ALU.is_equal).then_inc(gate_step[s], 1)
                    for s in range(NS):
                        dve.wait_ge(gate_step[s], it * GATE_STEPS + 4)
                        nc.vector.tensor_reduce(gate[s][:, :], key[s][:, :].rearrange("p (k e) -> p e k", e=E),
                                                AX.X, ALU.add).then_inc(gate_step[s], 1)
                    for e in range(E):
                        for s in range(NS):
                            h = hidden[s][:, e * D:(e + 1) * D]
                            if e == 0:
                                dve.wait_ge(gate_step[s], it * GATE_STEPS + 5)
                                dve.wait_ge(hidden_ready[s], it + 1)
                                nc.vector.tensor_scalar(acc[s][:, :], h, gate[s][:, 0:1], None,
                                                        ALU.mult).then_inc(mix_step[s], 1)
                            else:
                                dve.wait_ge(mix_step[s], it * MIX_STEPS + e)
                                nc.vector.scalar_tensor_tensor(acc[s][:, :], h, gate[s][:, e:e + 1], acc[s][:, :],
                                                               ALU.mult, ALU.add).then_inc(mix_step[s], 1)
                    for s in range(NS):
                        dve.wait_ge(exp_done[s], it + 1)
                        nc.vector.reciprocal(total[s][:, 1:2], total[s][:, 0:1]).then_inc(mix_step[s], 1)
                    for s in range(NS):
                        dve.wait_ge(mix_step[s], it * MIX_STEPS + E + 1)
                        nc.vector.tensor_scalar(acc[s][:, :], acc[s][:, :], 0.0, total[s][:, 1:2],
                                                ALU.max, ALU.mult).then_inc(relu_done[s], 1)
                    for s in range(NS):
                        t = it * NS + s
                        dve.wait_ge(relu_done[s], it + 1)
                        nc.vector.scalar_tensor_tensor(g.tile(t), acc[s][:, :], 0.5, g.tile(t),
                                                       ALU.mult, ALU.add).then_inc(slot_free[s], 1)

            @block.tensor
            def _(pe):
                with pe.Fori(0, TILES // NS) as it:
                    for s in range(NS):
                        pe.wait_ge(xn_ready[s], it + 1)
                        nc.tensor.transpose(small[s][:, 0:128], xn[s][:, :], g.c("ident")).then_inc(turned[s], 1)
                    for s in range(NS):
                        pe.wait_ge(xT_ready[s], it + 1)
                        nc.tensor.matmul(small[s][:, 128:256], xT[s][:, :], w[:, cols["wg"]], start=True, stop=False)
                        nc.tensor.matmul(small[s][:, 128:256], g.c("ones")[0:1, :], w[0:1, cols["bg"]],
                                         start=False, stop=True).then_inc(logits_ready[s], 1)
                        for half in range(2):
                            o = hidden[s][:, half * 512:half * 512 + 512]
                            a = half * 512
                            nc.tensor.matmul(o, xT[s][:, :], w[:, cols["we"]][:, a:a + 512], start=True, stop=False)
                            last = nc.tensor.matmul(o, g.c("ones")[0:1, :], w[0:1, cols["be"]][:, a:a + 512],
                                                    start=False, stop=True)
                        last.then_inc(hidden_ready[s], 1)

            @block.scalar
            def _(act):
                with act.Fori(0, TILES // NS) as it:
                    for s in range(NS):
                        act.wait_ge(turned[s], it + 1)
                        nc.scalar.copy(xT[s][:, :], small[s][:, 0:128]).then_inc(xT_ready[s], 1)
                    for s in range(NS):
                        act.wait_ge(logits_ready[s], it + 1)
                        nc.scalar.copy(logits[s][:, :], small[s][:, 128:256]).then_inc(logits_saved[s], 1)
                    for s in range(NS):
                        act.wait_ge(max_ready[s], it + 1)
                        nc.scalar.activation(prob[s][:, :], logits[s][:, :], ACT.Exp, bias=neg_max[s][:, :],
                                             accum_out=total[s][:, 0:1]).then_inc(exp_done[s], 1)


L0A_HEADS, L0A_HD = 16, 8
L0A_PARTS = [("wq", 128), ("wk", 128), ("wv", 128), ("phi", 128), ("bv", 128), ("bq", 1), ("bk", 1)]


def l0_attn(nc, g, name):
    cols, width = columns(L0A_PARTS)
    NS = 2
    N = SEQ
    with Stage(nc, name) as st:
        w = st.sb("w", [P, width])
        QT = st.sb("QT", [P, TOKENS])
        KT = st.sb("KT", [P, TOKENS])
        V = st.sb("V", [P, TILES, D])
        heads_scaled = st.sb("heads_scaled", [P, L0A_HEADS])
        norms = st.sb("norms", [P, 12])
        sums = [st.sb(f"sums{s}", [P, 2]) for s in range(NS)]
        row_statistics(nc, g, name, [(w[:, :], g.dram["w_l0a"])])

        with Stage(nc, name + "_a") as sa:
            xn = [sa.sb(f"xn{s}", [P, TPB, D]) for s in range(NS)]
            xT = [sa.sb(f"xT{s}", [P, N]) for s in range(NS)]
            square = [sa.sb(f"square{s}", [P, 2 * N]) for s in range(NS)]
            sq = [sa.sb(f"sq{s}", [P, 2]) for s in range(NS)]
            turn = [sa.ps(f"turn{s}", [P, 512]) for s in range(NS)]
            qk = [sa.ps(f"qk{s}", [P, 512]) for s in range(NS)]
            vps = [sa.ps(f"vps{s}", [P, 512]) for s in range(NS)]
            slot_free = sa.sems("slot_free", NS)
            sums_clear = sa.sem("sums_clear")
            xn_ready = sa.sems("xn_ready", NS)
            turned = sa.sems("turned", NS)
            xT_ready = sa.sems("xT_ready", NS)
            qk_ready = sa.sems("qk_ready", NS)
            v_ready = sa.sems("v_ready", NS)
            qk_saved = sa.sems("qk_saved", NS)
            v_saved = sa.sems("v_saved", NS)
            with nc.Block() as block:
                @block.vector
                def _(dve):
                    for s in range(NS):
                        nc.vector.memset(sums[s][:, :], 0.0).then_inc(slot_free[s], 1)
                    with dve.Fori(0, BATCH // NS) as it:
                        for s in range(NS):
                            dve.wait_ge(slot_free[s], it + 1)
                            for u in range(TPB):
                                t = (it * NS + s) * TPB + u
                                last = nc.vector.tensor_scalar(xn[s][:, u, :], g.tile(t), g.mean[:, bass.ds(t, 1)],
                                                               g.rstd[:, bass.ds(t, 1)], ALU.subtract, ALU.mult)
                            last.then_inc(xn_ready[s], 1)
                        for s in range(NS):
                            dve.wait_ge(v_ready[s], it + 1)
                            nc.vector.tensor_copy(V[:, bass.ds((it * NS + s) * TPB, TPB), :],
                                                  vps[s][:, 0:TPB * D].rearrange("p (u d) -> p u d", u=TPB)
                                                  ).then_inc(v_saved[s], 1)
                        for s in range(NS):
                            dve.wait_ge(qk_saved[s], it + 1)
                            dve.wait_ge(v_saved[s], it + 1)
                            nc.vector.tensor_tensor(sums[s][:, :], sums[s][:, :], sq[s][:, :],
                                                    ALU.add).then_inc(slot_free[s], 1)

                @block.tensor
                def _(pe):
                    with pe.Fori(0, BATCH // NS) as it:
                        for s in range(NS):
                            pe.wait_ge(xn_ready[s], it + 1)
                            for u in range(TPB):
                                last = nc.tensor.transpose(turn[s][:, u * P:(u + 1) * P], xn[s][:, u, :], g.c("ident"))
                            last.then_inc(turned[s], 1)
                        for s in range(NS):
                            pe.wait_ge(xT_ready[s], it + 1)
                            nc.tensor.matmul(qk[s][:, 0:N], w[:, cols["wq"]], xT[s][:, :], start=True, stop=True)
                            nc.tensor.matmul(qk[s][:, N:2 * N], w[:, cols["wk"]], xT[s][:, :], start=True,
                                             stop=True).then_inc(qk_ready[s], 1)
                            for u in range(TPB):
                                o = vps[s][:, u * D:(u + 1) * D]
                                nc.tensor.matmul(o, xT[s][:, u * P:(u + 1) * P], w[:, cols["wv"]], start=True, stop=False)
                                last = nc.tensor.matmul(o, g.c("ones")[0:1, :], w[0:1, cols["bv"]], start=False, stop=True)
                            last.then_inc(v_ready[s], 1)

                @block.scalar
                def _(act):
                    with act.Fori(0, BATCH // NS) as it:
                        for s in range(NS):
                            act.wait_ge(turned[s], it + 1)
                            nc.scalar.copy(xT[s][:, :], turn[s][:, 0:N]).then_inc(xT_ready[s], 1)
                        for s in range(NS):
                            act.wait_ge(qk_ready[s], it + 1)
                            b = it * NS + s
                            for k, (dst, bias) in enumerate(((QT, "bq"), (KT, "bk"))):
                                src = qk[s][:, k * N:(k + 1) * N]
                                nc.scalar.activation(dst[:, bass.ds(b * N, N)], src, ACT.Identity, bias=w[:, cols[bias]])
                                last = nc.scalar.activation(square[s][:, k * N:(k + 1) * N], src, ACT.Square, bias=w[:, cols[bias]],
                                                            accum_out=sq[s][:, k:k + 1])
                            last.then_inc(qk_saved[s], 1)

        with Stage(nc, name + "_n") as sn:
            total = sn.ps("total", [P, 512])
            step = sn.sem("step")
            summed = sn.sem("summed")
            rooted = sn.sem("rooted")
            scaled = sn.sem("scaled")
            exped = sn.sem("exped")
            with nc.Block() as block:
                @block.vector
                def _(dve):
                    nc.vector.tensor_tensor(norms[:, 0:2], sums[0][:, :], sums[1][:, :], ALU.add).then_inc(step, 1)
                    dve.wait_ge(rooted, 1)
                    nc.vector.reciprocal(norms[:, 4:6], norms[:, 2:4]).then_inc(step, 1)
                    dve.wait_ge(step, 2)
                    nc.vector.tensor_tensor(norms[:, 6:8], total[:, 0:2], norms[:, 4:6], ALU.mult).then_inc(step, 1)
                    dve.wait_ge(step, 3)
                    nc.vector.tensor_tensor(norms[:, 6:8], norms[:, 6:8], norms[:, 4:6], ALU.mult).then_inc(scaled, 1)
                    dve.wait_ge(exped, 1)
                    nc.vector.tensor_scalar(norms[:, 10:11], norms[:, 8:9], norms[:, 9:10], 1.0 / L0A_HD,
                                            ALU.mult, ALU.mult).then_inc(step, 1)
                    dve.wait_ge(step, 4)
                    nc.vector.tensor_scalar(heads_scaled[:, :], g.c("heads8"), norms[:, 10:11], None,
                                            ALU.mult).then_inc(step, 1)

                @block.tensor
                def _(pe):
                    pe.wait_ge(step, 1)
                    nc.tensor.matmul(total[:, 0:2], g.c("ones"), norms[:, 0:2], start=True, stop=True).then_inc(summed, 1)

                @block.scalar
                def _(act):
                    act.wait_ge(summed, 1)
                    nc.scalar.activation(norms[:, 2:4], total[:, 0:2], ACT.Sqrt).then_inc(rooted, 1)
                    act.wait_ge(scaled, 1)
                    nc.scalar.activation(norms[:, 8:10], norms[:, 6:8], ACT.Exp, scale=-0.5).then_inc(exped, 1)

        with Stage(nc, name + "_b") as sb:
            feats = [sb.sb(f"feats{s}", [P, 2 * N]) for s in range(NS)]
            prod = [sb.sb(f"prod{s}", [P, N]) for s in range(NS)]
            sim = [sb.sb(f"sim{s}", [P, TPB * L0A_HEADS]) for s in range(NS)]
            inv = [sb.sb(f"inv{s}", [P, TPB * L0A_HEADS]) for s in range(NS)]
            mix = [sb.sb(f"mix{s}", [P, TPB * D]) for s in range(NS)]
            proj = [sb.ps(f"proj{s}", [P, 512]) for s in range(NS)]
            sim_ps = [sb.ps(f"sim_ps{s}", [P, 512]) for s in range(NS)]
            slot_free = sb.sems("slot_free", NS)
            projected = sb.sems("projected", NS)
            exp_done = sb.sems("exp_done", NS)
            prod_ready = sb.sems("prod_ready", NS)
            sim_ready = sb.sems("sim_ready", NS)
            mix_step = sb.sems("mix_step", NS)
            MIX_STEPS = 4
            with nc.Block() as block:
                @block.tensor
                def _(pe):
                    for s in range(NS):
                        pe.sem_inc(slot_free[s], 1)
                    with pe.Fori(0, BATCH // NS) as it:
                        for s in range(NS):
                            pe.wait_ge(slot_free[s], it + 1)
                            b = it * NS + s
                            nc.tensor.matmul(proj[s][:, 0:N], w[:, cols["phi"]], QT[:, bass.ds(b * N, N)], start=True, stop=True)
                            nc.tensor.matmul(proj[s][:, N:2 * N], w[:, cols["phi"]], KT[:, bass.ds(b * N, N)], start=True,
                                             stop=True).then_inc(projected[s], 1)
                        for s in range(NS):
                            pe.wait_ge(prod_ready[s], it + 1)
                            for u in range(TPB):
                                last = nc.tensor.matmul(sim_ps[s][:, u * L0A_HEADS:(u + 1) * L0A_HEADS],
                                                        prod[s][:, u * P:(u + 1) * P], heads_scaled[:, :], start=True, stop=True)
                            last.then_inc(sim_ready[s], 1)

                @block.scalar
                def _(act):
                    with act.Fori(0, BATCH // NS) as it:
                        for s in range(NS):
                            act.wait_ge(projected[s], it + 1)
                            nc.scalar.activation(feats[s][:, 0:N], proj[s][:, 0:N], ACT.Exp, scale=norms[:, 4:5])
                            nc.scalar.activation(feats[s][:, N:2 * N], proj[s][:, N:2 * N], ACT.Exp,
                                                 scale=norms[:, 5:6]).then_inc(exp_done[s], 1)

                @block.gpsimd
                def _(pool):
                    with pool.Fori(0, BATCH // NS) as it:
                        for s in range(NS):
                            pool.wait_ge(exp_done[s], it + 1)
                            nc.gpsimd.tensor_tensor(prod[s][:, :], feats[s][:, 0:N], feats[s][:, N:2 * N],
                                                    ALU.mult).then_inc(prod_ready[s], 1)

                @block.vector
                def _(dve):
                    with dve.Fori(0, BATCH // NS) as it:
                        for s in range(NS):
                            dve.wait_ge(sim_ready[s], it + 1)
                            nc.vector.tensor_copy(sim[s][:, :], sim_ps[s][:, 0:TPB * L0A_HEADS]).then_inc(mix_step[s], 1)
                        for s in range(NS):
                            t = (it * NS + s) * TPB
                            dve.wait_ge(mix_step[s], it * MIX_STEPS + 1)
                            nc.vector.reciprocal(inv[s][:, :], sim[s][:, :]).then_inc(mix_step[s], 1)
                            nc.vector.tensor_tensor(
                                mix[s][:, :].rearrange("p (h e) -> p h e", e=L0A_HD),
                                V[:, bass.ds(t, TPB), :].rearrange("p u (h e) -> p (u h) e", e=L0A_HD),
                                sim[s][:, :].unsqueeze(2).broadcast_to([P, TPB * L0A_HEADS, L0A_HD]),
                                ALU.mult).then_inc(mix_step[s], 1)
                        for s in range(NS):
                            dve.wait_ge(mix_step[s], it * MIX_STEPS + 3)
                            nc.vector.tensor_tensor(
                                mix[s][:, :].rearrange("p (h e) -> p h e", e=L0A_HD),
                                mix[s][:, :].rearrange("p (h e) -> p h e", e=L0A_HD),
                                inv[s][:, :].unsqueeze(2).broadcast_to([P, TPB * L0A_HEADS, L0A_HD]),
                                ALU.mult).then_inc(mix_step[s], 1)
                        for s in range(NS):
                            t = (it * NS + s) * TPB
                            dve.wait_ge(mix_step[s], it * MIX_STEPS + 4)
                            nc.vector.tensor_tensor(g.X[:, bass.ds(t, TPB), :].rearrange("p u d -> p (u d)"),
                                                    g.X[:, bass.ds(t, TPB), :].rearrange("p u d -> p (u d)"),
                                                    mix[s][:, :], ALU.add).then_inc(slot_free[s], 1)


L1_G, L1_NQ, L1_NK, L1_H, L1_DH = 4, 128, 64, 8, 64
L1_DI = L1_H * L1_DH
L1_C = L1_DI // P
L1F_PARTS = [("route", 2 * L1_G), ("wq", L1_G * L1_DI), ("wk", L1_G * L1_DI), ("wv", L1_G * L1_DI),
             ("wo", L1_G * L1_C * D), ("null_kb", L1_G * L1_C * 2), ("null_token", D)]
LOWEST = -3.4028235e38


def l1_ffn(nc, g, name):
    G, NQ, NK, H, DH, C = L1_G, L1_NQ, L1_NK, L1_H, L1_DH, L1_C
    cols, width = columns(L1F_PARTS)
    N = SEQ
    NS = 2
    USES = G // NS
    ROWS = 2 * G
    with Stage(nc, name) as st:
        w = st.sb("w", [P, width])
        row_statistics(nc, g, name, [(w[:, :], g.dram["w_l1f"])])
        logits_d = nc.dram_tensor(name + "_logits", (BATCH, ROWS, N), F32, kind="Internal").ap()
        place_d = nc.dram_tensor(name + "_place", (P, N), F32, kind="Internal").ap()
        placeT = st.sb("placeT", [P, TPB, P])
        scoreT = st.sb("scoreT", [P, TPB, P])
        mean_by = st.sb("mean_by", [P, TPB, BATCH])
        unpicked = st.sb("unpicked", [P, TPB, BATCH])

        with Stage(nc, name + "_l") as sl:
            XT = sl.sb("XT", [P, TOKENS])
            row = sl.sb("row", [ROWS, TOKENS])
            turn_stream(nc, g, name, XT)
            bank = [sl.ps(f"bank{s}", [P, 512]) for s in range(4)]
            slot_free = sl.sems("slot_free", 4)
            ready = sl.sems("ready", 4)
            stored = sl.sem("stored")
            with nc.Block() as block:
                @block.tensor
                def _(pe):
                    for s in range(4):
                        pe.sem_inc(slot_free[s], 1)
                    with pe.Fori(0, TOKENS // 512 // 4) as it:
                        for s in range(4):
                            pe.wait_ge(slot_free[s], it + 1)
                            nc.tensor.matmul(bank[s][0:ROWS, :], w[:, cols["route"]], XT[:, bass.ds((it * 4 + s) * 512, 512)],
                                             start=True, stop=True).then_inc(ready[s], 1)

                @block.scalar
                def _(act):
                    with act.Fori(0, TOKENS // 512 // 4) as it:
                        for s in range(4):
                            act.wait_ge(ready[s], it + 1)
                            nc.scalar.copy(row[:, bass.ds((it * 4 + s) * 512, 512)], bank[s][0:ROWS, :]).then_inc(slot_free[s], 1)

                @block.sync
                def _(sp):
                    for s in range(4):
                        sp.wait_ge(slot_free[s], TOKENS // 512 // 4 + 1)
                    sp.dma_start(logits_d.rearrange("b k t -> k b t"), row[:, :].rearrange("k (b t) -> k b t", b=BATCH)
                                 ).then_inc(stored, 16)
                    sp.wait_ge(stored, 16)

        with Stage(nc, name + "_t") as sk:
            logit = sk.sb("logit", [P, N])
            left = [sk.sb(f"left{i}", [P, N]) for i in range(2)]
            top8 = sk.sb("top8", [P, 8])
            mark64 = sk.sb("mark64", [P, N])
            mark = sk.sb("mark", [P, N])
            count = sk.sb("count", [P, N])
            place = sk.sb("place", [P, N])
            score = sk.sb("score", [P, N])
            picks = sk.sb("picks", [P, TPB, P])
            num = sk.sb("num", [P, TPB, BATCH])
            turn = sk.ps("turn", [P, 512])
            loaded = sk.sem("loaded")
            pick = sk.sem("pick")
            step = sk.sem("step")
            placed = sk.sem("placed")
            scored = sk.sem("scored")
            turned = sk.sem("turned")
            stored = sk.sem("stored")
            with nc.Block() as block:
                @block.sync
                def _(sp):
                    sp.dma_start(logit[:, :], logits_d.rearrange("b k t -> (b k) t")).then_inc(loaded, 16)
                    sp.wait_ge(placed, 1)
                    sp.dma_start(place_d, place[:, :]).then_inc(stored, 16)
                    sp.wait_ge(stored, 16)

                @block.scalar
                def _(act):
                    act.wait_ge(loaded, 16)
                    nc.scalar.activation(score[:, :], logit[:, :], ACT.Sigmoid).then_inc(scored, 1)

                @block.vector
                def _(dve):
                    dve.wait_ge(loaded, 16)
                    done = 0
                    src = logit
                    for r in range(NQ // 8):
                        if done:
                            dve.wait_ge(pick, done)
                        nc.vector.max(top8[:, :], src[:, :]).then_inc(pick, 1)
                        dve.wait_ge(pick, done + 1)
                        dst = left[r % 2]
                        nc.vector.match_replace(dst[:, :], top8[:, :], src[:, :], LOWEST).then_inc(pick, 1)
                        done += 2
                        src = dst
                        if r == NK // 8 - 1:
                            dve.wait_ge(pick, done)
                            nc.vector.tensor_scalar(mark64[:, :], src[:, :], LOWEST, None, ALU.is_equal).then_inc(pick, 1)
                            done += 1
                    dve.wait_ge(pick, done)
                    nc.vector.tensor_scalar(count[:, :], src[:, :], LOWEST, None, ALU.is_equal).then_inc(step, 1)
                    dve.wait_ge(step, 1)
                    nc.vector.scalar_tensor_tensor(mark[:, :], count[:, :], g.c("is_query"), mark64[:, :], ALU.mult,
                                                   ALU.max).then_inc(step, 1)
                    dve.wait_ge(step, 2)
                    nc.vector.memset(mark64[:, :], 1.0).then_inc(step, 1)
                    dve.wait_ge(step, 3)
                    nc.vector.tensor_tensor_scan(count[:, :], mark64[:, :], mark[:, :], 0.0, ALU.mult, ALU.add).then_inc(step, 1)
                    dve.wait_ge(step, 4)
                    nc.vector.tensor_tensor(place[:, :], count[:, :], mark[:, :], ALU.mult).then_inc(step, 1)
                    dve.wait_ge(step, 5)
                    nc.vector.tensor_scalar(place[:, :], place[:, :], 1.0, None, ALU.subtract).then_inc(placed, 1)
                    dve.wait_ge(turned, 1)
                    nc.vector.tensor_copy(placeT[:, :, :], turn[:, 0:2 * P].rearrange("p (u r) -> p u r", u=TPB)).then_inc(step, 1)
                    nc.vector.tensor_copy(scoreT[:, :, :], turn[:, 2 * P:4 * P].rearrange("p (u r) -> p u r", u=TPB)).then_inc(step, 1)
                    dve.wait_ge(step, 7)
                    nc.vector.tensor_scalar(picks[:, :, :], placeT[:, :, :], 0.0, None, ALU.is_ge).then_inc(step, 1)
                    dve.wait_ge(step, 8)
                    nc.vector.tensor_reduce(num[:, :, :], picks[:, :, :].rearrange("p u (b r) -> p u b r", r=ROWS)[:, :, :, 0:G],
                                            AX.X, ALU.add).then_inc(step, 1)
                    dve.wait_ge(step, 9)
                    nc.vector.tensor_scalar(unpicked[:, :, :], num[:, :, :], 0.0, 0.5, ALU.is_equal, ALU.mult).then_inc(step, 1)
                    nc.vector.tensor_scalar(mean_by[:, :, :], num[:, :, :], 1e-5, None, ALU.max).then_inc(step, 1)
                    dve.wait_ge(step, 11)
                    nc.vector.reciprocal(mean_by[:, :, :], mean_by[:, :, :]).then_inc(step, 1)
                    dve.wait_ge(step, 12)
                    nc.vector.tensor_scalar(mean_by[:, :, :], mean_by[:, :, :], 0.5, None, ALU.mult).then_inc(step, 1)

                @block.tensor
                def _(pe):
                    pe.wait_ge(placed, 1)
                    pe.wait_ge(scored, 1)
                    for i, a in enumerate((place, score)):
                        for u in range(TPB):
                            last = nc.tensor.transpose(turn[:, (2 * i + u) * P:(2 * i + u + 1) * P], a[:, u * P:(u + 1) * P],
                                                       g.c("ident"))
                    last.then_inc(turned, 1)

        with Stage(nc, name + "_a") as sa:
            wq, wk, wv = (w[:, cols[n]].rearrange("p (g e) -> p g e", g=G) for n in ("wq", "wk", "wv"))
            wo = w[:, cols["wo"]].rearrange("p (g c d) -> p g c d", g=G, c=C)
            null_kb = w[:, cols["null_kb"]].rearrange("p (g c h) -> p g c h", g=G, c=C)
            xn = sa.sb("xn", [P, TPB, D])
            hot = sa.sb("hot", [P, TPB, G, NQ + NK])
            places = sa.sb("places", [P, G * N])
            hotT = sa.sb("hotT", [P, G, N])
            v = [sa.sb(f"v{k}", [NK + 1, L1_DI]) for k in range(G)]
            xg = [sa.sb(f"xg{s}", [P, NQ + NK]) for s in range(NS)]
            sg = [sa.sb(f"sg{s}", [P, 2]) for s in range(NS)]
            qT = [sa.sb(f"qT{s}", [P, C, NQ]) for s in range(NS)]
            kT = [sa.sb(f"kT{s}", [P, C, NK]) for s in range(NS)]
            top = [sa.sb(f"top{s}", [P, 2, C]) for s in range(NS)]
            prob = [sa.sb(f"prob{s}", [P, 2, C, NK + 1]) for s in range(NS)]
            den = [sa.sb(f"den{s}", [P, 2, C]) for s in range(NS)]
            probT = [sa.sb(f"probT{s}", [NK + 1, 2, C, NQ]) for s in range(NS)]
            oT = [sa.sb(f"oT{s}", [P, C, NQ]) for s in range(NS)]
            o = [sa.sb(f"o{s}", [P, D]) for s in range(NS)]
            bank_x = [sa.ps(f"bank_x{s}", [P, 512]) for s in range(NS)]
            bank_q = [sa.ps(f"bank_q{s}", [P, 512]) for s in range(NS)]
            bank_v = [sa.ps(f"bank_v{s}", [P, 512]) for s in range(NS)]
            bank_s = [sa.ps(f"bank_s{s}", [P, 512]) for s in range(NS)]
            null_loaded = sa.sem("null_loaded")
            batch_free = sa.sem("batch_free")
            places_loaded = sa.sem("places_loaded")
            hotT_ready = sa.sem("hotT_ready")
            xn_ready = sa.sem("xn_ready")
            hot_ready = sa.sem("hot_ready")
            null_added = sa.sem("null_added")
            gathered = sa.sems("gathered", NS)
            xg_saved = sa.sems("xg_saved", NS)
            q_ready = sa.sems("q_ready", NS)
            k_ready = sa.sems("k_ready", NS)
            v_ready = sa.sems("v_ready", NS)
            q_saved = sa.sems("q_saved", NS)
            k_saved = sa.sems("k_saved", NS)
            v_saved = sa.sems("v_saved", NS)
            s_ready = sa.sems("s_ready", NS)
            top_step = sa.sems("top_step", NS)
            shifted = sa.sems("shifted", NS)
            exp_done = sa.sems("exp_done", NS)
            den_step = sa.sems("den_step", NS)
            normed = sa.sems("normed", NS)
            pT_ready = sa.sems("pT_ready", NS)
            pTa_saved = sa.sems("pTa_saved", NS)
            pTb_saved = sa.sems("pTb_saved", NS)
            pv_ready = sa.sems("pv_ready", NS)
            oT_saved = sa.sems("oT_saved", NS)
            o_ready = sa.sems("o_ready", NS)
            o_saved = sa.sems("o_saved", NS)
            back_ready = sa.sems("back_ready", NS)
            slot_free = sa.sems("slot_free", NS)

            def use(it, k):
                return it * USES + k // NS + 1

            with nc.Block() as block:
                @block.sync
                def _(sp):
                    for k in range(G):
                        sp.dma_start(v[k][NK:NK + 1, :], g.dram["null_v"][k:k + 1, :]).then_inc(null_loaded, 16)
                    with sp.Fori(0, BATCH) as it:
                        sp.wait_ge(batch_free, it + 1)
                        sp.dma_start(places[:, :], place_d[bass.ds(it * ROWS, G), :].rearrange("r t -> (r t)").partition_broadcast(P)
                                     ).then_inc(places_loaded, 16)

                @block.gpsimd
                def _(pool):
                    with pool.Fori(0, BATCH) as it:
                        for pair in range(USES):
                            for s in range(NS):
                                k = pair * NS + s
                                pool.wait_ge(den_step[s], (use(it, k) - 1) * 2 + 2)
                                nc.gpsimd.tensor_tensor(prob[s][:, :, :, :].rearrange("p a c k -> p (a c) k"),
                                                        prob[s][:, :, :, :].rearrange("p a c k -> p (a c) k"),
                                                        den[s][:, :, :].rearrange("p a c -> p (a c)").unsqueeze(2)
                                                        .broadcast_to([P, H, NK + 1]), ALU.mult).then_inc(normed[s], 1)

                @block.vector
                def _(dve):
                    dve.sem_inc(batch_free, 1)
                    with dve.Fori(0, BATCH) as it:
                        for u in range(TPB):
                            t = it * TPB + u
                            last = nc.vector.tensor_scalar(xn[:, u, :], g.tile(t), g.mean[:, bass.ds(t, 1)],
                                                           g.rstd[:, bass.ds(t, 1)], ALU.subtract, ALU.mult)
                        last.then_inc(xn_ready, 1)
                        for u in range(TPB):
                            for at, n, r in ((0, NQ, 0), (NQ, NK, G)):
                                mine = placeT[:, u, bass.ds(it * ROWS + r, G)].unsqueeze(2).broadcast_to([P, G, n])
                                last = nc.vector.tensor_tensor(hot[:, u, :, at:at + n],
                                                               g.c("iota")[:, 0:n].unsqueeze(1).broadcast_to([P, G, n]),
                                                               mine, ALU.is_equal)
                        last.then_inc(hot_ready, 1)
                        dve.wait_ge(places_loaded, it * 16 + 16)
                        nc.vector.tensor_scalar(hotT[:, :, :].rearrange("p g t -> p (g t)"), places[:, :], g.c("row_index"), None,
                                                ALU.is_equal).then_inc(hotT_ready, 1)
                        dve.wait_ge(xn_ready, it + 1)
                        for u in range(TPB):
                            t = it * TPB + u
                            x = g.tile(t).rearrange("p t d -> p (t d)")
                            last = nc.vector.scalar_tensor_tensor(x, w[:, cols["null_token"]], unpicked[:, u, bass.ds(it, 1)], x,
                                                                  ALU.mult, ALU.add)
                        last.then_inc(null_added, 1)
                        for pair in range(USES):
                            ks = [(s, pair * NS + s) for s in range(NS)]
                            for s, k in ks:
                                n = use(it, k)
                                dve.wait_ge(k_ready[s], n)
                                nc.vector.tensor_copy(kT[s][:, :, :], bank_x[s][:, 192:448].rearrange("p (c k) -> p c k", c=C)
                                                      ).then_inc(k_saved[s], 1)
                                dve.wait_ge(v_ready[s], n)
                                dve.wait_ge(xg_saved[s], n)
                                nc.vector.tensor_scalar(v[k][0:NK, :], bank_v[s][0:NK, :], sg[s][0:NK, 1:2], None,
                                                        ALU.mult).then_inc(v_saved[s], 1)
                            for s, k in ks:
                                n = use(it, k)
                                dve.wait_ge(s_ready[s], n)
                                for a, bank in ((0, bank_s[s]), (1, bank_q[s])):
                                    nc.vector.tensor_reduce(top[s][:, a, :], bank[:, 0:C * NK].rearrange("p (c k) -> p c k", c=C),
                                                            AX.X, ALU.max).then_inc(top_step[s], 1)
                                null = bank_x[s][:, 448:448 + H].rearrange("p (c a) -> p a c", a=2)
                                dve.wait_ge(top_step[s], (n - 1) * 3 + 2)
                                nc.vector.tensor_tensor(top[s][:, :, :], top[s][:, :, :], null, ALU.max).then_inc(top_step[s], 1)
                                dve.wait_ge(top_step[s], (n - 1) * 3 + 3)
                                for a, bank in ((0, bank_s[s]), (1, bank_q[s])):
                                    nc.vector.tensor_tensor(prob[s][:, a, :, 0:NK], bank[:, 0:C * NK].rearrange("p (c k) -> p c k", c=C),
                                                            top[s][:, a, :].unsqueeze(2).broadcast_to([P, C, NK]), ALU.subtract)
                                nc.vector.tensor_tensor(prob[s][:, :, :, NK], null, top[s][:, :, :],
                                                        ALU.subtract).then_inc(shifted[s], 1)
                            for s, k in ks:
                                n = use(it, k)
                                dve.wait_ge(exp_done[s], n)
                                nc.vector.tensor_reduce(den[s][:, :, :], prob[s][:, :, :, :], AX.X, ALU.add).then_inc(den_step[s], 1)
                                dve.wait_ge(den_step[s], (n - 1) * 2 + 1)
                                nc.vector.reciprocal(den[s][:, :, :], den[s][:, :, :]).then_inc(den_step[s], 1)
                            for s, k in ks:
                                dve.wait_ge(pT_ready[s], use(it, k))
                                nc.vector.tensor_copy(probT[s][:, 1, :, :], bank_v[s][0:NK + 1, :].rearrange("p (c q) -> p c q", c=C)
                                                      ).then_inc(pTb_saved[s], 1)
                            for s, k in ks:
                                dve.wait_ge(o_ready[s], use(it, k))
                                nc.vector.tensor_scalar(o[s][:, :], bank_x[s][:, 0:D], sg[s][:, 0:1], None,
                                                        ALU.mult).then_inc(o_saved[s], 1)
                            for s, k in ks:
                                n = use(it, k)
                                dve.wait_ge(back_ready[s], n)
                                if k == 0:
                                    dve.wait_ge(null_added, it + 1)
                                else:
                                    dve.wait_ge(slot_free[1 - s], use(it, k - 1) + 1)
                                for u in range(TPB):
                                    t = it * TPB + u
                                    x = g.tile(t).rearrange("p t d -> p (t d)")
                                    last = nc.vector.scalar_tensor_tensor(x, bank_x[s][:, 128 + u * D:128 + (u + 1) * D],
                                                                          mean_by[:, u, bass.ds(it, 1)], x, ALU.mult, ALU.add)
                                last.then_inc(slot_free[s], 1)
                        dve.sem_inc(batch_free, 1)

                @block.scalar
                def _(act):
                    with act.Fori(0, BATCH) as it:
                        for pair in range(USES):
                            ks = [(s, pair * NS + s) for s in range(NS)]
                            for s, k in ks:
                                act.wait_ge(gathered[s], use(it, k))
                                nc.scalar.copy(xg[s][:, :], bank_x[s][:, 0:192])
                                nc.scalar.copy(sg[s][:, 0:1], bank_x[s][:, 448:449])
                                nc.scalar.copy(sg[s][0:NK, 1:2], bank_x[s][0:NK, 449:450]).then_inc(xg_saved[s], 1)
                            for s, k in ks:
                                act.wait_ge(q_ready[s], use(it, k))
                                nc.scalar.mul(qT[s][:, :, :], bank_q[s][:, :].rearrange("p (c q) -> p c q", c=C),
                                              float(DH) ** -0.5).then_inc(q_saved[s], 1)
                            for s, k in ks:
                                act.wait_ge(shifted[s], use(it, k))
                                nc.scalar.activation(prob[s][:, :, :, :], prob[s][:, :, :, :], ACT.Exp).then_inc(exp_done[s], 1)
                            for s, k in ks:
                                act.wait_ge(pT_ready[s], use(it, k))
                                nc.scalar.copy(probT[s][:, 0, :, :], bank_q[s][0:NK + 1, :].rearrange("p (c q) -> p c q", c=C)
                                               ).then_inc(pTa_saved[s], 1)
                            for s, k in ks:
                                act.wait_ge(pv_ready[s], use(it, k))
                                nc.scalar.copy(oT[s][:, :, :], bank_s[s][:, :].rearrange("p (c q) -> p c q", c=C)
                                               ).then_inc(oT_saved[s], 1)

                @block.tensor
                def _(pe):
                    for s in range(NS):
                        pe.sem_inc(slot_free[s], 1)
                    pe.wait_ge(null_loaded, 16 * G)
                    with pe.Fori(0, BATCH) as it:
                        pe.wait_ge(xn_ready, it + 1)
                        pe.wait_ge(hot_ready, it + 1)
                        for pair in range(USES):
                            ks = [(s, pair * NS + s) for s in range(NS)]
                            for s, k in ks:
                                pe.wait_ge(slot_free[s], use(it, k))
                                for u in range(TPB):
                                    nc.tensor.matmul(bank_x[s][:, 0:192], xn[:, u, :], hot[:, u, k, :], start=(u == 0), stop=(u == 1))
                                for u in range(TPB):
                                    nc.tensor.matmul(bank_x[s][:, 448:449], hot[:, u, k, 0:NQ],
                                                     scoreT[:, u, bass.ds(it * ROWS + k, 1)], start=(u == 0), stop=(u == 1))
                                for u in range(TPB):
                                    last = nc.tensor.matmul(bank_x[s][0:NK, 449:450], hot[:, u, k, NQ:NQ + NK],
                                                            scoreT[:, u, bass.ds(it * ROWS + G + k, 1)], start=(u == 0), stop=(u == 1))
                                last.then_inc(gathered[s], 1)
                            for s, k in ks:
                                pe.wait_ge(xg_saved[s], use(it, k))
                                for c in range(C):
                                    last = nc.tensor.matmul(bank_q[s][:, c * NQ:(c + 1) * NQ], wq[:, k, c * P:(c + 1) * P],
                                                            xg[s][:, 0:NQ], start=True, stop=True)
                                last.then_inc(q_ready[s], 1)
                                for c in range(C):
                                    last = nc.tensor.matmul(bank_x[s][:, 192 + c * NK:192 + (c + 1) * NK], wk[:, k, c * P:(c + 1) * P],
                                                            xg[s][:, NQ:NQ + NK], start=True, stop=True)
                                last.then_inc(k_ready[s], 1)
                                nc.tensor.matmul(bank_v[s][0:NK, :], xg[s][:, NQ:NQ + NK], wv[:, k, :], start=True,
                                                 stop=True).then_inc(v_ready[s], 1)
                            for s, k in ks:
                                pe.wait_ge(q_saved[s], use(it, k))
                                pe.wait_ge(k_saved[s], use(it, k))
                                for c in range(C):
                                    for a, bank in ((0, bank_s[s]), (1, bank_q[s])):
                                        r = slice(64 * a, 64 * a + 64)
                                        nc.tensor.matmul(bank[:, c * NK:(c + 1) * NK], qT[s][r, c, :], kT[s][r, c, :],
                                                         start=True, stop=True)
                                for c in range(C):
                                    last = nc.tensor.matmul(bank_x[s][:, 448 + 2 * c:450 + 2 * c], qT[s][:, c, :], null_kb[:, k, c, :],
                                                            start=True, stop=True)
                                last.then_inc(s_ready[s], 1)
                            for s, k in ks:
                                pe.wait_ge(normed[s], use(it, k))
                                pe.wait_ge(v_saved[s], use(it, k))
                                for a, bank in ((0, bank_q[s]), (1, bank_v[s])):
                                    for c in range(C):
                                        last = nc.tensor.transpose(bank[0:NK + 1, c * NQ:(c + 1) * NQ], prob[s][:, a, c, :], g.c("ident"))
                                last.then_inc(pT_ready[s], 1)
                            for s, k in ks:
                                pe.wait_ge(pTa_saved[s], use(it, k))
                                pe.wait_ge(pTb_saved[s], use(it, k))
                                for c in range(C):
                                    for a in range(2):
                                        h = 2 * c + a
                                        last = nc.tensor.matmul(bank_s[s][64 * a:64 * a + 64, c * NQ:(c + 1) * NQ],
                                                                v[k][:, h * DH:(h + 1) * DH], probT[s][:, a, c, :],
                                                                start=True, stop=True)
                                last.then_inc(pv_ready[s], 1)
                            for s, k in ks:
                                pe.wait_ge(oT_saved[s], use(it, k))
                                for c in range(C):
                                    last = nc.tensor.matmul(bank_x[s][:, 0:D], oT[s][:, c, :], wo[:, k, c, :], start=(c == 0),
                                                            stop=(c == C - 1))
                                last.then_inc(o_ready[s], 1)
                            for s, k in ks:
                                pe.wait_ge(o_saved[s], use(it, k))
                                pe.wait_ge(hotT_ready, it + 1)
                                for u in range(TPB):
                                    last = nc.tensor.matmul(bank_x[s][:, 128 + u * D:128 + (u + 1) * D],
                                                            hotT[:, k, u * P:(u + 1) * P], o[s][:, :], start=True, stop=True)
                                last.then_inc(back_ready[s], 1)


L1A_H, L1A_DK, L1A_DV, L1A_TAPS = 16, 64, 128, 4
L1A_HG = 4
L1A_GROUPS = L1A_H // L1A_HG
L1A_W = 2 * L1A_HG * L1A_DK + L1A_HG * L1A_DV
L1A_PARTS = [("wab", 2 * L1A_H), ("wgate", L1A_H * L1A_DV), ("wo", L1A_H * D), ("dt_bias", L1A_H), ("a_log", L1A_H),
             ("norm", 1)]
LEVELS = 6


def l1_attn(nc, g, name):
    H, HG, DK, DV, NG = L1A_H, L1A_HG, L1A_DK, L1A_DV, L1A_GROUPS
    cols, width = columns(L1A_PARTS)
    N = SEQ
    PAD = L1A_TAPS - 1
    W2 = 2 * HG * DK
    with Stage(nc, name) as st:
        w = st.sb("w", [P, width])
        XT = st.sb("XT", [P, TOKENS])
        folded = st.sb("folded", [P, NG, L1A_TAPS, L1A_W])
        beta = st.sb("beta", [P, TILES, H])
        decay = st.sb("decay", [P, TILES, H])
        grown = st.sb("grown", [P, TILES, H])

        with Stage(nc, name + "_p") as sp_:
            raw = sp_.sb("raw", [P, NG, L1A_W])
            ab = sp_.sb("ab", [P, TILES, 2 * H])
            z = sp_.sb("z", [P, TILES, H])
            away = sp_.sb("away", [P, TILES, H])
            rate = sp_.sb("rate", [P, H])
            row_statistics(nc, g, name, [(w[:, :], g.dram["w_l1a"]), (raw[:, :, :], g.dram["w_l1a_qkv"]),
                                         (folded[:, :, :, :].rearrange("p a b c -> p (a b c)"),
                                          g.dram["l1a_taps"].partition_broadcast(P))])
            turn_stream(nc, g, name, XT, w[:, cols["wab"]], ab[:, :, :])
            sums = sp_.ps("sums", [P, 512])
            step = sp_.sem("step")
            z_ready = sp_.sem("z_ready")
            away_ready = sp_.sem("away_ready")
            act_step = sp_.sem("act_step")
            decay_ready = sp_.sem("decay_ready")
            summed = sp_.sem("summed")

            def each(a):
                return a.unsqueeze(1).broadcast_to([P, TILES, H])

            with nc.Block() as block:
                @block.vector
                def _(dve):
                    nc.vector.tensor_tensor(z[:, :, :], ab[:, :, 0:H], each(w[:, cols["dt_bias"]]), ALU.add).then_inc(z_ready, 1)
                    dve.wait_ge(z_ready, 1)
                    nc.vector.scalar_tensor_tensor(away[:, :, :], z[:, :, :], -1.0, z[:, :, :], ALU.mult, ALU.max).then_inc(away_ready, 1)
                    for gi in range(NG):
                        for j in range(L1A_TAPS):
                            last = nc.vector.scalar_tensor_tensor(folded[:, gi, j, :], raw[:, gi, :], 0.5, folded[:, gi, j, :],
                                                                  ALU.mult, ALU.mult)
                    nc.vector.tensor_scalar(w[:, cols["wo"]], w[:, cols["wo"]], w[:, cols["norm"]], 0.5, ALU.mult,
                                            ALU.mult).then_inc(step, 1)
                    dve.wait_ge(act_step, 4)
                    nc.vector.scalar_tensor_tensor(z[:, :, :], z[:, :, :], 0.0, away[:, :, :], ALU.max, ALU.add).then_inc(step, 1)
                    dve.wait_ge(step, 2)
                    nc.vector.scalar_tensor_tensor(decay[:, :, :], z[:, :, :], -1.0, each(rate[:, :]), ALU.mult,
                                                   ALU.mult).then_inc(decay_ready, 1)
                    nc.vector.tensor_scalar(beta[:, :, :], beta[:, :, :], 2.0, None, ALU.mult).then_inc(step, 1)

                @block.scalar
                def _(act):
                    act.wait_ge(away_ready, 1)
                    nc.scalar.activation(beta[:, :, :], ab[:, :, H:2 * H], ACT.Sigmoid).then_inc(act_step, 1)
                    nc.scalar.activation(rate[:, :], w[:, cols["a_log"]], ACT.Exp).then_inc(act_step, 1)
                    nc.scalar.activation(away[:, :, :], away[:, :, :], ACT.Exp, scale=-1.0).then_inc(act_step, 1)
                    act.wait_ge(act_step, 3)
                    nc.scalar.activation(away[:, :, :], away[:, :, :], ACT.Ln, bias=g.c("ones")[:, 0:1]).then_inc(act_step, 1)
                    act.wait_ge(summed, 1)
                    nc.scalar.activation(grown[:, :, :].rearrange("p t h -> p (t h)"), sums[:, :], ACT.Exp).then_inc(act_step, 1)

                @block.tensor
                def _(pe):
                    pe.wait_ge(decay_ready, 1)
                    nc.tensor.matmul(sums[:, :], g.c("upto"), decay[:, :, :].rearrange("p t h -> p (t h)"), start=True,
                                     stop=True).then_inc(summed, 1)

        with Stage(nc, name + "_m") as sm:
            U = range(TPB)
            wgate = w[:, cols["wgate"]].rearrange("p (a n) -> p a n", a=NG)
            wo = w[:, cols["wo"]].rearrange("p (h d) -> p h d", h=H)
            xpad = sm.sb("xpad", [P, PAD + N])
            t0 = [sm.sb(f"t0{u}", [P, HG, P]) for u in U]
            t1 = [sm.sb(f"t1{u}", [P, HG, P]) for u in U]
            t2 = [sm.sb(f"t2{u}", [P, HG, P]) for u in U]
            qk = [sm.sb(f"qk{u}", [P, 2 * HG, DK]) for u in U]
            rhs = [sm.sb(f"rhs{u}", [P, HG, DV]) for u in U]
            gate = [sm.sb(f"gate{u}", [P, HG, DV]) for u in U]
            length = [sm.sb(f"length{u}", [P, 2 * HG]) for u in U]
            qkT = [sm.sb(f"qkT{u}", [P, 4, P]) for u in U]
            fade = [sm.sb(f"fade{u}", [P, HG, P]) for u in U]
            NT = [sm.sb(f"NT{u}", [P, HG, P]) for u in U]
            mixT = [sm.sb(f"mixT{u}", [P, HG, P]) for u in U]
            X = [sm.sb(f"X{u}", [P, HG, P]) for u in U]
            Y = [sm.sb(f"Y{u}", [P, HG, P]) for u in U]
            kfade = sm.sb("kfade", [P, HG, DK])
            state = sm.sb("state", [P, 2, DV])
            from_state = sm.sb("from_state", [P, HG, DV])
            ms = [sm.sb(f"ms{u}", [P, HG]) for u in U]
            yT = [sm.sb(f"yT{u}", [P, HG, P]) for u in U]
            bank = [[sm.ps(f"bank{u}_{i}", [P, 512]) for i in range(4)] for u in U]
            pad_clear = sm.sem("pad_clear")
            xpad_ready = sm.sem("xpad_ready")
            slot_free = sm.sems("slot_free", TPB)
            proj_ready = sm.sems("proj_ready", TPB)
            tanh_done = sm.sems("tanh_done", TPB)
            silu_done = sm.sems("silu_done", TPB)
            squared = sm.sems("squared", TPB)
            length_step = sm.sems("length_step", TPB)
            length_ready = sm.sems("length_ready", TPB)
            unit = sm.sems("unit", TPB)
            qk_turned = sm.sems("qk_turned", TPB)
            qkT_saved = sm.sems("qkT_saved", TPB)
            terms_ready = sm.sems("terms_ready", TPB)
            diff_ready = sm.sems("diff_ready", TPB)
            fade_done = sm.sems("fade_done", TPB)
            fade_step = sm.sems("fade_step", TPB)
            dots_ready = sm.sems("dots_ready", TPB)
            NT_ready = sm.sems("NT_ready", TPB)
            mixT_ready = sm.sems("mixT_ready", TPB)
            N_turned = sm.sems("N_turned", TPB)
            X_begun = sm.sems("X_begun", TPB)
            X_ready = sm.sems("X_ready", TPB)
            Y_step = sm.sems("Y_step", TPB)
            W_ready = sm.sems("W_ready", TPB)
            W_masked = sm.sems("W_masked", TPB)
            XW_ready = sm.sems("XW_ready", TPB)
            merged = sm.sems("merged", TPB)
            kfade_ready = sm.sem("kfade_ready")
            solved = sm.sems("solved", TPB)
            delta_ready = sm.sems("delta_ready", TPB)
            out_ready = sm.sems("out_ready", TPB)
            state_ready = sm.sem("state_ready")
            state_saved = sm.sem("state_saved")
            read_ready = sm.sem("read_ready")
            grown_done = sm.sem("grown_done")
            rhs_ready = sm.sem("rhs_ready")
            o_saved = sm.sems("o_saved", TPB)
            o_squared = sm.sems("o_squared", TPB)
            ms_step = sm.sems("ms_step", TPB)
            ms_ready = sm.sems("ms_ready", TPB)
            o_normed = sm.sems("o_normed", TPB)
            y_ready = sm.sems("y_ready", TPB)
            y_turned = sm.sems("y_turned", TPB)
            yT_saved = sm.sems("yT_saved", TPB)
            projected = sm.sems("projected", TPB)
            MERGES = LEVELS - 1

            def heads(a, n):
                return a.unsqueeze(2).broadcast_to([P, a.shape[1], n])

            def over_heads(a):
                return a.unsqueeze(1).broadcast_to([P, HG, P])

            def at_gate(a, b, u, hg):
                return a[:, :, :].rearrange("p t h -> p (t h)")[:, bass.ds((b * TPB + u) * H + hg * HG, HG)]

            def parity(a, half):
                return a[:, half:HG:2, :]

            def half_rows(hh):
                return slice(64 * (hh % 2), 64 * (hh % 2) + 64)

            with nc.Block() as block:
                @block.tensor
                def _(pe):
                    for u in U:
                        pe.sem_inc(slot_free[u], 1)
                    with pe.Fori(0, BATCH) as b:
                        with pe.Fori(0, NG) as hg:
                            n = b * NG + hg
                            pe.wait_ge(xpad_ready, b + 1)
                            for u in U:
                                pe.wait_ge(slot_free[u], n + 1)
                                for i in range(2):
                                    for j in range(L1A_TAPS):
                                        last = nc.tensor.matmul(bank[u][i][:, :], xpad[:, u * P + j:u * P + j + P],
                                                                folded[:, bass.ds(hg, 1), j, i * W2:(i + 1) * W2],
                                                                start=(j == 0), stop=(j == L1A_TAPS - 1))
                                    last.then_inc(proj_ready[u], 1)
                                nc.tensor.matmul(bank[u][2][:, :], xpad[:, u * P + PAD:u * P + PAD + P], wgate[:, bass.ds(hg, 1), :],
                                                 start=True, stop=True).then_inc(proj_ready[u], 1)
                            for u in U:
                                pe.wait_ge(terms_ready[u], n + 1)
                                nc.tensor.matmul(bank[u][1][:, :], g.c("after"), t2[u][:, :, :].rearrange("p h t -> p (h t)"),
                                                 start=True, stop=True).then_inc(diff_ready[u], 1)
                            for u in U:
                                pe.wait_ge(unit[u], n + 1)
                                for pair in range(2):
                                    for i, at in ((0, HG + 2 * pair), (1, 2 * pair)):
                                        last = nc.tensor.transpose(bank[u][0][:, (2 * pair + i) * P:(2 * pair + i + 1) * P],
                                                                   qk[u][:, at:at + 2, :].rearrange("p h d -> p (h d)"), g.c("ident"))
                                last.then_inc(qk_turned[u], 1)
                            for u in U:
                                pe.wait_ge(qkT_saved[u], n + 1)
                                for hh in range(HG):
                                    r, pair = half_rows(hh), hh // 2
                                    last = nc.tensor.matmul(bank[u][2 + hh % 2][:, pair * 256:pair * 256 + 256],
                                                            qkT[u][r, 2 * pair, :],
                                                            qkT[u][r, 2 * pair:2 * pair + 2, :].rearrange("p a t -> p (a t)"),
                                                            start=True, stop=True)
                                last.then_inc(dots_ready[u], 1)
                            for u in U:
                                pe.wait_ge(NT_ready[u], n + 1)
                                for hh in range(HG):
                                    last = nc.tensor.transpose(bank[u][0][:, hh * P:(hh + 1) * P], NT[u][:, hh, :], g.c("ident"))
                                last.then_inc(N_turned[u], 1)
                            for k in range(LEVELS):
                                for u in U:
                                    if k == 0:
                                        pe.wait_ge(X_ready[u], n + 1)
                                        pe.wait_ge(Y_step[u], n * 2 + 2)
                                        pe.wait_ge(mixT_ready[u], n + 1)
                                    else:
                                        pe.wait_ge(merged[u], n * LEVELS + k)
                                    for hh in range(HG):
                                        last = nc.tensor.matmul(bank[u][1][:, hh * P:(hh + 1) * P], NT[u][:, hh, :], X[u][:, hh, :],
                                                                start=True, stop=True)
                                    last.then_inc(W_ready[u], 1)
                                for u in U:
                                    pe.wait_ge(W_masked[u], n * LEVELS + k + 1)
                                    if k < MERGES:
                                        for hh in range(HG):
                                            last = nc.tensor.matmul(bank[u][2][:, hh * P:(hh + 1) * P], Y[u][:, hh, :], t0[u][:, hh, :],
                                                                    start=True, stop=True)
                                    for hh in range(HG):
                                        last = nc.tensor.matmul(bank[u][3][:, hh * P:(hh + 1) * P], t0[u][:, hh, :], Y[u][:, hh, :],
                                                                start=True, stop=True)
                                    last.then_inc(XW_ready[u], 1)

                            def solve(u):
                                for hh in range(HG):
                                    last = nc.tensor.matmul(bank[u][0][:, hh * P:(hh + 1) * P], Y[u][:, hh, :], rhs[u][:, hh, :],
                                                            start=True, stop=True)
                                last.then_inc(solved[u], 1)

                            def mix(u):
                                pe.wait_ge(delta_ready[u], n + 1)
                                for hh in range(HG):
                                    last = nc.tensor.matmul(bank[u][1][:, hh * P:(hh + 1) * P], mixT[u][:, hh, :], t1[u][:, hh, :],
                                                            start=True, stop=True)
                                last.then_inc(out_ready[u], 1)

                            def turn_y(u):
                                pe.wait_ge(y_ready[u], n + 1)
                                for hh in range(HG):
                                    last = nc.tensor.transpose(bank[u][0][:, hh * P:(hh + 1) * P], yT_src[u][:, hh, :], g.c("ident"))
                                last.then_inc(y_turned[u], 1)

                            def project(u):
                                pe.wait_ge(yT_saved[u], n + 1)
                                for hh in range(HG):
                                    last = nc.tensor.matmul(bank[u][1][:, 0:D], yT[u][:, hh, :],
                                                            wo[:, bass.ds(hg * HG + hh, 1), :], start=(hh == 0), stop=(hh == HG - 1))
                                last.then_inc(projected[u], 1)

                            yT_src = t2
                            pe.wait_ge(merged[0], n * LEVELS + LEVELS)
                            solve(0)
                            mix(0)
                            pe.wait_ge(kfade_ready, n + 1)
                            for hh in range(HG):
                                last = nc.tensor.matmul(bank[0][2][half_rows(hh), (hh // 2) * DV:(hh // 2 + 1) * DV], kfade[:, hh, :],
                                                        t1[0][:, hh, :], start=True, stop=True)
                            last.then_inc(state_ready, 1)
                            pe.wait_ge(merged[1], n * LEVELS + LEVELS)
                            pe.wait_ge(state_saved, n + 1)
                            for hh in range(HG):
                                r, pair = half_rows(hh), hh // 2
                                for i in range(2):
                                    last = nc.tensor.matmul(bank[1][2 + hh % 2][:, (2 * i + pair) * DV:(2 * i + pair + 1) * DV],
                                                            qkT[1][r, 2 * pair + i, :], state[r, pair, :], start=True, stop=True)
                            last.then_inc(read_ready, 1)
                            turn_y(0)
                            pe.wait_ge(rhs_ready, n + 1)
                            solve(1)
                            project(0)
                            mix(1)
                            turn_y(1)
                            project(1)

                @block.scalar
                def _(act):
                    with act.Fori(0, BATCH) as b:
                        with act.Fori(0, NG) as hg:
                            n = b * NG + hg
                            for i, (dst, scale) in enumerate(((t0, 1.0), (t1, 1.0), (t2, 0.5))):
                                for u in U:
                                    act.wait_ge(proj_ready[u], n * 3 + i + 1)
                                    nc.scalar.activation(dst[u][:, :, :].rearrange("p h t -> p (h t)"), bank[u][i][:, :], ACT.Tanh,
                                                         scale=scale).then_inc(tanh_done[u], 1)
                            for u in U:
                                act.wait_ge(diff_ready[u], n + 1)
                                nc.scalar.activation(fade[u][:, :, :].rearrange("p h t -> p (h t)"), bank[u][1][:, :],
                                                     ACT.Exp).then_inc(fade_done[u], 1)
                            for u in U:
                                act.wait_ge(qk_turned[u], n + 1)
                                nc.scalar.copy(qkT[u][:, :, :].rearrange("p a t -> p (a t)"), bank[u][0][:, :]).then_inc(qkT_saved[u], 1)
                            act.wait_ge(state_ready, n + 1)
                            nc.scalar.copy(state[:, :, :].rearrange("p a d -> p (a d)"), bank[0][2][:, 0:2 * DV]).then_inc(state_saved, 1)
                            act.wait_ge(out_ready[0], n + 1)
                            nc.scalar.copy(t2[0][:, :, :].rearrange("p h t -> p (h t)"), bank[0][1][:, :]).then_inc(o_saved[0], 1)
                            for u in U:
                                act.wait_ge(y_turned[u], n + 1)
                                nc.scalar.copy(yT[u][:, :, :].rearrange("p h t -> p (h t)"), bank[u][0][:, :]).then_inc(yT_saved[u], 1)

                @block.gpsimd
                def _(pool):
                    nc.gpsimd.memset(xpad[:, 0:PAD], 0.0).then_inc(pad_clear, 1)
                    pool.wait_ge(pad_clear, 1)
                    with pool.Fori(0, BATCH) as b:
                        nc.gpsimd.tensor_copy(xpad[:, PAD:PAD + N], XT[:, bass.ds(b * N, N)]).then_inc(xpad_ready, 1)
                        with pool.Fori(0, NG) as hg:
                            n = b * NG + hg
                            for u in U:
                                pool.wait_ge(silu_done[u], n * 3 + 3)
                                nc.gpsimd.tensor_tensor(t2[u][:, :, :], over_heads(g.c("upto")), heads(at_gate(decay, b, u, hg), P),
                                                        ALU.mult).then_inc(terms_ready[u], 1)
                            for u in U:
                                nc.gpsimd.tensor_tensor(t0[u][:, :, :].rearrange("p h t -> p (h t)"),
                                                        qk[u][:, :, :].rearrange("p h d -> p (h d)"),
                                                        qk[u][:, :, :].rearrange("p h d -> p (h d)"), ALU.mult).then_inc(squared[u], 1)
                            for u in U:
                                pool.wait_ge(length_step[u], n * 3 + 3)
                                nc.gpsimd.tensor_tensor(length[u][:, :], length[u][:, :], g.c("minus_half")[:, 0:2 * HG],
                                                        ALU.pow).then_inc(length_ready[u], 1)
                            for u in U:
                                pool.wait_ge(fade_done[u], n + 1)
                                nc.gpsimd.tensor_tensor(fade[u][:, :, :], fade[u][:, :, :], over_heads(g.c("upto")),
                                                        ALU.mult).then_inc(fade_step[u], 1)
                                pool.wait_ge(fade_step[u], n * 2 + 1)
                                nc.gpsimd.tensor_tensor(t1[u][:, :, :], fade[u][:, :, :], heads(at_gate(beta, b, u, hg), P),
                                                        ALU.mult).then_inc(fade_step[u], 1)
                            pool.wait_ge(unit[0], n + 1)
                            nc.gpsimd.tensor_tensor(kfade[:, :, :], qk[0][:, HG:2 * HG, :],
                                                    fade[0][:, :, P - 1:P].broadcast_to([P, HG, DK]),
                                                    ALU.mult).then_inc(kfade_ready, 1)
                            for u in U:
                                pool.wait_ge(NT_ready[u], n + 1)
                                nc.gpsimd.tensor_tensor(Y[u][:, :, :], NT[u][:, :, :], over_heads(g.c("level1tn")),
                                                        ALU.mult).then_inc(Y_step[u], 1)
                                pool.wait_ge(Y_step[u], n * 2 + 1)
                                nc.gpsimd.tensor_tensor(Y[u][:, :, :], Y[u][:, :, :], over_heads(g.c("ident")),
                                                        ALU.add).then_inc(Y_step[u], 1)
                            for u in U:
                                pool.wait_ge(X_begun[u], n + 1)
                                nc.gpsimd.tensor_tensor(X[u][:, :, :], X[u][:, :, :], over_heads(g.c("ident")),
                                                        ALU.add).then_inc(X_ready[u], 1)

                            def finish(u):
                                pool.wait_ge(o_saved[u], n + 1)
                                nc.gpsimd.tensor_tensor(yT[u][:, :, :], t2[u][:, :, :], t2[u][:, :, :], ALU.mult).then_inc(o_squared[u], 1)
                                pool.wait_ge(ms_step[u], n * 2 + 2)
                                nc.gpsimd.tensor_tensor(ms[u][:, :], ms[u][:, :], g.c("minus_half")[:, 0:HG],
                                                        ALU.pow).then_inc(ms_ready[u], 1)
                                pool.wait_ge(o_normed[u], n + 1)
                                nc.gpsimd.tensor_tensor(t2[u][:, :, :], t2[u][:, :, :], gate[u][:, :, :], ALU.mult).then_inc(y_ready[u], 1)

                            finish(0)
                            pool.wait_ge(grown_done, n * 2 + 1)
                            nc.gpsimd.tensor_tensor(rhs[1][:, :, :], rhs[1][:, :, :], NT[1][:, :, :], ALU.subtract).then_inc(rhs_ready, 1)
                            finish(1)

                @block.vector
                def _(dve):
                    with dve.Fori(0, BATCH) as b:
                        with dve.Fori(0, NG) as hg:
                            n = b * NG + hg
                            for i, (src, dst) in enumerate(((t0, qk), (t1, rhs), (t2, gate))):
                                for u in U:
                                    dve.wait_ge(tanh_done[u], n * 3 + i + 1)
                                    nc.vector.scalar_tensor_tensor(dst[u][:, :, :].rearrange("p h d -> p (h d)"),
                                                                   src[u][:, :, :].rearrange("p h d -> p (h d)"), 1.0,
                                                                   bank[u][i][:, :], ALU.add, ALU.mult).then_inc(silu_done[u], 1)
                            for u in U:
                                dve.wait_ge(squared[u], n + 1)
                                nc.vector.tensor_reduce(length[u][:, :], t0[u][:, :, :].rearrange("p h t -> p (h t)").rearrange(
                                    "p (h d) -> p h d", d=DK), AX.X, ALU.add).then_inc(length_step[u], 1)
                            for u in U:
                                dve.wait_ge(length_step[u], n * 3 + 1)
                                nc.vector.tensor_scalar(length[u][:, 0:HG], length[u][:, 0:HG], 1e-6, float(DK), ALU.add,
                                                        ALU.mult).then_inc(length_step[u], 1)
                                nc.vector.tensor_scalar(length[u][:, HG:], length[u][:, HG:], 1e-6, None,
                                                        ALU.add).then_inc(length_step[u], 1)
                            for u in U:
                                dve.wait_ge(length_ready[u], n + 1)
                                nc.vector.tensor_tensor(qk[u][:, :, :], qk[u][:, :, :], heads(length[u][:, :], DK),
                                                        ALU.mult).then_inc(unit[u], 1)
                            for u in U:
                                dve.wait_ge(dots_ready[u], n + 1)
                                dve.wait_ge(fade_step[u], n * 2 + 2)
                                for half in range(2):
                                    dots = bank[u][2 + half][:, :].rearrange("p (a k t) -> p a k t", a=2, k=2)
                                    last = nc.vector.tensor_tensor(parity(NT[u], half), dots[:, :, 0, :], parity(t1[u], half), ALU.mult)
                                last.then_inc(NT_ready[u], 1)
                                for half in range(2):
                                    dots = bank[u][2 + half][:, :].rearrange("p (a k t) -> p a k t", a=2, k=2)
                                    last = nc.vector.tensor_tensor(parity(mixT[u], half), dots[:, :, 1, :], parity(fade[u], half), ALU.mult)
                                last.then_inc(mixT_ready[u], 1)
                            for u in U:
                                dve.wait_ge(N_turned[u], n + 1)
                                nc.vector.tensor_tensor(X[u][:, :, :], bank[u][0][:, :].rearrange("p (h t) -> p h t", h=HG),
                                                        over_heads(g.c("level1n")), ALU.mult).then_inc(X_begun[u], 1)
                            for k in range(LEVELS):
                                for u in U:
                                    dve.wait_ge(W_ready[u], n * LEVELS + k + 1)
                                    nc.vector.tensor_tensor(t0[u][:, :, :], bank[u][1][:, :].rearrange("p (h t) -> p h t", h=HG),
                                                            over_heads(g.c("level")[:, k * P:(k + 1) * P]),
                                                            ALU.mult).then_inc(W_masked[u], 1)
                                for u in U:
                                    dve.wait_ge(XW_ready[u], n * LEVELS + k + 1)
                                    if k < MERGES:
                                        nc.vector.tensor_tensor(X[u][:, :, :].rearrange("p h t -> p (h t)"),
                                                                X[u][:, :, :].rearrange("p h t -> p (h t)"), bank[u][2][:, :], ALU.subtract)
                                    nc.vector.tensor_tensor(Y[u][:, :, :].rearrange("p h t -> p (h t)"),
                                                            Y[u][:, :, :].rearrange("p h t -> p (h t)"), bank[u][3][:, :],
                                                            ALU.subtract).then_inc(merged[u], 1)

                            def delta(u):
                                dve.wait_ge(solved[u], n + 1)
                                nc.vector.tensor_tensor(t1[u][:, :, :], bank[u][0][:, :].rearrange("p (h t) -> p h t", h=HG),
                                                        heads(at_gate(beta, b, u, hg), P), ALU.mult).then_inc(delta_ready[u], 1)

                            def mean_square(u):
                                dve.wait_ge(o_squared[u], n + 1)
                                nc.vector.tensor_reduce(ms[u][:, :], yT[u][:, :, :], AX.X, ALU.add).then_inc(ms_step[u], 1)
                                dve.wait_ge(ms_step[u], n * 2 + 1)
                                nc.vector.tensor_scalar(ms[u][:, :], ms[u][:, :], 1.0 / DV, 1e-5, ALU.mult, ALU.add).then_inc(ms_step[u], 1)

                            def norm(u):
                                dve.wait_ge(ms_ready[u], n + 1)
                                nc.vector.tensor_tensor(t2[u][:, :, :], t2[u][:, :, :], heads(ms[u][:, :], DV),
                                                        ALU.mult).then_inc(o_normed[u], 1)

                            def add(u):
                                x = g.tile(b * TPB + u).rearrange("p t d -> p (t d)")
                                dve.wait_ge(projected[u], n + 1)
                                nc.vector.tensor_tensor(x, x, bank[u][1][:, 0:D], ALU.add).then_inc(slot_free[u], 1)

                            delta(0)
                            mean_square(0)
                            norm(0)
                            dve.wait_ge(read_ready, n + 1)
                            for i, dst in ((0, NT[1]), (1, from_state)):
                                for half in range(2):
                                    src = bank[1][2 + half][:, i * 256:i * 256 + 256].rearrange("p (a d) -> p a d", a=2)
                                    last = nc.vector.tensor_tensor(parity(dst, half), src,
                                                                   heads(at_gate(grown, b, 1, hg)[:, half:HG:2], DV), ALU.mult)
                                last.then_inc(grown_done, 1)
                            delta(1)
                            add(0)
                            dve.wait_ge(out_ready[1], n + 1)
                            dve.wait_ge(grown_done, n * 2 + 2)
                            nc.vector.tensor_tensor(t2[1][:, :, :].rearrange("p h t -> p (h t)"), bank[1][1][:, :],
                                                    from_state[:, :, :].rearrange("p h d -> p (h d)"), ALU.add).then_inc(o_saved[1], 1)
                            mean_square(1)
                            norm(1)
                            add(1)


def turn_stream(nc, g, name, XT, wide=None, wide_out=None):
    NS = 4
    n = wide.shape[1] if wide is not None else 0
    with Stage(nc, name + "_turn") as st:
        xn = [st.sb(f"xn{s}", [P, D]) for s in range(NS)]
        xt = [st.sb(f"xt{s}", [P, P]) for s in range(NS)]
        turn = [st.ps(f"turn{s}", [P, 512]) for s in range(NS)]
        prod = st.ps("prod", [P, max(512, TILES * n)])
        slot_free = st.sems("slot_free", NS)
        xn_ready = st.sems("xn_ready", NS)
        turned = st.sems("turned", NS)
        xt_ready = st.sems("xt_ready", NS)
        xt_used = st.sems("xt_used", NS)
        prod_saved = st.sem("prod_saved")
        with nc.Block() as block:
            @block.vector
            def _(dve):
                for s in range(NS):
                    dve.sem_inc(slot_free[s], 1)
                with dve.Fori(0, TILES // NS) as it:
                    for s in range(NS):
                        t = it * NS + s
                        dve.wait_ge(slot_free[s], it + 1)
                        nc.vector.tensor_scalar(xn[s][:, :], g.tile(t), g.mean[:, bass.ds(t, 1)],
                                                g.rstd[:, bass.ds(t, 1)], ALU.subtract, ALU.mult).then_inc(xn_ready[s], 1)
                if n:
                    for s in range(NS):
                        dve.wait_ge(xt_used[s], TILES // NS + 1)
                    nc.vector.tensor_copy(wide_out.rearrange("p t n -> p (t n)"), prod[:, 0:TILES * n]).then_inc(prod_saved, 1)

            @block.tensor
            def _(pe):
                with pe.Fori(0, TILES // NS) as it:
                    for s in range(NS):
                        pe.wait_ge(xn_ready[s], it + 1)
                        nc.tensor.transpose(turn[s][:, 0:P], xn[s][:, :], g.c("ident")).then_inc(turned[s], 1)
                    if n:
                        for s in range(NS):
                            pe.wait_ge(xt_ready[s], it + 1)
                            nc.tensor.matmul(prod[:, bass.ds((it * NS + s) * n, n)], xt[s][:, :], wide, start=True,
                                             stop=True).then_inc(xt_used[s], 1)

            @block.scalar
            def _(act):
                for s in range(NS):
                    act.sem_inc(xt_used[s], 1)
                with act.Fori(0, TILES // NS) as it:
                    for s in range(NS):
                        act.wait_ge(turned[s], it + 1)
                        if n:
                            act.wait_ge(xt_used[s], it + 1)
                        nc.scalar.copy(xt[s][:, :], turn[s][:, 0:P]).then_inc(xt_ready[s], 1)

            @block.gpsimd
            def _(pool):
                with pool.Fori(0, TILES // NS) as it:
                    for s in range(NS):
                        pool.wait_ge(xt_ready[s], it + 1)
                        nc.gpsimd.tensor_copy(XT[:, bass.ds((it * NS + s) * P, P)], xt[s][:, :]).then_inc(slot_free[s], 1)


L2_EXPERTS, L2_SHARED, L2_TOP = 8, 2, 2
L2F_ALL = L2_EXPERTS + L2_SHARED
L2F_PARTS = [("gate", L2_EXPERTS), ("bias", L2_EXPERTS), ("w1", L2F_ALL * 128), ("w3", L2F_ALL * 128),
             ("w2", L2F_ALL * 128)]


def l2_ffn(nc, g, name):
    E, EA = L2_EXPERTS, L2F_ALL
    cols, width = columns(L2F_PARTS)
    N = 512
    JT = N // P
    NS = 2
    USES = EA // NS
    with Stage(nc, name) as st:
        w = st.sb("w", [P, width])
        XT = st.sb("XT", [P, TOKENS])
        logits = st.sb("logits", [P, TILES, E])
        gate = st.sb("gate", [P, TILES, E])
        row_statistics(nc, g, name, [(w[:, :], g.dram["w_l2f"])])
        turn_stream(nc, g, name, XT, w[:, cols["gate"]], logits[:, :, :])

        with Stage(nc, name + "_gate") as sg:
            top = sg.sb("top", [P, TILES])
            score = sg.sb("score", [P, TILES, E])
            picked = sg.sb("picked", [P, TILES, E])
            above = sg.sb("above", [P, TILES, E, E])
            equal = sg.sb("equal", [P, TILES, E, E])
            rank = sg.sb("rank", [P, TILES, E])
            step = sg.sem("step")
            shifted = sg.sem("shifted")
            exped = sg.sem("exped")

            def each(a):
                return a.unsqueeze(2).broadcast_to([P, TILES, E])

            mine = picked[:, :, :].unsqueeze(3).broadcast_to([P, TILES, E, E])
            other = picked[:, :, :].unsqueeze(2).broadcast_to([P, TILES, E, E])
            before = g.c("before8").rearrange("p (e j) -> p e j", e=E).unsqueeze(1).broadcast_to([P, TILES, E, E])
            with nc.Block() as block:
                @block.vector
                def _(dve):
                    nc.vector.tensor_reduce(top[:, :], logits[:, :, :], AX.X, ALU.max).then_inc(step, 1)
                    dve.wait_ge(step, 1)
                    nc.vector.tensor_tensor(score[:, :, :], logits[:, :, :], each(top[:, :]),
                                            ALU.subtract).then_inc(shifted, 1)
                    dve.wait_ge(exped, 1)
                    nc.vector.tensor_reduce(top[:, :], score[:, :, :], AX.X, ALU.add).then_inc(step, 1)
                    dve.wait_ge(step, 2)
                    nc.vector.reciprocal(top[:, :], top[:, :]).then_inc(step, 1)
                    dve.wait_ge(step, 3)
                    nc.vector.tensor_tensor(score[:, :, :], score[:, :, :], each(top[:, :]), ALU.mult).then_inc(step, 1)
                    dve.wait_ge(step, 4)
                    nc.vector.tensor_tensor(picked[:, :, :], score[:, :, :],
                                            w[:, cols["bias"]].unsqueeze(1).broadcast_to([P, TILES, E]),
                                            ALU.add).then_inc(step, 1)
                    dve.wait_ge(step, 5)
                    nc.vector.tensor_tensor(above[:, :, :, :], other, mine, ALU.is_gt).then_inc(step, 1)
                    nc.vector.tensor_tensor(equal[:, :, :, :], other, mine, ALU.is_equal).then_inc(step, 1)
                    dve.wait_ge(step, 7)
                    nc.vector.tensor_tensor(equal[:, :, :, :], equal[:, :, :, :], before, ALU.mult).then_inc(step, 1)
                    dve.wait_ge(step, 8)
                    nc.vector.tensor_tensor(above[:, :, :, :], above[:, :, :, :], equal[:, :, :, :],
                                            ALU.add).then_inc(step, 1)
                    dve.wait_ge(step, 9)
                    nc.vector.tensor_reduce(rank[:, :, :], above[:, :, :, :], AX.X, ALU.add).then_inc(step, 1)
                    dve.wait_ge(step, 10)
                    nc.vector.tensor_scalar(rank[:, :, :], rank[:, :, :], float(L2_TOP), 0.5, ALU.is_lt,
                                            ALU.mult).then_inc(step, 1)
                    dve.wait_ge(step, 11)
                    nc.vector.tensor_tensor(gate[:, :, :], rank[:, :, :], score[:, :, :], ALU.mult).then_inc(step, 1)

                @block.scalar
                def _(act):
                    act.wait_ge(shifted, 1)
                    nc.scalar.activation(score[:, :, :], score[:, :, :], ACT.Exp).then_inc(exped, 1)

        with Stage(nc, name + "_mix") as sm:
            silu = [sm.sb(f"silu{s}", [P, N]) for s in range(NS)]
            hid = [sm.sb(f"hid{s}", [P, N]) for s in range(NS)]
            up1 = [sm.ps(f"up1{s}", [P, N]) for s in range(NS)]
            up3 = [sm.ps(f"up3{s}", [P, N]) for s in range(NS)]
            down = [sm.ps(f"down{s}", [P, N]) for s in range(NS)]
            up1_ready = sm.sems("up1_ready", NS)
            up3_ready = sm.sems("up3_ready", NS)
            silu_done = sm.sems("silu_done", NS)
            hid_ready = sm.sems("hid_ready", NS)
            down_ready = sm.sems("down_ready", NS)
            mixed = sm.sems("mixed", NS)
            with nc.Block() as block:
                @block.tensor
                def _(pe):
                    def up(it, e):
                        s, use = e % NS, it * USES + e // NS + 1
                        x = XT[:, bass.ds(it * N, N)]
                        pe.wait_ge(mixed[s], use)
                        nc.tensor.matmul(up1[s][:, :], w[:, cols["w1"]][:, e * P:(e + 1) * P], x, start=True,
                                         stop=True).then_inc(up1_ready[s], 1)
                        nc.tensor.matmul(up3[s][:, :], w[:, cols["w3"]][:, e * P:(e + 1) * P], x, start=True,
                                         stop=True).then_inc(up3_ready[s], 1)

                    def turn_down(it, e):
                        s, use = e % NS, it * USES + e // NS + 1
                        pe.wait_ge(hid_ready[s], use)
                        for j in range(JT):
                            last = nc.tensor.matmul(down[s][:, j * D:(j + 1) * D], hid[s][:, j * P:(j + 1) * P],
                                                    w[:, cols["w2"]][:, e * D:(e + 1) * D], start=True, stop=True)
                        last.then_inc(down_ready[s], 1)

                    for s in range(NS):
                        pe.sem_inc(mixed[s], 1)
                    with pe.Fori(0, TOKENS // N) as it:
                        up(it, 0)
                        for e in range(1, EA):
                            up(it, e)
                            turn_down(it, e - 1)
                        turn_down(it, EA - 1)

                @block.scalar
                def _(act):
                    with act.Fori(0, TOKENS // N) as it:
                        for e in range(EA):
                            s, use = e % NS, it * USES + e // NS + 1
                            act.wait_ge(up1_ready[s], use)
                            nc.scalar.activation(silu[s][:, :], up1[s][:, :], ACT.Silu).then_inc(silu_done[s], 1)

                @block.vector
                def _(dve):
                    def gated(it, e):
                        s, use = e % NS, it * USES + e // NS + 1
                        dve.wait_ge(silu_done[s], use)
                        dve.wait_ge(up3_ready[s], use)
                        nc.vector.tensor_tensor(hid[s][:, :], silu[s][:, :], up3[s][:, :], ALU.mult).then_inc(hid_ready[s], 1)

                    def mix(it, e):
                        s, use = e % NS, it * USES + e // NS + 1
                        dve.wait_ge(down_ready[s], use)
                        dve.wait_ge(mixed[1 - s], use + s)
                        if e < E:
                            for j in range(JT):
                                t = it * JT + j
                                last = nc.vector.scalar_tensor_tensor(
                                    g.tile(t), down[s][:, j * D:(j + 1) * D], gate[:, bass.ds(t, 1), e:e + 1], g.tile(t),
                                    ALU.mult, ALU.add)
                        else:
                            x = g.X[:, bass.ds(it * JT, JT), :].rearrange("p t d -> p (t d)")
                            last = nc.vector.scalar_tensor_tensor(x, down[s][:, :], 0.5, x, ALU.mult, ALU.add)
                        last.then_inc(mixed[s], 1)

                    with dve.Fori(0, TOKENS // N) as it:
                        gated(it, 0)
                        for e in range(1, EA):
                            gated(it, e)
                            mix(it, e - 1)
                        mix(it, EA - 1)


BF16 = mybir.dt.bfloat16
RMS_EPS = 1e-6


def rms_scales(nc, g, name, scale_out):
    NS = 4
    with Stage(nc, name + "_rms") as st:
        x1 = [st.sb(f"x1{s}", [P, D]) for s in range(NS)]
        square = [st.sb(f"square{s}", [P, D]) for s in range(NS)]
        ss = st.sb("ss", [P, TILES])
        slot_free = st.sems("slot_free", NS)
        x1_ready = st.sems("x1_ready", NS)
        rooted = st.sem("rooted")
        step = st.sem("step")
        with nc.Block() as block:
            @block.vector
            def _(dve):
                for s in range(NS):
                    dve.sem_inc(slot_free[s], 1)
                with dve.Fori(0, TILES // NS) as it:
                    for s in range(NS):
                        t = it * NS + s
                        dve.wait_ge(slot_free[s], it + 1)
                        nc.vector.tensor_scalar(x1[s][:, :], g.tile(t), g.mean[:, bass.ds(t, 1)],
                                                g.rstd[:, bass.ds(t, 1)], ALU.subtract, ALU.mult).then_inc(x1_ready[s], 1)
                dve.wait_ge(rooted, 1)
                nc.vector.reciprocal(ss[:, :], ss[:, :]).then_inc(step, 1)
                dve.wait_ge(step, 1)
                nc.vector.tensor_tensor(scale_out, ss[:, :], g.rstd[:, :], ALU.mult).then_inc(step, 1)

            @block.scalar
            def _(act):
                with act.Fori(0, TILES // NS) as it:
                    for s in range(NS):
                        act.wait_ge(x1_ready[s], it + 1)
                        nc.scalar.activation(square[s][:, :], x1[s][:, :], ACT.Square,
                                             accum_out=ss[:, bass.ds(it * NS + s, 1)]).then_inc(slot_free[s], 1)
                for s in range(NS):
                    act.wait_ge(slot_free[s], TILES // NS + 1)
                nc.scalar.activation(ss[:, :], ss[:, :], ACT.Sqrt, scale=1.0 / D, bias=g.c("eps_l2")).then_inc(rooted, 1)


L2A_HEADS, L2A_HD = 16, 8
L2A_PARTS = [("wq", D), ("wk", D), ("wv", D), ("wo", D), ("norm", D), ("bv", D), ("bo", D), ("bq", 1), ("bk", 1)]


def l2_attn(nc, g, name):
    H, HD = L2A_HEADS, L2A_HD
    cols, width = columns(L2A_PARTS)
    SCALE = float(HD) ** -0.5
    N = SEQ
    NS = 3
    PAIRS = H // 2
    uses = [len(range(s, PAIRS, NS)) for s in range(NS)]
    with Stage(nc, name) as st:
        w = st.sb("w", [P, width])
        scale = st.sb("scale", [P, TILES])
        row_statistics(nc, g, name, [(w[:, :], g.dram["w_l2a"])])
        rms_scales(nc, g, name, scale[:, :])
        ident_b = st.ctx.enter_context(nc.sbuf_tensor(name + "_ident_b", [P, P], BF16))
        causal_b = st.ctx.enter_context(nc.sbuf_tensor(name + "_causal_b", [P, P], BF16))
        bq4 = st.sb("bq4", [P, 4])
        x0 = st.sb("x0", [P, TPB, D])
        xn = st.sb("xn", [P, TPB, D])
        xT = st.sb("xT", [P, N])
        kT = st.sb("kT", [P, N])
        q4 = st.sb("q4", [P, 4, N])
        v = st.sb("v", [P, TPB, D])
        den = st.sb("den", [P, TPB, H])
        rden = st.sb("rden", [P, TPB, H])
        on = st.sb("on", [P, TPB * D])
        onT = st.sb("onT", [P, N])
        low = [st.sb(f"low{s}", [P, TPB, 2]) for s in range(NS)]
        bias = [st.sb(f"bias{s}", [P, TPB, 2]) for s in range(NS)]
        prob = [st.sb(f"prob{s}", [P, 2, 3 * P]) for s in range(NS)]
        probT = [st.sb(f"probT{s}", [P, 6, P]) for s in range(NS)]
        misc = st.ps("misc", [P, 512])
        O = st.ps("O", [P, 512])
        wideS = [st.ps(f"wideS{s}", [P, 512]) for s in range(NS)]
        slimS = [st.ps(f"slimS{s}", [P, 512]) for s in range(NS)]
        cast = st.sem("cast")
        batch_free = st.sem("batch_free")
        x0_ready = st.sem("x0_ready")
        xn_ready = st.sem("xn_ready")
        turned = st.sem("turned")
        xT_ready = st.sem("xT_ready")
        qk_ready = st.sem("qk_ready")
        qk_saved = st.sem("qk_saved")
        v_ready = st.sem("v_ready")
        v_saved = st.sem("v_saved")
        s_ready = st.sems("s_ready", NS)
        low_ready = st.sems("low_ready", NS)
        bias_ready = st.sems("bias_ready", NS)
        exp_done = st.sems("exp_done", NS)
        pT_ready = st.sems("pT_ready", NS)
        wide_saved = st.sems("wide_saved", NS)
        slim_saved = st.sems("slim_saved", NS)
        pv_done = st.sems("pv_done", NS)
        rden_ready = st.sem("rden_ready")
        on_ready = st.sem("on_ready")
        on_turned = st.sem("on_turned")
        onT_ready = st.sem("onT_ready")
        out_ready = st.sem("out_ready")
        out_added = st.sem("out_added")

        with nc.Block() as block:
            @block.vector
            def _(dve):
                nc.vector.tensor_copy(ident_b[:, :], g.c("ident")).then_inc(cast, 1)
                nc.vector.tensor_copy(causal_b[:, :], g.c("causal")).then_inc(cast, 1)
                nc.vector.tensor_scalar(bq4[:, :], g.c("quarter"), w[:, cols["bq"]], None, ALU.mult).then_inc(cast, 1)
                dve.sem_inc(batch_free, 1)

                def shift(it, i):
                    s, use = i % NS, it * uses[i % NS] + i // NS + 1
                    dve.wait_ge(s_ready[s], use)
                    nc.vector.tensor_reduce(low[s][:, 0, :], slimS[s][:, 0:2 * P].rearrange("p (h k) -> p h k", h=2), AX.X,
                                            ALU.max, negate=True)
                    nc.vector.tensor_reduce(low[s][:, 1, :], wideS[s][:, :].rearrange("p (h k) -> p h k", h=2), AX.X,
                                            ALU.max, negate=True).then_inc(low_ready[s], 1)
                    dve.wait_ge(low_ready[s], use)
                    nc.vector.tensor_scalar(bias[s][:, :, :], low[s][:, :, :], SCALE, None, ALU.mult).then_inc(bias_ready[s], 1)

                def save(it, i):
                    s, use = i % NS, it * uses[i % NS] + i // NS + 1
                    dve.wait_ge(pT_ready[s], use)
                    nc.vector.tensor_copy(probT[s][:, 4:6, :], slimS[s][:, 0:2 * P].rearrange("p (b q) -> p b q", b=2)
                                          ).then_inc(slim_saved[s], 1)

                with dve.Fori(0, BATCH) as it:
                    dve.wait_ge(batch_free, it + 1)
                    for u in range(TPB):
                        t = it * TPB + u
                        last = nc.vector.tensor_scalar(x0[:, u, :], g.tile(t), g.mean[:, bass.ds(t, 1)],
                                                       scale[:, bass.ds(t, 1)], ALU.subtract, ALU.mult)
                    last.then_inc(x0_ready, 1)
                    dve.wait_ge(x0_ready, it + 1)
                    nc.vector.tensor_tensor(xn[:, :, :], x0[:, :, :], w[:, cols["norm"]].unsqueeze(1).broadcast_to([P, TPB, D]),
                                            ALU.mult).then_inc(xn_ready, 1)
                    for i in range(PAIRS + 1):
                        if i < PAIRS:
                            shift(it, i)
                        if i >= 1:
                            save(it, i - 1)
                    for s in range(NS):
                        dve.wait_ge(exp_done[s], it * uses[s] + uses[s])
                    nc.vector.reciprocal(rden[:, :, :], den[:, :, :]).then_inc(rden_ready, 1)
                    dve.wait_ge(rden_ready, it + 1)
                    for s in range(NS):
                        dve.wait_ge(pv_done[s], it * uses[s] + uses[s])
                    nc.vector.tensor_tensor(on[:, :].rearrange("p (h e) -> p h e", e=HD),
                                            O[:, 0:TPB * D].rearrange("p (h e) -> p h e", e=HD),
                                            rden[:, :, :].rearrange("p u h -> p (u h)").unsqueeze(2)
                                            .broadcast_to([P, TPB * H, HD]), ALU.mult).then_inc(on_ready, 1)
                    x = g.X[:, bass.ds(it * TPB, TPB), :].rearrange("p u d -> p (u d)")
                    dve.wait_ge(out_ready, it + 1)
                    nc.vector.tensor_tensor(on[:, :], misc[:, 256:512], xn[:, :, :].rearrange("p u d -> p (u d)"),
                                            ALU.add).then_inc(out_added, 1)
                    dve.wait_ge(out_added, it + 1)
                    nc.vector.tensor_tensor(x, x, on[:, :], ALU.add).then_inc(batch_free, 1)

            @block.tensor
            def _(pe):
                def scores(it, i):
                    s, k = i % NS, i // NS
                    pe.wait_ge(wide_saved[s], it * uses[s] + k + 1)
                    pe.wait_ge(slim_saved[s], it * uses[s] + k + 1)
                    for hh in range(2):
                        h = 2 * i + hh
                        r = slice(32 * (h // 4), 32 * (h // 4) + 32)
                        o = wideS[s][:, hh * 256:hh * 256 + 256]
                        nc.tensor.matmul(o[:, 0:P], q4[r, h % 4, P:2 * P], kT[r, 0:P], start=True, stop=True)
                        nc.tensor.matmul(o[:, P:2 * P], q4[r, h % 4, P:2 * P], kT[r, P:2 * P], start=True, stop=False)
                        nc.tensor.matmul(o[:, P:2 * P], ident_b[:, :], causal_b[:, :], start=False, stop=True)
                        o = slimS[s][:, hh * P:hh * P + P]
                        nc.tensor.matmul(o, q4[r, h % 4, 0:P], kT[r, 0:P], start=True, stop=False)
                        last = nc.tensor.matmul(o, ident_b[:, :], causal_b[:, :], start=False, stop=True)
                    last.then_inc(s_ready[s], 1)

                def turn(it, i):
                    s, use = i % NS, it * uses[i % NS] + i // NS + 1
                    pe.wait_ge(exp_done[s], use)
                    for n in range(6):
                        o = wideS[s][:, n * P:n * P + P] if n < 4 else slimS[s][:, (n - 4) * P:(n - 3) * P]
                        last = nc.tensor.transpose(o, prob[s][:, n // 3, (n % 3) * P:(n % 3) * P + P], g.c("ident"))
                    last.then_inc(pT_ready[s], 1)

                def weigh(it, i):
                    s, use = i % NS, it * uses[i % NS] + i // NS + 1
                    pe.wait_ge(wide_saved[s], use + 1)
                    pe.wait_ge(slim_saved[s], use + 1)
                    for hh in range(2):
                        e = slice((2 * i + hh) * HD, (2 * i + hh + 1) * HD)
                        nc.tensor.matmul(O[:, e], probT[s][:, 3 * hh, :], v[:, 0, e], start=True, stop=True)
                        o = O[:, D + e.start:D + e.stop]
                        nc.tensor.matmul(o, probT[s][:, 3 * hh + 1, :], v[:, 0, e], start=True, stop=False)
                        last = nc.tensor.matmul(o, probT[s][:, 3 * hh + 2, :], v[:, 1, e], start=False, stop=True)
                    last.then_inc(pv_done[s], 1)

                for s in range(NS):
                    pe.sem_inc(wide_saved[s], 1)
                    pe.sem_inc(slim_saved[s], 1)
                pe.wait_ge(cast, 3)
                with pe.Fori(0, BATCH) as it:
                    pe.wait_ge(xn_ready, it + 1)
                    for u in range(TPB):
                        last = nc.tensor.transpose(misc[:, u * P:(u + 1) * P], xn[:, u, :], g.c("ident"))
                    last.then_inc(turned, 1)
                    pe.wait_ge(xT_ready, it + 1)
                    nc.tensor.matmul(misc[:, 0:N], w[:, cols["wq"]], xT[:, :], start=True, stop=True)
                    nc.tensor.matmul(misc[:, N:2 * N], w[:, cols["wk"]], xT[:, :], start=True, stop=True).then_inc(qk_ready, 1)
                    for u in range(TPB):
                        o = O[:, u * D:(u + 1) * D]
                        nc.tensor.matmul(o, xT[:, u * P:(u + 1) * P], w[:, cols["wv"]], start=True, stop=False)
                        last = nc.tensor.matmul(o, g.c("ones")[0:1, :], w[0:1, cols["bv"]], start=False, stop=True)
                    last.then_inc(v_ready, 1)
                    pe.wait_ge(qk_saved, it + 1)
                    pe.wait_ge(v_saved, it + 1)
                    for i in range(PAIRS + 2):
                        if i < PAIRS:
                            scores(it, i)
                        if 1 <= i <= PAIRS:
                            turn(it, i - 1)
                        if i >= 2:
                            weigh(it, i - 2)
                    pe.wait_ge(on_ready, it + 1)
                    for u in range(TPB):
                        last = nc.tensor.transpose(misc[:, u * P:(u + 1) * P], on[:, u * P:(u + 1) * P], g.c("ident"))
                    last.then_inc(on_turned, 1)
                    pe.wait_ge(onT_ready, it + 1)
                    for u in range(TPB):
                        o = misc[:, 256 + u * D:256 + (u + 1) * D]
                        nc.tensor.matmul(o, onT[:, u * P:(u + 1) * P], w[:, cols["wo"]], start=True, stop=False)
                        last = nc.tensor.matmul(o, g.c("ones")[0:1, :], w[0:1, cols["bo"]], start=False, stop=True)
                    last.then_inc(out_ready, 1)

            @block.scalar
            def _(act):
                def exps(it, i):
                    s, use = i % NS, it * uses[i % NS] + i // NS + 1
                    act.wait_ge(bias_ready[s], use)
                    for hh in range(2):
                        h = 2 * i + hh
                        nc.scalar.activation(prob[s][:, hh, 0:P], slimS[s][:, hh * P:hh * P + P], ACT.Exp, scale=SCALE,
                                             bias=bias[s][:, 0, hh:hh + 1], accum_out=den[:, 0, h:h + 1])
                        last = nc.scalar.activation(prob[s][:, hh, P:3 * P], wideS[s][:, hh * 256:hh * 256 + 256], ACT.Exp,
                                                    scale=SCALE, bias=bias[s][:, 1, hh:hh + 1], accum_out=den[:, 1, h:h + 1])
                    last.then_inc(exp_done[s], 1)

                def save(it, i):
                    s, use = i % NS, it * uses[i % NS] + i // NS + 1
                    act.wait_ge(pT_ready[s], use)
                    nc.scalar.copy(probT[s][:, 0:4, :], wideS[s][:, :].rearrange("p (b q) -> p b q", b=4)).then_inc(wide_saved[s], 1)

                act.wait_ge(cast, 3)
                with act.Fori(0, BATCH) as it:
                    act.wait_ge(turned, it + 1)
                    nc.scalar.copy(xT[:, :], misc[:, 0:N]).then_inc(xT_ready, 1)
                    act.wait_ge(qk_ready, it + 1)
                    nc.scalar.activation(kT[:, :], misc[:, N:2 * N], ACT.Identity, bias=w[:, cols["bk"]])
                    for c in range(4):
                        last = nc.scalar.activation(q4[:, c, :], misc[:, 0:N], ACT.Identity, bias=bq4[:, c:c + 1],
                                                    scale=g.c("quarter")[:, c:c + 1])
                    last.then_inc(qk_saved, 1)
                    act.wait_ge(v_ready, it + 1)
                    nc.scalar.copy(v[:, :, :], O[:, 0:TPB * D].rearrange("p (u d) -> p u d", u=TPB)).then_inc(v_saved, 1)
                    for i in range(PAIRS + 1):
                        if i < PAIRS:
                            exps(it, i)
                        if i >= 1:
                            save(it, i - 1)
                    act.wait_ge(on_turned, it + 1)
                    nc.scalar.copy(onT[:, :], misc[:, 0:N]).then_inc(onT_ready, 1)


L3_HID = 512
L3_C = L3_HID // P
L3F_PARTS = [("w1", L3_HID), ("w2", L3_HID), ("h1", L3_C * L3_HID), ("h2", L3_C * L3_HID), ("w3", L3_C * D),
             ("s1", L3_C), ("s2", L3_C), ("sh1", L3_C), ("sh2", L3_C), ("s3", D)]


def l3_ffn(nc, g, name):
    cols, width = columns(L3F_PARTS)
    C = L3_C
    N = 512
    JT = N // P
    NS = 2
    with Stage(nc, name) as st:
        w = st.sb("w", [P, width])
        XT = st.sb("XT", [P, TOKENS])
        row_statistics(nc, g, name, [(w[:, :], g.dram["w_l3f"])])
        turn_stream(nc, g, name, XT)
        h1 = w[:, cols["h1"]].rearrange("p (k o) -> p k o", k=C)
        h2 = w[:, cols["h2"]].rearrange("p (k o) -> p k o", k=C)
        w3 = w[:, cols["w3"]].rearrange("p (k o) -> p k o", k=C)
        silu = [st.sb(f"silu{s}", [P, C, N]) for s in range(NS)]
        hid = [st.sb(f"hid{s}", [P, C, N]) for s in range(NS)]
        gelu1 = [st.sb(f"gelu1{s}", [P, C, N]) for s in range(NS)]
        gelu2 = [st.sb(f"gelu2{s}", [P, C, N]) for s in range(NS)]
        scaled = [st.sb(f"scaled{s}", [P, N]) for s in range(NS)]
        bank = [[st.ps(f"bank{s}_{c}", [P, N]) for c in range(C)] for s in range(NS)]
        slot_free = st.sems("slot_free", NS)
        a_ready = st.sems("a_ready", NS)
        b_ready = st.sems("b_ready", NS)
        silu_done = st.sems("silu_done", NS)
        hid_ready = st.sems("hid_ready", NS)
        sq1_ready = st.sems("sq1_ready", NS)
        gelu1_done = st.sems("gelu1_done", NS)
        sq2_ready = st.sems("sq2_ready", NS)
        gelu2_done = st.sems("gelu2_done", NS)
        out_ready = st.sems("out_ready", NS)
        scale_done = st.sems("scale_done", NS)
        with nc.Block() as block:
            @block.tensor
            def _(pe):
                for s in range(NS):
                    pe.sem_inc(slot_free[s], 1)
                with pe.Fori(0, TOKENS // N // NS) as it:
                    for c in range(C):
                        for s in range(NS):
                            x = XT[:, bass.ds((it * NS + s) * N, N)]
                            if c == 0:
                                pe.wait_ge(slot_free[s], it + 1)
                            if c >= 2:
                                pe.wait_ge(hid_ready[s], it * C + c - 1)
                            nc.tensor.matmul(bank[s][c % 2][:, :], w[:, cols["w1"]][:, c * P:(c + 1) * P], x, start=True,
                                             stop=True).then_inc(a_ready[s], 1)
                            nc.tensor.matmul(bank[s][2 + c % 2][:, :], w[:, cols["w2"]][:, c * P:(c + 1) * P], x, start=True,
                                             stop=True).then_inc(b_ready[s], 1)
                    for layer, src, needs, ready in ((h1, hid, hid_ready, sq1_ready), (h2, gelu1, gelu1_done, sq2_ready)):
                        for s in range(NS):
                            pe.wait_ge(needs[s], it * C + C)
                            for c in range(C):
                                for k in range(C):
                                    last = nc.tensor.matmul(bank[s][c][:, :], layer[:, k, c * P:(c + 1) * P], src[s][:, k, :],
                                                            start=(k == 0), stop=(k == C - 1))
                                last.then_inc(ready[s], 1)
                    for s in range(NS):
                        pe.wait_ge(gelu2_done[s], it * C + C)
                        for j in range(JT):
                            for k in range(C):
                                last = nc.tensor.matmul(bank[s][0][:, j * D:(j + 1) * D], gelu2[s][:, k, j * P:(j + 1) * P],
                                                        w3[:, k, :], start=(k == 0), stop=(k == C - 1))
                        last.then_inc(out_ready[s], 1)

            @block.scalar
            def _(act):
                with act.Fori(0, TOKENS // N // NS) as it:
                    for c in range(C):
                        for s in range(NS):
                            act.wait_ge(a_ready[s], it * C + c + 1)
                            nc.scalar.activation(silu[s][:, c, :], bank[s][c % 2][:, :], ACT.Silu,
                                                 scale=w[:, cols["s1"]][:, c:c + 1]).then_inc(silu_done[s], 1)
                    for dst, scale, ready, done in ((gelu1, "sh1", sq1_ready, gelu1_done), (gelu2, "sh2", sq2_ready, gelu2_done)):
                        for s in range(NS):
                            for c in range(C):
                                act.wait_ge(ready[s], it * C + c + 1)
                                nc.scalar.activation(dst[s][:, c, :], bank[s][c][:, :], ACT.Gelu,
                                                     scale=w[:, cols[scale]][:, c:c + 1]).then_inc(done[s], 1)

            @block.vector
            def _(dve):
                with dve.Fori(0, TOKENS // N // NS) as it:
                    for c in range(C):
                        for s in range(NS):
                            dve.wait_ge(silu_done[s], it * C + c + 1)
                            dve.wait_ge(b_ready[s], it * C + c + 1)
                            nc.vector.scalar_tensor_tensor(hid[s][:, c, :], bank[s][2 + c % 2][:, :],
                                                           w[:, cols["s2"]][:, c:c + 1], silu[s][:, c, :],
                                                           ALU.mult, ALU.mult).then_inc(hid_ready[s], 1)
                    for s in range(NS):
                        dve.wait_ge(out_ready[s], it + 1)
                        nc.vector.tensor_tensor(scaled[s][:, :].rearrange("p (j d) -> p j d", j=JT),
                                                bank[s][0][:, :].rearrange("p (j d) -> p j d", j=JT),
                                                w[:, cols["s3"]].unsqueeze(1).broadcast_to([P, JT, D]),
                                                ALU.mult).then_inc(scale_done[s], 1)
                    for s in range(NS):
                        x = g.X[:, bass.ds((it * NS + s) * JT, JT), :].rearrange("p t d -> p (t d)")
                        dve.wait_ge(scale_done[s], it + 1)
                        nc.vector.scalar_tensor_tensor(x, scaled[s][:, :], 0.5, x, ALU.mult, ALU.add).then_inc(slot_free[s], 1)


L3A_HEADS, L3A_HD, L3A_TAPS, L3A_INNER = 16, 8, 4, 345
L3A_ALPHA_BIAS = 4.0
L3A_PARTS = [("wq", D), ("wk", D), ("wv", D), ("wba", 2 * L3A_HEADS), ("wo", D), ("wg", L3A_INNER), ("wu", L3A_INNER),
             ("wd", 3 * D), ("norm1", D), ("norm2", D), ("taps", L3A_TAPS), ("conv_b", 1)]


def l3_attn(nc, g, name):
    H, HD = L3A_HEADS, L3A_HD
    cols, width = columns(L3A_PARTS)
    N = SEQ
    NS = 2
    G = BATCH * H // P
    STEP = 32
    ROUNDS = SEQ // STEP
    PAD = L3A_TAPS - 1
    inner = [(c * P, min(P, L3A_INNER - c * P)) for c in range(3)]
    with Stage(nc, name) as st:
        w = st.sb("w", [P, width])
        scale = st.sb("scale", [P, TILES])
        row_statistics(nc, g, name, [(w[:, :], g.dram["w_l3a"])])
        rms_scales(nc, g, name, scale[:, :])
        qkv_d = nc.dram_tensor(name + "_qkv", (3, BATCH, P, N), F32, kind="Internal").ap()
        gates_d = nc.dram_tensor(name + "_gates", (2, BATCH, H, N), F32, kind="Internal").ap()
        o_d = nc.dram_tensor(name + "_o", (BATCH, P, N), F32, kind="Internal").ap()

        with Stage(nc, name + "_a") as sa:
            x0 = [sa.sb(f"x0{s}", [P, TPB, D]) for s in range(NS)]
            xn = [sa.sb(f"xn{s}", [P, TPB, D]) for s in range(NS)]
            xT = [sa.sb(f"xT{s}", [P, PAD + N]) for s in range(NS)]
            conv = [sa.sb(f"conv{s}", [P, L3A_TAPS, N]) for s in range(NS)]
            xc = [sa.sb(f"xc{s}", [P, N]) for s in range(NS)]
            qkv = [sa.sb(f"qkv{s}", [P, 3, N]) for s in range(NS)]
            gates = [sa.sb(f"gates{s}", [2 * H, N]) for s in range(NS)]
            turn = [sa.ps(f"turn{s}", [P, 512]) for s in range(NS)]
            qk = [sa.ps(f"qk{s}", [P, 512]) for s in range(NS)]
            vg = [sa.ps(f"vg{s}", [P, 512]) for s in range(NS)]
            x0_ready = sa.sems("x0_ready", NS)
            xn_ready = sa.sems("xn_ready", NS)
            turned = sa.sems("turned", NS)
            xT_ready = sa.sems("xT_ready", NS)
            conv_step = sa.sems("conv_step", NS)
            xc_ready = sa.sems("xc_ready", NS)
            proj_ready = sa.sems("proj_ready", NS)
            saved = sa.sems("saved", NS)
            stored = sa.sems("stored", NS)
            with nc.Block() as block:
                @block.vector
                def _(dve):
                    for s in range(NS):
                        nc.vector.memset(xT[s][:, 0:PAD], 0.0).then_inc(conv_step[s], 1)
                    for s in range(NS):
                        dve.sem_inc(stored[s], 1)
                    with dve.Fori(0, BATCH // NS) as it:
                        for s in range(NS):
                            dve.wait_ge(stored[s], it * 48 + 1)
                            for u in range(TPB):
                                t = (it * NS + s) * TPB + u
                                last = nc.vector.tensor_scalar(x0[s][:, u, :], g.tile(t), g.mean[:, bass.ds(t, 1)],
                                                               scale[:, bass.ds(t, 1)], ALU.subtract, ALU.mult)
                            last.then_inc(x0_ready[s], 1)
                        for s in range(NS):
                            dve.wait_ge(x0_ready[s], it + 1)
                            nc.vector.tensor_tensor(xn[s][:, :, :], x0[s][:, :, :],
                                                    w[:, cols["norm1"]].unsqueeze(1).broadcast_to([P, TPB, D]),
                                                    ALU.mult).then_inc(xn_ready[s], 1)
                        for j in range(L3A_TAPS):
                            for s in range(NS):
                                tap = w[:, cols["taps"]][:, j:j + 1]
                                if j == 0:
                                    dve.wait_ge(xT_ready[s], it + 1)
                                    nc.vector.tensor_scalar(conv[s][:, 0, :], xT[s][:, 0:N], tap, w[:, cols["conv_b"]],
                                                            ALU.mult, ALU.add).then_inc(conv_step[s], 1)
                                else:
                                    dve.wait_ge(conv_step[s], it * L3A_TAPS + j + 1)
                                    nc.vector.scalar_tensor_tensor(conv[s][:, j, :], xT[s][:, j:j + N], tap,
                                                                   conv[s][:, j - 1, :], ALU.mult, ALU.add
                                                                   ).then_inc(conv_step[s], 1)

                @block.tensor
                def _(pe):
                    with pe.Fori(0, BATCH // NS) as it:
                        for s in range(NS):
                            pe.wait_ge(xn_ready[s], it + 1)
                            for u in range(TPB):
                                last = nc.tensor.transpose(turn[s][:, u * P:(u + 1) * P], xn[s][:, u, :], g.c("ident"))
                            last.then_inc(turned[s], 1)
                        for s in range(NS):
                            pe.wait_ge(xc_ready[s], it + 1)
                            nc.tensor.matmul(qk[s][:, 0:N], w[:, cols["wq"]], xc[s][:, :], start=True, stop=True)
                            nc.tensor.matmul(qk[s][:, N:2 * N], w[:, cols["wk"]], xc[s][:, :], start=True, stop=True)
                            nc.tensor.matmul(vg[s][:, 0:N], w[:, cols["wv"]], xc[s][:, :], start=True, stop=True)
                            nc.tensor.matmul(vg[s][0:2 * H, N:2 * N], w[:, cols["wba"]], xc[s][:, :], start=True,
                                             stop=True).then_inc(proj_ready[s], 1)

                @block.scalar
                def _(act):
                    with act.Fori(0, BATCH // NS) as it:
                        for s in range(NS):
                            if s == 0:
                                for z in range(NS):
                                    act.wait_ge(conv_step[z], 1)
                            act.wait_ge(turned[s], it + 1)
                            nc.scalar.copy(xT[s][:, PAD:PAD + N], turn[s][:, 0:N]).then_inc(xT_ready[s], 1)
                        for s in range(NS):
                            act.wait_ge(conv_step[s], it * L3A_TAPS + L3A_TAPS + 1)
                            nc.scalar.activation(xc[s][:, :], conv[s][:, L3A_TAPS - 1, :], ACT.Silu).then_inc(xc_ready[s], 1)
                        for s in range(NS):
                            act.wait_ge(proj_ready[s], it + 1)
                            nc.scalar.copy(qkv[s][:, 0:2, :], qk[s][:, :].rearrange("p (k t) -> p k t", k=2))
                            nc.scalar.copy(qkv[s][:, 2, :], vg[s][:, 0:N])
                            nc.scalar.copy(gates[s][:, :], vg[s][0:2 * H, N:2 * N]).then_inc(saved[s], 1)

                @block.sync
                def _(sp):
                    with sp.Fori(0, BATCH // NS) as it:
                        for s in range(NS):
                            b = it * NS + s
                            sp.wait_ge(saved[s], it + 1)
                            sp.dma_start(qkv_d[:, bass.ds(b, 1), :, :].rearrange("k b p t -> p (k b) t"), qkv[s][:, :, :]
                                         ).then_inc(stored[s], 16)
                            for k in range(2):
                                sp.dma_start(gates_d[k, bass.ds(b, 1), :, :].rearrange("b h t -> (b h) t"),
                                             gates[s][k * H:(k + 1) * H, :]).then_inc(stored[s], 16)
                    for s in range(NS):
                        sp.wait_ge(stored[s], BATCH // NS * 48 + 1)

        with Stage(nc, name + "_s") as ss:
            qkv = ss.sb("qkv", [P, 3, G, HD, N])
            kg = ss.sb("kg", [P, G, HD, N])
            gates = ss.sb("gates", [P, 2, G, N])
            both = ss.sb("both", [P, G, N])
            length = ss.sb("length", [P, 2, G, N])
            hist = [ss.sb(f"hist{z}", [P, STEP + 1, G, HD, HD]) for z in range(2)]
            prod = ss.sb("prod", [P, 2, G, HD, HD])
            pred = ss.sb("pred", [P, G, HD])
            delta = ss.sb("delta", [P, G, HD])
            outer = ss.sb("outer", [P, G, HD, HD])
            read = ss.sb("read", [P, STEP, HD, HD])
            o = ss.sb("o", [P, G, HD, N])
            loaded = ss.sem("loaded")
            gates_done = ss.sem("gates_done")
            step = ss.sem("step")
            squared = ss.sem("squared")
            rooted = ss.sem("rooted")
            ready = ss.sem("ready")
            cell = ss.sem("cell")
            round_done = ss.sem("round_done")
            read_done = ss.sem("read_done")
            summed = ss.sem("summed")
            stored = ss.sem("stored")
            q, k, v = (qkv[:, i, :, :, :] for i in range(3))
            CELLS = 6

            def over_d(a):
                return a.unsqueeze(2).broadcast_to([P, G, HD, N])

            with nc.Block() as block:
                @block.sync
                def _(sp):
                    for i in range(3):
                        sp.dma_start(qkv[:, i, :, :, :].rearrange("p g d t -> p g (d t)"),
                                     qkv_d[i].rearrange("(g b) (h d) t -> (b h) g (d t)", g=G, h=H)).then_inc(loaded, 16)
                    for i in range(2):
                        sp.dma_start(gates[:, i, :, :], gates_d[i].rearrange("(g b) h t -> (b h) g t", g=G)).then_inc(loaded, 16)
                    sp.wait_ge(summed, ROUNDS * G)
                    sp.dma_start(o_d.rearrange("(g b) (h d) t -> (b h) g (d t)", g=G, h=H),
                                 o[:, :, :, :].rearrange("p g d t -> p g (d t)")).then_inc(stored, 16)
                    sp.wait_ge(stored, 16)

                @block.scalar
                def _(act):
                    act.wait_ge(loaded, 80)
                    nc.scalar.activation(gates[:, 0, :, :], gates[:, 0, :, :], ACT.Sigmoid)
                    nc.scalar.activation(gates[:, 1, :, :], gates[:, 1, :, :], ACT.Sigmoid,
                                         bias=g.c("alpha_bias")).then_inc(gates_done, 1)
                    act.wait_ge(squared, 1)
                    nc.scalar.activation(length[:, :, :, :], length[:, :, :, :], ACT.Sqrt, bias=g.c("eps_l2")).then_inc(rooted, 1)

                @block.vector
                def _(dve):
                    square = hist[0][:, 0:STEP, :, :, :].rearrange("p s g a b -> p (s g a b)").rearrange(
                        "p (g d t) -> p g d t", g=G, d=HD)
                    dve.wait_ge(loaded, 80)
                    for i, a in enumerate((q, k)):
                        if i:
                            dve.wait_ge(step, 2)
                        nc.vector.tensor_tensor(square, a, a, ALU.mult).then_inc(step, 1)
                        dve.wait_ge(step, 2 * i + 1)
                        last = nc.vector.tensor_reduce(length[:, i, :, :], square.rearrange("p g d t -> p g t d"), AX.X, ALU.add)
                        last.then_inc(squared if i else step, 1)
                    dve.wait_ge(rooted, 1)
                    nc.vector.reciprocal(length[:, :, :, :], length[:, :, :, :]).then_inc(step, 1)
                    dve.wait_ge(step, 4)
                    nc.vector.tensor_tensor(q, q, over_d(length[:, 0, :, :]), ALU.mult)
                    nc.vector.tensor_tensor(k, k, over_d(length[:, 1, :, :]), ALU.mult).then_inc(step, 1)
                    dve.wait_ge(gates_done, 1)
                    nc.vector.tensor_tensor(v, v, over_d(gates[:, 0, :, :]), ALU.mult).then_inc(step, 1)
                    nc.vector.tensor_tensor(both[:, :, :], gates[:, 0, :, :], gates[:, 1, :, :], ALU.mult).then_inc(step, 1)
                    dve.wait_ge(step, 7)
                    nc.vector.tensor_tensor(kg[:, :, :, :], k, over_d(both[:, :, :]), ALU.mult).then_inc(step, 1)
                    nc.vector.memset(hist[1][:, STEP, :, :, :], 0.0).then_inc(step, 1)
                    dve.wait_ge(step, 9)

                    def readout(r, z):
                        for gi in range(G):
                            dve.wait_ge(read_done, (r * 2 + z) * G + gi + 1)
                            nc.vector.tensor_reduce(o[:, gi, :, bass.ds((r * 2 + z) * STEP, STEP)].rearrange("p d t -> p t d"),
                                                    read[:, :, :, :], AX.X, ALU.add).then_inc(summed, 1)

                    with dve.Fori(0, ROUNDS // 2) as r:
                        for z in range(2):
                            for i in range(STEP):
                                t = (r * 2 + z) * STEP + i
                                done = ((r * 2 + z) * STEP + i) * CELLS
                                old = hist[z][:, i, :, :, :] if i else hist[1 - z][:, STEP, :, :, :]
                                new = hist[z][:, i + 1, :, :, :]

                                def along_k(a):
                                    return a[:, :, :, bass.ds(t, 1)].rearrange("p g d t -> p g (t d)").unsqueeze(2).broadcast_to(
                                        [P, G, HD, HD])

                                if i or z:
                                    dve.wait_ge(cell, done)
                                else:
                                    dve.wait_ge(ready, r + 1)
                                nc.vector.tensor_tensor(prod[:, 0, :, :, :], old, along_k(kg), ALU.mult).then_inc(cell, 1)
                                dve.wait_ge(cell, done + 1)
                                nc.vector.tensor_reduce(pred[:, :, :], prod[:, 0, :, :, :], AX.X, ALU.add,
                                                        negate=True).then_inc(cell, 1)
                                dve.wait_ge(cell, done + 2)
                                nc.vector.tensor_tensor(delta[:, :, :], pred[:, :, :],
                                                        v[:, :, :, bass.ds(t, 1)].rearrange("p g d t -> p g (d t)"),
                                                        ALU.add).then_inc(cell, 1)
                                dve.wait_ge(cell, done + 3)
                                nc.vector.tensor_tensor(outer[:, :, :, :],
                                                        delta[:, :, :].unsqueeze(3).broadcast_to([P, G, HD, HD]),
                                                        along_k(k), ALU.mult).then_inc(cell, 1)
                                dve.wait_ge(cell, done + 4)
                                if i == 0:
                                    pass
                                for gi in range(G):
                                    last = nc.vector.scalar_tensor_tensor(
                                        new[:, gi, :, :], old[:, gi, :, :], gates[:, 1, gi, bass.ds(t, 1)], outer[:, gi, :, :],
                                        ALU.mult, ALU.add)
                                    last.then_inc(cell, 1)
                            dve.wait_ge(cell, ((r * 2 + z) * STEP + STEP) * CELLS)
                            dve.sem_inc(round_done, 1)
                            readout(r, z)
                        dve.sem_inc(ready, 1)

                @block.gpsimd
                def _(pool):
                    with pool.Fori(0, ROUNDS // 2) as r:
                        for z in range(2):
                            pool.wait_ge(round_done, r * 2 + z + 1)
                            for gi in range(G):
                                if gi:
                                    pool.wait_ge(summed, (r * 2 + z) * G + gi)
                                qt = q[:, gi, :, bass.ds((r * 2 + z) * STEP, STEP)].rearrange("p d t -> p t d").unsqueeze(
                                    2).broadcast_to([P, STEP, HD, HD])
                                nc.gpsimd.tensor_tensor(read[:, :, :, :], hist[z][:, 1:STEP + 1, gi, :, :], qt,
                                                        ALU.mult).then_inc(read_done, 1)

                @block.tensor
                def _(pe):
                    pe.sem_inc(ready, 1)

        hid = st.sb("hid", [P, TILES, D])
        hscale = st.sb("hscale", [P, TILES])
        with Stage(nc, name + "_h") as sh:
            x1 = [sh.sb(f"x1{s}", [P, TPB, D]) for s in range(NS)]
            oT = [sh.sb(f"oT{s}", [P, N]) for s in range(NS)]
            hs = [sh.sb(f"hs{s}", [P, TPB, D]) for s in range(NS)]
            square = [sh.sb(f"square{s}", [P, TPB, D]) for s in range(NS)]
            mix = [sh.ps(f"mix{s}", [P, 512]) for s in range(NS)]
            o_loaded = sh.sems("o_loaded", NS)
            slot_free = sh.sems("slot_free", NS)
            mix_ready = sh.sems("mix_ready", NS)
            x1_ready = sh.sems("x1_ready", NS)
            h_ready = sh.sems("h_ready", NS)
            rooted = sh.sem("rooted")
            with nc.Block() as block:
                @block.sync
                def _(sp):
                    for s in range(NS):
                        sp.sem_inc(slot_free[s], 1)
                    with sp.Fori(0, BATCH // NS) as it:
                        for s in range(NS):
                            sp.wait_ge(slot_free[s], it + 1)
                            sp.dma_start(oT[s][:, :], o_d[bass.ds(it * NS + s, 1), :, :].rearrange("b p t -> (b p) t")
                                         ).then_inc(o_loaded[s], 16)

                @block.tensor
                def _(pe):
                    with pe.Fori(0, BATCH // NS) as it:
                        for s in range(NS):
                            pe.wait_ge(o_loaded[s], it * 16 + 16)
                            for u in range(TPB):
                                last = nc.tensor.matmul(mix[s][:, u * D:(u + 1) * D], oT[s][:, u * P:(u + 1) * P],
                                                        w[:, cols["wo"]], start=True, stop=True)
                            last.then_inc(mix_ready[s], 1)

                @block.vector
                def _(dve):
                    with dve.Fori(0, BATCH // NS) as it:
                        for s in range(NS):
                            dve.wait_ge(mix_ready[s], it + 1)
                            for u in range(TPB):
                                t = (it * NS + s) * TPB + u
                                last = nc.vector.tensor_scalar(x1[s][:, u, :], g.tile(t), g.mean[:, bass.ds(t, 1)],
                                                               g.rstd[:, bass.ds(t, 1)], ALU.subtract, ALU.mult)
                            last.then_inc(x1_ready[s], 1)
                        for s in range(NS):
                            t = (it * NS + s) * TPB
                            dve.wait_ge(x1_ready[s], it + 1)
                            nc.vector.tensor_tensor(hid[:, bass.ds(t, TPB), :].rearrange("p u d -> p (u d)"),
                                                    x1[s][:, :, :].rearrange("p u d -> p (u d)"),
                                                    mix[s][:, 0:TPB * D], ALU.add).then_inc(h_ready[s], 1)
                    dve.wait_ge(rooted, 1)
                    nc.vector.reciprocal(hscale[:, :], hscale[:, :]).then_inc(rooted, 1)

                @block.scalar
                def _(act):
                    with act.Fori(0, BATCH // NS) as it:
                        for s in range(NS):
                            act.wait_ge(h_ready[s], it + 1)
                            for u in range(TPB):
                                t = (it * NS + s) * TPB + u
                                last = nc.scalar.activation(square[s][:, u, :], hid[:, bass.ds(t, 1), :], ACT.Square,
                                                            accum_out=hscale[:, bass.ds(t, 1)])
                            last.then_inc(slot_free[s], 1)
                    for s in range(NS):
                        act.wait_ge(slot_free[s], BATCH // NS + 1)
                    nc.scalar.activation(hscale[:, :], hscale[:, :], ACT.Sqrt, scale=1.0 / D, bias=g.c("eps_l2")).then_inc(rooted, 1)

        with Stage(nc, name + "_f") as sf:
            h0 = [sf.sb(f"h0{s}", [P, D]) for s in range(NS)]
            hn = [sf.sb(f"hn{s}", [P, D]) for s in range(NS)]
            hT = [sf.sb(f"hT{s}", [P, P]) for s in range(NS)]
            silu = [sf.sb(f"silu{s}", [P, 3, P]) for s in range(NS)]
            act_ = [sf.sb(f"act{s}", [P, 3, P]) for s in range(NS)]
            total = [sf.sb(f"total{s}", [P, D]) for s in range(NS)]
            turn = [sf.ps(f"turn{s}", [P, 512]) for s in range(NS)]
            gate = [sf.ps(f"gate{s}", [P, 512]) for s in range(NS)]
            up = [sf.ps(f"up{s}", [P, 512]) for s in range(NS)]
            slot_free = sf.sems("slot_free", NS)
            h0_ready = sf.sems("h0_ready", NS)
            hn_ready = sf.sems("hn_ready", NS)
            turned = sf.sems("turned", NS)
            hT_ready = sf.sems("hT_ready", NS)
            gate_ready = sf.sems("gate_ready", NS)
            up_ready = sf.sems("up_ready", NS)
            silu_done = sf.sems("silu_done", NS)
            act_ready = sf.sems("act_ready", NS)
            down_ready = sf.sems("down_ready", NS)
            total_ready = sf.sems("total_ready", NS)
            with nc.Block() as block:
                @block.vector
                def _(dve):
                    for s in range(NS):
                        dve.sem_inc(slot_free[s], 1)
                    with dve.Fori(0, TILES // NS) as it:
                        for s in range(NS):
                            t = it * NS + s
                            dve.wait_ge(slot_free[s], it + 1)
                            nc.vector.tensor_scalar(h0[s][:, :], hid[:, bass.ds(t, 1), :], hscale[:, bass.ds(t, 1)], None,
                                                    ALU.mult).then_inc(h0_ready[s], 1)
                        for s in range(NS):
                            dve.wait_ge(h0_ready[s], it + 1)
                            nc.vector.tensor_tensor(hn[s][:, :], h0[s][:, :], w[:, cols["norm2"]], ALU.mult).then_inc(hn_ready[s], 1)
                        for s in range(NS):
                            dve.wait_ge(silu_done[s], it + 1)
                            dve.wait_ge(up_ready[s], it + 1)
                            for c, (at, m) in enumerate(inner):
                                last = nc.vector.tensor_tensor(act_[s][0:m, c, :], silu[s][0:m, c, :],
                                                               up[s][0:m, c * P:(c + 1) * P], ALU.mult)
                            last.then_inc(act_ready[s], 1)
                        for s in range(NS):
                            t = it * NS + s
                            dve.wait_ge(down_ready[s], it + 1)
                            nc.vector.tensor_tensor(total[s][:, :], turn[s][:, 128:256],
                                                    hid[:, bass.ds(t, 1), :].rearrange("p t d -> p (t d)"), ALU.add
                                                    ).then_inc(total_ready[s], 1)
                        for s in range(NS):
                            t = it * NS + s
                            x = g.tile(t).rearrange("p t d -> p (t d)")
                            dve.wait_ge(total_ready[s], it + 1)
                            nc.vector.tensor_tensor(x, x, total[s][:, :], ALU.add).then_inc(slot_free[s], 1)

                @block.tensor
                def _(pe):
                    with pe.Fori(0, TILES // NS) as it:
                        for s in range(NS):
                            pe.wait_ge(hn_ready[s], it + 1)
                            nc.tensor.transpose(turn[s][:, 0:P], hn[s][:, :], g.c("ident")).then_inc(turned[s], 1)
                        for s in range(NS):
                            pe.wait_ge(hT_ready[s], it + 1)
                            for bank, part, done in ((gate[s], "wg", gate_ready[s]), (up[s], "wu", up_ready[s])):
                                for c, (at, m) in enumerate(inner):
                                    last = nc.tensor.matmul(bank[0:m, c * P:(c + 1) * P], w[:, cols[part]][:, at:at + m],
                                                            hT[s][:, :], start=True, stop=True)
                                last.then_inc(done, 1)
                        for s in range(NS):
                            pe.wait_ge(act_ready[s], it + 1)
                            for c, (at, m) in enumerate(inner):
                                last = nc.tensor.matmul(turn[s][:, 128:256], act_[s][0:m, c, :],
                                                        w[0:m, cols["wd"]][:, c * D:(c + 1) * D], start=(c == 0), stop=(c == 2))
                            last.then_inc(down_ready[s], 1)

                @block.scalar
                def _(act):
                    with act.Fori(0, TILES // NS) as it:
                        for s in range(NS):
                            act.wait_ge(turned[s], it + 1)
                            nc.scalar.copy(hT[s][:, :], turn[s][:, 0:P]).then_inc(hT_ready[s], 1)
                        for s in range(NS):
                            act.wait_ge(gate_ready[s], it + 1)
                            for c, (at, m) in enumerate(inner):
                                last = nc.scalar.activation(silu[s][0:m, c, :], gate[s][0:m, c * P:(c + 1) * P], ACT.Silu)
                            last.then_inc(silu_done[s], 1)


PIPELINE = {0: (l0_ffn, "l0f"), 1: (l0_attn, "l0a"), 2: (l0_ffn, "l0f"),
            3: (l1_ffn, "l1f"), 4: (l1_attn, "l1a"), 5: (l1_ffn, "l1f"), 6: (l2_ffn, "l2f"), 7: (l2_attn, "l2a"), 8: (l2_ffn, "l2f"), 9: (l3_ffn, "l3f"), 10: (l3_attn, "l3a"),
            11: (l3_ffn, "l3f")}


def build(nc, dram, out):
    Stage.pool = [nc.alloc_semaphore(f"s{i}") for i in range(SEMAPHORES)]
    Stage.taken = 0
    with ExitStack() as ctx:
        g = Globals(nc, ctx, dram, out)
        load_stream(nc, g)
        for n in STEPS:
            step, name = PIPELINE[n]
            step(nc, g, f"{name}_{n}")
        store_stream(nc, g)


def constants():
    import numpy as np
    p = np.arange(P)[:, None]
    j = np.arange(P)[None, :]
    levels = []
    for k in range(1, 7):
        s = 1 << k
        levels.append((p // s == j // s + 1) & ((j // s) % 2 == 0))
    level1 = (p == j + 1) & (j % 2 == 0)
    rows = np.arange(P)[:, None]
    tables = {
        "ident": p == j, "ones": np.ones((P, P)), "iota": j + 0 * p, "rev_iota": P - j + 0 * p,
        "upto": p <= j, "after": p > j, "blocks8": p // 8 == j // 8, "heads8": p // 8 == np.arange(16)[None, :],
        "level1n": -1.0 * level1, "level1tn": -1.0 * level1.T, "level": np.concatenate(levels, axis=1),
        "row_index": rows, "is_query": (rows % 8) < 4, "quarter": (rows % 32) // 8 == np.arange(4)[None, :],
        "minus_half": np.full((P, 512), -0.5), "eps_ln": np.full((P, 1), LN_EPS), "eps_l2": np.full((P, 1), 1e-6),
        "causal": np.where(j <= p, 0.0, -1e30),
        "alpha_bias": np.full((P, 1), L3A_ALPHA_BIAS),
        "before8": np.broadcast_to((np.arange(8)[None, :] < np.arange(8)[:, None]).reshape(1, 64), (P, 64)),
    }
    return np.ascontiguousarray(np.concatenate([tables[n] for n, _ in CONST_PARTS], axis=1).astype(np.float32))


def lay_out(inputs):
    import numpy as np

    def rows(a):
        return np.broadcast_to(np.reshape(a, (1, -1)), (P, a.size))

    def side(*parts):
        return np.ascontiguousarray(np.concatenate(parts, axis=1))

    i = inputs
    arrays = {"x": np.ascontiguousarray(np.reshape(i["L0_attn_x"], (TOKENS, D))), "consts": constants()}
    we = np.reshape(np.transpose(i["L0_ffn_We"], (1, 0, 2)), (D, -1))
    arrays["w_l0f"] = side(i["L0_ffn_Wg"], we, rows(i["L0_ffn_bg"]), rows(i["L0_ffn_be"]))
    w_phi = i["L0_attn_weights"]
    phi = np.zeros((L0A_HEADS, L0A_HD, L0A_HEADS, L0A_HD), np.float32)
    for h in range(L0A_HEADS):
        phi[h, :, h, :] = w_phi[h].T
    arrays["w_l0a"] = side(i["L0_attn_Wq"].T, i["L0_attn_Wk"].T, i["L0_attn_Wv"].T, phi.reshape(D, D),
                           rows(i["L0_attn_bv"]), i["L0_attn_bq"][:, None], i["L0_attn_bk"][:, None])

    def chunks(a):
        return np.reshape(np.transpose(np.reshape(a, (-1, P, a.shape[1])), (1, 0, 2)), (P, -1))

    w1 = np.reshape(np.transpose(i["L2_ffn_w1"], (2, 0, 1)), (D, -1))
    w3 = np.reshape(np.transpose(i["L2_ffn_w3"], (2, 0, 1)), (D, -1))
    w2 = np.reshape(np.transpose(i["L2_ffn_w2"], (2, 0, 1)), (P, -1))
    arrays["w_l2f"] = side(i["L2_ffn_gate_w"].T, rows(i["L2_ffn_gate_bias"]), w1, i["L2_ffn_sw1"].T,
                           w3, i["L2_ffn_sw3"].T, w2, chunks(i["L2_ffn_sw2"].T))
    arrays["w_l3f"] = side(i["L3_ffn_w1_w"].T, i["L3_ffn_w2_w"].T, chunks(i["L3_ffn_h1_w"].T), chunks(i["L3_ffn_h2_w"].T),
                           chunks(i["L3_ffn_w3_w"].T), *[i["L3_ffn_" + s][:, None].reshape(L3_C, P).T
                                                         for s in ("w1_s", "w2_s", "h1_s", "h2_s")],
                           rows(i["L3_ffn_w3_s"]))
    arrays["w_l2a"] = side(*[i["L2_attn_" + n].T for n in ("Wq", "Wk", "Wv", "Wo")], rows(i["L2_attn_norm_w"]),
                           rows(i["L2_attn_bv"]), rows(i["L2_attn_bo"]), i["L2_attn_bq"][:, None], i["L2_attn_bk"][:, None])
    down = np.zeros((3 * P, D), np.float32)
    down[:L3A_INNER] = i["L3_attn_wd"]
    arrays["w_l3a"] = side(i["L3_attn_wq"], i["L3_attn_wk"], i["L3_attn_wv"], i["L3_attn_wb"], i["L3_attn_wa"],
                           i["L3_attn_wo"], i["L3_attn_wg"], i["L3_attn_wu"], chunks(down), rows(i["L3_attn_norm1_w"]),
                           rows(i["L3_attn_norm2_w"]), i["L3_attn_conv_w"], i["L3_attn_conv_b"][:, None])
    null_k = i["L1_ffn_null_kv"][0, :, :, 0, :]
    null_kb = np.zeros((L1_G, L1_C, 2, L1_DH, 2), np.float32)
    for a in range(2):
        null_kb[:, :, a, :, a] = null_k[:, a::2, :]
    null_kb = np.reshape(np.transpose(null_kb, (2, 3, 0, 1, 4)), (P, -1))
    w_kv = i["L1_ffn_w_kv"]

    def by_group(a):
        return np.reshape(np.transpose(a, (2, 0, 1)), (D, -1))

    wo = np.reshape(i["L1_ffn_w_out"], (L1_G, D, L1_C, P))
    arrays["w_l1f"] = side(i["L1_ffn_w_qr"].T, i["L1_ffn_w_kvr"].T, by_group(i["L1_ffn_w_q"]),
                           by_group(w_kv[:, :L1_DI]), by_group(w_kv[:, L1_DI:]),
                           np.reshape(np.transpose(wo, (3, 0, 2, 1)), (P, -1)), null_kb, rows(i["L1_ffn_null_token"]))
    arrays["null_v"] = np.ascontiguousarray(np.reshape(i["L1_ffn_null_kv"][1], (L1_G, L1_DI)))

    def by_heads(q, k, v):
        return np.concatenate([np.reshape(a, (a.shape[0], L1A_GROUPS, -1)) for a in (q, k, v)], axis=2)

    arrays["w_l1a_qkv"] = np.ascontiguousarray(by_heads(i["L1_attn_w_q"], i["L1_attn_w_k"], i["L1_attn_w_v"]))
    taps = by_heads(i["L1_attn_conv_q"].T, i["L1_attn_conv_k"].T, i["L1_attn_conv_v"].T)
    arrays["l1a_taps"] = np.ascontiguousarray(np.transpose(taps, (1, 0, 2))).reshape(-1)
    arrays["w_l1a"] = side(i["L1_attn_w_a"], i["L1_attn_w_b"], i["L1_attn_w_g"], chunks(i["L1_attn_w_out"]),
                           rows(i["L1_attn_dt_bias"]), rows(i["L1_attn_A_log"]), i["L1_attn_norm_w"][:, None])
    return arrays


def kernel(**inputs):
    import numpy as np
    import concourse.bacc as bacc
    from concourse.bass_utils import run_bass_kernel_spmd

    nc = bacc.Bacc("TRN2", target_bir_lowering=False, num_devices=1)
    arrays = lay_out({k: np.asarray(v) for k, v in inputs.items()})
    dram = {k: nc.dram_tensor(f"in_{k}", a.shape, mybir.dt.from_np(a.dtype), kind="ExternalInput").ap()
            for k, a in arrays.items()}
    out = nc.dram_tensor("out_x", (TOKENS, D), F32, kind="ExternalOutput").ap()
    build(nc, dram, out)
    r = run_bass_kernel_spmd(nc, [{f"in_{k}": a for k, a in arrays.items()}], core_ids=[0])
    return np.reshape(r.results[0]["out_x"], (BATCH, SEQ, D))
```

```python
from contextlib import ExitStack

import concourse.bass as bass
from concourse import mybir

F32 = mybir.dt.float32
ACT = mybir.ActivationFunctionType
ALU = mybir.AluOpType
AX = mybir.AxisListType

P = 128
D = 128
BATCH = 16
SEQ = 256
TOKENS = BATCH * SEQ
TILES = TOKENS // P
TPB = SEQ // P
LN_EPS = 1e-5
SEMAPHORES = 120
STEPS = tuple(range(12))

CONST_PARTS = [("ident", 128), ("ones", 128), ("iota", 128), ("rev_iota", 128), ("upto", 128),
               ("after", 128), ("blocks8", 128), ("heads8", 16), ("level1n", 128), 
               ("level", 6 * 64), ("row_index", 1), ("is_query", 1), ("quarter", 4), ("minus_half", 8), ("dk_scale", 8),
               ("eps_ln", 1), ("eps_l2", 1), ("causal", 128), ("before8", 64), ("alpha_bias", 1)]
CONST_AT = {}
_at = 0
for _name, _width in CONST_PARTS:
    CONST_AT[_name] = (_at, _width)
    _at += _width
CONST_COLS = _at


class Stage:
    pool = []
    taken = 0

    def __init__(self, nc, name):
        self.nc, self.name, self.ctx, self.first = nc, name, ExitStack(), Stage.taken

    def __enter__(self):
        return self

    def sb(self, name, shape):
        return self.ctx.enter_context(self.nc.sbuf_tensor(f"{self.name}_{name}", shape, F32))

    def ps(self, name, shape):
        return self.ctx.enter_context(self.nc.psum_tensor(f"{self.name}_{name}", shape, F32))

    def sem(self, name):
        Stage.taken += 1
        return Stage.pool[Stage.taken - 1]

    def sems(self, name, n):
        return [self.sem(f"{name}{i}") for i in range(n)]

    def __exit__(self, kind, value, trace):
        if kind is None and Stage.taken > self.first:
            used = [s.num for s in Stage.pool[self.first:Stage.taken]]
            self.nc.all_engine_barrier(sems_to_clear=range(used[0], used[-1] + 1))
            Stage.taken = self.first
        self.ctx.close()


class Globals:

    def __init__(self, nc, ctx, dram, out):
        self.dram, self.out = dram, out
        self.X = ctx.enter_context(nc.sbuf_tensor("X", [P, TILES, D], F32))
        self.const = ctx.enter_context(nc.sbuf_tensor("const", [P, CONST_COLS], F32))
        self.mean = ctx.enter_context(nc.sbuf_tensor("mean", [P, TILES], F32))
        self.rstd = ctx.enter_context(nc.sbuf_tensor("rstd", [P, TILES], F32))

    def c(self, name):
        at, width = CONST_AT[name]
        return self.const[:, at:at + width]

    def tile(self, t):
        return self.X[:, bass.ds(t, 1), :]


def load_stream(nc, g):
    with Stage(nc, "load") as st:
        s_in = st.sem("in")
        with nc.Block() as block:
            @block.sync
            def _(sp):
                sp.dma_start(g.X[:, :, :], g.dram["x"].rearrange("(t p) d -> p t d", p=P)).then_inc(s_in, 16)
                sp.dma_start(g.const[:, :], g.dram["consts"]).then_inc(s_in, 16)
                sp.wait_ge(s_in, 32)


def store_stream(nc, g):
    with Stage(nc, "store") as st:
        s_out = st.sem("out")
        with nc.Block() as block:
            @block.sync
            def _(sp):
                sp.dma_start(g.out.rearrange("(t p) d -> p t d", p=P), g.X[:, :, :]).then_inc(s_out, 16)
                sp.wait_ge(s_out, 16)


def row_statistics(nc, g, name, loads=()):
    with Stage(nc, name + "_stat") as st:
        parts = st.sb("parts", [P, TILES, 6])
        tmp = st.sb("tmp", [P, 3, TILES])
        s_load = st.sem("load")
        s_parts = st.sem("parts")
        s_step = st.sem("step")
        s_var = st.sem("var")
        s_std = st.sem("std")
        with nc.Block() as block:
            @block.sync
            def _(sp):
                for dst, src in loads:
                    sp.dma_start(dst, src).then_inc(s_load, 16)
                if loads:
                    sp.wait_ge(s_load, 16 * len(loads))

            @block.vector
            def _(dve):
                with dve.Fori(0, TILES) as t:
                    nc.vector.bn_stats(parts[:, bass.ds(t, 1), :], g.X[:, bass.ds(t, 1), :]).then_inc(s_parts, 1)
                dve.wait_ge(s_parts, TILES)
                nc.vector.tensor_tensor(g.mean[:, :], parts[:, :, 1], parts[:, :, 4], ALU.add).then_inc(s_step, 1)
                nc.vector.tensor_tensor(tmp[:, 0, :], parts[:, :, 1], parts[:, :, 4], ALU.subtract).then_inc(s_step, 1)
                nc.vector.tensor_tensor(tmp[:, 1, :], parts[:, :, 2], parts[:, :, 5], ALU.add).then_inc(s_step, 1)
                dve.wait_ge(s_step, 3)
                nc.vector.tensor_scalar(g.mean[:, :], g.mean[:, :], 0.5, None, ALU.mult).then_inc(s_step, 1)
                nc.vector.scalar_tensor_tensor(tmp[:, 2, :], tmp[:, 0, :], 0.25, tmp[:, 0, :],
                                               ALU.mult, ALU.mult).then_inc(s_step, 1)
                dve.wait_ge(s_step, 5)
                nc.vector.scalar_tensor_tensor(tmp[:, 0, :], tmp[:, 1, :], 1.0 / D, tmp[:, 2, :],
                                               ALU.mult, ALU.add).then_inc(s_var, 1)
                dve.wait_ge(s_std, 1)
                nc.vector.reciprocal(g.rstd[:, :], tmp[:, 1, :]).then_inc(s_step, 1)

            @block.scalar
            def _(act):
                act.wait_ge(s_var, 1)
                nc.scalar.activation(tmp[:, 1, :], tmp[:, 0, :], ACT.Sqrt, bias=g.c("eps_ln")).then_inc(s_std, 1)


L0_EXPERTS = 8
L0F_PARTS = [("wg", 128), ("we", L0_EXPERTS * 128), ("bg", 128), ("be", L0_EXPERTS * 128)]


def columns(parts):
    at, out = 0, {}
    for name, width in parts:
        out[name] = slice(at, at + width)
        at += width
    return out, at


def l0_ffn(nc, g, name):
    E = L0_EXPERTS
    cols, width = columns(L0F_PARTS)
    NS = 2
    with Stage(nc, name) as st:
        w = st.sb("w", [P, width])
        row_statistics(nc, g, name, [(w[:, :], g.dram["w_l0f"])])
        xn = [st.sb(f"xn{s}", [P, D]) for s in range(NS)]
        xT = [st.sb(f"xT{s}", [P, P]) for s in range(NS)]
        logits = [st.sb(f"logits{s}", [P, D]) for s in range(NS)]
        neg_max = [st.sb(f"neg_max{s}", [P, 1]) for s in range(NS)]
        key = [st.sb(f"key{s}", [P, D]) for s in range(NS)]
        first = [st.sb(f"first{s}", [P, 1]) for s in range(NS)]
        gate = [st.sb(f"gate{s}", [P, E]) for s in range(NS)]
        prob = [st.sb(f"prob{s}", [P, D]) for s in range(NS)]
        total = [st.sb(f"total{s}", [P, 2]) for s in range(NS)]
        acc = [st.sb(f"acc{s}", [P, D]) for s in range(NS)]
        small = [st.ps(f"small{s}", [P, 512]) for s in range(NS)]
        hidden = [st.ps(f"hidden{s}", [P, E * D]) for s in range(NS)]
        xn_ready = st.sems("xn_ready", NS)
        turned = st.sems("turned", NS)
        xT_ready = st.sems("xT_ready", NS)
        logits_ready = st.sems("logits_ready", NS)
        logits_saved = st.sems("logits_saved", NS)
        hidden_ready = st.sems("hidden_ready", NS)
        max_ready = st.sems("max_ready", NS)
        exp_done = st.sems("exp_done", NS)
        gate_step = st.sems("gate_step", NS)
        relu_done = st.sems("relu_done", NS)
        slot_free = st.sems("slot_free", NS)
        mix_step = st.sems("mix_step", NS)
        GATE_STEPS, MIX_STEPS = 5, E + 1

        with nc.Block() as block:
            @block.vector
            def _(dve):
                for s in range(NS):
                    dve.sem_inc(slot_free[s], 1)
                with dve.Fori(0, TILES // NS) as it:
                    for s in range(NS):
                        t = it * NS + s
                        dve.wait_ge(slot_free[s], it + 1)
                        nc.vector.tensor_scalar(xn[s][:, :], g.tile(t), g.mean[:, bass.ds(t, 1)],
                                                g.rstd[:, bass.ds(t, 1)], ALU.subtract, ALU.mult).then_inc(xn_ready[s], 1)
                    for s in range(NS):
                        dve.wait_ge(logits_saved[s], it + 1)
                        nc.vector.tensor_reduce(neg_max[s][:, :], logits[s][:, :], AX.X, ALU.max,
                                                negate=True).then_inc(max_ready[s], 1)
                        nc.vector.tensor_reduce(total[s][:, 1:2], logits[s][:, :], AX.X,
                                                ALU.max).then_inc(gate_step[s], 1)
                    for s in range(NS):
                        dve.wait_ge(gate_step[s], it * GATE_STEPS + 1)
                        nc.vector.scalar_tensor_tensor(key[s][:, :], logits[s][:, :], total[s][:, 1:2],
                                                       g.c("rev_iota"), ALU.is_equal, ALU.mult).then_inc(gate_step[s], 1)
                    for s in range(NS):
                        dve.wait_ge(gate_step[s], it * GATE_STEPS + 2)
                        nc.vector.tensor_reduce(first[s][:, :], key[s][:, :], AX.X, ALU.max).then_inc(gate_step[s], 1)
                    for s in range(NS):
                        dve.wait_ge(gate_step[s], it * GATE_STEPS + 3)
                        nc.vector.tensor_scalar(key[s][:, :], g.c("rev_iota"), first[s][:, :], None,
                                                ALU.is_equal).then_inc(gate_step[s], 1)
                    for s in range(NS):
                        dve.wait_ge(gate_step[s], it * GATE_STEPS + 4)
                        nc.vector.tensor_reduce(gate[s][:, :], key[s][:, :].rearrange("p (k e) -> p e k", e=E),
                                                AX.X, ALU.add).then_inc(gate_step[s], 1)
                    for e in range(E):
                        for s in range(NS):
                            h = hidden[s][:, e * D:(e + 1) * D]
                            if e == 0:
                                dve.wait_ge(gate_step[s], it * GATE_STEPS + 5)
                                dve.wait_ge(hidden_ready[s], it + 1)
                                nc.vector.tensor_scalar(acc[s][:, :], h, gate[s][:, 0:1], None,
                                                        ALU.mult).then_inc(mix_step[s], 1)
                            else:
                                dve.wait_ge(mix_step[s], it * MIX_STEPS + e)
                                nc.vector.scalar_tensor_tensor(acc[s][:, :], h, gate[s][:, e:e + 1], acc[s][:, :],
                                                               ALU.mult, ALU.add).then_inc(mix_step[s], 1)
                    for s in range(NS):
                        dve.wait_ge(exp_done[s], it + 1)
                        nc.vector.reciprocal(total[s][:, 1:2], total[s][:, 0:1]).then_inc(mix_step[s], 1)
                    for s in range(NS):
                        dve.wait_ge(mix_step[s], it * MIX_STEPS + E + 1)
                        nc.vector.tensor_scalar(acc[s][:, :], acc[s][:, :], 0.0, total[s][:, 1:2],
                                                ALU.max, ALU.mult).then_inc(relu_done[s], 1)
                    for s in range(NS):
                        t = it * NS + s
                        dve.wait_ge(relu_done[s], it + 1)
                        nc.vector.scalar_tensor_tensor(g.tile(t), acc[s][:, :], 0.5, g.tile(t),
                                                       ALU.mult, ALU.add).then_inc(slot_free[s], 1)

            @block.tensor
            def _(pe):
                with pe.Fori(0, TILES // NS) as it:
                    for s in range(NS):
                        pe.wait_ge(xn_ready[s], it + 1)
                        nc.tensor.transpose(small[s][:, 0:128], xn[s][:, :], g.c("ident")).then_inc(turned[s], 1)
                    for s in range(NS):
                        pe.wait_ge(xT_ready[s], it + 1)
                        nc.tensor.matmul(small[s][:, 128:256], xT[s][:, :], w[:, cols["wg"]], start=True, stop=False)
                        nc.tensor.matmul(small[s][:, 128:256], g.c("ones")[0:1, :], w[0:1, cols["bg"]],
                                         start=False, stop=True).then_inc(logits_ready[s], 1)
                        for half in range(2):
                            o = hidden[s][:, half * 512:half * 512 + 512]
                            a = half * 512
                            nc.tensor.matmul(o, xT[s][:, :], w[:, cols["we"]][:, a:a + 512], start=True, stop=False)
                            last = nc.tensor.matmul(o, g.c("ones")[0:1, :], w[0:1, cols["be"]][:, a:a + 512],
                                                    start=False, stop=True)
                        last.then_inc(hidden_ready[s], 1)

            @block.scalar
            def _(act):
                with act.Fori(0, TILES // NS) as it:
                    for s in range(NS):
                        act.wait_ge(turned[s], it + 1)
                        nc.scalar.copy(xT[s][:, :], small[s][:, 0:128]).then_inc(xT_ready[s], 1)
                    for s in range(NS):
                        act.wait_ge(logits_ready[s], it + 1)
                        nc.scalar.copy(logits[s][:, :], small[s][:, 128:256]).then_inc(logits_saved[s], 1)
                    for s in range(NS):
                        act.wait_ge(max_ready[s], it + 1)
                        nc.scalar.activation(prob[s][:, :], logits[s][:, :], ACT.Exp, bias=neg_max[s][:, :],
                                             accum_out=total[s][:, 0:1]).then_inc(exp_done[s], 1)


L0A_HEADS, L0A_HD = 16, 8
L0A_PARTS = [("wq", 128), ("wk", 128), ("wv", 128), ("phi", 128), ("bv", 128), ("bq", 1), ("bk", 1)]


def l0_attn(nc, g, name):
    cols, width = columns(L0A_PARTS)
    NS = 2
    N = SEQ
    with Stage(nc, name) as st:
        w = st.sb("w", [P, width])
        QT = st.sb("QT", [P, TOKENS])
        KT = st.sb("KT", [P, TOKENS])
        V = st.sb("V", [P, TILES, D])
        heads_scaled = st.sb("heads_scaled", [P, L0A_HEADS])
        norms = st.sb("norms", [P, 12])
        sums = [st.sb(f"sums{s}", [P, 2]) for s in range(NS)]
        row_statistics(nc, g, name, [(w[:, :], g.dram["w_l0a"])])

        with Stage(nc, name + "_a") as sa:
            xn = [sa.sb(f"xn{s}", [P, TPB, D]) for s in range(NS)]
            xT = [sa.sb(f"xT{s}", [P, N]) for s in range(NS)]
            square = [sa.sb(f"square{s}", [P, 2 * N]) for s in range(NS)]
            sq = [sa.sb(f"sq{s}", [P, 2]) for s in range(NS)]
            turn = [sa.ps(f"turn{s}", [P, 512]) for s in range(NS)]
            qk = [sa.ps(f"qk{s}", [P, 512]) for s in range(NS)]
            vps = [sa.ps(f"vps{s}", [P, 512]) for s in range(NS)]
            slot_free = sa.sems("slot_free", NS)
            sums_clear = sa.sem("sums_clear")
            xn_ready = sa.sems("xn_ready", NS)
            turned = sa.sems("turned", NS)
            xT_ready = sa.sems("xT_ready", NS)
            qk_ready = sa.sems("qk_ready", NS)
            v_ready = sa.sems("v_ready", NS)
            qk_saved = sa.sems("qk_saved", NS)
            v_saved = sa.sems("v_saved", NS)
            with nc.Block() as block:
                @block.vector
                def _(dve):
                    for s in range(NS):
                        nc.vector.memset(sums[s][:, :], 0.0).then_inc(slot_free[s], 1)
                    with dve.Fori(0, BATCH // NS) as it:
                        for s in range(NS):
                            dve.wait_ge(slot_free[s], it + 1)
                            for u in range(TPB):
                                t = (it * NS + s) * TPB + u
                                last = nc.vector.tensor_scalar(xn[s][:, u, :], g.tile(t), g.mean[:, bass.ds(t, 1)],
                                                               g.rstd[:, bass.ds(t, 1)], ALU.subtract, ALU.mult)
                            last.then_inc(xn_ready[s], 1)
                        for s in range(NS):
                            dve.wait_ge(v_ready[s], it + 1)
                            nc.vector.tensor_copy(V[:, bass.ds((it * NS + s) * TPB, TPB), :],
                                                  vps[s][:, 0:TPB * D].rearrange("p (u d) -> p u d", u=TPB)
                                                  ).then_inc(v_saved[s], 1)
                        for s in range(NS):
                            dve.wait_ge(qk_saved[s], it + 1)
                            dve.wait_ge(v_saved[s], it + 1)
                            nc.vector.tensor_tensor(sums[s][:, :], sums[s][:, :], sq[s][:, :],
                                                    ALU.add).then_inc(slot_free[s], 1)

                @block.tensor
                def _(pe):
                    with pe.Fori(0, BATCH // NS) as it:
                        for s in range(NS):
                            pe.wait_ge(xn_ready[s], it + 1)
                            for u in range(TPB):
                                last = nc.tensor.transpose(turn[s][:, u * P:(u + 1) * P], xn[s][:, u, :], g.c("ident"))
                            last.then_inc(turned[s], 1)
                        for s in range(NS):
                            pe.wait_ge(xT_ready[s], it + 1)
                            nc.tensor.matmul(qk[s][:, 0:N], w[:, cols["wq"]], xT[s][:, :], start=True, stop=True)
                            nc.tensor.matmul(qk[s][:, N:2 * N], w[:, cols["wk"]], xT[s][:, :], start=True,
                                             stop=True).then_inc(qk_ready[s], 1)
                            for u in range(TPB):
                                o = vps[s][:, u * D:(u + 1) * D]
                                nc.tensor.matmul(o, xT[s][:, u * P:(u + 1) * P], w[:, cols["wv"]], start=True, stop=False)
                                last = nc.tensor.matmul(o, g.c("ones")[0:1, :], w[0:1, cols["bv"]], start=False, stop=True)
                            last.then_inc(v_ready[s], 1)

                @block.scalar
                def _(act):
                    with act.Fori(0, BATCH // NS) as it:
                        for s in range(NS):
                            act.wait_ge(turned[s], it + 1)
                            nc.scalar.copy(xT[s][:, :], turn[s][:, 0:N]).then_inc(xT_ready[s], 1)
                        for s in range(NS):
                            act.wait_ge(qk_ready[s], it + 1)
                            b = it * NS + s
                            for k, (dst, bias) in enumerate(((QT, "bq"), (KT, "bk"))):
                                src = qk[s][:, k * N:(k + 1) * N]
                                nc.scalar.activation(dst[:, bass.ds(b * N, N)], src, ACT.Identity, bias=w[:, cols[bias]])
                                last = nc.scalar.activation(square[s][:, k * N:(k + 1) * N], src, ACT.Square, bias=w[:, cols[bias]],
                                                            accum_out=sq[s][:, k:k + 1])
                            last.then_inc(qk_saved[s], 1)

        with Stage(nc, name + "_n") as sn:
            total = sn.ps("total", [P, 512])
            step = sn.sem("step")
            summed = sn.sem("summed")
            rooted = sn.sem("rooted")
            scaled = sn.sem("scaled")
            exped = sn.sem("exped")
            with nc.Block() as block:
                @block.vector
                def _(dve):
                    nc.vector.tensor_tensor(norms[:, 0:2], sums[0][:, :], sums[1][:, :], ALU.add).then_inc(step, 1)
                    dve.wait_ge(rooted, 1)
                    nc.vector.reciprocal(norms[:, 4:6], norms[:, 2:4]).then_inc(step, 1)
                    dve.wait_ge(step, 2)
                    nc.vector.tensor_tensor(norms[:, 6:8], total[:, 0:2], norms[:, 4:6], ALU.mult).then_inc(step, 1)
                    dve.wait_ge(step, 3)
                    nc.vector.tensor_tensor(norms[:, 6:8], norms[:, 6:8], norms[:, 4:6], ALU.mult).then_inc(scaled, 1)
                    dve.wait_ge(exped, 1)
                    nc.vector.tensor_scalar(norms[:, 10:11], norms[:, 8:9], norms[:, 9:10], 1.0 / L0A_HD,
                                            ALU.mult, ALU.mult).then_inc(step, 1)
                    dve.wait_ge(step, 4)
                    nc.vector.tensor_scalar(heads_scaled[:, :], g.c("heads8"), norms[:, 10:11], None,
                                            ALU.mult).then_inc(step, 1)

                @block.tensor
                def _(pe):
                    pe.wait_ge(step, 1)
                    nc.tensor.matmul(total[:, 0:2], g.c("ones"), norms[:, 0:2], start=True, stop=True).then_inc(summed, 1)

                @block.scalar
                def _(act):
                    act.wait_ge(summed, 1)
                    nc.scalar.activation(norms[:, 2:4], total[:, 0:2], ACT.Sqrt).then_inc(rooted, 1)
                    act.wait_ge(scaled, 1)
                    nc.scalar.activation(norms[:, 8:10], norms[:, 6:8], ACT.Exp, scale=-0.5).then_inc(exped, 1)

        with Stage(nc, name + "_b") as sb:
            feats = [sb.sb(f"feats{s}", [P, 2 * N]) for s in range(NS)]
            prod = [sb.sb(f"prod{s}", [P, N]) for s in range(NS)]
            sim = [sb.sb(f"sim{s}", [P, TPB * L0A_HEADS]) for s in range(NS)]
            inv = [sb.sb(f"inv{s}", [P, TPB * L0A_HEADS]) for s in range(NS)]
            mix = [sb.sb(f"mix{s}", [P, TPB * D]) for s in range(NS)]
            proj = [sb.ps(f"proj{s}", [P, 512]) for s in range(NS)]
            sim_ps = [sb.ps(f"sim_ps{s}", [P, 512]) for s in range(NS)]
            slot_free = sb.sems("slot_free", NS)
            projected = sb.sems("projected", NS)
            exp_done = sb.sems("exp_done", NS)
            prod_ready = sb.sems("prod_ready", NS)
            sim_ready = sb.sems("sim_ready", NS)
            mix_step = sb.sems("mix_step", NS)
            MIX_STEPS = 4
            with nc.Block() as block:
                @block.tensor
                def _(pe):
                    for s in range(NS):
                        pe.sem_inc(slot_free[s], 1)
                    with pe.Fori(0, BATCH // NS) as it:
                        for s in range(NS):
                            pe.wait_ge(slot_free[s], it + 1)
                            b = it * NS + s
                            nc.tensor.matmul(proj[s][:, 0:N], w[:, cols["phi"]], QT[:, bass.ds(b * N, N)], start=True, stop=True)
                            nc.tensor.matmul(proj[s][:, N:2 * N], w[:, cols["phi"]], KT[:, bass.ds(b * N, N)], start=True,
                                             stop=True).then_inc(projected[s], 1)
                        for s in range(NS):
                            pe.wait_ge(prod_ready[s], it + 1)
                            for u in range(TPB):
                                last = nc.tensor.matmul(sim_ps[s][:, u * L0A_HEADS:(u + 1) * L0A_HEADS],
                                                        prod[s][:, u * P:(u + 1) * P], heads_scaled[:, :], start=True, stop=True)
                            last.then_inc(sim_ready[s], 1)

                @block.scalar
                def _(act):
                    with act.Fori(0, BATCH // NS) as it:
                        for s in range(NS):
                            act.wait_ge(projected[s], it + 1)
                            nc.scalar.activation(feats[s][:, 0:N], proj[s][:, 0:N], ACT.Exp, scale=norms[:, 4:5])
                            nc.scalar.activation(feats[s][:, N:2 * N], proj[s][:, N:2 * N], ACT.Exp,
                                                 scale=norms[:, 5:6]).then_inc(exp_done[s], 1)

                @block.gpsimd
                def _(pool):
                    with pool.Fori(0, BATCH // NS) as it:
                        for s in range(NS):
                            pool.wait_ge(exp_done[s], it + 1)
                            nc.gpsimd.tensor_tensor(prod[s][:, :], feats[s][:, 0:N], feats[s][:, N:2 * N],
                                                    ALU.mult).then_inc(prod_ready[s], 1)

                @block.vector
                def _(dve):
                    with dve.Fori(0, BATCH // NS) as it:
                        for s in range(NS):
                            dve.wait_ge(sim_ready[s], it + 1)
                            nc.vector.tensor_copy(sim[s][:, :], sim_ps[s][:, 0:TPB * L0A_HEADS]).then_inc(mix_step[s], 1)
                        for s in range(NS):
                            t = (it * NS + s) * TPB
                            dve.wait_ge(mix_step[s], it * MIX_STEPS + 1)
                            nc.vector.reciprocal(inv[s][:, :], sim[s][:, :]).then_inc(mix_step[s], 1)
                            nc.vector.tensor_tensor(
                                mix[s][:, :].rearrange("p (h e) -> p h e", e=L0A_HD),
                                V[:, bass.ds(t, TPB), :].rearrange("p u (h e) -> p (u h) e", e=L0A_HD),
                                sim[s][:, :].unsqueeze(2).broadcast_to([P, TPB * L0A_HEADS, L0A_HD]),
                                ALU.mult).then_inc(mix_step[s], 1)
                        for s in range(NS):
                            dve.wait_ge(mix_step[s], it * MIX_STEPS + 3)
                            nc.vector.tensor_tensor(
                                mix[s][:, :].rearrange("p (h e) -> p h e", e=L0A_HD),
                                mix[s][:, :].rearrange("p (h e) -> p h e", e=L0A_HD),
                                inv[s][:, :].unsqueeze(2).broadcast_to([P, TPB * L0A_HEADS, L0A_HD]),
                                ALU.mult).then_inc(mix_step[s], 1)
                        for s in range(NS):
                            t = (it * NS + s) * TPB
                            dve.wait_ge(mix_step[s], it * MIX_STEPS + 4)
                            nc.vector.tensor_tensor(g.X[:, bass.ds(t, TPB), :].rearrange("p u d -> p (u d)"),
                                                    g.X[:, bass.ds(t, TPB), :].rearrange("p u d -> p (u d)"),
                                                    mix[s][:, :], ALU.add).then_inc(slot_free[s], 1)


L1_G, L1_NQ, L1_NK, L1_H, L1_DH = 4, 128, 64, 8, 64
L1_DI = L1_H * L1_DH
L1_C = L1_DI // P
L1F_PARTS = [("route", 2 * L1_G), ("wq", L1_G * L1_DI), ("wk", L1_G * L1_DI), ("wv", L1_G * L1_DI),
             ("wo", L1_G * L1_C * D), ("null_k", L1_G * L1_C), ("null_token", D)]
LOWEST = -3.4028235e38


def l1_ffn(nc, g, name):
    G, NQ, NK, H, DH, C = L1_G, L1_NQ, L1_NK, L1_H, L1_DH, L1_C
    cols, width = columns(L1F_PARTS)
    N = SEQ
    NS = 2
    USES = G // NS
    ROWS = 2 * G
    with Stage(nc, name) as st:
        w = st.sb("w", [P, width])
        row_statistics(nc, g, name, [(w[:, :], g.dram["w_l1f"])])
        logits_d = nc.dram_tensor(name + "_logits", (BATCH, ROWS, N), F32, kind="Internal").ap()
        place_d = nc.dram_tensor(name + "_place", (P, N), F32, kind="Internal").ap()
        placeT = st.sb("placeT", [P, TPB, P])
        scoreT = st.sb("scoreT", [P, TPB, P])
        mean_by = st.sb("mean_by", [P, TPB, BATCH])
        unpicked = st.sb("unpicked", [P, TPB, BATCH])

        with Stage(nc, name + "_l") as sl:
            XT = sl.sb("XT", [P, TOKENS])
            row = sl.sb("row", [ROWS, TOKENS])
            turn_stream(nc, g, name, XT)
            bank = [sl.ps(f"bank{s}", [P, 512]) for s in range(4)]
            slot_free = sl.sems("slot_free", 4)
            ready = sl.sems("ready", 4)
            stored = sl.sem("stored")
            with nc.Block() as block:
                @block.tensor
                def _(pe):
                    for s in range(4):
                        pe.sem_inc(slot_free[s], 1)
                    with pe.Fori(0, TOKENS // 512 // 4) as it:
                        for s in range(4):
                            pe.wait_ge(slot_free[s], it + 1)
                            nc.tensor.matmul(bank[s][0:ROWS, :], w[:, cols["route"]], XT[:, bass.ds((it * 4 + s) * 512, 512)],
                                             start=True, stop=True).then_inc(ready[s], 1)

                @block.scalar
                def _(act):
                    with act.Fori(0, TOKENS // 512 // 4) as it:
                        for s in range(4):
                            act.wait_ge(ready[s], it + 1)
                            nc.scalar.copy(row[:, bass.ds((it * 4 + s) * 512, 512)], bank[s][0:ROWS, :]).then_inc(slot_free[s], 1)

                @block.sync
                def _(sp):
                    for s in range(4):
                        sp.wait_ge(slot_free[s], TOKENS // 512 // 4 + 1)
                    sp.dma_start(logits_d.rearrange("b k t -> k b t"), row[:, :].rearrange("k (b t) -> k b t", b=BATCH)
                                 ).then_inc(stored, 16)
                    sp.wait_ge(stored, 16)

        with Stage(nc, name + "_t") as sk:
            logit = sk.sb("logit", [P, N])
            left = [sk.sb(f"left{i}", [P, N]) for i in range(2)]
            top8 = sk.sb("top8", [P, 8])
            mark64 = sk.sb("mark64", [P, N])
            mark = sk.sb("mark", [P, N])
            count = sk.sb("count", [P, N])
            place = sk.sb("place", [P, N])
            score = sk.sb("score", [P, N])
            picks = sk.sb("picks", [P, TPB, P])
            num = sk.sb("num", [P, TPB, BATCH])
            turn = sk.ps("turn", [P, 512])
            loaded = sk.sem("loaded")
            pick = sk.sem("pick")
            step = sk.sem("step")
            placed = sk.sem("placed")
            scored = sk.sem("scored")
            turned = sk.sem("turned")
            stored = sk.sem("stored")
            with nc.Block() as block:
                @block.sync
                def _(sp):
                    sp.dma_start(logit[:, :], logits_d.rearrange("b k t -> (b k) t")).then_inc(loaded, 16)
                    sp.wait_ge(placed, 1)
                    sp.dma_start(place_d, place[:, :]).then_inc(stored, 16)
                    sp.wait_ge(stored, 16)

                @block.scalar
                def _(act):
                    act.wait_ge(loaded, 16)
                    nc.scalar.activation(score[:, :], logit[:, :], ACT.Sigmoid).then_inc(scored, 1)

                @block.vector
                def _(dve):
                    dve.wait_ge(loaded, 16)
                    done = 0
                    src = logit
                    for r in range(NQ // 8):
                        if done:
                            dve.wait_ge(pick, done)
                        nc.vector.max(top8[:, :], src[:, :]).then_inc(pick, 1)
                        dve.wait_ge(pick, done + 1)
                        dst = left[r % 2]
                        nc.vector.match_replace(dst[:, :], top8[:, :], src[:, :], LOWEST).then_inc(pick, 1)
                        done += 2
                        src = dst
                        if r == NK // 8 - 1:
                            dve.wait_ge(pick, done)
                            nc.vector.tensor_scalar(mark64[:, :], src[:, :], LOWEST, None, ALU.is_equal).then_inc(pick, 1)
                            done += 1
                    dve.wait_ge(pick, done)
                    nc.vector.tensor_scalar(count[:, :], src[:, :], LOWEST, None, ALU.is_equal).then_inc(step, 1)
                    dve.wait_ge(step, 1)
                    nc.vector.scalar_tensor_tensor(mark[:, :], count[:, :], g.c("is_query"), mark64[:, :], ALU.mult,
                                                   ALU.max).then_inc(step, 1)
                    dve.wait_ge(step, 2)
                    nc.vector.memset(mark64[:, :], 1.0).then_inc(step, 1)
                    dve.wait_ge(step, 3)
                    nc.vector.tensor_tensor_scan(count[:, :], mark64[:, :], mark[:, :], 0.0, ALU.mult, ALU.add).then_inc(step, 1)
                    dve.wait_ge(step, 4)
                    nc.vector.tensor_tensor(place[:, :], count[:, :], mark[:, :], ALU.mult).then_inc(step, 1)
                    dve.wait_ge(step, 5)
                    nc.vector.tensor_scalar(place[:, :], place[:, :], 1.0, None, ALU.subtract).then_inc(placed, 1)
                    dve.wait_ge(turned, 1)
                    nc.vector.tensor_copy(placeT[:, :, :], turn[:, 0:2 * P].rearrange("p (u r) -> p u r", u=TPB)).then_inc(step, 1)
                    nc.vector.tensor_copy(scoreT[:, :, :], turn[:, 2 * P:4 * P].rearrange("p (u r) -> p u r", u=TPB)).then_inc(step, 1)
                    dve.wait_ge(step, 7)
                    nc.vector.tensor_scalar(picks[:, :, :], placeT[:, :, :], 0.0, None, ALU.is_ge).then_inc(step, 1)
                    dve.wait_ge(step, 8)
                    nc.vector.tensor_reduce(num[:, :, :], picks[:, :, :].rearrange("p u (b r) -> p u b r", r=ROWS)[:, :, :, 0:G],
                                            AX.X, ALU.add).then_inc(step, 1)
                    dve.wait_ge(step, 9)
                    nc.vector.tensor_scalar(unpicked[:, :, :], num[:, :, :], 0.0, 0.5, ALU.is_equal, ALU.mult).then_inc(step, 1)
                    nc.vector.tensor_scalar(mean_by[:, :, :], num[:, :, :], 1e-5, None, ALU.max).then_inc(step, 1)
                    dve.wait_ge(step, 11)
                    nc.vector.reciprocal(mean_by[:, :, :], mean_by[:, :, :]).then_inc(step, 1)
                    dve.wait_ge(step, 12)
                    nc.vector.tensor_scalar(mean_by[:, :, :], mean_by[:, :, :], 0.5, None, ALU.mult).then_inc(step, 1)

                @block.tensor
                def _(pe):
                    pe.wait_ge(placed, 1)
                    pe.wait_ge(scored, 1)
                    for i, a in enumerate((place, score)):
                        for u in range(TPB):
                            last = nc.tensor.transpose(turn[:, (2 * i + u) * P:(2 * i + u + 1) * P], a[:, u * P:(u + 1) * P],
                                                       g.c("ident"))
                    last.then_inc(turned, 1)

        with Stage(nc, name + "_a") as sa:
            wq, wk, wv = (w[:, cols[n]].rearrange("p (g e) -> p g e", g=G) for n in ("wq", "wk", "wv"))
            wo = w[:, cols["wo"]].rearrange("p (g c d) -> p g c d", g=G, c=C)
            null_k = w[:, cols["null_k"]].rearrange("p (g c) -> p g c", g=G)
            xn = sa.sb("xn", [P, TPB, D])
            hot = sa.sb("hot", [P, TPB, G, NQ + NK])
            places = sa.sb("places", [P, G * N])
            hotT = sa.sb("hotT", [P, G, N])
            kT = [sa.sb(f"kT{k}", [P, C, NK + 1]) for k in range(G)]
            v = [sa.sb(f"v{k}", [NK + 1, L1_DI]) for k in range(G)]
            sg = [sa.sb(f"sg{k}", [P, 2]) for k in range(G)]
            xg = [sa.sb(f"xg{s}", [P, NQ + NK]) for s in range(NS)]
            qT = [sa.sb(f"qT{s}", [P, C, NQ]) for s in range(NS)]
            top = [sa.sb(f"top{s}", [P, 2, C]) for s in range(NS)]
            prob = [sa.sb(f"prob{s}", [P, 2, C, NK + 1]) for s in range(NS)]
            den = [sa.sb(f"den{s}", [P, 2, C]) for s in range(NS)]
            probT = [sa.sb(f"probT{s}", [NK + 1, 2, C, NQ]) for s in range(NS)]
            oT = [sa.sb(f"oT{s}", [P, C, NQ]) for s in range(NS)]
            o = [sa.sb(f"o{s}", [P, D]) for s in range(NS)]
            bank_x = sa.ps("bank_x", [P, 512])
            bank_q = sa.ps("bank_q", [P, 512])
            bank_v = sa.ps("bank_v", [P, 512])
            bank_s = [sa.ps(f"bank_s{a}", [P, 512]) for a in range(2)]
            bank_p = [sa.ps(f"bank_p{a}", [P, 512]) for a in range(2)]
            bank_o = sa.ps("bank_o", [P, 512])
            null_loaded = sa.sem("null_loaded")
            null_k_ready = sa.sem("null_k_ready")
            places_loaded = sa.sem("places_loaded")
            hotT_ready = sa.sem("hotT_ready")
            xn_ready = sa.sem("xn_ready")
            hot_ready = sa.sem("hot_ready")
            null_added = sa.sem("null_added")
            added = sa.sem("added")
            gathered = sa.sems("gathered", NS)
            xg_saved = sa.sems("xg_saved", NS)
            q_ready = sa.sems("q_ready", NS)
            k_ready = sa.sems("k_ready", NS)
            v_ready = sa.sems("v_ready", NS)
            q_saved = sa.sems("q_saved", NS)
            k_saved = sa.sems("k_saved", NS)
            v_saved = sa.sems("v_saved", NS)
            s_ready = sa.sems("s_ready", NS)
            top_step = sa.sems("top_step", NS)
            shifted = sa.sems("shifted", NS)
            exp_done = sa.sems("exp_done", NS)
            den_step = sa.sems("den_step", NS)
            normed = sa.sems("normed", NS)
            pT_ready = sa.sems("pT_ready", NS)
            pT_saved = sa.sems("pT_saved", NS)
            pv_ready = sa.sems("pv_ready", NS)
            oT_saved = sa.sems("oT_saved", NS)
            o_ready = sa.sems("o_ready", NS)
            o_saved = sa.sems("o_saved", NS)
            back_ready = sa.sems("back_ready", NS)

            def use(unit):
                return unit[0] * USES + unit[1] // NS + 1

            last_batch = BATCH - 1

            def run(engine, step):
                step((0, 0), None, None)
                step((0, 1), (0, 0), None)
                with engine.Fori(0, BATCH - 1) as it:
                    step((it, 2), (it, 1), (it, 0))
                    step((it, 3), (it, 2), (it, 1))
                    step((it + 1, 0), (it, 3), (it, 2))
                    step((it + 1, 1), (it + 1, 0), (it, 3))
                step((last_batch, 2), (last_batch, 1), (last_batch, 0))
                step((last_batch, 3), (last_batch, 2), (last_batch, 1))
                step(None, (last_batch, 3), (last_batch, 2))
                step(None, None, (last_batch, 3))

            with nc.Block() as block:
                @block.sync
                def _(sp):
                    for k in range(G):
                        sp.dma_start(v[k][NK:NK + 1, :], g.dram["null_v"][k:k + 1, :]).then_inc(null_loaded, 16)

                    def load_places(it):
                        sp.dma_start(places[:, :], place_d[bass.ds(it * ROWS, G), :].rearrange("r t -> (r t)").partition_broadcast(P)
                                     ).then_inc(places_loaded, 16)

                    load_places(0)
                    with sp.Fori(1, BATCH) as it:
                        sp.wait_ge(hotT_ready, it)
                        load_places(it)

                @block.gpsimd
                def _(pool):
                    def step(front, soft, back):
                        if soft is not None:
                            s = soft[1] % NS
                            pool.wait_ge(den_step[s], use(soft) * 2)
                            nc.gpsimd.tensor_tensor(prob[s][:, :, :, :].rearrange("p a c k -> p (a c) k"),
                                                    prob[s][:, :, :, :].rearrange("p a c k -> p (a c) k"),
                                                    den[s][:, :, :].rearrange("p a c -> p (a c)").unsqueeze(2)
                                                    .broadcast_to([P, H, NK + 1]), ALU.mult).then_inc(normed[s], 1)

                    run(pool, step)

                @block.vector
                def _(dve):
                    def norm_tokens(it):
                        for u in range(TPB):
                            t = it * TPB + u
                            last = nc.vector.tensor_scalar(xn[:, u, :], g.tile(t), g.mean[:, bass.ds(t, 1)],
                                                           g.rstd[:, bass.ds(t, 1)], ALU.subtract, ALU.mult)
                        last.then_inc(xn_ready, 1)

                    def make_hot(it, k):
                        for u in range(TPB):
                            for at, n, r in ((0, NQ, 0), (NQ, NK, G)):
                                last = nc.vector.tensor_scalar(hot[:, u, k, at:at + n], g.c("iota")[:, 0:n],
                                                               placeT[:, u, bass.ds(it * ROWS + r + k, 1)], None, ALU.is_equal)
                        last.then_inc(hot_ready, 1)

                    def hotT_and_null(it):
                        dve.wait_ge(places_loaded, it * 16 + 16)
                        nc.vector.tensor_scalar(hotT[:, :, :].rearrange("p g t -> p (g t)"), places[:, :], g.c("row_index"), None,
                                                ALU.is_equal).then_inc(hotT_ready, 1)
                        dve.wait_ge(xn_ready, it + 1)
                        for u in range(TPB):
                            t = it * TPB + u
                            x = g.tile(t).rearrange("p t d -> p (t d)")
                            last = nc.vector.scalar_tensor_tensor(x, w[:, cols["null_token"]], unpicked[:, u, bass.ds(it, 1)], x,
                                                                  ALU.mult, ALU.add)
                        last.then_inc(null_added, 1)

                    def step(front, soft, back):
                        if soft is not None:
                            s, n = soft[1] % NS, use(soft)
                            dve.wait_ge(s_ready[s], n)
                            for a in range(2):
                                nc.vector.tensor_reduce(top[s][:, a, :], bank_s[a][:, 0:C * (NK + 1)].rearrange("p (c k) -> p c k", c=C),
                                                        AX.X, ALU.max).then_inc(top_step[s], 1)
                            dve.wait_ge(top_step[s], n * 2)
                            for a in range(2):
                                last = nc.vector.tensor_tensor(prob[s][:, a, :, :],
                                                               bank_s[a][:, 0:C * (NK + 1)].rearrange("p (c k) -> p c k", c=C),
                                                               top[s][:, a, :].unsqueeze(2).broadcast_to([P, C, NK + 1]), ALU.subtract)
                            last.then_inc(shifted[s], 1)
                        if front is not None:
                            s, n, k = front[1] % NS, use(front), front[1]
                            ends = k >= 2 and front[0] is not last_batch
                            if ends:
                                dve.wait_ge(gathered[s], n)
                                if k == G - 1:
                                    norm_tokens(front[0] + 1)
                            dve.wait_ge(k_ready[s], n)
                            nc.vector.tensor_copy(kT[k][:, :, 0:NK], bank_x[:, 192:448].rearrange("p (c k) -> p c k", c=C)
                                                  ).then_inc(k_saved[s], 1)
                        if soft is not None:
                            s, n = soft[1] % NS, use(soft)
                            dve.wait_ge(exp_done[s], n)
                            nc.vector.tensor_reduce(den[s][:, :, :], prob[s][:, :, :, :], AX.X, ALU.add).then_inc(den_step[s], 1)
                            dve.wait_ge(den_step[s], n * 2 - 1)
                            nc.vector.reciprocal(den[s][:, :, :], den[s][:, :, :]).then_inc(den_step[s], 1)
                        if front is not None:
                            s, n, k = front[1] % NS, use(front), front[1]
                            dve.wait_ge(v_ready[s], n)
                            dve.wait_ge(xg_saved[s], n)
                            nc.vector.tensor_scalar(v[k][0:NK, :], bank_v[0:NK, :], sg[k][0:NK, 1:2], None,
                                                    ALU.mult).then_inc(v_saved[s], 1)
                        if back is not None:
                            (it, k), s, n = back, back[1] % NS, use(back)
                            dve.wait_ge(o_ready[s], n)
                            nc.vector.tensor_scalar(o[s][:, :], bank_p[0][:, 0:D], sg[k][:, 0:1], None, ALU.mult).then_inc(o_saved[s], 1)
                            dve.wait_ge(back_ready[s], n)
                            if k == 0:
                                dve.wait_ge(null_added, it + 1)
                            else:
                                dve.wait_ge(added, it * G + k)
                            for u in range(TPB):
                                x = g.tile(it * TPB + u).rearrange("p t d -> p (t d)")
                                last = nc.vector.scalar_tensor_tensor(x, bank_o[:, u * D:(u + 1) * D],
                                                                      mean_by[:, u, bass.ds(it, 1)], x, ALU.mult, ALU.add)
                            last.then_inc(added, 1)
                        if front is not None and ends:
                            for k in (0, 1) if front[1] == 2 else (2, 3):
                                make_hot(front[0] + 1, k)
                        if front is not None and front[1] == 1:
                            hotT_and_null(front[0])
                    for k in range(G):
                        nc.vector.tensor_copy(kT[k][:, :, NK], null_k[:, k, :]).then_inc(null_k_ready, 1)
                    norm_tokens(0)
                    for k in range(G):
                        make_hot(0, k)
                    run(dve, step)

                @block.scalar
                def _(act):
                    def step(front, soft, back):
                        if front is not None:
                            s, k = front[1] % NS, front[1]
                            act.wait_ge(gathered[s], use(front))
                            nc.scalar.copy(xg[s][:, :], bank_x[:, 0:192])
                            nc.scalar.copy(sg[k][:, 0:1], bank_x[:, 448:449])
                            nc.scalar.copy(sg[k][0:NK, 1:2], bank_x[0:NK, 449:450]).then_inc(xg_saved[s], 1)
                        if back is not None:
                            s = back[1] % NS
                            act.wait_ge(pT_ready[s], use(back))
                            for a in range(2):
                                nc.scalar.copy(probT[s][:, a, :, :], bank_p[a][0:NK + 1, :].rearrange("p (c q) -> p c q", c=C)
                                               ).then_inc(pT_saved[s], 1)
                        if soft is not None:
                            s = soft[1] % NS
                            act.wait_ge(shifted[s], use(soft))
                            nc.scalar.activation(prob[s][:, :, :, :], prob[s][:, :, :, :], ACT.Exp).then_inc(exp_done[s], 1)
                        if front is not None:
                            s = front[1] % NS
                            act.wait_ge(q_ready[s], use(front))
                            nc.scalar.mul(qT[s][:, :, :], bank_q[:, :].rearrange("p (c q) -> p c q", c=C),
                                          float(DH) ** -0.5).then_inc(q_saved[s], 1)
                        if back is not None:
                            s = back[1] % NS
                            act.wait_ge(pv_ready[s], use(back))
                            nc.scalar.copy(oT[s][:, :, :], bank_o[:, :].rearrange("p (c q) -> p c q", c=C)).then_inc(oT_saved[s], 1)

                    run(act, step)

                @block.tensor
                def _(pe):
                    def gather(unit):
                        (it, k), s = unit, unit[1] % NS
                        if k == 0:
                            pe.wait_ge(xn_ready, it + 1)
                        pe.wait_ge(hot_ready, it * G + k + 1)
                        for u in range(TPB):
                            nc.tensor.matmul(bank_x[:, 0:192], xn[:, u, :], hot[:, u, k, :], start=(u == 0), stop=(u == 1))
                        for u in range(TPB):
                            nc.tensor.matmul(bank_x[:, 448:449], hot[:, u, k, 0:NQ],
                                             scoreT[:, u, bass.ds(it * ROWS + k, 1)], start=(u == 0), stop=(u == 1))
                        for u in range(TPB):
                            last = nc.tensor.matmul(bank_x[0:NK, 449:450], hot[:, u, k, NQ:NQ + NK],
                                                    scoreT[:, u, bass.ds(it * ROWS + G + k, 1)], start=(u == 0), stop=(u == 1))
                        last.then_inc(gathered[s], 1)

                    def turn_probs(unit):
                        s = unit[1] % NS
                        pe.wait_ge(normed[s], use(unit))
                        for a in range(2):
                            for c in range(C):
                                last = nc.tensor.transpose(bank_p[a][0:NK + 1, c * NQ:(c + 1) * NQ], prob[s][:, a, c, :], g.c("ident"))
                        last.then_inc(pT_ready[s], 1)

                    def project_qk(unit):
                        s, k = unit[1] % NS, unit[1]
                        pe.wait_ge(xg_saved[s], use(unit))
                        for c in range(C):
                            last = nc.tensor.matmul(bank_x[:, 192 + c * NK:192 + (c + 1) * NK], wk[:, k, c * P:(c + 1) * P],
                                                    xg[s][:, NQ:NQ + NK], start=True, stop=True)
                        last.then_inc(k_ready[s], 1)
                        for c in range(C):
                            last = nc.tensor.matmul(bank_q[:, c * NQ:(c + 1) * NQ], wq[:, k, c * P:(c + 1) * P],
                                                    xg[s][:, 0:NQ], start=True, stop=True)
                        last.then_inc(q_ready[s], 1)

                    def project_v(unit, before):
                        s, k = unit[1] % NS, unit[1]
                        if before is not None:
                            pe.wait_ge(v_saved[before[1] % NS], use(before))
                        nc.tensor.matmul(bank_v[0:NK, :], xg[s][:, NQ:NQ + NK], wv[:, k, :], start=True,
                                         stop=True).then_inc(v_ready[s], 1)

                    def values(unit):
                        (it, k), s = unit, unit[1] % NS
                        pe.wait_ge(v_saved[s], use(unit))
                        pe.wait_ge(pT_saved[s], use(unit) * 2)
                        if not (isinstance(it, int) and it == 0 and k == 0):
                            pe.wait_ge(added, it * G + k)
                        for c in range(C):
                            for a in range(2):
                                h = 2 * c + a
                                last = nc.tensor.matmul(bank_o[64 * a:64 * a + 64, c * NQ:(c + 1) * NQ],
                                                        v[k][:, h * DH:(h + 1) * DH], probT[s][:, a, c, :],
                                                        start=True, stop=True)
                        last.then_inc(pv_ready[s], 1)

                    def project_out(unit):
                        s, k = unit[1] % NS, unit[1]
                        pe.wait_ge(oT_saved[s], use(unit))
                        for c in range(C):
                            last = nc.tensor.matmul(bank_p[0][:, 0:D], oT[s][:, c, :], wo[:, k, c, :], start=(c == 0),
                                                    stop=(c == C - 1))
                        last.then_inc(o_ready[s], 1)

                    def scores(unit, before):
                        s, k = unit[1] % NS, unit[1]
                        pe.wait_ge(q_saved[s], use(unit))
                        pe.wait_ge(k_saved[s], use(unit))
                        if before is not None:
                            pe.wait_ge(shifted[before[1] % NS], use(before))
                        for c in range(C):
                            for a in range(2):
                                r = slice(64 * a, 64 * a + 64)
                                last = nc.tensor.matmul(bank_s[a][:, c * (NK + 1):(c + 1) * (NK + 1)], qT[s][r, c, :], kT[k][r, c, :],
                                                        start=True, stop=True)
                        last.then_inc(s_ready[s], 1)

                    def scatter(unit):
                        (it, k), s = unit, unit[1] % NS
                        pe.wait_ge(o_saved[s], use(unit))
                        if k == 0:
                            pe.wait_ge(hotT_ready, it + 1)
                        for u in range(TPB):
                            last = nc.tensor.matmul(bank_o[:, u * D:(u + 1) * D], hotT[:, k, u * P:(u + 1) * P], o[s][:, :],
                                                    start=True, stop=True)
                        last.then_inc(back_ready[s], 1)

                    def step(front, soft, back):
                        if front is not None:
                            gather(front)
                        if back is not None:
                            turn_probs(back)
                        if front is not None:
                            project_qk(front)
                        if back is not None:
                            values(back)
                        if front is not None:
                            project_v(front, soft)
                        if back is not None:
                            project_out(back)
                        if front is not None:
                            scores(front, soft)
                        if back is not None:
                            scatter(back)

                    pe.wait_ge(null_loaded, 16 * G)
                    pe.wait_ge(null_k_ready, G)
                    run(pe, step)

L1A_H, L1A_DK, L1A_DV, L1A_TAPS = 16, 64, 128, 4
L1A_HG = 4
L1A_GROUPS = L1A_H // L1A_HG
GROUP_BITS = L1A_GROUPS.bit_length() - 1
L1A_W = 2 * L1A_HG * L1A_DK + L1A_HG * L1A_DV
L1A_PARTS = [("wab", 2 * L1A_H), ("wgate", L1A_H * L1A_DV), ("wo", L1A_H * D), ("dt_bias", L1A_H), ("a_log", L1A_H),
             ("norm", 1)]
LEVELS = 6
HALF = P // 2


def l1_attn(nc, g, name):
    H, HG, DK, DV, NG = L1A_H, L1A_HG, L1A_DK, L1A_DV, L1A_GROUPS
    cols, width = columns(L1A_PARTS)
    N = SEQ
    PAD = L1A_TAPS - 1
    W2 = 2 * HG * DK
    with Stage(nc, name) as st:
        w = st.sb("w", [P, width])
        XT = st.sb("XT", [P, TOKENS])
        folded = st.sb("folded", [P, NG, L1A_TAPS, L1A_W])
        beta = st.sb("beta", [P, TILES, H])
        decay = st.sb("decay", [P, TILES, H])
        grown = st.sb("grown", [P, TILES, H])

        with Stage(nc, name + "_p") as sp_:
            raw = sp_.sb("raw", [P, NG, L1A_W])
            ab = sp_.sb("ab", [P, TILES, 2 * H])
            z = sp_.sb("z", [P, TILES, H])
            away = sp_.sb("away", [P, TILES, H])
            rate = sp_.sb("rate", [P, H])
            row_statistics(nc, g, name, [(w[:, :], g.dram["w_l1a"]), (raw[:, :, :], g.dram["w_l1a_qkv"]),
                                         (folded[:, :, :, :].rearrange("p a b c -> p (a b c)"),
                                          g.dram["l1a_taps"].partition_broadcast(P))])
            turn_stream(nc, g, name, XT, w[:, cols["wab"]], ab[:, :, :])
            sums = sp_.ps("sums", [P, 512])
            step = sp_.sem("step")
            z_ready = sp_.sem("z_ready")
            away_ready = sp_.sem("away_ready")
            act_step = sp_.sem("act_step")
            decay_ready = sp_.sem("decay_ready")
            summed = sp_.sem("summed")

            def each(a):
                return a.unsqueeze(1).broadcast_to([P, TILES, H])

            with nc.Block() as block:
                @block.vector
                def _(dve):
                    nc.vector.tensor_tensor(z[:, :, :], ab[:, :, 0:H], each(w[:, cols["dt_bias"]]), ALU.add).then_inc(z_ready, 1)
                    dve.wait_ge(z_ready, 1)
                    nc.vector.scalar_tensor_tensor(away[:, :, :], z[:, :, :], -1.0, z[:, :, :], ALU.mult, ALU.max).then_inc(away_ready, 1)
                    for gi in range(NG):
                        for j in range(L1A_TAPS):
                            last = nc.vector.scalar_tensor_tensor(folded[:, gi, j, :], raw[:, gi, :], 0.5, folded[:, gi, j, :],
                                                                  ALU.mult, ALU.mult)
                    nc.vector.tensor_scalar(w[:, cols["wo"]], w[:, cols["wo"]], w[:, cols["norm"]], 0.5, ALU.mult,
                                            ALU.mult).then_inc(step, 1)
                    dve.wait_ge(act_step, 4)
                    nc.vector.scalar_tensor_tensor(z[:, :, :], z[:, :, :], 0.0, away[:, :, :], ALU.max, ALU.add).then_inc(step, 1)
                    dve.wait_ge(step, 2)
                    nc.vector.scalar_tensor_tensor(decay[:, :, :], z[:, :, :], -1.0, each(rate[:, :]), ALU.mult,
                                                   ALU.mult).then_inc(decay_ready, 1)
                    nc.vector.tensor_scalar(beta[:, :, :], beta[:, :, :], 2.0, None, ALU.mult).then_inc(step, 1)

                @block.scalar
                def _(act):
                    act.wait_ge(away_ready, 1)
                    nc.scalar.activation(beta[:, :, :], ab[:, :, H:2 * H], ACT.Sigmoid).then_inc(act_step, 1)
                    nc.scalar.activation(rate[:, :], w[:, cols["a_log"]], ACT.Exp).then_inc(act_step, 1)
                    nc.scalar.activation(away[:, :, :], away[:, :, :], ACT.Exp, scale=-1.0).then_inc(act_step, 1)
                    act.wait_ge(act_step, 3)
                    nc.scalar.activation(away[:, :, :], away[:, :, :], ACT.Ln, bias=g.c("ones")[:, 0:1]).then_inc(act_step, 1)
                    act.wait_ge(summed, 1)
                    nc.scalar.activation(grown[:, :, :].rearrange("p t h -> p (t h)"), sums[:, :], ACT.Exp).then_inc(act_step, 1)

                @block.tensor
                def _(pe):
                    pe.wait_ge(decay_ready, 1)
                    nc.tensor.matmul(sums[:, :], g.c("upto"), decay[:, :, :].rearrange("p t h -> p (t h)"), start=True,
                                     stop=True).then_inc(summed, 1)

        with Stage(nc, name + "_m") as sm:
            U = range(TPB)
            UNITS = BATCH * NG
            wgate = w[:, cols["wgate"]].rearrange("p (a n) -> p a n", a=NG)
            wo = w[:, cols["wo"]].rearrange("p (h d) -> p h d", h=H)
            xpad = [sm.sb(f"xpad{u}", [P, PAD + P]) for u in U]
            t0 = [sm.sb(f"t0{u}", [P, HG, P]) for u in U]
            t1 = [sm.sb(f"t1{u}", [P, HG, P]) for u in U]
            t2 = [sm.sb(f"t2{u}", [P, HG, P]) for u in U]
            qk = [sm.sb(f"qk{u}", [P, 2 * HG, DK]) for u in U]
            rhs = [sm.sb(f"rhs{u}", [P, HG, DV]) for u in U]
            gate = [sm.sb(f"gate{u}", [P, HG, DV]) for u in U]
            length = [sm.sb(f"length{u}", [P, 2 * HG]) for u in U]
            qkT = [sm.sb(f"qkT{u}", [P, 4, P]) for u in U]
            terms = [sm.sb(f"terms{u}", [P, HG, P]) for u in U]
            fade = [sm.sb(f"fade{u}", [P, HG, P]) for u in U]
            NT = [sm.sb(f"NT{u}", [P, HG, P]) for u in U]
            mixT = [sm.sb(f"mixT{u}", [P, HG, P]) for u in U]
            W = [sm.sb(f"W{u}", [P, HG, HALF]) for u in U]
            X = [sm.sb(f"X{u}", [P, HG, P]) for u in U]
            Y = [sm.sb(f"Y{u}", [P, HG, P]) for u in U]
            kfade = sm.sb("kfade", [P, HG, DK])
            state = sm.sb("state", [P, 2, DV])
            read_k = sm.sb("read_k", [P, HG, DV])
            read_q = sm.sb("read_q", [P, HG, DV])
            ms = [sm.sb(f"ms{u}", [P, HG]) for u in U]
            bank = [[sm.ps(f"bank{u}_{i}", [P, 512]) for i in range(4)] for u in U]
            pad_clear = sm.sem("pad_clear")
            xpad_ready = sm.sems("xpad_ready", TPB)
            qk_projected = sm.sems("qk_projected", TPB)
            v_projected = sm.sems("v_projected", TPB)
            gate_projected = sm.sems("gate_projected", TPB)
            qk_tanh = sm.sems("qk_tanh", TPB)
            v_tanh = sm.sems("v_tanh", TPB)
            gate_tanh = sm.sems("gate_tanh", TPB)
            qk_silu = sm.sems("qk_silu", TPB)
            v_silu = sm.sems("v_silu", TPB)
            gate_silu = sm.sems("gate_silu", TPB)
            squared = sm.sems("squared", TPB)
            length_step = sm.sems("length_step", TPB)
            length_ready = sm.sems("length_ready", TPB)
            unit = sm.sems("unit", TPB)
            qk_turned = sm.sems("qk_turned", TPB)
            qkT_saved = sm.sems("qkT_saved", TPB)
            terms_ready = sm.sems("terms_ready", TPB)
            diff_ready = sm.sems("diff_ready", TPB)
            fade_done = sm.sems("fade_done", TPB)
            faded_beta = sm.sems("faded_beta", TPB)
            dots_ready = sm.sems("dots_ready", TPB)
            NT_ready = sm.sems("NT_ready", TPB)
            mixT_begun = sm.sems("mixT_begun", TPB)
            mixT_ready = sm.sems("mixT_ready", TPB)
            N_turned = sm.sems("N_turned", TPB)
            X_begun = sm.sems("X_begun", TPB)
            X_ready = sm.sems("X_ready", TPB)
            X_turned = sm.sems("X_turned", TPB)
            Y_saved = sm.sems("Y_saved", TPB)
            W_ready = sm.sems("W_ready", TPB)
            W_masked = sm.sems("W_masked", TPB)
            XW_ready = sm.sems("XW_ready", TPB)
            merged = sm.sems("merged", TPB)
            kfade_ready = sm.sem("kfade_ready")
            solved = sm.sems("solved", TPB)
            delta_ready = sm.sems("delta_ready", TPB)
            out_ready = sm.sems("out_ready", TPB)
            state_ready = sm.sem("state_ready")
            state_saved = sm.sem("state_saved")
            read_ready = sm.sem("read_ready")
            read_saved = sm.sem("read_saved")
            rhs_ready = sm.sem("rhs_ready")
            o_saved = sm.sems("o_saved", TPB)
            o_squared = sm.sems("o_squared", TPB)
            ms_step = sm.sems("ms_step", TPB)
            ms_ready = sm.sems("ms_ready", TPB)
            o_normed = sm.sems("o_normed", TPB)
            y_ready = sm.sems("y_ready", TPB)
            y_turned = sm.sems("y_turned", TPB)
            yT_saved = sm.sems("yT_saved", TPB)
            projected = sm.sems("projected", TPB)

            def left(a, k):
                return a.rearrange("p (i two s) -> p i two s", two=2, s=2 << k)[:, :, 0, :]

            def flat(a):
                return a[:, :, :].rearrange("p a b -> p (a b)")

            def by_head(a):
                return a[:, :].rearrange("p (h t) -> p h t", h=HG)

            def heads(a, n):
                return a.unsqueeze(2).broadcast_to([P, a.shape[1], n])

            def over_heads(a):
                return a.unsqueeze(1).broadcast_to([P, HG, P])

            def group(n):
                return n & (NG - 1)

            def tile_of(u, n):
                b = n >> GROUP_BITS
                return (b if isinstance(b, int) else b.with_bounds(min_val=0, max_val=BATCH - 1)) * TPB + u

            def at_gate(a, u, n, first=0, count=HG):
                return flat(a)[:, bass.ds(tile_of(u, n) * H + group(n) * HG + first, count)]

            def parity(a, half):
                return a[:, half:HG:2, :]

            def half_rows(hh):
                return slice(64 * (hh % 2), 64 * (hh % 2) + 64)

            def run(engine, first, phase):
                first()
                phase(0, 0, 1, None, 0)
                with engine.Fori(0, UNITS - 1) as n:
                    phase(1, n, 0, n, n + 1)
                    phase(0, n + 1, 1, n, n + 1)
                phase(1, UNITS - 1, 0, UNITS - 1, None)
                phase(None, None, 1, UNITS - 1, None)

            with nc.Block() as block:
                @block.tensor
                def _(pe):
                    def project_qk(u, n, taps):
                        for j in taps:
                            if j == 0:
                                pe.wait_ge(xpad_ready[u], n + 1)
                            last = nc.tensor.matmul(bank[u][0][:, :], xpad[u][:, j:j + P], folded[:, bass.ds(group(n), 1), j, 0:W2],
                                                    start=(j == 0), stop=(j == L1A_TAPS - 1))
                            if j == L1A_TAPS - 1:
                                last.then_inc(qk_projected[u], 1)

                    def project_v(u, n, taps):
                        for j in taps:
                            if j == 0:
                                pe.wait_ge(fade_done[u], n + 1)
                            last = nc.tensor.matmul(bank[u][1][:, :], xpad[u][:, j:j + P],
                                                    folded[:, bass.ds(group(n), 1), j, W2:2 * W2],
                                                    start=(j == 0), stop=(j == L1A_TAPS - 1))
                            if j == L1A_TAPS - 1:
                                last.then_inc(v_projected[u], 1)

                    def project_gate(u, n):
                        nc.tensor.matmul(bank[u][2][:, :], xpad[u][:, PAD:PAD + P], wgate[:, bass.ds(group(n), 1), :],
                                         start=True, stop=True).then_inc(gate_projected[u], 1)

                    def decays(u, n):
                        pe.wait_ge(terms_ready[u], n + 1)
                        nc.tensor.matmul(bank[u][1][:, :], g.c("after"), flat(terms[u]), start=True,
                                         stop=True).then_inc(diff_ready[u], 1)

                    def turn_qk(u, n):
                        pe.wait_ge(unit[u], n + 1)
                        for pair in range(2):
                            for i, at in ((0, HG + 2 * pair), (1, 2 * pair)):
                                last = nc.tensor.transpose(bank[u][0][:, (2 * pair + i) * P:(2 * pair + i + 1) * P],
                                                           qk[u][:, at:at + 2, :].rearrange("p h d -> p (h d)"), g.c("ident"))
                        last.then_inc(qk_turned[u], 1)

                    def dots(u, n):
                        pe.wait_ge(qkT_saved[u], n + 1)
                        pe.wait_ge(v_silu[u], n + 1)
                        for hh in range(HG):
                            r, pair = half_rows(hh), hh // 2
                            last = nc.tensor.matmul(bank[u][hh % 2][:, pair * 256:pair * 256 + 256], qkT[u][r, 2 * pair, :],
                                                    qkT[u][r, 2 * pair:2 * pair + 2, :].rearrange("p a t -> p (a t)"),
                                                    start=True, stop=True)
                        last.then_inc(dots_ready[u], 1)

                    def turn_N(u, n):
                        pe.wait_ge(gate_silu[u], n + 1)
                        pe.wait_ge(NT_ready[u], n + 1)
                        for hh in range(HG):
                            last = nc.tensor.transpose(bank[u][2][:, hh * P:(hh + 1) * P], NT[u][:, hh, :], g.c("ident"))
                        last.then_inc(N_turned[u], 1)

                    def turn_X(u, n, k):
                        if k == 0:
                            pe.wait_ge(X_ready[u], n + 1)
                        else:
                            pe.wait_ge(merged[u], n * LEVELS + k)
                        for hh in range(HG):
                            last = nc.tensor.transpose(bank[u][2][:, hh * P:(hh + 1) * P], X[u][:, hh, :], g.c("ident"))
                        last.then_inc(X_turned[u], 1)

                    def products_NX(u, n, k):
                        if k == 0:
                            pe.wait_ge(mixT_begun[u], n + 1)
                        for hh in range(HG):
                            last = nc.tensor.matmul(bank[u][0][:, hh * HALF:(hh + 1) * HALF], NT[u][:, hh, :],
                                                    left(X[u][:, hh, :], k), start=True, stop=True)
                        last.then_inc(W_ready[u], 1)

                    def products_XW(u, n, k):
                        pe.wait_ge(Y_saved[u], n * (LEVELS + 1) + k + 1)
                        pe.wait_ge(W_masked[u], n * LEVELS + k + 1)
                        for hh in range(HG):
                            last = nc.tensor.matmul(bank[u][1][:, hh * HALF:(hh + 1) * HALF], Y[u][:, hh, :],
                                                    W[u][:, hh, :], start=True, stop=True)
                        last.then_inc(XW_ready[u], 1)

                    def solve(u, n):
                        pe.wait_ge(Y_saved[u], n * (LEVELS + 1) + LEVELS + 1)
                        if u == 1:
                            pe.wait_ge(rhs_ready, n + 1)
                        for hh in range(HG):
                            last = nc.tensor.matmul(bank[u][2][:, hh * P:(hh + 1) * P], Y[u][:, hh, :], rhs[u][:, hh, :],
                                                    start=True, stop=True)
                        last.then_inc(solved[u], 1)

                    def mix(u, n):
                        pe.wait_ge(mixT_ready[u], n + 1)
                        pe.wait_ge(delta_ready[u], n + 1)
                        for hh in range(HG):
                            last = nc.tensor.matmul(bank[u][3][:, hh * P:(hh + 1) * P], mixT[u][:, hh, :], t1[u][:, hh, :],
                                                    start=True, stop=True)
                        last.then_inc(out_ready[u], 1)

                    def new_state(n):
                        pe.wait_ge(kfade_ready, n + 1)
                        for hh in range(HG):
                            last = nc.tensor.matmul(bank[0][2][half_rows(hh), (hh // 2) * DV:(hh // 2 + 1) * DV], kfade[:, hh, :],
                                                    t1[0][:, hh, :], start=True, stop=True)
                        last.then_inc(state_ready, 1)

                    def read_state(n, half):
                        if half == 0:
                            pe.wait_ge(state_saved, n + 1)
                        else:
                            pe.wait_ge(read_saved, n * 2 + 1)
                        for pair in range(HG // 2):
                            for i in range(2):
                                last = nc.tensor.matmul(bank[1][3][:, (2 * i + pair) * DV:(2 * i + pair + 1) * DV],
                                                        qkT[1][half_rows(half), 2 * pair + i, :], state[half_rows(half), pair, :],
                                                        start=True, stop=True)
                        last.then_inc(read_ready, 1)

                    def turn_y(u, n):
                        pe.wait_ge(y_ready[u], n + 1)
                        for hh in range(HG):
                            last = nc.tensor.transpose(bank[u][3][:, hh * P:(hh + 1) * P], X[u][:, hh, :], g.c("ident"))
                        last.then_inc(y_turned[u], 1)

                    def project_out(u, n):
                        pe.wait_ge(yT_saved[u], n + 1)
                        for hh in range(HG):
                            last = nc.tensor.matmul(bank[u][3][:, 0:D], Y[u][:, hh, :],
                                                    wo[:, bass.ds(group(n) * HG + hh, 1), :], start=(hh == 0), stop=(hh == HG - 1))
                        last.then_inc(projected[u], 1)

                    def prepare(u, n):
                        project_qk(u, n, range(L1A_TAPS))
                        decays(u, n)
                        project_v(u, n, range(L1A_TAPS))
                        project_gate(u, n)
                        turn_qk(u, n)
                        dots(u, n)
                        turn_N(u, n)

                    def phase(at, n, other, done, ahead):
                        if at is None:
                            solve(other, done)
                            mix(other, done)
                            turn_y(other, done)
                            project_out(other, done)
                            return
                        turn_X(at, n, 0)
                        products_NX(at, n, 0)
                        if done is not None:
                            solve(other, done)
                        if ahead is not None:
                            project_qk(other, ahead, [0])
                        products_XW(at, n, 0)
                        if ahead is not None:
                            project_qk(other, ahead, [1])
                        if done is not None:
                            mix(other, done)
                        turn_X(at, n, 1)
                        if ahead is not None:
                            project_qk(other, ahead, [2])
                        if done is not None and other == 0:
                            new_state(done)
                        products_NX(at, n, 1)
                        if ahead is not None:
                            project_qk(other, ahead, [3])
                        products_XW(at, n, 1)
                        if ahead is not None:
                            decays(other, ahead)
                        turn_X(at, n, 2)
                        if at == 1:
                            read_state(n, 0)
                        products_NX(at, n, 2)
                        if ahead is not None:
                            project_gate(other, ahead)
                        products_XW(at, n, 2)
                        if ahead is not None:
                            project_v(other, ahead, [0])
                        turn_X(at, n, 3)
                        if at == 1:
                            read_state(n, 1)
                        if ahead is not None:
                            project_v(other, ahead, [1])
                        products_NX(at, n, 3)
                        if ahead is not None:
                            project_v(other, ahead, [2])
                        products_XW(at, n, 3)
                        if ahead is not None:
                            project_v(other, ahead, [3])
                            turn_qk(other, ahead)
                        turn_X(at, n, 4)
                        if done is not None:
                            turn_y(other, done)
                        products_NX(at, n, 4)
                        if ahead is not None:
                            dots(other, ahead)
                        products_XW(at, n, 4)
                        if done is not None:
                            project_out(other, done)
                        turn_X(at, n, 5)
                        products_NX(at, n, 5)
                        if ahead is not None:
                            turn_N(other, ahead)
                        products_XW(at, n, 5)
                        turn_X(at, n, 6)

                    run(pe, lambda: prepare(0, 0), phase)

                @block.scalar
                def _(act):
                    def load_x(u, n):
                        if u == 0:
                            act.wait_ge(pad_clear, 1)
                            nc.scalar.copy(xpad[0][:, PAD:PAD + P], XT[:, bass.ds(tile_of(u, n) * P, P)]).then_inc(xpad_ready[u], 1)
                        else:
                            nc.scalar.copy(xpad[1][:, :], XT[:, bass.ds(tile_of(u, n) * P - PAD, P + PAD)]).then_inc(xpad_ready[u], 1)

                    def tanh_qk(u, n):
                        act.wait_ge(qk_projected[u], n + 1)
                        nc.scalar.activation(flat(t0[u]), bank[u][0][:, :], ACT.Tanh).then_inc(qk_tanh[u], 1)

                    def tanh_v(u, n):
                        act.wait_ge(v_projected[u], n + 1)
                        nc.scalar.activation(flat(t1[u]), bank[u][1][:, :], ACT.Tanh).then_inc(v_tanh[u], 1)

                    def tanh_gate(u, n):
                        act.wait_ge(gate_projected[u], n + 1)
                        nc.scalar.activation(flat(t2[u]), bank[u][2][:, :], ACT.Tanh, scale=0.5).then_inc(gate_tanh[u], 1)

                    def square(u, n):
                        act.wait_ge(qk_silu[u], n + 1)
                        nc.scalar.activation(flat(t0[u]), flat(qk[u]), ACT.Square).then_inc(squared[u], 1)

                    def exp_decays(u, n):
                        act.wait_ge(diff_ready[u], n + 1)
                        nc.scalar.activation(flat(fade[u]), bank[u][1][:, :], ACT.Exp).then_inc(fade_done[u], 1)

                    def save_qkT(u, n):
                        act.wait_ge(qk_turned[u], n + 1)
                        nc.scalar.copy(flat(qkT[u]), bank[u][0][:, :]).then_inc(qkT_saved[u], 1)

                    def save_Y(u, n, k):
                        act.wait_ge(X_turned[u], n * (LEVELS + 1) + k + 1)
                        nc.scalar.copy(flat(Y[u]), bank[u][2][:, :]).then_inc(Y_saved[u], 1)

                    def save_state(n):
                        act.wait_ge(state_ready, n + 1)
                        nc.scalar.copy(flat(state), bank[0][2][:, 0:2 * DV]).then_inc(state_saved, 1)

                    def save_out(n):
                        act.wait_ge(out_ready[0], n + 1)
                        nc.scalar.copy(flat(X[0]), bank[0][3][:, :]).then_inc(o_saved[0], 1)

                    def square_out(u, n):
                        act.wait_ge(o_saved[u], n + 1)
                        nc.scalar.activation(flat(Y[u]), flat(X[u]), ACT.Square).then_inc(o_squared[u], 1)

                    def save_yT(u, n):
                        act.wait_ge(y_turned[u], n + 1)
                        nc.scalar.copy(flat(Y[u]), bank[u][3][:, :]).then_inc(yT_saved[u], 1)

                    def prepare(u, n):
                        load_x(u, n)
                        tanh_qk(u, n)
                        exp_decays(u, n)
                        square(u, n)
                        tanh_v(u, n)
                        tanh_gate(u, n)
                        save_qkT(u, n)

                    def phase(at, n, other, done, ahead):
                        if ahead is not None:
                            load_x(other, ahead)
                        if at is not None:
                            save_Y(at, n, 0)
                        if done is not None and other == 0:
                            save_out(done)
                        if at is not None:
                            save_Y(at, n, 1)
                        if done is not None:
                            square_out(other, done)
                            if other == 0:
                                save_state(done)
                        if at is None:
                            save_yT(other, done)
                            return
                        if ahead is not None:
                            tanh_qk(other, ahead)
                        save_Y(at, n, 2)
                        if ahead is not None:
                            square(other, ahead)
                            exp_decays(other, ahead)
                            tanh_gate(other, ahead)
                        save_Y(at, n, 3)
                        if ahead is not None:
                            tanh_v(other, ahead)
                            save_qkT(other, ahead)
                        save_Y(at, n, 4)
                        if done is not None:
                            save_yT(other, done)
                        save_Y(at, n, 5)
                        save_Y(at, n, 6)

                    run(act, lambda: prepare(0, 0), phase)

                @block.gpsimd
                def _(pool):
                    def decay_terms(u, n):
                        nc.gpsimd.tensor_tensor(terms[u][:, :, :], over_heads(g.c("upto")), heads(at_gate(decay, u, n), P),
                                                ALU.mult).then_inc(terms_ready[u], 1)

                    def invert_length(u, n):
                        pool.wait_ge(length_step[u], n * 2 + 2)
                        nc.gpsimd.tensor_tensor(length[u][:, :], length[u][:, :], g.c("minus_half")[:, 0:2 * HG],
                                                ALU.pow).then_inc(length_ready[u], 1)

                    def fade_beta(u, n):
                        pool.wait_ge(fade_done[u], n + 1)
                        nc.gpsimd.tensor_tensor(terms[u][:, :, :], fade[u][:, :, :], heads(at_gate(beta, u, n), P),
                                                ALU.mult).then_inc(faded_beta[u], 1)

                    def fade_k(n):
                        pool.wait_ge(unit[0], n + 1)
                        nc.gpsimd.tensor_tensor(kfade[:, :, :], qk[0][:, HG:2 * HG, :],
                                                fade[0][:, :, P - 1:P].broadcast_to([P, HG, DK]), ALU.mult).then_inc(kfade_ready, 1)

                    def mask_mixT(u, n):
                        pool.wait_ge(mixT_begun[u], n + 1)
                        nc.gpsimd.tensor_tensor(mixT[u][:, :, :], mixT[u][:, :, :], over_heads(g.c("upto")),
                                                ALU.mult).then_inc(mixT_ready[u], 1)

                    def invert_ms(u, n):
                        pool.wait_ge(ms_step[u], n * 2 + 2)
                        nc.gpsimd.tensor_tensor(ms[u][:, :], ms[u][:, :], g.c("minus_half")[:, 0:HG], ALU.pow).then_inc(ms_ready[u], 1)

                    def gate_out(u, n):
                        pool.wait_ge(o_normed[u], n + 1)
                        nc.gpsimd.tensor_tensor(X[u][:, :, :], X[u][:, :, :], gate[u][:, :, :], ALU.mult).then_inc(y_ready[u], 1)

                    def prepare(u, n):
                        decay_terms(u, n)
                        invert_length(u, n)
                        fade_beta(u, n)
                        if u == 0:
                            fade_k(n)
                        mask_mixT(u, n)

                    def phase(at, n, other, done, ahead):
                        if ahead is not None:
                            decay_terms(other, ahead)
                        if done is not None:
                            invert_ms(other, done)
                            gate_out(other, done)
                        if ahead is not None:
                            invert_length(other, ahead)
                            fade_beta(other, ahead)
                            if other == 0:
                                fade_k(ahead)
                            mask_mixT(other, ahead)

                    def first():
                        nc.gpsimd.memset(xpad[0][:, 0:PAD], 0.0).then_inc(pad_clear, 1)
                        prepare(0, 0)

                    run(pool, first, phase)

                @block.vector
                def _(dve):
                    def silu(dst, tanh, src, u, done):
                        nc.vector.scalar_tensor_tensor(flat(dst[u]), flat(tanh[u]), 1.0, src[:, :], ALU.add, ALU.mult).then_inc(done[u], 1)

                    def silu_qk(u, n):
                        dve.wait_ge(qk_tanh[u], n + 1)
                        silu(qk, t0, bank[u][0], u, qk_silu)

                    def silu_v(u, n):
                        dve.wait_ge(v_tanh[u], n + 1)
                        silu(rhs, t1, bank[u][1], u, v_silu)

                    def silu_gate(u, n, done):
                        if done is not None:
                            dve.wait_ge(y_ready[u], done + 1)
                        dve.wait_ge(gate_tanh[u], n + 1)
                        silu(gate, t2, bank[u][2], u, gate_silu)

                    def lengths(u, n):
                        dve.wait_ge(squared[u], n + 1)
                        nc.vector.tensor_reduce(length[u][:, :], flat(t0[u]).rearrange("p (h d) -> p h d", d=DK), AX.X,
                                                ALU.add).then_inc(length_step[u], 1)
                        dve.wait_ge(length_step[u], n * 2 + 1)
                        nc.vector.scalar_tensor_tensor(length[u][:, :], length[u][:, :], 1e-6, g.c("dk_scale"), ALU.add,
                                                       ALU.mult).then_inc(length_step[u], 1)

                    def to_unit(u, n):
                        dve.wait_ge(length_ready[u], n + 1)
                        nc.vector.tensor_tensor(qk[u][:, :, :], qk[u][:, :, :], heads(length[u][:, :], DK), ALU.mult).then_inc(unit[u], 1)

                    def fade_dots(u, n):
                        dve.wait_ge(faded_beta[u], n + 1)
                        dve.wait_ge(dots_ready[u], n + 1)
                        for half in range(2):
                            kk = bank[u][half][:, :].rearrange("p (a k t) -> p a k t", a=2, k=2)[:, :, 0, :]
                            last = nc.vector.tensor_tensor(parity(NT[u], half), kk, parity(terms[u], half), ALU.mult)
                        last.then_inc(NT_ready[u], 1)

                    def begin_mixT(u, n):
                        for half in range(2):
                            kq = bank[u][half][:, :].rearrange("p (a k t) -> p a k t", a=2, k=2)[:, :, 1, :]
                            last = nc.vector.tensor_tensor(parity(mixT[u], half), kq, parity(fade[u], half), ALU.mult)
                        last.then_inc(mixT_begun[u], 1)

                    def begin_X(u, n):
                        dve.wait_ge(N_turned[u], n + 1)
                        nc.vector.tensor_tensor(X[u][:, :, :], by_head(bank[u][2]), over_heads(g.c("level1n")),
                                                ALU.mult).then_inc(X_begun[u], 1)

                    def add_one(u, n):
                        dve.wait_ge(X_begun[u], n + 1)
                        nc.vector.tensor_tensor(X[u][:, :, :], X[u][:, :, :], over_heads(g.c("ident")), ALU.add).then_inc(X_ready[u], 1)

                    def mask_W(u, n, k):
                        dve.wait_ge(W_ready[u], n * LEVELS + k + 1)
                        nc.vector.tensor_tensor(W[u][:, :, :], bank[u][0][:, 0:HG * HALF].rearrange("p (h t) -> p h t", h=HG),
                                                g.c("level")[:, k * HALF:(k + 1) * HALF].unsqueeze(1).broadcast_to([P, HG, HALF]),
                                                ALU.mult).then_inc(W_masked[u], 1)

                    def merge(u, n, k):
                        x = left(flat(X[u]), k)
                        dve.wait_ge(XW_ready[u], n * LEVELS + k + 1)
                        nc.vector.tensor_tensor(x, x, bank[u][1][:, 0:HG * HALF].rearrange("p (i s) -> p i s", s=2 << k),
                                                ALU.subtract).then_inc(merged[u], 1)

                    def delta(u, n):
                        dve.wait_ge(solved[u], n + 1)
                        nc.vector.tensor_tensor(t1[u][:, :, :], by_head(bank[u][2]), heads(at_gate(beta, u, n), P),
                                                ALU.mult).then_inc(delta_ready[u], 1)

                    def take_read(n, half):
                        dve.wait_ge(read_ready, n * 2 + half + 1)
                        for i, dst in ((0, read_k), (1, read_q)):
                            src = bank[1][3][:, i * 256:i * 256 + 256].rearrange("p (a d) -> p a d", a=2)
                            last = nc.vector.tensor_tensor(parity(dst, half), src, heads(at_gate(grown, 1, n)[:, half:HG:2], DV), ALU.mult)
                        last.then_inc(read_saved, 1)

                    def subtract_read(n):
                        dve.wait_ge(read_saved, n * 2 + 2)
                        nc.vector.tensor_tensor(flat(rhs[1]), flat(rhs[1]), flat(read_k), ALU.subtract).then_inc(rhs_ready, 1)

                    def add_read(n):
                        dve.wait_ge(out_ready[1], n + 1)
                        nc.vector.tensor_tensor(flat(X[1]), bank[1][3][:, :], flat(read_q), ALU.add).then_inc(o_saved[1], 1)

                    def mean_square(u, n):
                        dve.wait_ge(o_squared[u], n + 1)
                        nc.vector.tensor_reduce(ms[u][:, :], Y[u][:, :, :], AX.X, ALU.add).then_inc(ms_step[u], 1)
                        dve.wait_ge(ms_step[u], n * 2 + 1)
                        nc.vector.tensor_scalar(ms[u][:, :], ms[u][:, :], 1.0 / DV, 1e-5, ALU.mult, ALU.add).then_inc(ms_step[u], 1)

                    def norm(u, n):
                        dve.wait_ge(ms_ready[u], n + 1)
                        nc.vector.tensor_tensor(X[u][:, :, :], X[u][:, :, :], heads(ms[u][:, :], DV), ALU.mult).then_inc(o_normed[u], 1)

                    def add(u, n):
                        x = g.tile(tile_of(u, n)).rearrange("p t d -> p (t d)")
                        dve.wait_ge(projected[u], n + 1)
                        nc.vector.tensor_tensor(x, x, bank[u][3][:, 0:D], ALU.add)

                    def prepare(u, n):
                        silu_qk(u, n)
                        lengths(u, n)
                        to_unit(u, n)
                        silu_v(u, n)
                        silu_gate(u, n, None)
                        fade_dots(u, n)
                        begin_mixT(u, n)
                        begin_X(u, n)
                        add_one(u, n)

                    def phase(at, n, other, done, ahead):
                        if at is None:
                            delta(other, done)
                            add_read(done)
                            mean_square(other, done)
                            norm(other, done)
                            add(other, done)
                            return
                        mask_W(at, n, 0)
                        if done is not None:
                            delta(other, done)
                        merge(at, n, 0)
                        if done is not None and other == 1:
                            add_read(done)
                        mask_W(at, n, 1)
                        if done is not None:
                            mean_square(other, done)
                        merge(at, n, 1)
                        if done is not None:
                            norm(other, done)
                        if ahead is not None:
                            silu_qk(other, ahead)
                        mask_W(at, n, 2)
                        if at == 1:
                            take_read(n, 0)
                        if ahead is not None:
                            lengths(other, ahead)
                        merge(at, n, 2)
                        mask_W(at, n, 3)
                        if ahead is not None:
                            to_unit(other, ahead)
                        if at == 1:
                            take_read(n, 1)
                        merge(at, n, 3)
                        if ahead is not None:
                            silu_gate(other, ahead, done)
                            silu_v(other, ahead)
                        mask_W(at, n, 4)
                        if at == 1:
                            subtract_read(n)
                        merge(at, n, 4)
                        if ahead is not None:
                            fade_dots(other, ahead)
                        mask_W(at, n, 5)
                        if ahead is not None:
                            begin_X(other, ahead)
                        merge(at, n, 5)
                        if ahead is not None:
                            add_one(other, ahead)
                            begin_mixT(other, ahead)
                        if done is not None:
                            add(other, done)

                    run(dve, lambda: prepare(0, 0), phase)


def turn_stream(nc, g, name, XT, wide=None, wide_out=None):
    NS = 4
    n = wide.shape[1] if wide is not None else 0
    with Stage(nc, name + "_turn") as st:
        xn = [st.sb(f"xn{s}", [P, D]) for s in range(NS)]
        xt = [st.sb(f"xt{s}", [P, P]) for s in range(NS)]
        turn = [st.ps(f"turn{s}", [P, 512]) for s in range(NS)]
        prod = st.ps("prod", [P, max(512, TILES * n)])
        slot_free = st.sems("slot_free", NS)
        xn_ready = st.sems("xn_ready", NS)
        turned = st.sems("turned", NS)
        xt_ready = st.sems("xt_ready", NS)
        xt_used = st.sems("xt_used", NS)
        prod_saved = st.sem("prod_saved")
        with nc.Block() as block:
            @block.vector
            def _(dve):
                for s in range(NS):
                    dve.sem_inc(slot_free[s], 1)
                with dve.Fori(0, TILES // NS) as it:
                    for s in range(NS):
                        t = it * NS + s
                        dve.wait_ge(slot_free[s], it + 1)
                        nc.vector.tensor_scalar(xn[s][:, :], g.tile(t), g.mean[:, bass.ds(t, 1)],
                                                g.rstd[:, bass.ds(t, 1)], ALU.subtract, ALU.mult).then_inc(xn_ready[s], 1)
                if n:
                    for s in range(NS):
                        dve.wait_ge(xt_used[s], TILES // NS + 1)
                    nc.vector.tensor_copy(wide_out.rearrange("p t n -> p (t n)"), prod[:, 0:TILES * n]).then_inc(prod_saved, 1)

            @block.tensor
            def _(pe):
                with pe.Fori(0, TILES // NS) as it:
                    for s in range(NS):
                        pe.wait_ge(xn_ready[s], it + 1)
                        nc.tensor.transpose(turn[s][:, 0:P], xn[s][:, :], g.c("ident")).then_inc(turned[s], 1)
                    if n:
                        for s in range(NS):
                            pe.wait_ge(xt_ready[s], it + 1)
                            nc.tensor.matmul(prod[:, bass.ds((it * NS + s) * n, n)], xt[s][:, :], wide, start=True,
                                             stop=True).then_inc(xt_used[s], 1)

            @block.scalar
            def _(act):
                for s in range(NS):
                    act.sem_inc(xt_used[s], 1)
                with act.Fori(0, TILES // NS) as it:
                    for s in range(NS):
                        act.wait_ge(turned[s], it + 1)
                        if n:
                            act.wait_ge(xt_used[s], it + 1)
                        nc.scalar.copy(xt[s][:, :], turn[s][:, 0:P]).then_inc(xt_ready[s], 1)

            @block.gpsimd
            def _(pool):
                with pool.Fori(0, TILES // NS) as it:
                    for s in range(NS):
                        pool.wait_ge(xt_ready[s], it + 1)
                        nc.gpsimd.tensor_copy(XT[:, bass.ds((it * NS + s) * P, P)], xt[s][:, :]).then_inc(slot_free[s], 1)


L2_EXPERTS, L2_SHARED, L2_TOP = 8, 2, 2
L2F_ALL = L2_EXPERTS + L2_SHARED
L2F_PARTS = [("gate", L2_EXPERTS), ("bias", L2_EXPERTS), ("w1", L2F_ALL * 128), ("w3", L2F_ALL * 128),
             ("w2", L2F_ALL * 128)]


def l2_ffn(nc, g, name):
    E, EA = L2_EXPERTS, L2F_ALL
    cols, width = columns(L2F_PARTS)
    N = 512
    JT = N // P
    NS = 2
    USES = EA // NS
    with Stage(nc, name) as st:
        w = st.sb("w", [P, width])
        XT = st.sb("XT", [P, TOKENS])
        logits = st.sb("logits", [P, TILES, E])
        gate = st.sb("gate", [P, TILES, E])
        row_statistics(nc, g, name, [(w[:, :], g.dram["w_l2f"])])
        turn_stream(nc, g, name, XT, w[:, cols["gate"]], logits[:, :, :])

        with Stage(nc, name + "_gate") as sg:
            top = sg.sb("top", [P, TILES])
            score = sg.sb("score", [P, TILES, E])
            picked = sg.sb("picked", [P, TILES, E])
            above = sg.sb("above", [P, TILES, E, E])
            equal = sg.sb("equal", [P, TILES, E, E])
            rank = sg.sb("rank", [P, TILES, E])
            step = sg.sem("step")
            shifted = sg.sem("shifted")
            exped = sg.sem("exped")

            def each(a):
                return a.unsqueeze(2).broadcast_to([P, TILES, E])

            mine = picked[:, :, :].unsqueeze(3).broadcast_to([P, TILES, E, E])
            other = picked[:, :, :].unsqueeze(2).broadcast_to([P, TILES, E, E])
            before = g.c("before8").rearrange("p (e j) -> p e j", e=E).unsqueeze(1).broadcast_to([P, TILES, E, E])
            with nc.Block() as block:
                @block.vector
                def _(dve):
                    nc.vector.tensor_reduce(top[:, :], logits[:, :, :], AX.X, ALU.max).then_inc(step, 1)
                    dve.wait_ge(step, 1)
                    nc.vector.tensor_tensor(score[:, :, :], logits[:, :, :], each(top[:, :]),
                                            ALU.subtract).then_inc(shifted, 1)
                    dve.wait_ge(exped, 1)
                    nc.vector.tensor_reduce(top[:, :], score[:, :, :], AX.X, ALU.add).then_inc(step, 1)
                    dve.wait_ge(step, 2)
                    nc.vector.reciprocal(top[:, :], top[:, :]).then_inc(step, 1)
                    dve.wait_ge(step, 3)
                    nc.vector.tensor_tensor(score[:, :, :], score[:, :, :], each(top[:, :]), ALU.mult).then_inc(step, 1)
                    dve.wait_ge(step, 4)
                    nc.vector.tensor_tensor(picked[:, :, :], score[:, :, :],
                                            w[:, cols["bias"]].unsqueeze(1).broadcast_to([P, TILES, E]),
                                            ALU.add).then_inc(step, 1)
                    dve.wait_ge(step, 5)
                    nc.vector.tensor_tensor(above[:, :, :, :], other, mine, ALU.is_gt).then_inc(step, 1)
                    nc.vector.tensor_tensor(equal[:, :, :, :], other, mine, ALU.is_equal).then_inc(step, 1)
                    dve.wait_ge(step, 7)
                    nc.vector.tensor_tensor(equal[:, :, :, :], equal[:, :, :, :], before, ALU.mult).then_inc(step, 1)
                    dve.wait_ge(step, 8)
                    nc.vector.tensor_tensor(above[:, :, :, :], above[:, :, :, :], equal[:, :, :, :],
                                            ALU.add).then_inc(step, 1)
                    dve.wait_ge(step, 9)
                    nc.vector.tensor_reduce(rank[:, :, :], above[:, :, :, :], AX.X, ALU.add).then_inc(step, 1)
                    dve.wait_ge(step, 10)
                    nc.vector.tensor_scalar(rank[:, :, :], rank[:, :, :], float(L2_TOP), 0.5, ALU.is_lt,
                                            ALU.mult).then_inc(step, 1)
                    dve.wait_ge(step, 11)
                    nc.vector.tensor_tensor(gate[:, :, :], rank[:, :, :], score[:, :, :], ALU.mult).then_inc(step, 1)

                @block.scalar
                def _(act):
                    act.wait_ge(shifted, 1)
                    nc.scalar.activation(score[:, :, :], score[:, :, :], ACT.Exp).then_inc(exped, 1)

        with Stage(nc, name + "_mix") as sm:
            silu = [sm.sb(f"silu{s}", [P, N]) for s in range(NS)]
            hid = [sm.sb(f"hid{s}", [P, N]) for s in range(NS)]
            up1 = [sm.ps(f"up1{s}", [P, N]) for s in range(NS)]
            up3 = [sm.ps(f"up3{s}", [P, N]) for s in range(NS)]
            down = [sm.ps(f"down{s}", [P, N]) for s in range(NS)]
            up1_ready = sm.sems("up1_ready", NS)
            up3_ready = sm.sems("up3_ready", NS)
            silu_done = sm.sems("silu_done", NS)
            hid_ready = sm.sems("hid_ready", NS)
            down_ready = sm.sems("down_ready", NS)
            mixed = sm.sems("mixed", NS)
            with nc.Block() as block:
                @block.tensor
                def _(pe):
                    def up(it, e):
                        s, use = e % NS, it * USES + e // NS + 1
                        x = XT[:, bass.ds(it * N, N)]
                        pe.wait_ge(mixed[s], use)
                        nc.tensor.matmul(up1[s][:, :], w[:, cols["w1"]][:, e * P:(e + 1) * P], x, start=True,
                                         stop=True).then_inc(up1_ready[s], 1)
                        nc.tensor.matmul(up3[s][:, :], w[:, cols["w3"]][:, e * P:(e + 1) * P], x, start=True,
                                         stop=True).then_inc(up3_ready[s], 1)

                    def turn_down(it, e):
                        s, use = e % NS, it * USES + e // NS + 1
                        pe.wait_ge(hid_ready[s], use)
                        for j in range(JT):
                            last = nc.tensor.matmul(down[s][:, j * D:(j + 1) * D], hid[s][:, j * P:(j + 1) * P],
                                                    w[:, cols["w2"]][:, e * D:(e + 1) * D], start=True, stop=True)
                        last.then_inc(down_ready[s], 1)

                    for s in range(NS):
                        pe.sem_inc(mixed[s], 1)
                    with pe.Fori(0, TOKENS // N) as it:
                        up(it, 0)
                        for e in range(1, EA):
                            up(it, e)
                            turn_down(it, e - 1)
                        turn_down(it, EA - 1)

                @block.scalar
                def _(act):
                    with act.Fori(0, TOKENS // N) as it:
                        for e in range(EA):
                            s, use = e % NS, it * USES + e // NS + 1
                            act.wait_ge(up1_ready[s], use)
                            nc.scalar.activation(silu[s][:, :], up1[s][:, :], ACT.Silu).then_inc(silu_done[s], 1)

                @block.vector
                def _(dve):
                    def gated(it, e):
                        s, use = e % NS, it * USES + e // NS + 1
                        dve.wait_ge(silu_done[s], use)
                        dve.wait_ge(up3_ready[s], use)
                        nc.vector.tensor_tensor(hid[s][:, :], silu[s][:, :], up3[s][:, :], ALU.mult).then_inc(hid_ready[s], 1)

                    def mix(it, e):
                        s, use = e % NS, it * USES + e // NS + 1
                        dve.wait_ge(down_ready[s], use)
                        dve.wait_ge(mixed[1 - s], use + s)
                        if e < E:
                            for j in range(JT):
                                t = it * JT + j
                                last = nc.vector.scalar_tensor_tensor(
                                    g.tile(t), down[s][:, j * D:(j + 1) * D], gate[:, bass.ds(t, 1), e:e + 1], g.tile(t),
                                    ALU.mult, ALU.add)
                        else:
                            x = g.X[:, bass.ds(it * JT, JT), :].rearrange("p t d -> p (t d)")
                            last = nc.vector.scalar_tensor_tensor(x, down[s][:, :], 0.5, x, ALU.mult, ALU.add)
                        last.then_inc(mixed[s], 1)

                    with dve.Fori(0, TOKENS // N) as it:
                        gated(it, 0)
                        for e in range(1, EA):
                            gated(it, e)
                            mix(it, e - 1)
                        mix(it, EA - 1)


BF16 = mybir.dt.bfloat16
RMS_EPS = 1e-6


def rms_scales(nc, g, name, scale_out):
    NS = 4
    with Stage(nc, name + "_rms") as st:
        x1 = [st.sb(f"x1{s}", [P, D]) for s in range(NS)]
        square = [st.sb(f"square{s}", [P, D]) for s in range(NS)]
        ss = st.sb("ss", [P, TILES])
        slot_free = st.sems("slot_free", NS)
        x1_ready = st.sems("x1_ready", NS)
        rooted = st.sem("rooted")
        step = st.sem("step")
        with nc.Block() as block:
            @block.vector
            def _(dve):
                for s in range(NS):
                    dve.sem_inc(slot_free[s], 1)
                with dve.Fori(0, TILES // NS) as it:
                    for s in range(NS):
                        t = it * NS + s
                        dve.wait_ge(slot_free[s], it + 1)
                        nc.vector.tensor_scalar(x1[s][:, :], g.tile(t), g.mean[:, bass.ds(t, 1)],
                                                g.rstd[:, bass.ds(t, 1)], ALU.subtract, ALU.mult).then_inc(x1_ready[s], 1)
                dve.wait_ge(rooted, 1)
                nc.vector.reciprocal(ss[:, :], ss[:, :]).then_inc(step, 1)
                dve.wait_ge(step, 1)
                nc.vector.tensor_tensor(scale_out, ss[:, :], g.rstd[:, :], ALU.mult).then_inc(step, 1)

            @block.scalar
            def _(act):
                with act.Fori(0, TILES // NS) as it:
                    for s in range(NS):
                        act.wait_ge(x1_ready[s], it + 1)
                        nc.scalar.activation(square[s][:, :], x1[s][:, :], ACT.Square,
                                             accum_out=ss[:, bass.ds(it * NS + s, 1)]).then_inc(slot_free[s], 1)
                for s in range(NS):
                    act.wait_ge(slot_free[s], TILES // NS + 1)
                nc.scalar.activation(ss[:, :], ss[:, :], ACT.Sqrt, scale=1.0 / D, bias=g.c("eps_l2")).then_inc(rooted, 1)


L2A_HEADS, L2A_HD = 16, 8
L2A_PARTS = [("wq", D), ("wk", D), ("wv", D), ("wo", D), ("norm", D), ("bv", D), ("bo", D), ("bq", 1), ("bk", 1)]


def l2_attn(nc, g, name):
    H, HD = L2A_HEADS, L2A_HD
    cols, width = columns(L2A_PARTS)
    SCALE = float(HD) ** -0.5
    N = SEQ
    NS = 3
    PAIRS = H // 2
    uses = [len(range(s, PAIRS, NS)) for s in range(NS)]
    with Stage(nc, name) as st:
        w = st.sb("w", [P, width])
        scale = st.sb("scale", [P, TILES])
        row_statistics(nc, g, name, [(w[:, :], g.dram["w_l2a"])])
        rms_scales(nc, g, name, scale[:, :])
        ident_b = st.ctx.enter_context(nc.sbuf_tensor(name + "_ident_b", [P, P], BF16))
        causal_b = st.ctx.enter_context(nc.sbuf_tensor(name + "_causal_b", [P, P], BF16))
        bq4 = st.sb("bq4", [P, 4])
        x0 = st.sb("x0", [P, TPB, D])
        xn = st.sb("xn", [P, TPB, D])
        xT = st.sb("xT", [P, N])
        kT = st.sb("kT", [P, N])
        q4 = st.sb("q4", [P, 4, N])
        v = st.sb("v", [P, TPB, D])
        den = st.sb("den", [P, TPB, H])
        rden = st.sb("rden", [P, TPB, H])
        on = st.sb("on", [P, TPB * D])
        onT = st.sb("onT", [P, N])
        low = [st.sb(f"low{s}", [P, TPB, 2]) for s in range(NS)]
        bias = [st.sb(f"bias{s}", [P, TPB, 2]) for s in range(NS)]
        prob = [st.sb(f"prob{s}", [P, 2, 3 * P]) for s in range(NS)]
        probT = [st.sb(f"probT{s}", [P, 6, P]) for s in range(NS)]
        misc = st.ps("misc", [P, 512])
        O = st.ps("O", [P, 512])
        wideS = [st.ps(f"wideS{s}", [P, 512]) for s in range(NS)]
        slimS = [st.ps(f"slimS{s}", [P, 512]) for s in range(NS)]
        cast = st.sem("cast")
        batch_free = st.sem("batch_free")
        x0_ready = st.sem("x0_ready")
        xn_ready = st.sem("xn_ready")
        turned = st.sem("turned")
        xT_ready = st.sem("xT_ready")
        qk_ready = st.sem("qk_ready")
        qk_saved = st.sem("qk_saved")
        v_ready = st.sem("v_ready")
        v_saved = st.sem("v_saved")
        s_ready = st.sems("s_ready", NS)
        low_ready = st.sems("low_ready", NS)
        bias_ready = st.sems("bias_ready", NS)
        exp_done = st.sems("exp_done", NS)
        pT_ready = st.sems("pT_ready", NS)
        wide_saved = st.sems("wide_saved", NS)
        slim_saved = st.sems("slim_saved", NS)
        pv_done = st.sems("pv_done", NS)
        rden_ready = st.sem("rden_ready")
        on_ready = st.sem("on_ready")
        on_turned = st.sem("on_turned")
        onT_ready = st.sem("onT_ready")
        out_ready = st.sem("out_ready")
        out_added = st.sem("out_added")

        with nc.Block() as block:
            @block.vector
            def _(dve):
                nc.vector.tensor_copy(ident_b[:, :], g.c("ident")).then_inc(cast, 1)
                nc.vector.tensor_copy(causal_b[:, :], g.c("causal")).then_inc(cast, 1)
                nc.vector.tensor_scalar(bq4[:, :], g.c("quarter"), w[:, cols["bq"]], None, ALU.mult).then_inc(cast, 1)
                dve.sem_inc(batch_free, 1)

                def shift(it, i):
                    s, use = i % NS, it * uses[i % NS] + i // NS + 1
                    dve.wait_ge(s_ready[s], use)
                    nc.vector.tensor_reduce(low[s][:, 0, :], slimS[s][:, 0:2 * P].rearrange("p (h k) -> p h k", h=2), AX.X,
                                            ALU.max, negate=True)
                    nc.vector.tensor_reduce(low[s][:, 1, :], wideS[s][:, :].rearrange("p (h k) -> p h k", h=2), AX.X,
                                            ALU.max, negate=True).then_inc(low_ready[s], 1)
                    dve.wait_ge(low_ready[s], use)
                    nc.vector.tensor_scalar(bias[s][:, :, :], low[s][:, :, :], SCALE, None, ALU.mult).then_inc(bias_ready[s], 1)

                def save(it, i):
                    s, use = i % NS, it * uses[i % NS] + i // NS + 1
                    dve.wait_ge(pT_ready[s], use)
                    nc.vector.tensor_copy(probT[s][:, 4:6, :], slimS[s][:, 0:2 * P].rearrange("p (b q) -> p b q", b=2)
                                          ).then_inc(slim_saved[s], 1)

                with dve.Fori(0, BATCH) as it:
                    dve.wait_ge(batch_free, it + 1)
                    for u in range(TPB):
                        t = it * TPB + u
                        last = nc.vector.tensor_scalar(x0[:, u, :], g.tile(t), g.mean[:, bass.ds(t, 1)],
                                                       scale[:, bass.ds(t, 1)], ALU.subtract, ALU.mult)
                    last.then_inc(x0_ready, 1)
                    dve.wait_ge(x0_ready, it + 1)
                    nc.vector.tensor_tensor(xn[:, :, :], x0[:, :, :], w[:, cols["norm"]].unsqueeze(1).broadcast_to([P, TPB, D]),
                                            ALU.mult).then_inc(xn_ready, 1)
                    for i in range(PAIRS + 1):
                        if i < PAIRS:
                            shift(it, i)
                        if i >= 1:
                            save(it, i - 1)
                    for s in range(NS):
                        dve.wait_ge(exp_done[s], it * uses[s] + uses[s])
                    nc.vector.reciprocal(rden[:, :, :], den[:, :, :]).then_inc(rden_ready, 1)
                    dve.wait_ge(rden_ready, it + 1)
                    for s in range(NS):
                        dve.wait_ge(pv_done[s], it * uses[s] + uses[s])
                    nc.vector.tensor_tensor(on[:, :].rearrange("p (h e) -> p h e", e=HD),
                                            O[:, 0:TPB * D].rearrange("p (h e) -> p h e", e=HD),
                                            rden[:, :, :].rearrange("p u h -> p (u h)").unsqueeze(2)
                                            .broadcast_to([P, TPB * H, HD]), ALU.mult).then_inc(on_ready, 1)
                    x = g.X[:, bass.ds(it * TPB, TPB), :].rearrange("p u d -> p (u d)")
                    dve.wait_ge(out_ready, it + 1)
                    nc.vector.tensor_tensor(on[:, :], misc[:, 256:512], xn[:, :, :].rearrange("p u d -> p (u d)"),
                                            ALU.add).then_inc(out_added, 1)
                    dve.wait_ge(out_added, it + 1)
                    nc.vector.tensor_tensor(x, x, on[:, :], ALU.add).then_inc(batch_free, 1)

            @block.tensor
            def _(pe):
                def scores(it, i):
                    s, k = i % NS, i // NS
                    pe.wait_ge(wide_saved[s], it * uses[s] + k + 1)
                    pe.wait_ge(slim_saved[s], it * uses[s] + k + 1)
                    for hh in range(2):
                        h = 2 * i + hh
                        r = slice(32 * (h // 4), 32 * (h // 4) + 32)
                        o = wideS[s][:, hh * 256:hh * 256 + 256]
                        nc.tensor.matmul(o[:, 0:P], q4[r, h % 4, P:2 * P], kT[r, 0:P], start=True, stop=True)
                        nc.tensor.matmul(o[:, P:2 * P], q4[r, h % 4, P:2 * P], kT[r, P:2 * P], start=True, stop=False)
                        nc.tensor.matmul(o[:, P:2 * P], ident_b[:, :], causal_b[:, :], start=False, stop=True)
                        o = slimS[s][:, hh * P:hh * P + P]
                        nc.tensor.matmul(o, q4[r, h % 4, 0:P], kT[r, 0:P], start=True, stop=False)
                        last = nc.tensor.matmul(o, ident_b[:, :], causal_b[:, :], start=False, stop=True)
                    last.then_inc(s_ready[s], 1)

                def turn(it, i):
                    s, use = i % NS, it * uses[i % NS] + i // NS + 1
                    pe.wait_ge(exp_done[s], use)
                    for n in range(6):
                        o = wideS[s][:, n * P:n * P + P] if n < 4 else slimS[s][:, (n - 4) * P:(n - 3) * P]
                        last = nc.tensor.transpose(o, prob[s][:, n // 3, (n % 3) * P:(n % 3) * P + P], g.c("ident"))
                    last.then_inc(pT_ready[s], 1)

                def weigh(it, i):
                    s, use = i % NS, it * uses[i % NS] + i // NS + 1
                    pe.wait_ge(wide_saved[s], use + 1)
                    pe.wait_ge(slim_saved[s], use + 1)
                    for hh in range(2):
                        e = slice((2 * i + hh) * HD, (2 * i + hh + 1) * HD)
                        nc.tensor.matmul(O[:, e], probT[s][:, 3 * hh, :], v[:, 0, e], start=True, stop=True)
                        o = O[:, D + e.start:D + e.stop]
                        nc.tensor.matmul(o, probT[s][:, 3 * hh + 1, :], v[:, 0, e], start=True, stop=False)
                        last = nc.tensor.matmul(o, probT[s][:, 3 * hh + 2, :], v[:, 1, e], start=False, stop=True)
                    last.then_inc(pv_done[s], 1)

                for s in range(NS):
                    pe.sem_inc(wide_saved[s], 1)
                    pe.sem_inc(slim_saved[s], 1)
                pe.wait_ge(cast, 3)
                with pe.Fori(0, BATCH) as it:
                    pe.wait_ge(xn_ready, it + 1)
                    for u in range(TPB):
                        last = nc.tensor.transpose(misc[:, u * P:(u + 1) * P], xn[:, u, :], g.c("ident"))
                    last.then_inc(turned, 1)
                    pe.wait_ge(xT_ready, it + 1)
                    nc.tensor.matmul(misc[:, 0:N], w[:, cols["wq"]], xT[:, :], start=True, stop=True)
                    nc.tensor.matmul(misc[:, N:2 * N], w[:, cols["wk"]], xT[:, :], start=True, stop=True).then_inc(qk_ready, 1)
                    for u in range(TPB):
                        o = O[:, u * D:(u + 1) * D]
                        nc.tensor.matmul(o, xT[:, u * P:(u + 1) * P], w[:, cols["wv"]], start=True, stop=False)
                        last = nc.tensor.matmul(o, g.c("ones")[0:1, :], w[0:1, cols["bv"]], start=False, stop=True)
                    last.then_inc(v_ready, 1)
                    pe.wait_ge(qk_saved, it + 1)
                    pe.wait_ge(v_saved, it + 1)
                    for i in range(PAIRS + 2):
                        if i < PAIRS:
                            scores(it, i)
                        if 1 <= i <= PAIRS:
                            turn(it, i - 1)
                        if i >= 2:
                            weigh(it, i - 2)
                    pe.wait_ge(on_ready, it + 1)
                    for u in range(TPB):
                        last = nc.tensor.transpose(misc[:, u * P:(u + 1) * P], on[:, u * P:(u + 1) * P], g.c("ident"))
                    last.then_inc(on_turned, 1)
                    pe.wait_ge(onT_ready, it + 1)
                    for u in range(TPB):
                        o = misc[:, 256 + u * D:256 + (u + 1) * D]
                        nc.tensor.matmul(o, onT[:, u * P:(u + 1) * P], w[:, cols["wo"]], start=True, stop=False)
                        last = nc.tensor.matmul(o, g.c("ones")[0:1, :], w[0:1, cols["bo"]], start=False, stop=True)
                    last.then_inc(out_ready, 1)

            @block.scalar
            def _(act):
                def exps(it, i):
                    s, use = i % NS, it * uses[i % NS] + i // NS + 1
                    act.wait_ge(bias_ready[s], use)
                    for hh in range(2):
                        h = 2 * i + hh
                        nc.scalar.activation(prob[s][:, hh, 0:P], slimS[s][:, hh * P:hh * P + P], ACT.Exp, scale=SCALE,
                                             bias=bias[s][:, 0, hh:hh + 1], accum_out=den[:, 0, h:h + 1])
                        last = nc.scalar.activation(prob[s][:, hh, P:3 * P], wideS[s][:, hh * 256:hh * 256 + 256], ACT.Exp,
                                                    scale=SCALE, bias=bias[s][:, 1, hh:hh + 1], accum_out=den[:, 1, h:h + 1])
                    last.then_inc(exp_done[s], 1)

                def save(it, i):
                    s, use = i % NS, it * uses[i % NS] + i // NS + 1
                    act.wait_ge(pT_ready[s], use)
                    nc.scalar.copy(probT[s][:, 0:4, :], wideS[s][:, :].rearrange("p (b q) -> p b q", b=4)).then_inc(wide_saved[s], 1)

                act.wait_ge(cast, 3)
                with act.Fori(0, BATCH) as it:
                    act.wait_ge(turned, it + 1)
                    nc.scalar.copy(xT[:, :], misc[:, 0:N]).then_inc(xT_ready, 1)
                    act.wait_ge(qk_ready, it + 1)
                    nc.scalar.activation(kT[:, :], misc[:, N:2 * N], ACT.Identity, bias=w[:, cols["bk"]])
                    for c in range(4):
                        last = nc.scalar.activation(q4[:, c, :], misc[:, 0:N], ACT.Identity, bias=bq4[:, c:c + 1],
                                                    scale=g.c("quarter")[:, c:c + 1])
                    last.then_inc(qk_saved, 1)
                    act.wait_ge(v_ready, it + 1)
                    nc.scalar.copy(v[:, :, :], O[:, 0:TPB * D].rearrange("p (u d) -> p u d", u=TPB)).then_inc(v_saved, 1)
                    for i in range(PAIRS + 1):
                        if i < PAIRS:
                            exps(it, i)
                        if i >= 1:
                            save(it, i - 1)
                    act.wait_ge(on_turned, it + 1)
                    nc.scalar.copy(onT[:, :], misc[:, 0:N]).then_inc(onT_ready, 1)


L3_HID = 512
L3_C = L3_HID // P
L3F_PARTS = [("w1", L3_HID), ("w2", L3_HID), ("h1", L3_C * L3_HID), ("h2", L3_C * L3_HID), ("w3", L3_C * D),
             ("s1", L3_C), ("s2", L3_C), ("sh1", L3_C), ("sh2", L3_C), ("s3", D)]


def l3_ffn(nc, g, name):
    cols, width = columns(L3F_PARTS)
    C = L3_C
    N = 512
    JT = N // P
    NS = 2
    with Stage(nc, name) as st:
        w = st.sb("w", [P, width])
        XT = st.sb("XT", [P, TOKENS])
        row_statistics(nc, g, name, [(w[:, :], g.dram["w_l3f"])])
        turn_stream(nc, g, name, XT)
        h1 = w[:, cols["h1"]].rearrange("p (k o) -> p k o", k=C)
        h2 = w[:, cols["h2"]].rearrange("p (k o) -> p k o", k=C)
        w3 = w[:, cols["w3"]].rearrange("p (k o) -> p k o", k=C)
        silu = [st.sb(f"silu{s}", [P, C, N]) for s in range(NS)]
        hid = [st.sb(f"hid{s}", [P, C, N]) for s in range(NS)]
        gelu1 = [st.sb(f"gelu1{s}", [P, C, N]) for s in range(NS)]
        gelu2 = [st.sb(f"gelu2{s}", [P, C, N]) for s in range(NS)]
        scaled = [st.sb(f"scaled{s}", [P, N]) for s in range(NS)]
        bank = [[st.ps(f"bank{s}_{c}", [P, N]) for c in range(C)] for s in range(NS)]
        slot_free = st.sems("slot_free", NS)
        a_ready = st.sems("a_ready", NS)
        b_ready = st.sems("b_ready", NS)
        silu_done = st.sems("silu_done", NS)
        hid_ready = st.sems("hid_ready", NS)
        sq1_ready = st.sems("sq1_ready", NS)
        gelu1_done = st.sems("gelu1_done", NS)
        sq2_ready = st.sems("sq2_ready", NS)
        gelu2_done = st.sems("gelu2_done", NS)
        out_ready = st.sems("out_ready", NS)
        scale_done = st.sems("scale_done", NS)
        with nc.Block() as block:
            @block.tensor
            def _(pe):
                for s in range(NS):
                    pe.sem_inc(slot_free[s], 1)
                with pe.Fori(0, TOKENS // N // NS) as it:
                    for c in range(C):
                        for s in range(NS):
                            x = XT[:, bass.ds((it * NS + s) * N, N)]
                            if c == 0:
                                pe.wait_ge(slot_free[s], it + 1)
                            if c >= 2:
                                pe.wait_ge(hid_ready[s], it * C + c - 1)
                            nc.tensor.matmul(bank[s][c % 2][:, :], w[:, cols["w1"]][:, c * P:(c + 1) * P], x, start=True,
                                             stop=True).then_inc(a_ready[s], 1)
                            nc.tensor.matmul(bank[s][2 + c % 2][:, :], w[:, cols["w2"]][:, c * P:(c + 1) * P], x, start=True,
                                             stop=True).then_inc(b_ready[s], 1)
                    for layer, src, needs, ready in ((h1, hid, hid_ready, sq1_ready), (h2, gelu1, gelu1_done, sq2_ready)):
                        for s in range(NS):
                            pe.wait_ge(needs[s], it * C + C)
                            for c in range(C):
                                for k in range(C):
                                    last = nc.tensor.matmul(bank[s][c][:, :], layer[:, k, c * P:(c + 1) * P], src[s][:, k, :],
                                                            start=(k == 0), stop=(k == C - 1))
                                last.then_inc(ready[s], 1)
                    for s in range(NS):
                        pe.wait_ge(gelu2_done[s], it * C + C)
                        for j in range(JT):
                            for k in range(C):
                                last = nc.tensor.matmul(bank[s][0][:, j * D:(j + 1) * D], gelu2[s][:, k, j * P:(j + 1) * P],
                                                        w3[:, k, :], start=(k == 0), stop=(k == C - 1))
                        last.then_inc(out_ready[s], 1)

            @block.scalar
            def _(act):
                with act.Fori(0, TOKENS // N // NS) as it:
                    for c in range(C):
                        for s in range(NS):
                            act.wait_ge(a_ready[s], it * C + c + 1)
                            nc.scalar.activation(silu[s][:, c, :], bank[s][c % 2][:, :], ACT.Silu,
                                                 scale=w[:, cols["s1"]][:, c:c + 1]).then_inc(silu_done[s], 1)
                    for dst, scale, ready, done in ((gelu1, "sh1", sq1_ready, gelu1_done), (gelu2, "sh2", sq2_ready, gelu2_done)):
                        for s in range(NS):
                            for c in range(C):
                                act.wait_ge(ready[s], it * C + c + 1)
                                nc.scalar.activation(dst[s][:, c, :], bank[s][c][:, :], ACT.Gelu,
                                                     scale=w[:, cols[scale]][:, c:c + 1]).then_inc(done[s], 1)

            @block.vector
            def _(dve):
                with dve.Fori(0, TOKENS // N // NS) as it:
                    for c in range(C):
                        for s in range(NS):
                            dve.wait_ge(silu_done[s], it * C + c + 1)
                            dve.wait_ge(b_ready[s], it * C + c + 1)
                            nc.vector.scalar_tensor_tensor(hid[s][:, c, :], bank[s][2 + c % 2][:, :],
                                                           w[:, cols["s2"]][:, c:c + 1], silu[s][:, c, :],
                                                           ALU.mult, ALU.mult).then_inc(hid_ready[s], 1)
                    for s in range(NS):
                        dve.wait_ge(out_ready[s], it + 1)
                        nc.vector.tensor_tensor(scaled[s][:, :].rearrange("p (j d) -> p j d", j=JT),
                                                bank[s][0][:, :].rearrange("p (j d) -> p j d", j=JT),
                                                w[:, cols["s3"]].unsqueeze(1).broadcast_to([P, JT, D]),
                                                ALU.mult).then_inc(scale_done[s], 1)
                    for s in range(NS):
                        x = g.X[:, bass.ds((it * NS + s) * JT, JT), :].rearrange("p t d -> p (t d)")
                        dve.wait_ge(scale_done[s], it + 1)
                        nc.vector.scalar_tensor_tensor(x, scaled[s][:, :], 0.5, x, ALU.mult, ALU.add).then_inc(slot_free[s], 1)


L3A_HEADS, L3A_HD, L3A_TAPS, L3A_INNER = 16, 8, 4, 345
L3A_ALPHA_BIAS = 4.0
L3A_PARTS = [("wq", D), ("wk", D), ("wv", D), ("wba", 2 * L3A_HEADS), ("wo", D), ("wg", L3A_INNER), ("wu", L3A_INNER),
             ("wd", 3 * D), ("norm1", D), ("norm2", D), ("taps", L3A_TAPS), ("conv_b", 1)]


def l3_attn(nc, g, name):
    H, HD = L3A_HEADS, L3A_HD
    cols, width = columns(L3A_PARTS)
    N = SEQ
    NS = 2
    G = BATCH * H // P
    STEP = 32
    ROUNDS = SEQ // STEP
    PAD = L3A_TAPS - 1
    inner = [(c * P, min(P, L3A_INNER - c * P)) for c in range(3)]
    with Stage(nc, name) as st:
        w = st.sb("w", [P, width])
        scale = st.sb("scale", [P, TILES])
        row_statistics(nc, g, name, [(w[:, :], g.dram["w_l3a"])])
        rms_scales(nc, g, name, scale[:, :])
        qkv_d = nc.dram_tensor(name + "_qkv", (3, BATCH, P, N), F32, kind="Internal").ap()
        gates_d = nc.dram_tensor(name + "_gates", (2, BATCH, H, N), F32, kind="Internal").ap()
        o_d = nc.dram_tensor(name + "_o", (BATCH, P, N), F32, kind="Internal").ap()

        with Stage(nc, name + "_a") as sa:
            x0 = [sa.sb(f"x0{s}", [P, TPB, D]) for s in range(NS)]
            xn = [sa.sb(f"xn{s}", [P, TPB, D]) for s in range(NS)]
            xT = [sa.sb(f"xT{s}", [P, PAD + N]) for s in range(NS)]
            conv = [sa.sb(f"conv{s}", [P, L3A_TAPS, N]) for s in range(NS)]
            xc = [sa.sb(f"xc{s}", [P, N]) for s in range(NS)]
            qkv = [sa.sb(f"qkv{s}", [P, 3, N]) for s in range(NS)]
            gates = [sa.sb(f"gates{s}", [2 * H, N]) for s in range(NS)]
            turn = [sa.ps(f"turn{s}", [P, 512]) for s in range(NS)]
            qk = [sa.ps(f"qk{s}", [P, 512]) for s in range(NS)]
            vg = [sa.ps(f"vg{s}", [P, 512]) for s in range(NS)]
            x0_ready = sa.sems("x0_ready", NS)
            xn_ready = sa.sems("xn_ready", NS)
            turned = sa.sems("turned", NS)
            xT_ready = sa.sems("xT_ready", NS)
            conv_step = sa.sems("conv_step", NS)
            xc_ready = sa.sems("xc_ready", NS)
            proj_ready = sa.sems("proj_ready", NS)
            saved = sa.sems("saved", NS)
            stored = sa.sems("stored", NS)
            with nc.Block() as block:
                @block.vector
                def _(dve):
                    for s in range(NS):
                        nc.vector.memset(xT[s][:, 0:PAD], 0.0).then_inc(conv_step[s], 1)
                    for s in range(NS):
                        dve.sem_inc(stored[s], 1)
                    with dve.Fori(0, BATCH // NS) as it:
                        for s in range(NS):
                            dve.wait_ge(stored[s], it * 48 + 1)
                            for u in range(TPB):
                                t = (it * NS + s) * TPB + u
                                last = nc.vector.tensor_scalar(x0[s][:, u, :], g.tile(t), g.mean[:, bass.ds(t, 1)],
                                                               scale[:, bass.ds(t, 1)], ALU.subtract, ALU.mult)
                            last.then_inc(x0_ready[s], 1)
                        for s in range(NS):
                            dve.wait_ge(x0_ready[s], it + 1)
                            nc.vector.tensor_tensor(xn[s][:, :, :], x0[s][:, :, :],
                                                    w[:, cols["norm1"]].unsqueeze(1).broadcast_to([P, TPB, D]),
                                                    ALU.mult).then_inc(xn_ready[s], 1)
                        for j in range(L3A_TAPS):
                            for s in range(NS):
                                tap = w[:, cols["taps"]][:, j:j + 1]
                                if j == 0:
                                    dve.wait_ge(xT_ready[s], it + 1)
                                    nc.vector.tensor_scalar(conv[s][:, 0, :], xT[s][:, 0:N], tap, w[:, cols["conv_b"]],
                                                            ALU.mult, ALU.add).then_inc(conv_step[s], 1)
                                else:
                                    dve.wait_ge(conv_step[s], it * L3A_TAPS + j + 1)
                                    nc.vector.scalar_tensor_tensor(conv[s][:, j, :], xT[s][:, j:j + N], tap,
                                                                   conv[s][:, j - 1, :], ALU.mult, ALU.add
                                                                   ).then_inc(conv_step[s], 1)

                @block.tensor
                def _(pe):
                    with pe.Fori(0, BATCH // NS) as it:
                        for s in range(NS):
                            pe.wait_ge(xn_ready[s], it + 1)
                            for u in range(TPB):
                                last = nc.tensor.transpose(turn[s][:, u * P:(u + 1) * P], xn[s][:, u, :], g.c("ident"))
                            last.then_inc(turned[s], 1)
                        for s in range(NS):
                            pe.wait_ge(xc_ready[s], it + 1)
                            nc.tensor.matmul(qk[s][:, 0:N], w[:, cols["wq"]], xc[s][:, :], start=True, stop=True)
                            nc.tensor.matmul(qk[s][:, N:2 * N], w[:, cols["wk"]], xc[s][:, :], start=True, stop=True)
                            nc.tensor.matmul(vg[s][:, 0:N], w[:, cols["wv"]], xc[s][:, :], start=True, stop=True)
                            nc.tensor.matmul(vg[s][0:2 * H, N:2 * N], w[:, cols["wba"]], xc[s][:, :], start=True,
                                             stop=True).then_inc(proj_ready[s], 1)

                @block.scalar
                def _(act):
                    with act.Fori(0, BATCH // NS) as it:
                        for s in range(NS):
                            if s == 0:
                                for z in range(NS):
                                    act.wait_ge(conv_step[z], 1)
                            act.wait_ge(turned[s], it + 1)
                            nc.scalar.copy(xT[s][:, PAD:PAD + N], turn[s][:, 0:N]).then_inc(xT_ready[s], 1)
                        for s in range(NS):
                            act.wait_ge(conv_step[s], it * L3A_TAPS + L3A_TAPS + 1)
                            nc.scalar.activation(xc[s][:, :], conv[s][:, L3A_TAPS - 1, :], ACT.Silu).then_inc(xc_ready[s], 1)
                        for s in range(NS):
                            act.wait_ge(proj_ready[s], it + 1)
                            nc.scalar.copy(qkv[s][:, 0:2, :], qk[s][:, :].rearrange("p (k t) -> p k t", k=2))
                            nc.scalar.copy(qkv[s][:, 2, :], vg[s][:, 0:N])
                            nc.scalar.copy(gates[s][:, :], vg[s][0:2 * H, N:2 * N]).then_inc(saved[s], 1)

                @block.sync
                def _(sp):
                    with sp.Fori(0, BATCH // NS) as it:
                        for s in range(NS):
                            b = it * NS + s
                            sp.wait_ge(saved[s], it + 1)
                            sp.dma_start(qkv_d[:, bass.ds(b, 1), :, :].rearrange("k b p t -> p (k b) t"), qkv[s][:, :, :]
                                         ).then_inc(stored[s], 16)
                            for k in range(2):
                                sp.dma_start(gates_d[k, bass.ds(b, 1), :, :].rearrange("b h t -> (b h) t"),
                                             gates[s][k * H:(k + 1) * H, :]).then_inc(stored[s], 16)
                    for s in range(NS):
                        sp.wait_ge(stored[s], BATCH // NS * 48 + 1)

        with Stage(nc, name + "_s") as ss:
            qkv = ss.sb("qkv", [P, 3, G, HD, N])
            kg = ss.sb("kg", [P, G, HD, N])
            gates = ss.sb("gates", [P, 2, G, N])
            both = ss.sb("both", [P, G, N])
            length = ss.sb("length", [P, 2, G, N])
            hist = [ss.sb(f"hist{z}", [P, STEP + 1, G, HD, HD]) for z in range(2)]
            prod = ss.sb("prod", [P, 2, G, HD, HD])
            pred = ss.sb("pred", [P, G, HD])
            delta = ss.sb("delta", [P, G, HD])
            outer = ss.sb("outer", [P, G, HD, HD])
            read = ss.sb("read", [P, STEP, HD, HD])
            o = ss.sb("o", [P, G, HD, N])
            loaded = ss.sem("loaded")
            gates_done = ss.sem("gates_done")
            step = ss.sem("step")
            squared = ss.sem("squared")
            rooted = ss.sem("rooted")
            ready = ss.sem("ready")
            cell = ss.sem("cell")
            round_done = ss.sem("round_done")
            read_done = ss.sem("read_done")
            summed = ss.sem("summed")
            stored = ss.sem("stored")
            q, k, v = (qkv[:, i, :, :, :] for i in range(3))
            CELLS = 6

            def over_d(a):
                return a.unsqueeze(2).broadcast_to([P, G, HD, N])

            with nc.Block() as block:
                @block.sync
                def _(sp):
                    for i in range(3):
                        sp.dma_start(qkv[:, i, :, :, :].rearrange("p g d t -> p g (d t)"),
                                     qkv_d[i].rearrange("(g b) (h d) t -> (b h) g (d t)", g=G, h=H)).then_inc(loaded, 16)
                    for i in range(2):
                        sp.dma_start(gates[:, i, :, :], gates_d[i].rearrange("(g b) h t -> (b h) g t", g=G)).then_inc(loaded, 16)
                    sp.wait_ge(summed, ROUNDS * G)
                    sp.dma_start(o_d.rearrange("(g b) (h d) t -> (b h) g (d t)", g=G, h=H),
                                 o[:, :, :, :].rearrange("p g d t -> p g (d t)")).then_inc(stored, 16)
                    sp.wait_ge(stored, 16)

                @block.scalar
                def _(act):
                    act.wait_ge(loaded, 80)
                    nc.scalar.activation(gates[:, 0, :, :], gates[:, 0, :, :], ACT.Sigmoid)
                    nc.scalar.activation(gates[:, 1, :, :], gates[:, 1, :, :], ACT.Sigmoid,
                                         bias=g.c("alpha_bias")).then_inc(gates_done, 1)
                    act.wait_ge(squared, 1)
                    nc.scalar.activation(length[:, :, :, :], length[:, :, :, :], ACT.Sqrt, bias=g.c("eps_l2")).then_inc(rooted, 1)

                @block.vector
                def _(dve):
                    square = hist[0][:, 0:STEP, :, :, :].rearrange("p s g a b -> p (s g a b)").rearrange(
                        "p (g d t) -> p g d t", g=G, d=HD)
                    dve.wait_ge(loaded, 80)
                    for i, a in enumerate((q, k)):
                        if i:
                            dve.wait_ge(step, 2)
                        nc.vector.tensor_tensor(square, a, a, ALU.mult).then_inc(step, 1)
                        dve.wait_ge(step, 2 * i + 1)
                        last = nc.vector.tensor_reduce(length[:, i, :, :], square.rearrange("p g d t -> p g t d"), AX.X, ALU.add)
                        last.then_inc(squared if i else step, 1)
                    dve.wait_ge(rooted, 1)
                    nc.vector.reciprocal(length[:, :, :, :], length[:, :, :, :]).then_inc(step, 1)
                    dve.wait_ge(step, 4)
                    nc.vector.tensor_tensor(q, q, over_d(length[:, 0, :, :]), ALU.mult)
                    nc.vector.tensor_tensor(k, k, over_d(length[:, 1, :, :]), ALU.mult).then_inc(step, 1)
                    dve.wait_ge(gates_done, 1)
                    nc.vector.tensor_tensor(v, v, over_d(gates[:, 0, :, :]), ALU.mult).then_inc(step, 1)
                    nc.vector.tensor_tensor(both[:, :, :], gates[:, 0, :, :], gates[:, 1, :, :], ALU.mult).then_inc(step, 1)
                    dve.wait_ge(step, 7)
                    nc.vector.tensor_tensor(kg[:, :, :, :], k, over_d(both[:, :, :]), ALU.mult).then_inc(step, 1)
                    nc.vector.memset(hist[1][:, STEP, :, :, :], 0.0).then_inc(step, 1)
                    dve.wait_ge(step, 9)

                    def readout(r, z):
                        for gi in range(G):
                            dve.wait_ge(read_done, (r * 2 + z) * G + gi + 1)
                            nc.vector.tensor_reduce(o[:, gi, :, bass.ds((r * 2 + z) * STEP, STEP)].rearrange("p d t -> p t d"),
                                                    read[:, :, :, :], AX.X, ALU.add).then_inc(summed, 1)

                    with dve.Fori(0, ROUNDS // 2) as r:
                        for z in range(2):
                            for i in range(STEP):
                                t = (r * 2 + z) * STEP + i
                                done = ((r * 2 + z) * STEP + i) * CELLS
                                old = hist[z][:, i, :, :, :] if i else hist[1 - z][:, STEP, :, :, :]
                                new = hist[z][:, i + 1, :, :, :]

                                def along_k(a):
                                    return a[:, :, :, bass.ds(t, 1)].rearrange("p g d t -> p g (t d)").unsqueeze(2).broadcast_to(
                                        [P, G, HD, HD])

                                if i or z:
                                    dve.wait_ge(cell, done)
                                else:
                                    dve.wait_ge(ready, r + 1)
                                nc.vector.tensor_tensor(prod[:, 0, :, :, :], old, along_k(kg), ALU.mult).then_inc(cell, 1)
                                dve.wait_ge(cell, done + 1)
                                nc.vector.tensor_reduce(pred[:, :, :], prod[:, 0, :, :, :], AX.X, ALU.add,
                                                        negate=True).then_inc(cell, 1)
                                dve.wait_ge(cell, done + 2)
                                nc.vector.tensor_tensor(delta[:, :, :], pred[:, :, :],
                                                        v[:, :, :, bass.ds(t, 1)].rearrange("p g d t -> p g (d t)"),
                                                        ALU.add).then_inc(cell, 1)
                                dve.wait_ge(cell, done + 3)
                                nc.vector.tensor_tensor(outer[:, :, :, :],
                                                        delta[:, :, :].unsqueeze(3).broadcast_to([P, G, HD, HD]),
                                                        along_k(k), ALU.mult).then_inc(cell, 1)
                                dve.wait_ge(cell, done + 4)
                                if i == 0:
                                    pass
                                for gi in range(G):
                                    last = nc.vector.scalar_tensor_tensor(
                                        new[:, gi, :, :], old[:, gi, :, :], gates[:, 1, gi, bass.ds(t, 1)], outer[:, gi, :, :],
                                        ALU.mult, ALU.add)
                                    last.then_inc(cell, 1)
                            dve.wait_ge(cell, ((r * 2 + z) * STEP + STEP) * CELLS)
                            dve.sem_inc(round_done, 1)
                            readout(r, z)
                        dve.sem_inc(ready, 1)

                @block.gpsimd
                def _(pool):
                    with pool.Fori(0, ROUNDS // 2) as r:
                        for z in range(2):
                            pool.wait_ge(round_done, r * 2 + z + 1)
                            for gi in range(G):
                                if gi:
                                    pool.wait_ge(summed, (r * 2 + z) * G + gi)
                                qt = q[:, gi, :, bass.ds((r * 2 + z) * STEP, STEP)].rearrange("p d t -> p t d").unsqueeze(
                                    2).broadcast_to([P, STEP, HD, HD])
                                nc.gpsimd.tensor_tensor(read[:, :, :, :], hist[z][:, 1:STEP + 1, gi, :, :], qt,
                                                        ALU.mult).then_inc(read_done, 1)

                @block.tensor
                def _(pe):
                    pe.sem_inc(ready, 1)

        hid = st.sb("hid", [P, TILES, D])
        hscale = st.sb("hscale", [P, TILES])
        with Stage(nc, name + "_h") as sh:
            x1 = [sh.sb(f"x1{s}", [P, TPB, D]) for s in range(NS)]
            oT = [sh.sb(f"oT{s}", [P, N]) for s in range(NS)]
            hs = [sh.sb(f"hs{s}", [P, TPB, D]) for s in range(NS)]
            square = [sh.sb(f"square{s}", [P, TPB, D]) for s in range(NS)]
            mix = [sh.ps(f"mix{s}", [P, 512]) for s in range(NS)]
            o_loaded = sh.sems("o_loaded", NS)
            slot_free = sh.sems("slot_free", NS)
            mix_ready = sh.sems("mix_ready", NS)
            x1_ready = sh.sems("x1_ready", NS)
            h_ready = sh.sems("h_ready", NS)
            rooted = sh.sem("rooted")
            with nc.Block() as block:
                @block.sync
                def _(sp):
                    for s in range(NS):
                        sp.sem_inc(slot_free[s], 1)
                    with sp.Fori(0, BATCH // NS) as it:
                        for s in range(NS):
                            sp.wait_ge(slot_free[s], it + 1)
                            sp.dma_start(oT[s][:, :], o_d[bass.ds(it * NS + s, 1), :, :].rearrange("b p t -> (b p) t")
                                         ).then_inc(o_loaded[s], 16)

                @block.tensor
                def _(pe):
                    with pe.Fori(0, BATCH // NS) as it:
                        for s in range(NS):
                            pe.wait_ge(o_loaded[s], it * 16 + 16)
                            for u in range(TPB):
                                last = nc.tensor.matmul(mix[s][:, u * D:(u + 1) * D], oT[s][:, u * P:(u + 1) * P],
                                                        w[:, cols["wo"]], start=True, stop=True)
                            last.then_inc(mix_ready[s], 1)

                @block.vector
                def _(dve):
                    with dve.Fori(0, BATCH // NS) as it:
                        for s in range(NS):
                            dve.wait_ge(mix_ready[s], it + 1)
                            for u in range(TPB):
                                t = (it * NS + s) * TPB + u
                                last = nc.vector.tensor_scalar(x1[s][:, u, :], g.tile(t), g.mean[:, bass.ds(t, 1)],
                                                               g.rstd[:, bass.ds(t, 1)], ALU.subtract, ALU.mult)
                            last.then_inc(x1_ready[s], 1)
                        for s in range(NS):
                            t = (it * NS + s) * TPB
                            dve.wait_ge(x1_ready[s], it + 1)
                            nc.vector.tensor_tensor(hid[:, bass.ds(t, TPB), :].rearrange("p u d -> p (u d)"),
                                                    x1[s][:, :, :].rearrange("p u d -> p (u d)"),
                                                    mix[s][:, 0:TPB * D], ALU.add).then_inc(h_ready[s], 1)
                    dve.wait_ge(rooted, 1)
                    nc.vector.reciprocal(hscale[:, :], hscale[:, :]).then_inc(rooted, 1)

                @block.scalar
                def _(act):
                    with act.Fori(0, BATCH // NS) as it:
                        for s in range(NS):
                            act.wait_ge(h_ready[s], it + 1)
                            for u in range(TPB):
                                t = (it * NS + s) * TPB + u
                                last = nc.scalar.activation(square[s][:, u, :], hid[:, bass.ds(t, 1), :], ACT.Square,
                                                            accum_out=hscale[:, bass.ds(t, 1)])
                            last.then_inc(slot_free[s], 1)
                    for s in range(NS):
                        act.wait_ge(slot_free[s], BATCH // NS + 1)
                    nc.scalar.activation(hscale[:, :], hscale[:, :], ACT.Sqrt, scale=1.0 / D, bias=g.c("eps_l2")).then_inc(rooted, 1)

        with Stage(nc, name + "_f") as sf:
            h0 = [sf.sb(f"h0{s}", [P, D]) for s in range(NS)]
            hn = [sf.sb(f"hn{s}", [P, D]) for s in range(NS)]
            hT = [sf.sb(f"hT{s}", [P, P]) for s in range(NS)]
            silu = [sf.sb(f"silu{s}", [P, 3, P]) for s in range(NS)]
            act_ = [sf.sb(f"act{s}", [P, 3, P]) for s in range(NS)]
            total = [sf.sb(f"total{s}", [P, D]) for s in range(NS)]
            turn = [sf.ps(f"turn{s}", [P, 512]) for s in range(NS)]
            gate = [sf.ps(f"gate{s}", [P, 512]) for s in range(NS)]
            up = [sf.ps(f"up{s}", [P, 512]) for s in range(NS)]
            slot_free = sf.sems("slot_free", NS)
            h0_ready = sf.sems("h0_ready", NS)
            hn_ready = sf.sems("hn_ready", NS)
            turned = sf.sems("turned", NS)
            hT_ready = sf.sems("hT_ready", NS)
            gate_ready = sf.sems("gate_ready", NS)
            up_ready = sf.sems("up_ready", NS)
            silu_done = sf.sems("silu_done", NS)
            act_ready = sf.sems("act_ready", NS)
            down_ready = sf.sems("down_ready", NS)
            total_ready = sf.sems("total_ready", NS)
            with nc.Block() as block:
                @block.vector
                def _(dve):
                    for s in range(NS):
                        dve.sem_inc(slot_free[s], 1)
                    with dve.Fori(0, TILES // NS) as it:
                        for s in range(NS):
                            t = it * NS + s
                            dve.wait_ge(slot_free[s], it + 1)
                            nc.vector.tensor_scalar(h0[s][:, :], hid[:, bass.ds(t, 1), :], hscale[:, bass.ds(t, 1)], None,
                                                    ALU.mult).then_inc(h0_ready[s], 1)
                        for s in range(NS):
                            dve.wait_ge(h0_ready[s], it + 1)
                            nc.vector.tensor_tensor(hn[s][:, :], h0[s][:, :], w[:, cols["norm2"]], ALU.mult).then_inc(hn_ready[s], 1)
                        for s in range(NS):
                            dve.wait_ge(silu_done[s], it + 1)
                            dve.wait_ge(up_ready[s], it + 1)
                            for c, (at, m) in enumerate(inner):
                                last = nc.vector.tensor_tensor(act_[s][0:m, c, :], silu[s][0:m, c, :],
                                                               up[s][0:m, c * P:(c + 1) * P], ALU.mult)
                            last.then_inc(act_ready[s], 1)
                        for s in range(NS):
                            t = it * NS + s
                            dve.wait_ge(down_ready[s], it + 1)
                            nc.vector.tensor_tensor(total[s][:, :], turn[s][:, 128:256],
                                                    hid[:, bass.ds(t, 1), :].rearrange("p t d -> p (t d)"), ALU.add
                                                    ).then_inc(total_ready[s], 1)
                        for s in range(NS):
                            t = it * NS + s
                            x = g.tile(t).rearrange("p t d -> p (t d)")
                            dve.wait_ge(total_ready[s], it + 1)
                            nc.vector.tensor_tensor(x, x, total[s][:, :], ALU.add).then_inc(slot_free[s], 1)

                @block.tensor
                def _(pe):
                    with pe.Fori(0, TILES // NS) as it:
                        for s in range(NS):
                            pe.wait_ge(hn_ready[s], it + 1)
                            nc.tensor.transpose(turn[s][:, 0:P], hn[s][:, :], g.c("ident")).then_inc(turned[s], 1)
                        for s in range(NS):
                            pe.wait_ge(hT_ready[s], it + 1)
                            for bank, part, done in ((gate[s], "wg", gate_ready[s]), (up[s], "wu", up_ready[s])):
                                for c, (at, m) in enumerate(inner):
                                    last = nc.tensor.matmul(bank[0:m, c * P:(c + 1) * P], w[:, cols[part]][:, at:at + m],
                                                            hT[s][:, :], start=True, stop=True)
                                last.then_inc(done, 1)
                        for s in range(NS):
                            pe.wait_ge(act_ready[s], it + 1)
                            for c, (at, m) in enumerate(inner):
                                last = nc.tensor.matmul(turn[s][:, 128:256], act_[s][0:m, c, :],
                                                        w[0:m, cols["wd"]][:, c * D:(c + 1) * D], start=(c == 0), stop=(c == 2))
                            last.then_inc(down_ready[s], 1)

                @block.scalar
                def _(act):
                    with act.Fori(0, TILES // NS) as it:
                        for s in range(NS):
                            act.wait_ge(turned[s], it + 1)
                            nc.scalar.copy(hT[s][:, :], turn[s][:, 0:P]).then_inc(hT_ready[s], 1)
                        for s in range(NS):
                            act.wait_ge(gate_ready[s], it + 1)
                            for c, (at, m) in enumerate(inner):
                                last = nc.scalar.activation(silu[s][0:m, c, :], gate[s][0:m, c * P:(c + 1) * P], ACT.Silu)
                            last.then_inc(silu_done[s], 1)


PIPELINE = {0: (l0_ffn, "l0f"), 1: (l0_attn, "l0a"), 2: (l0_ffn, "l0f"),
            3: (l1_ffn, "l1f"), 4: (l1_attn, "l1a"), 5: (l1_ffn, "l1f"), 6: (l2_ffn, "l2f"), 7: (l2_attn, "l2a"), 8: (l2_ffn, "l2f"), 9: (l3_ffn, "l3f"), 10: (l3_attn, "l3a"),
            11: (l3_ffn, "l3f")}


def build(nc, dram, out):
    Stage.pool = [nc.alloc_semaphore(f"s{i}") for i in range(SEMAPHORES)]
    Stage.taken = 0
    with ExitStack() as ctx:
        g = Globals(nc, ctx, dram, out)
        load_stream(nc, g)
        for n in STEPS:
            step, name = PIPELINE[n]
            step(nc, g, f"{name}_{n}")
        store_stream(nc, g)


def constants():
    import numpy as np
    p = np.arange(P)[:, None]
    j = np.arange(P)[None, :]
    levels = []
    for k in range(1, 7):
        s = 1 << k
        c = np.arange(P // 2)[None, :]
        levels.append(p // s == 2 * (c // s) + 1)
    level1 = (p == j + 1) & (j % 2 == 0)
    rows = np.arange(P)[:, None]
    tables = {
        "ident": p == j, "ones": np.ones((P, P)), "iota": j + 0 * p, "rev_iota": P - j + 0 * p,
        "upto": p <= j, "after": p > j, "blocks8": p // 8 == j // 8, "heads8": p // 8 == np.arange(16)[None, :],
        "level1n": -1.0 * level1, "level": np.concatenate(levels, axis=1),
        "row_index": rows, "is_query": (rows % 8) < 4, "quarter": (rows % 32) // 8 == np.arange(4)[None, :],
        "minus_half": np.full((P, 8), -0.5),
        "dk_scale": np.where(np.arange(8) < L1A_HG, L1A_DK, 1.0) + 0.0 * p, "eps_ln": np.full((P, 1), LN_EPS), "eps_l2": np.full((P, 1), 1e-6),
        "causal": np.where(j <= p, 0.0, -1e30),
        "alpha_bias": np.full((P, 1), L3A_ALPHA_BIAS),
        "before8": np.broadcast_to((np.arange(8)[None, :] < np.arange(8)[:, None]).reshape(1, 64), (P, 64)),
    }
    return np.ascontiguousarray(np.concatenate([tables[n] for n, _ in CONST_PARTS], axis=1).astype(np.float32))


def lay_out(inputs):
    import numpy as np

    def rows(a):
        return np.broadcast_to(np.reshape(a, (1, -1)), (P, a.size))

    def side(*parts):
        return np.ascontiguousarray(np.concatenate(parts, axis=1))

    i = inputs
    arrays = {"x": np.ascontiguousarray(np.reshape(i["L0_attn_x"], (TOKENS, D))), "consts": constants()}
    we = np.reshape(np.transpose(i["L0_ffn_We"], (1, 0, 2)), (D, -1))
    arrays["w_l0f"] = side(i["L0_ffn_Wg"], we, rows(i["L0_ffn_bg"]), rows(i["L0_ffn_be"]))
    w_phi = i["L0_attn_weights"]
    phi = np.zeros((L0A_HEADS, L0A_HD, L0A_HEADS, L0A_HD), np.float32)
    for h in range(L0A_HEADS):
        phi[h, :, h, :] = w_phi[h].T
    arrays["w_l0a"] = side(i["L0_attn_Wq"].T, i["L0_attn_Wk"].T, i["L0_attn_Wv"].T, phi.reshape(D, D),
                           rows(i["L0_attn_bv"]), i["L0_attn_bq"][:, None], i["L0_attn_bk"][:, None])

    def chunks(a):
        return np.reshape(np.transpose(np.reshape(a, (-1, P, a.shape[1])), (1, 0, 2)), (P, -1))

    w1 = np.reshape(np.transpose(i["L2_ffn_w1"], (2, 0, 1)), (D, -1))
    w3 = np.reshape(np.transpose(i["L2_ffn_w3"], (2, 0, 1)), (D, -1))
    w2 = np.reshape(np.transpose(i["L2_ffn_w2"], (2, 0, 1)), (P, -1))
    arrays["w_l2f"] = side(i["L2_ffn_gate_w"].T, rows(i["L2_ffn_gate_bias"]), w1, i["L2_ffn_sw1"].T,
                           w3, i["L2_ffn_sw3"].T, w2, chunks(i["L2_ffn_sw2"].T))
    arrays["w_l3f"] = side(i["L3_ffn_w1_w"].T, i["L3_ffn_w2_w"].T, chunks(i["L3_ffn_h1_w"].T), chunks(i["L3_ffn_h2_w"].T),
                           chunks(i["L3_ffn_w3_w"].T), *[i["L3_ffn_" + s][:, None].reshape(L3_C, P).T
                                                         for s in ("w1_s", "w2_s", "h1_s", "h2_s")],
                           rows(i["L3_ffn_w3_s"]))
    arrays["w_l2a"] = side(*[i["L2_attn_" + n].T for n in ("Wq", "Wk", "Wv", "Wo")], rows(i["L2_attn_norm_w"]),
                           rows(i["L2_attn_bv"]), rows(i["L2_attn_bo"]), i["L2_attn_bq"][:, None], i["L2_attn_bk"][:, None])
    down = np.zeros((3 * P, D), np.float32)
    down[:L3A_INNER] = i["L3_attn_wd"]
    arrays["w_l3a"] = side(i["L3_attn_wq"], i["L3_attn_wk"], i["L3_attn_wv"], i["L3_attn_wb"], i["L3_attn_wa"],
                           i["L3_attn_wo"], i["L3_attn_wg"], i["L3_attn_wu"], chunks(down), rows(i["L3_attn_norm1_w"]),
                           rows(i["L3_attn_norm2_w"]), i["L3_attn_conv_w"], i["L3_attn_conv_b"][:, None])
    null_k = i["L1_ffn_null_kv"][0, :, :, 0, :]
    null_k = np.reshape(np.transpose(np.reshape(null_k, (L1_G, L1_C, 2, L1_DH)), (2, 3, 0, 1)), (P, -1))
    w_kv = i["L1_ffn_w_kv"]

    def by_group(a):
        return np.reshape(np.transpose(a, (2, 0, 1)), (D, -1))

    wo = np.reshape(i["L1_ffn_w_out"], (L1_G, D, L1_C, P))
    arrays["w_l1f"] = side(i["L1_ffn_w_qr"].T, i["L1_ffn_w_kvr"].T, by_group(i["L1_ffn_w_q"]),
                           by_group(w_kv[:, :L1_DI]), by_group(w_kv[:, L1_DI:]),
                           np.reshape(np.transpose(wo, (3, 0, 2, 1)), (P, -1)), null_k, rows(i["L1_ffn_null_token"]))
    arrays["null_v"] = np.ascontiguousarray(np.reshape(i["L1_ffn_null_kv"][1], (L1_G, L1_DI)))

    def by_heads(q, k, v):
        return np.concatenate([np.reshape(a, (a.shape[0], L1A_GROUPS, -1)) for a in (q, k, v)], axis=2)

    arrays["w_l1a_qkv"] = np.ascontiguousarray(by_heads(i["L1_attn_w_q"], i["L1_attn_w_k"], i["L1_attn_w_v"]))
    taps = by_heads(i["L1_attn_conv_q"].T, i["L1_attn_conv_k"].T, i["L1_attn_conv_v"].T)
    arrays["l1a_taps"] = np.ascontiguousarray(np.transpose(taps, (1, 0, 2))).reshape(-1)
    arrays["w_l1a"] = side(i["L1_attn_w_a"], i["L1_attn_w_b"], i["L1_attn_w_g"], chunks(i["L1_attn_w_out"]),
                           rows(i["L1_attn_dt_bias"]), rows(i["L1_attn_A_log"]), i["L1_attn_norm_w"][:, None])
    return arrays


def kernel(**inputs):
    import numpy as np
    import concourse.bacc as bacc
    from concourse.bass_utils import run_bass_kernel_spmd

    nc = bacc.Bacc("TRN2", target_bir_lowering=False, num_devices=1)
    arrays = lay_out({k: np.asarray(v) for k, v in inputs.items()})
    dram = {k: nc.dram_tensor(f"in_{k}", a.shape, mybir.dt.from_np(a.dtype), kind="ExternalInput").ap()
            for k, a in arrays.items()}
    out = nc.dram_tensor("out_x", (TOKENS, D), F32, kind="ExternalOutput").ap()
    build(nc, dram, out)
    r = run_bass_kernel_spmd(nc, [{f"in_{k}": a for k, a in arrays.items()}], core_ids=[0])
    return np.reshape(r.results[0]["out_x"], (BATCH, SEQ, D))
```

```python
from contextlib import ExitStack

import concourse.bass as bass
from concourse import mybir

F32 = mybir.dt.float32
ACT = mybir.ActivationFunctionType
ALU = mybir.AluOpType
AX = mybir.AxisListType

P = 128
D = 128
BATCH = 16
SEQ = 256
TOKENS = BATCH * SEQ
TILES = TOKENS // P
TPB = SEQ // P
LN_EPS = 1e-5
SEMAPHORES = 120
STEPS = tuple(range(12))

CONST_PARTS = [("ident", 128), ("ones", 128), ("iota", 128), ("rev_iota", 128), ("upto", 128),
               ("after", 128), ("blocks8", 128), ("heads8", 16), ("level1nT", 128), 
               ("level", 6 * 64), ("row_index", 1), ("is_query", 1), ("quarter", 4), ("minus_half", 8), ("dk_scale", 8),
               ("eps_ln", 1), ("eps_l2", 1), ("causal", 128), ("before8", 64), ("alpha_bias", 1)]
CONST_AT = {}
_at = 0
for _name, _width in CONST_PARTS:
    CONST_AT[_name] = (_at, _width)
    _at += _width
CONST_COLS = _at


class Stage:
    pool = []
    taken = 0

    def __init__(self, nc, name):
        self.nc, self.name, self.ctx, self.first = nc, name, ExitStack(), Stage.taken

    def __enter__(self):
        return self

    def sb(self, name, shape):
        return self.ctx.enter_context(self.nc.sbuf_tensor(f"{self.name}_{name}", shape, F32))

    def ps(self, name, shape):
        return self.ctx.enter_context(self.nc.psum_tensor(f"{self.name}_{name}", shape, F32))

    def sem(self, name):
        Stage.taken += 1
        return Stage.pool[Stage.taken - 1]

    def sems(self, name, n):
        return [self.sem(f"{name}{i}") for i in range(n)]

    def __exit__(self, kind, value, trace):
        if kind is None and Stage.taken > self.first:
            used = [s.num for s in Stage.pool[self.first:Stage.taken]]
            self.nc.all_engine_barrier(sems_to_clear=range(used[0], used[-1] + 1))
            Stage.taken = self.first
        self.ctx.close()


class Globals:

    def __init__(self, nc, ctx, dram, out):
        self.dram, self.out = dram, out
        self.X = ctx.enter_context(nc.sbuf_tensor("X", [P, TILES, D], F32))
        self.const = ctx.enter_context(nc.sbuf_tensor("const", [P, CONST_COLS], F32))
        self.mean = ctx.enter_context(nc.sbuf_tensor("mean", [P, TILES], F32))
        self.rstd = ctx.enter_context(nc.sbuf_tensor("rstd", [P, TILES], F32))

    def c(self, name):
        at, width = CONST_AT[name]
        return self.const[:, at:at + width]

    def tile(self, t):
        return self.X[:, bass.ds(t, 1), :]


def load_stream(nc, g):
    with Stage(nc, "load") as st:
        s_in = st.sem("in")
        with nc.Block() as block:
            @block.sync
            def _(sp):
                sp.dma_start(g.X[:, :, :], g.dram["x"].rearrange("(t p) d -> p t d", p=P)).then_inc(s_in, 16)
                sp.dma_start(g.const[:, :], g.dram["consts"]).then_inc(s_in, 16)
                sp.wait_ge(s_in, 32)


def store_stream(nc, g):
    with Stage(nc, "store") as st:
        s_out = st.sem("out")
        with nc.Block() as block:
            @block.sync
            def _(sp):
                sp.dma_start(g.out.rearrange("(t p) d -> p t d", p=P), g.X[:, :, :]).then_inc(s_out, 16)
                sp.wait_ge(s_out, 16)


def row_statistics(nc, g, name, loads=()):
    with Stage(nc, name + "_stat") as st:
        parts = st.sb("parts", [P, TILES, 6])
        tmp = st.sb("tmp", [P, 3, TILES])
        s_load = st.sem("load")
        s_parts = st.sem("parts")
        s_step = st.sem("step")
        s_var = st.sem("var")
        s_std = st.sem("std")
        with nc.Block() as block:
            @block.sync
            def _(sp):
                for dst, src in loads:
                    sp.dma_start(dst, src).then_inc(s_load, 16)
                if loads:
                    sp.wait_ge(s_load, 16 * len(loads))

            @block.vector
            def _(dve):
                with dve.Fori(0, TILES // 8) as it:
                    for i in range(8):
                        t = it * 8 + i
                        nc.vector.bn_stats(parts[:, bass.ds(t, 1), :], g.X[:, bass.ds(t, 1), :]).then_inc(s_parts, 1)
                dve.wait_ge(s_parts, TILES)
                nc.vector.tensor_tensor(g.mean[:, :], parts[:, :, 1], parts[:, :, 4], ALU.add).then_inc(s_step, 1)
                nc.vector.tensor_tensor(tmp[:, 0, :], parts[:, :, 1], parts[:, :, 4], ALU.subtract).then_inc(s_step, 1)
                nc.vector.tensor_tensor(tmp[:, 1, :], parts[:, :, 2], parts[:, :, 5], ALU.add).then_inc(s_step, 1)
                dve.wait_ge(s_step, 3)
                nc.vector.tensor_scalar(g.mean[:, :], g.mean[:, :], 0.5, None, ALU.mult).then_inc(s_step, 1)
                nc.vector.scalar_tensor_tensor(tmp[:, 2, :], tmp[:, 0, :], 0.25, tmp[:, 0, :],
                                               ALU.mult, ALU.mult).then_inc(s_step, 1)
                dve.wait_ge(s_step, 5)
                nc.vector.scalar_tensor_tensor(tmp[:, 0, :], tmp[:, 1, :], 1.0 / D, tmp[:, 2, :],
                                               ALU.mult, ALU.add).then_inc(s_var, 1)
                dve.wait_ge(s_std, 1)
                nc.vector.reciprocal(g.rstd[:, :], tmp[:, 1, :]).then_inc(s_step, 1)

            @block.scalar
            def _(act):
                act.wait_ge(s_var, 1)
                nc.scalar.activation(tmp[:, 1, :], tmp[:, 0, :], ACT.Sqrt, bias=g.c("eps_ln")).then_inc(s_std, 1)


L0_EXPERTS = 8
L0F_PARTS = [("wg", 128), ("we", L0_EXPERTS * 128), ("bg", 128)]


def columns(parts):
    at, out = 0, {}
    for name, width in parts:
        out[name] = slice(at, at + width)
        at += width
    return out, at


def l0_ffn(nc, g, name):
    E = L0_EXPERTS
    cols, width = columns(L0F_PARTS)
    NS = 2
    ROUNDS = TILES // NS
    with Stage(nc, name) as st:
        w = st.sb("w", [P, width])
        be = st.sb("be", [E, D])
        row_statistics(nc, g, name, [(w[:, :], g.dram["w_l0f"]), (be[:, :], g.dram["l0f_be"])])
        xn = [st.sb(f"xn{s}", [P, D]) for s in range(NS)]
        xT = [st.sb(f"xT{s}", [P, P]) for s in range(NS)]
        logits = [st.sb(f"logits{s}", [P, D]) for s in range(NS)]
        neg_max = [st.sb(f"neg_max{s}", [P, 1]) for s in range(NS)]
        key = [st.sb(f"key{s}", [P, D]) for s in range(NS)]
        first = [st.sb(f"first{s}", [P, 1]) for s in range(NS)]
        gate = [st.sb(f"gate{s}", [P, E]) for s in range(NS)]
        gateT = [st.sb(f"gateT{s}", [E, P]) for s in range(NS)]
        prob = [st.sb(f"prob{s}", [P, D]) for s in range(NS)]
        total = [st.sb(f"total{s}", [P, 2]) for s in range(NS)]
        acc = [st.sb(f"acc{s}", [P, D]) for s in range(NS)]
        logit_bank = [st.ps(f"logit_bank{s}", [P, 512]) for s in range(NS)]
        pick_bank = [st.ps(f"pick_bank{s}", [P, 512]) for s in range(NS)]
        hidden = [st.ps(f"hidden{s}", [P, E * D]) for s in range(NS)]
        xn_ready = st.sems("xn_ready", NS)
        turned = st.sems("turned", NS)
        xT_ready = st.sems("xT_ready", NS)
        logits_ready = st.sems("logits_ready", NS)
        logits_saved = st.sems("logits_saved", NS)
        hidden_ready = st.sems("hidden_ready", NS)
        max_ready = st.sems("max_ready", NS)
        exp_done = st.sems("exp_done", NS)
        gate_step = st.sems("gate_step", NS)
        gate_turned = st.sems("gate_turned", NS)
        gateT_saved = st.sems("gateT_saved", NS)
        bias_ready = st.sems("bias_ready", NS)
        mix_step = st.sems("mix_step", NS)
        relu_done = st.sems("relu_done", NS)
        GATE_STEPS, MIX_STEPS = 5, E + 1

        def run(engine, ahead, rest):
            ahead(0)
            with engine.Fori(0, ROUNDS - 1) as it:
                rest(it, it + 1)
            rest(ROUNDS - 1, None)

        with nc.Block() as block:
            @block.vector
            def _(dve):
                def normed(it):
                    for s in range(NS):
                        t = it * NS + s
                        nc.vector.tensor_scalar(xn[s][:, :], g.tile(t), g.mean[:, bass.ds(t, 1)],
                                                g.rstd[:, bass.ds(t, 1)], ALU.subtract, ALU.mult).then_inc(xn_ready[s], 1)

                def rest(it, following):
                    for s in range(NS):
                        dve.wait_ge(logits_saved[s], it + 1)
                        nc.vector.tensor_reduce(neg_max[s][:, :], logits[s][:, :], AX.X, ALU.max,
                                                negate=True).then_inc(max_ready[s], 1)
                        nc.vector.tensor_reduce(total[s][:, 1:2], logits[s][:, :], AX.X,
                                                ALU.max).then_inc(gate_step[s], 1)
                    for s in range(NS):
                        dve.wait_ge(gate_step[s], it * GATE_STEPS + 1)
                        nc.vector.scalar_tensor_tensor(key[s][:, :], logits[s][:, :], total[s][:, 1:2],
                                                       g.c("rev_iota"), ALU.is_equal, ALU.mult).then_inc(gate_step[s], 1)
                    for s in range(NS):
                        dve.wait_ge(gate_step[s], it * GATE_STEPS + 2)
                        nc.vector.tensor_reduce(first[s][:, :], key[s][:, :], AX.X, ALU.max).then_inc(gate_step[s], 1)
                    for s in range(NS):
                        dve.wait_ge(gate_step[s], it * GATE_STEPS + 3)
                        nc.vector.tensor_scalar(key[s][:, :], g.c("rev_iota"), first[s][:, :], None,
                                                ALU.is_equal).then_inc(gate_step[s], 1)
                    for s in range(NS):
                        dve.wait_ge(gate_step[s], it * GATE_STEPS + 4)
                        nc.vector.tensor_reduce(gate[s][:, :], key[s][:, :].rearrange("p (k e) -> p e k", e=E),
                                                AX.X, ALU.add).then_inc(gate_step[s], 1)
                    if following is not None:
                        normed(following)
                    for e in range(E):
                        for s in range(NS):
                            h = hidden[s][:, e * D:(e + 1) * D]
                            if e == 0:
                                dve.wait_ge(gate_step[s], it * GATE_STEPS + 5)
                                dve.wait_ge(hidden_ready[s], it + 1)
                                nc.vector.tensor_scalar(acc[s][:, :], h, gate[s][:, 0:1], None, ALU.mult).then_inc(mix_step[s], 1)
                            else:
                                dve.wait_ge(mix_step[s], it * MIX_STEPS + e)
                                nc.vector.scalar_tensor_tensor(acc[s][:, :], h, gate[s][:, e:e + 1], acc[s][:, :],
                                                               ALU.mult, ALU.add).then_inc(mix_step[s], 1)
                    for s in range(NS):
                        dve.wait_ge(exp_done[s], it + 1)
                        nc.vector.reciprocal(total[s][:, 1:2], total[s][:, 0:1])
                        dve.wait_ge(bias_ready[s], it + 1)
                        dve.wait_ge(mix_step[s], it * MIX_STEPS + E)
                        nc.vector.tensor_tensor(acc[s][:, :], acc[s][:, :], pick_bank[s][:, 128:256], ALU.add).then_inc(mix_step[s], 1)
                    for s in range(NS):
                        dve.wait_ge(mix_step[s], it * MIX_STEPS + E + 1)
                        nc.vector.tensor_scalar(acc[s][:, :], acc[s][:, :], 0.0, total[s][:, 1:2],
                                                ALU.max, ALU.mult).then_inc(relu_done[s], 1)
                    for s in range(NS):
                        t = it * NS + s
                        dve.wait_ge(relu_done[s], it + 1)
                        nc.vector.scalar_tensor_tensor(g.tile(t), acc[s][:, :], 0.5, g.tile(t), ALU.mult, ALU.add)

                run(dve, normed, rest)

            @block.tensor
            def _(pe):
                def take_logits(it):
                    for s in range(NS):
                        pe.wait_ge(xn_ready[s], it + 1)
                        nc.tensor.transpose(logit_bank[s][:, 0:128], xn[s][:, :], g.c("ident")).then_inc(turned[s], 1)
                    for s in range(NS):
                        pe.wait_ge(xT_ready[s], it + 1)
                        nc.tensor.matmul(logit_bank[s][:, 128:256], xT[s][:, :], w[:, cols["wg"]], start=True, stop=False)
                        nc.tensor.matmul(logit_bank[s][:, 128:256], g.c("ones")[0:1, :], w[0:1, cols["bg"]],
                                         start=False, stop=True).then_inc(logits_ready[s], 1)

                def experts(it):
                    for s in range(NS):
                        if not isinstance(it, int):
                            pe.wait_ge(mix_step[s], it * MIX_STEPS)
                        for half in range(2):
                            last = nc.tensor.matmul(hidden[s][:, half * 512:half * 512 + 512], xT[s][:, :],
                                                    w[:, cols["we"]][:, half * 512:half * 512 + 512], start=True, stop=True)
                        last.then_inc(hidden_ready[s], 1)

                def ahead(it):
                    take_logits(it)
                    experts(it)

                def rest(it, following):
                    for s in range(NS):
                        pe.wait_ge(gate_step[s], it * GATE_STEPS + 5)
                        nc.tensor.transpose(pick_bank[s][0:E, 0:P], gate[s][:, :], g.c("ident")).then_inc(gate_turned[s], 1)
                    if following is not None:
                        take_logits(following)
                    for s in range(NS):
                        pe.wait_ge(gateT_saved[s], it + 1)
                        nc.tensor.matmul(pick_bank[s][:, 128:256], gateT[s][:, :], be[:, :], start=True, stop=True).then_inc(bias_ready[s], 1)
                    if following is not None:
                        experts(following)

                run(pe, ahead, rest)

            @block.scalar
            def _(act):
                def take_logits(it):
                    for s in range(NS):
                        act.wait_ge(turned[s], it + 1)
                        nc.scalar.copy(xT[s][:, :], logit_bank[s][:, 0:128]).then_inc(xT_ready[s], 1)
                    for s in range(NS):
                        act.wait_ge(logits_ready[s], it + 1)
                        nc.scalar.copy(logits[s][:, :], logit_bank[s][:, 128:256]).then_inc(logits_saved[s], 1)

                def rest(it, following):
                    for s in range(NS):
                        act.wait_ge(max_ready[s], it + 1)
                        nc.scalar.activation(prob[s][:, :], logits[s][:, :], ACT.Exp, bias=neg_max[s][:, :],
                                             accum_out=total[s][:, 0:1]).then_inc(exp_done[s], 1)
                    for s in range(NS):
                        act.wait_ge(gate_turned[s], it + 1)
                        nc.scalar.copy(gateT[s][:, :], pick_bank[s][0:E, 0:P]).then_inc(gateT_saved[s], 1)
                    if following is not None:
                        take_logits(following)

                run(act, take_logits, rest)


L0A_HEADS, L0A_HD = 16, 8
L0A_PARTS = [("wq", 128), ("wk", 128), ("wv", 128), ("phi", 128), ("bv", 128), ("bq", 1), ("bk", 1)]


def l0_attn(nc, g, name):
    cols, width = columns(L0A_PARTS)
    NS = 2
    N = SEQ
    last = BATCH // NS - 1
    with Stage(nc, name) as st:
        w = st.sb("w", [P, width])
        QT = st.sb("QT", [P, TOKENS])
        KT = st.sb("KT", [P, TOKENS])
        V = st.sb("V", [P, TILES, D])
        heads_scaled = st.sb("heads_scaled", [P, L0A_HEADS])
        norms = st.sb("norms", [P, 12])
        sums = [st.sb(f"sums{s}", [P, 2]) for s in range(NS)]
        row_statistics(nc, g, name, [(w[:, :], g.dram["w_l0a"])])

        with Stage(nc, name + "_a") as sa:
            xn = [sa.sb(f"xn{s}", [P, TPB, D]) for s in range(NS)]
            xT = [sa.sb(f"xT{s}", [P, N]) for s in range(NS)]
            square = [sa.sb(f"square{s}", [P, 2 * N]) for s in range(NS)]
            sq = [sa.sb(f"sq{s}", [P, 2]) for s in range(NS)]
            turn = [sa.ps(f"turn{s}", [P, 512]) for s in range(NS)]
            qk = [sa.ps(f"qk{s}", [P, 512]) for s in range(NS)]
            vps = [sa.ps(f"vps{s}", [P, 512]) for s in range(NS)]
            sums_clear = sa.sem("sums_clear")
            squares_added = sa.sems("squares_added", NS)
            xn_ready = sa.sems("xn_ready", NS)
            turned = sa.sems("turned", NS)
            xT_ready = sa.sems("xT_ready", NS)
            qk_ready = sa.sems("qk_ready", NS)
            v_ready = sa.sems("v_ready", NS)
            qk_saved = sa.sems("qk_saved", NS)
            v_saved = sa.sems("v_saved", NS)
            with nc.Block() as block:
                @block.vector
                def _(dve):
                    def norm(it, s):
                        for u in range(TPB):
                            t = (it * NS + s) * TPB + u
                            done = nc.vector.tensor_scalar(xn[s][:, u, :], g.tile(t), g.mean[:, bass.ds(t, 1)],
                                                           g.rstd[:, bass.ds(t, 1)], ALU.subtract, ALU.mult)
                        done.then_inc(xn_ready[s], 1)

                    def save_v(it, s):
                        dve.wait_ge(v_ready[s], it + 1)
                        nc.vector.tensor_copy(V[:, bass.ds((it * NS + s) * TPB, TPB), :],
                                              vps[s][:, 0:TPB * D].rearrange("p (u d) -> p u d", u=TPB)).then_inc(v_saved[s], 1)

                    def add_squares(it, s):
                        dve.wait_ge(qk_saved[s], it + 1)
                        nc.vector.tensor_tensor(sums[s][:, :], sums[s][:, :], sq[s][:, :], ALU.add).then_inc(squares_added[s], 1)

                    for s in range(NS):
                        nc.vector.memset(sums[s][:, :], 0.0).then_inc(sums_clear, 1)
                    for s in range(NS):
                        norm(0, s)
                    dve.wait_ge(sums_clear, NS)
                    with dve.Fori(0, last) as it:
                        for s in range(NS):
                            dve.wait_ge(turned[s], it + 1)
                            norm(it + 1, s)
                            save_v(it, s)
                            add_squares(it, s)
                            dve.wait_ge(squares_added[s], it + 1)
                    for s in range(NS):
                        save_v(last, s)
                        add_squares(last, s)

                @block.tensor
                def _(pe):
                    def turn_tokens(it, s):
                        pe.wait_ge(xn_ready[s], it + 1)
                        for u in range(TPB):
                            done = nc.tensor.transpose(turn[s][:, u * P:(u + 1) * P], xn[s][:, u, :], g.c("ident"))
                        done.then_inc(turned[s], 1)

                    def project(it, s):
                        pe.wait_ge(xT_ready[s], it + 1)
                        nc.tensor.matmul(qk[s][:, 0:N], w[:, cols["wq"]], xT[s][:, :], start=True, stop=True)
                        nc.tensor.matmul(qk[s][:, N:2 * N], w[:, cols["wk"]], xT[s][:, :], start=True,
                                         stop=True).then_inc(qk_ready[s], 1)
                        for u in range(TPB):
                            o = vps[s][:, u * D:(u + 1) * D]
                            nc.tensor.matmul(o, xT[s][:, u * P:(u + 1) * P], w[:, cols["wv"]], start=True, stop=False)
                            done = nc.tensor.matmul(o, g.c("ones")[0:1, :], w[0:1, cols["bv"]], start=False, stop=True)
                        done.then_inc(v_ready[s], 1)

                    for s in range(NS):
                        turn_tokens(0, s)
                    for s in range(NS):
                        project(0, s)
                        turn_tokens(1, s)
                    with pe.Fori(1, last) as it:
                        for s in range(NS):
                            pe.wait_ge(qk_saved[s], it)
                            pe.wait_ge(v_saved[s], it)
                            project(it, s)
                            turn_tokens(it + 1, s)
                    for s in range(NS):
                        pe.wait_ge(qk_saved[s], last)
                        pe.wait_ge(v_saved[s], last)
                        project(last, s)

                @block.scalar
                def _(act):
                    def save_turned(it, s):
                        act.wait_ge(turned[s], it + 1)
                        nc.scalar.copy(xT[s][:, :], turn[s][:, 0:N]).then_inc(xT_ready[s], 1)

                    def save_qk(it, s):
                        act.wait_ge(qk_ready[s], it + 1)
                        b = it * NS + s
                        for k, (dst, bias) in enumerate(((QT, "bq"), (KT, "bk"))):
                            src = qk[s][:, k * N:(k + 1) * N]
                            nc.scalar.activation(dst[:, bass.ds(b * N, N)], src, ACT.Identity, bias=w[:, cols[bias]])
                            done = nc.scalar.activation(square[s][:, k * N:(k + 1) * N], src, ACT.Square, bias=w[:, cols[bias]],
                                                        accum_out=sq[s][:, k:k + 1])
                        done.then_inc(qk_saved[s], 1)

                    for s in range(NS):
                        save_turned(0, s)
                    for s in range(NS):
                        act.wait_ge(v_ready[s], 1)
                        save_turned(1, s)
                        save_qk(0, s)
                    with act.Fori(1, last) as it:
                        for s in range(NS):
                            act.wait_ge(v_ready[s], it + 1)
                            save_turned(it + 1, s)
                            act.wait_ge(squares_added[s], it)
                            save_qk(it, s)
                    for s in range(NS):
                        act.wait_ge(squares_added[s], last)
                        save_qk(last, s)

        with Stage(nc, name + "_n") as sn:
            total = sn.ps("total", [P, 512])
            step = sn.sem("step")
            summed = sn.sem("summed")
            rooted = sn.sem("rooted")
            scaled = sn.sem("scaled")
            exped = sn.sem("exped")
            with nc.Block() as block:
                @block.vector
                def _(dve):
                    nc.vector.tensor_tensor(norms[:, 0:2], sums[0][:, :], sums[1][:, :], ALU.add).then_inc(step, 1)
                    dve.wait_ge(rooted, 1)
                    nc.vector.reciprocal(norms[:, 4:6], norms[:, 2:4]).then_inc(step, 1)
                    dve.wait_ge(step, 2)
                    nc.vector.tensor_tensor(norms[:, 6:8], total[:, 0:2], norms[:, 4:6], ALU.mult).then_inc(step, 1)
                    dve.wait_ge(step, 3)
                    nc.vector.tensor_tensor(norms[:, 6:8], norms[:, 6:8], norms[:, 4:6], ALU.mult).then_inc(scaled, 1)
                    dve.wait_ge(exped, 1)
                    nc.vector.tensor_scalar(norms[:, 10:11], norms[:, 8:9], norms[:, 9:10], 1.0 / L0A_HD,
                                            ALU.mult, ALU.mult).then_inc(step, 1)
                    dve.wait_ge(step, 4)
                    nc.vector.tensor_scalar(heads_scaled[:, :], g.c("heads8"), norms[:, 10:11], None,
                                            ALU.mult).then_inc(step, 1)

                @block.tensor
                def _(pe):
                    pe.wait_ge(step, 1)
                    nc.tensor.matmul(total[:, 0:2], g.c("ones"), norms[:, 0:2], start=True, stop=True).then_inc(summed, 1)

                @block.scalar
                def _(act):
                    act.wait_ge(summed, 1)
                    nc.scalar.activation(norms[:, 2:4], total[:, 0:2], ACT.Sqrt).then_inc(rooted, 1)
                    act.wait_ge(scaled, 1)
                    nc.scalar.activation(norms[:, 8:10], norms[:, 6:8], ACT.Exp, scale=-0.5).then_inc(exped, 1)

        with Stage(nc, name + "_b") as sb:
            feats = [sb.sb(f"feats{s}", [P, 2 * N]) for s in range(NS)]
            prod = [sb.sb(f"prod{s}", [P, N]) for s in range(NS)]
            sim = [sb.sb(f"sim{s}", [P, TPB * L0A_HEADS]) for s in range(NS)]
            inv = [sb.sb(f"inv{s}", [P, TPB * L0A_HEADS]) for s in range(NS)]
            mix = [sb.sb(f"mix{s}", [P, TPB * D]) for s in range(NS)]
            proj = [sb.ps(f"proj{s}", [P, 512]) for s in range(NS)]
            sim_ps = [sb.ps(f"sim_ps{s}", [P, 512]) for s in range(NS)]
            projected = sb.sems("projected", NS)
            exp_done = sb.sems("exp_done", NS)
            prod_ready = sb.sems("prod_ready", NS)
            sim_ready = sb.sems("sim_ready", NS)
            mix_step = sb.sems("mix_step", NS)
            MIX_STEPS = 4
            with nc.Block() as block:
                @block.tensor
                def _(pe):
                    def project(it, s):
                        b = it * NS + s
                        nc.tensor.matmul(proj[s][:, 0:N], w[:, cols["phi"]], QT[:, bass.ds(b * N, N)], start=True, stop=True)
                        nc.tensor.matmul(proj[s][:, N:2 * N], w[:, cols["phi"]], KT[:, bass.ds(b * N, N)], start=True,
                                         stop=True).then_inc(projected[s], 1)

                    def sum_heads(it, s):
                        pe.wait_ge(prod_ready[s], it + 1)
                        for u in range(TPB):
                            done = nc.tensor.matmul(sim_ps[s][:, u * L0A_HEADS:(u + 1) * L0A_HEADS],
                                                    prod[s][:, u * P:(u + 1) * P], heads_scaled[:, :], start=True, stop=True)
                        done.then_inc(sim_ready[s], 1)

                    for s in range(NS):
                        project(0, s)
                    for s in range(NS):
                        pe.wait_ge(exp_done[s], 1)
                        project(1, s)
                        sum_heads(0, s)
                    with pe.Fori(1, last) as it:
                        for s in range(NS):
                            pe.wait_ge(exp_done[s], it + 1)
                            project(it + 1, s)
                            pe.wait_ge(mix_step[s], it * MIX_STEPS - MIX_STEPS + 1)
                            sum_heads(it, s)
                    for s in range(NS):
                        pe.wait_ge(mix_step[s], (last - 1) * MIX_STEPS + 1)
                        sum_heads(last, s)

                @block.scalar
                def _(act):
                    def features(it, s):
                        act.wait_ge(projected[s], it + 1)
                        nc.scalar.activation(feats[s][:, 0:N], proj[s][:, 0:N], ACT.Exp, scale=norms[:, 4:5])
                        nc.scalar.activation(feats[s][:, N:2 * N], proj[s][:, N:2 * N], ACT.Exp,
                                             scale=norms[:, 5:6]).then_inc(exp_done[s], 1)

                    for s in range(NS):
                        features(0, s)
                    with act.Fori(1, BATCH // NS) as it:
                        for s in range(NS):
                            act.wait_ge(prod_ready[s], it)
                            features(it, s)

                @block.gpsimd
                def _(pool):
                    def multiply(it, s):
                        pool.wait_ge(exp_done[s], it + 1)
                        nc.gpsimd.tensor_tensor(prod[s][:, :], feats[s][:, 0:N], feats[s][:, N:2 * N],
                                                ALU.mult).then_inc(prod_ready[s], 1)

                    for s in range(NS):
                        multiply(0, s)
                    with pool.Fori(1, BATCH // NS) as it:
                        for s in range(NS):
                            pool.wait_ge(sim_ready[s], it)
                            multiply(it, s)

                @block.vector
                def _(dve):
                    with dve.Fori(0, BATCH // NS) as it:
                        for s in range(NS):
                            dve.wait_ge(sim_ready[s], it + 1)
                            nc.vector.tensor_copy(sim[s][:, :], sim_ps[s][:, 0:TPB * L0A_HEADS]).then_inc(mix_step[s], 1)
                        for s in range(NS):
                            t = (it * NS + s) * TPB
                            dve.wait_ge(mix_step[s], it * MIX_STEPS + 1)
                            nc.vector.reciprocal(inv[s][:, :], sim[s][:, :]).then_inc(mix_step[s], 1)
                            nc.vector.tensor_tensor(
                                mix[s][:, :].rearrange("p (h e) -> p h e", e=L0A_HD),
                                V[:, bass.ds(t, TPB), :].rearrange("p u (h e) -> p (u h) e", e=L0A_HD),
                                sim[s][:, :].unsqueeze(2).broadcast_to([P, TPB * L0A_HEADS, L0A_HD]),
                                ALU.mult).then_inc(mix_step[s], 1)
                        for s in range(NS):
                            dve.wait_ge(mix_step[s], it * MIX_STEPS + 3)
                            nc.vector.tensor_tensor(
                                mix[s][:, :].rearrange("p (h e) -> p h e", e=L0A_HD),
                                mix[s][:, :].rearrange("p (h e) -> p h e", e=L0A_HD),
                                inv[s][:, :].unsqueeze(2).broadcast_to([P, TPB * L0A_HEADS, L0A_HD]),
                                ALU.mult).then_inc(mix_step[s], 1)
                        for s in range(NS):
                            t = (it * NS + s) * TPB
                            dve.wait_ge(mix_step[s], it * MIX_STEPS + 4)
                            nc.vector.tensor_tensor(g.X[:, bass.ds(t, TPB), :].rearrange("p u d -> p (u d)"),
                                                    g.X[:, bass.ds(t, TPB), :].rearrange("p u d -> p (u d)"),
                                                    mix[s][:, :], ALU.add)


L1_G, L1_NQ, L1_NK, L1_H, L1_DH = 4, 128, 64, 8, 64
L1_DI = L1_H * L1_DH
L1_C = L1_DI // P
L1F_PARTS = [("route", 2 * L1_G), ("wq", L1_G * L1_DI), ("wk", L1_G * L1_DI), ("wv", L1_G * L1_DI),
             ("wo", L1_G * L1_C * D), ("null_k", L1_G * L1_C), ("null_token", D)]
LOWEST = -3.4028235e38


def l1_ffn(nc, g, name):
    G, NQ, NK, H, DH, C = L1_G, L1_NQ, L1_NK, L1_H, L1_DH, L1_C
    cols, width = columns(L1F_PARTS)
    N = SEQ
    NS = 2
    USES = G // NS
    ROWS = 2 * G
    with Stage(nc, name) as st:
        w = st.sb("w", [P, width])
        row_statistics(nc, g, name, [(w[:, :], g.dram["w_l1f"])])
        logits_d = nc.dram_tensor(name + "_logits", (BATCH, ROWS, N), F32, kind="Internal").ap()
        place_d = nc.dram_tensor(name + "_place", (P, N), F32, kind="Internal").ap()
        placeT = st.sb("placeT", [P, TPB, P])
        scoreT = st.sb("scoreT", [P, TPB, P])
        mean_by = st.sb("mean_by", [P, TPB, BATCH])
        unpicked = st.sb("unpicked", [P, TPB, BATCH])

        with Stage(nc, name + "_l") as sl:
            XT = sl.sb("XT", [P, TOKENS])
            row = sl.sb("row", [ROWS, TOKENS])
            turn_stream(nc, g, name, XT)
            bank = [sl.ps(f"bank{s}", [P, 512]) for s in range(4)]
            slot_free = sl.sems("slot_free", 4)
            ready = sl.sems("ready", 4)
            stored = sl.sem("stored")
            with nc.Block() as block:
                @block.tensor
                def _(pe):
                    for s in range(4):
                        pe.sem_inc(slot_free[s], 1)
                    with pe.Fori(0, TOKENS // 512 // 4) as it:
                        for s in range(4):
                            pe.wait_ge(slot_free[s], it + 1)
                            nc.tensor.matmul(bank[s][0:ROWS, :], w[:, cols["route"]], XT[:, bass.ds((it * 4 + s) * 512, 512)],
                                             start=True, stop=True).then_inc(ready[s], 1)

                @block.scalar
                def _(act):
                    with act.Fori(0, TOKENS // 512 // 4) as it:
                        for s in range(4):
                            act.wait_ge(ready[s], it + 1)
                            nc.scalar.copy(row[:, bass.ds((it * 4 + s) * 512, 512)], bank[s][0:ROWS, :]).then_inc(slot_free[s], 1)

                @block.sync
                def _(sp):
                    for s in range(4):
                        sp.wait_ge(slot_free[s], TOKENS // 512 // 4 + 1)
                    sp.dma_start(logits_d.rearrange("b k t -> k b t"), row[:, :].rearrange("k (b t) -> k b t", b=BATCH)
                                 ).then_inc(stored, 16)
                    sp.wait_ge(stored, 16)

        with Stage(nc, name + "_t") as sk:
            logit = sk.sb("logit", [P, N])
            left = [sk.sb(f"left{i}", [P, N]) for i in range(2)]
            top8 = sk.sb("top8", [P, 8])
            mark64 = sk.sb("mark64", [P, N])
            mark = sk.sb("mark", [P, N])
            count = sk.sb("count", [P, N])
            place = sk.sb("place", [P, N])
            score = sk.sb("score", [P, N])
            picks = sk.sb("picks", [P, TPB, P])
            num = sk.sb("num", [P, TPB, BATCH])
            turn = sk.ps("turn", [P, 512])
            loaded = sk.sem("loaded")
            pick = sk.sem("pick")
            step = sk.sem("step")
            placed = sk.sem("placed")
            scored = sk.sem("scored")
            turned = sk.sem("turned")
            stored = sk.sem("stored")
            with nc.Block() as block:
                @block.sync
                def _(sp):
                    sp.dma_start(logit[:, :], logits_d.rearrange("b k t -> (b k) t")).then_inc(loaded, 16)
                    sp.wait_ge(placed, 1)
                    sp.dma_start(place_d, place[:, :]).then_inc(stored, 16)
                    sp.wait_ge(stored, 16)

                @block.scalar
                def _(act):
                    act.wait_ge(loaded, 16)
                    nc.scalar.activation(score[:, :], logit[:, :], ACT.Sigmoid).then_inc(scored, 1)

                @block.vector
                def _(dve):
                    dve.wait_ge(loaded, 16)
                    done = 0
                    src = logit
                    for r in range(NQ // 8):
                        if done:
                            dve.wait_ge(pick, done)
                        nc.vector.max(top8[:, :], src[:, :]).then_inc(pick, 1)
                        dve.wait_ge(pick, done + 1)
                        dst = left[r % 2]
                        nc.vector.match_replace(dst[:, :], top8[:, :], src[:, :], LOWEST).then_inc(pick, 1)
                        done += 2
                        src = dst
                        if r == NK // 8 - 1:
                            dve.wait_ge(pick, done)
                            nc.vector.tensor_scalar(mark64[:, :], src[:, :], LOWEST, None, ALU.is_equal).then_inc(pick, 1)
                            done += 1
                    dve.wait_ge(pick, done)
                    nc.vector.tensor_scalar(count[:, :], src[:, :], LOWEST, None, ALU.is_equal).then_inc(step, 1)
                    dve.wait_ge(step, 1)
                    nc.vector.scalar_tensor_tensor(mark[:, :], count[:, :], g.c("is_query"), mark64[:, :], ALU.mult,
                                                   ALU.max).then_inc(step, 1)
                    dve.wait_ge(step, 2)
                    nc.vector.memset(mark64[:, :], 1.0).then_inc(step, 1)
                    dve.wait_ge(step, 3)
                    nc.vector.tensor_tensor_scan(count[:, :], mark64[:, :], mark[:, :], 0.0, ALU.mult, ALU.add).then_inc(step, 1)
                    dve.wait_ge(step, 4)
                    nc.vector.tensor_tensor(place[:, :], count[:, :], mark[:, :], ALU.mult).then_inc(step, 1)
                    dve.wait_ge(step, 5)
                    nc.vector.tensor_scalar(place[:, :], place[:, :], 1.0, None, ALU.subtract).then_inc(placed, 1)
                    dve.wait_ge(turned, 1)
                    nc.vector.tensor_copy(placeT[:, :, :], turn[:, 0:2 * P].rearrange("p (u r) -> p u r", u=TPB)).then_inc(step, 1)
                    nc.vector.tensor_copy(scoreT[:, :, :], turn[:, 2 * P:4 * P].rearrange("p (u r) -> p u r", u=TPB)).then_inc(step, 1)
                    dve.wait_ge(step, 7)
                    nc.vector.tensor_scalar(picks[:, :, :], placeT[:, :, :], 0.0, None, ALU.is_ge).then_inc(step, 1)
                    dve.wait_ge(step, 8)
                    nc.vector.tensor_reduce(num[:, :, :], picks[:, :, :].rearrange("p u (b r) -> p u b r", r=ROWS)[:, :, :, 0:G],
                                            AX.X, ALU.add).then_inc(step, 1)
                    dve.wait_ge(step, 9)
                    nc.vector.tensor_scalar(unpicked[:, :, :], num[:, :, :], 0.0, 0.5, ALU.is_equal, ALU.mult).then_inc(step, 1)
                    nc.vector.tensor_scalar(mean_by[:, :, :], num[:, :, :], 1e-5, None, ALU.max).then_inc(step, 1)
                    dve.wait_ge(step, 11)
                    nc.vector.reciprocal(mean_by[:, :, :], mean_by[:, :, :]).then_inc(step, 1)
                    dve.wait_ge(step, 12)
                    nc.vector.tensor_scalar(mean_by[:, :, :], mean_by[:, :, :], 0.5, None, ALU.mult).then_inc(step, 1)
                    dve.wait_ge(step, 13)
                    query = scoreT[:, :, :].rearrange("p u (b r) -> p u b r", r=ROWS)[:, :, :, 0:G]
                    nc.vector.tensor_tensor(query, query, mean_by[:, :, :].unsqueeze(3).broadcast_to([P, TPB, BATCH, G]),
                                            ALU.mult).then_inc(step, 1)

                @block.tensor
                def _(pe):
                    pe.wait_ge(placed, 1)
                    pe.wait_ge(scored, 1)
                    for i, a in enumerate((place, score)):
                        for u in range(TPB):
                            last = nc.tensor.transpose(turn[:, (2 * i + u) * P:(2 * i + u + 1) * P], a[:, u * P:(u + 1) * P],
                                                       g.c("ident"))
                    last.then_inc(turned, 1)

        with Stage(nc, name + "_a") as sa:
            wq, wk, wv = (w[:, cols[n]].rearrange("p (g e) -> p g e", g=G) for n in ("wq", "wk", "wv"))
            wo = w[:, cols["wo"]].rearrange("p (g c d) -> p g c d", g=G, c=C)
            null_k = w[:, cols["null_k"]].rearrange("p (g c) -> p g c", g=G)
            xn = sa.sb("xn", [P, TPB, D])
            hot = sa.sb("hot", [P, TPB, G, NQ + NK])
            places = sa.sb("places", [P, G * N])
            hotT = sa.sb("hotT", [P, G, N])
            kT = [sa.sb(f"kT{k}", [P, C, NK + 1]) for k in range(G)]
            v = [sa.sb(f"v{k}", [NK + 1, L1_DI]) for k in range(G)]
            sg = [sa.sb(f"sg{k}", [NK, 1]) for k in range(G)]
            xg = [sa.sb(f"xg{s}", [P, NQ + NK]) for s in range(NS)]
            qT = [sa.sb(f"qT{s}", [P, C, NQ]) for s in range(NS)]
            top = [sa.sb(f"top{s}", [P, 2, C]) for s in range(NS)]
            prob = [sa.sb(f"prob{s}", [P, 2, C, NK + 1]) for s in range(NS)]
            den = [sa.sb(f"den{s}", [P, 2, C]) for s in range(NS)]
            probT = [sa.sb(f"probT{s}", [NK + 1, 2, C, NQ]) for s in range(NS)]
            oT = [sa.sb(f"oT{s}", [P, C, NQ]) for s in range(NS)]
            o = [sa.sb(f"o{s}", [P, D]) for s in range(NS)]
            bank_x = sa.ps("bank_x", [P, 512])
            bank_q = sa.ps("bank_q", [P, 512])
            bank_v = sa.ps("bank_v", [P, 512])
            bank_s = [sa.ps(f"bank_s{a}", [P, 512]) for a in range(2)]
            bank_p = [sa.ps(f"bank_p{a}", [P, 512]) for a in range(2)]
            bank_o = sa.ps("bank_o", [P, 512])
            null_loaded = sa.sem("null_loaded")
            null_k_ready = sa.sem("null_k_ready")
            places_loaded = sa.sem("places_loaded")
            hotT_ready = sa.sem("hotT_ready")
            xn_ready = sa.sem("xn_ready")
            hot_ready = sa.sem("hot_ready")
            null_added = sa.sem("null_added")
            added = sa.sem("added")
            gathered = sa.sems("gathered", NS)
            xg_saved = sa.sems("xg_saved", NS)
            q_ready = sa.sems("q_ready", NS)
            k_ready = sa.sems("k_ready", NS)
            v_ready = sa.sems("v_ready", NS)
            q_saved = sa.sems("q_saved", NS)
            k_saved = sa.sems("k_saved", NS)
            v_saved = sa.sems("v_saved", NS)
            s_ready = sa.sems("s_ready", NS)
            top_step = sa.sems("top_step", NS)
            shifted = sa.sems("shifted", NS)
            exp_done = sa.sems("exp_done", NS)
            den_step = sa.sems("den_step", NS)
            normed = sa.sems("normed", NS)
            pT_ready = sa.sems("pT_ready", NS)
            pT_saved = sa.sems("pT_saved", NS)
            pv_ready = sa.sems("pv_ready", NS)
            oT_saved = sa.sems("oT_saved", NS)
            o_ready = sa.sems("o_ready", NS)
            o_saved = sa.sems("o_saved", NS)
            back_ready = sa.sems("back_ready", NS)

            def use(unit):
                return unit[0] * USES + unit[1] // NS + 1

            last_batch = BATCH - 1

            def run(engine, step):
                step((0, 0), None, None)
                step((0, 1), (0, 0), None)
                with engine.Fori(0, BATCH - 1) as it:
                    step((it, 2), (it, 1), (it, 0))
                    step((it, 3), (it, 2), (it, 1))
                    step((it + 1, 0), (it, 3), (it, 2))
                    step((it + 1, 1), (it + 1, 0), (it, 3))
                step((last_batch, 2), (last_batch, 1), (last_batch, 0))
                step((last_batch, 3), (last_batch, 2), (last_batch, 1))
                step(None, (last_batch, 3), (last_batch, 2))
                step(None, None, (last_batch, 3))

            with nc.Block() as block:
                @block.sync
                def _(sp):
                    for k in range(G):
                        sp.dma_start(v[k][NK:NK + 1, :], g.dram["null_v"][k:k + 1, :]).then_inc(null_loaded, 16)

                    def load_places(it):
                        sp.dma_start(places[:, :], place_d[bass.ds(it * ROWS, G), :].rearrange("r t -> (r t)").partition_broadcast(P)
                                     ).then_inc(places_loaded, 16)

                    load_places(0)
                    with sp.Fori(1, BATCH) as it:
                        sp.wait_ge(hotT_ready, it)
                        load_places(it)

                @block.gpsimd
                def _(pool):
                    def step(front, soft, back):
                        if soft is not None:
                            s = soft[1] % NS
                            pool.wait_ge(den_step[s], use(soft) * 2)
                            nc.gpsimd.tensor_tensor(prob[s][:, :, :, :].rearrange("p a c k -> p (a c) k"),
                                                    prob[s][:, :, :, :].rearrange("p a c k -> p (a c) k"),
                                                    den[s][:, :, :].rearrange("p a c -> p (a c)").unsqueeze(2)
                                                    .broadcast_to([P, H, NK + 1]), ALU.mult).then_inc(normed[s], 1)

                    run(pool, step)

                @block.vector
                def _(dve):
                    def norm_tokens(it):
                        for u in range(TPB):
                            t = it * TPB + u
                            last = nc.vector.tensor_scalar(xn[:, u, :], g.tile(t), g.mean[:, bass.ds(t, 1)],
                                                           g.rstd[:, bass.ds(t, 1)], ALU.subtract, ALU.mult)
                        last.then_inc(xn_ready, 1)

                    def make_hot(it, k):
                        for u in range(TPB):
                            for at, n, r in ((0, NQ, 0), (NQ, NK, G)):
                                last = nc.vector.tensor_scalar(hot[:, u, k, at:at + n], g.c("iota")[:, 0:n],
                                                               placeT[:, u, bass.ds(it * ROWS + r + k, 1)], None, ALU.is_equal)
                        last.then_inc(hot_ready, 1)

                    def hotT_and_null(it):
                        dve.wait_ge(places_loaded, it * 16 + 16)
                        nc.vector.tensor_scalar(hotT[:, :, :].rearrange("p g t -> p (g t)"), places[:, :], g.c("row_index"), None,
                                                ALU.is_equal).then_inc(hotT_ready, 1)
                        dve.wait_ge(xn_ready, it + 1)
                        for u in range(TPB):
                            t = it * TPB + u
                            x = g.tile(t).rearrange("p t d -> p (t d)")
                            last = nc.vector.scalar_tensor_tensor(x, w[:, cols["null_token"]], unpicked[:, u, bass.ds(it, 1)], x,
                                                                  ALU.mult, ALU.add)
                        last.then_inc(null_added, 1)

                    def step(front, soft, back):
                        if soft is not None:
                            s, n = soft[1] % NS, use(soft)
                            dve.wait_ge(s_ready[s], n)
                            for a in range(2):
                                nc.vector.tensor_reduce(top[s][:, a, :], bank_s[a][:, 0:C * (NK + 1)].rearrange("p (c k) -> p c k", c=C),
                                                        AX.X, ALU.max).then_inc(top_step[s], 1)
                            dve.wait_ge(top_step[s], n * 2)
                            for a in range(2):
                                last = nc.vector.tensor_tensor(prob[s][:, a, :, :],
                                                               bank_s[a][:, 0:C * (NK + 1)].rearrange("p (c k) -> p c k", c=C),
                                                               top[s][:, a, :].unsqueeze(2).broadcast_to([P, C, NK + 1]), ALU.subtract)
                            last.then_inc(shifted[s], 1)
                        if front is not None:
                            s, n, k = front[1] % NS, use(front), front[1]
                            ends = k >= 2 and front[0] is not last_batch
                            if ends:
                                dve.wait_ge(gathered[s], n)
                                if k == G - 1:
                                    norm_tokens(front[0] + 1)
                            dve.wait_ge(k_ready[s], n)
                            nc.vector.tensor_copy(kT[k][:, :, 0:NK], bank_x[:, 192:448].rearrange("p (c k) -> p c k", c=C)
                                                  ).then_inc(k_saved[s], 1)
                        if soft is not None:
                            s, n = soft[1] % NS, use(soft)
                            dve.wait_ge(exp_done[s], n)
                            nc.vector.tensor_reduce(den[s][:, :, :], prob[s][:, :, :, :], AX.X, ALU.add).then_inc(den_step[s], 1)
                            dve.wait_ge(den_step[s], n * 2 - 1)
                            nc.vector.reciprocal(den[s][:, :, :], den[s][:, :, :]).then_inc(den_step[s], 1)
                        if front is not None:
                            s, n, k = front[1] % NS, use(front), front[1]
                            dve.wait_ge(v_ready[s], n)
                            dve.wait_ge(xg_saved[s], n)
                            nc.vector.tensor_scalar(v[k][0:NK, :], bank_v[0:NK, :], sg[k][:, :], None,
                                                    ALU.mult).then_inc(v_saved[s], 1)
                        if back is not None:
                            (it, k), s, n = back, back[1] % NS, use(back)
                            dve.wait_ge(o_ready[s], n)
                            nc.vector.tensor_copy(o[s][:, :], bank_p[0][:, 0:D]).then_inc(o_saved[s], 1)
                            dve.wait_ge(back_ready[s], n)
                            if k == 0:
                                dve.wait_ge(null_added, it + 1)
                            else:
                                dve.wait_ge(added, it * G + k)
                            for u in range(TPB):
                                x = g.tile(it * TPB + u).rearrange("p t d -> p (t d)")
                                last = nc.vector.scalar_tensor_tensor(x, bank_o[:, u * D:(u + 1) * D],
                                                                      scoreT[:, u, bass.ds(it * ROWS + k, 1)], x, ALU.mult, ALU.add)
                            last.then_inc(added, 1)
                        if front is not None and ends:
                            for k in (0, 1) if front[1] == 2 else (2, 3):
                                make_hot(front[0] + 1, k)
                        if front is not None and front[1] == 1:
                            hotT_and_null(front[0])
                    for k in range(G):
                        nc.vector.tensor_copy(kT[k][:, :, NK], null_k[:, k, :]).then_inc(null_k_ready, 1)
                    norm_tokens(0)
                    for k in range(G):
                        make_hot(0, k)
                    run(dve, step)

                @block.scalar
                def _(act):
                    def step(front, soft, back):
                        if front is not None:
                            s, k = front[1] % NS, front[1]
                            act.wait_ge(gathered[s], use(front))
                            nc.scalar.copy(xg[s][:, :], bank_x[:, 0:192])
                            nc.scalar.copy(sg[k][:, :], bank_x[0:NK, 448:449]).then_inc(xg_saved[s], 1)
                        if back is not None:
                            s = back[1] % NS
                            act.wait_ge(pT_ready[s], use(back))
                            for a in range(2):
                                nc.scalar.copy(probT[s][:, a, :, :], bank_p[a][0:NK + 1, :].rearrange("p (c q) -> p c q", c=C)
                                               ).then_inc(pT_saved[s], 1)
                        if soft is not None:
                            s = soft[1] % NS
                            act.wait_ge(shifted[s], use(soft))
                            nc.scalar.activation(prob[s][:, :, :, :], prob[s][:, :, :, :], ACT.Exp).then_inc(exp_done[s], 1)
                        if front is not None:
                            s = front[1] % NS
                            act.wait_ge(q_ready[s], use(front))
                            nc.scalar.mul(qT[s][:, :, :], bank_q[:, :].rearrange("p (c q) -> p c q", c=C),
                                          float(DH) ** -0.5).then_inc(q_saved[s], 1)
                        if back is not None:
                            s = back[1] % NS
                            act.wait_ge(pv_ready[s], use(back))
                            nc.scalar.copy(oT[s][:, :, :], bank_o[:, :].rearrange("p (c q) -> p c q", c=C)).then_inc(oT_saved[s], 1)

                    run(act, step)

                @block.tensor
                def _(pe):
                    def gather(unit):
                        (it, k), s = unit, unit[1] % NS
                        if k == 0:
                            pe.wait_ge(xn_ready, it + 1)
                        pe.wait_ge(hot_ready, it * G + k + 1)
                        for u in range(TPB):
                            nc.tensor.matmul(bank_x[:, 0:192], xn[:, u, :], hot[:, u, k, :], start=(u == 0), stop=(u == 1))
                        for u in range(TPB):
                            last = nc.tensor.matmul(bank_x[0:NK, 448:449], hot[:, u, k, NQ:NQ + NK],
                                                    scoreT[:, u, bass.ds(it * ROWS + G + k, 1)], start=(u == 0), stop=(u == 1))
                        last.then_inc(gathered[s], 1)

                    def turn_probs(unit):
                        s = unit[1] % NS
                        pe.wait_ge(normed[s], use(unit))
                        for a in range(2):
                            for c in range(C):
                                last = nc.tensor.transpose(bank_p[a][0:NK + 1, c * NQ:(c + 1) * NQ], prob[s][:, a, c, :], g.c("ident"))
                        last.then_inc(pT_ready[s], 1)

                    def project_qk(unit):
                        s, k = unit[1] % NS, unit[1]
                        pe.wait_ge(xg_saved[s], use(unit))
                        for c in range(C):
                            last = nc.tensor.matmul(bank_x[:, 192 + c * NK:192 + (c + 1) * NK], wk[:, k, c * P:(c + 1) * P],
                                                    xg[s][:, NQ:NQ + NK], start=True, stop=True)
                        last.then_inc(k_ready[s], 1)
                        for c in range(C):
                            last = nc.tensor.matmul(bank_q[:, c * NQ:(c + 1) * NQ], wq[:, k, c * P:(c + 1) * P],
                                                    xg[s][:, 0:NQ], start=True, stop=True)
                        last.then_inc(q_ready[s], 1)

                    def project_v(unit, before):
                        s, k = unit[1] % NS, unit[1]
                        if before is not None:
                            pe.wait_ge(v_saved[before[1] % NS], use(before))
                        nc.tensor.matmul(bank_v[0:NK, :], xg[s][:, NQ:NQ + NK], wv[:, k, :], start=True,
                                         stop=True).then_inc(v_ready[s], 1)

                    def values(unit):
                        (it, k), s = unit, unit[1] % NS
                        pe.wait_ge(v_saved[s], use(unit))
                        pe.wait_ge(pT_saved[s], use(unit) * 2)
                        if not (isinstance(it, int) and it == 0 and k == 0):
                            pe.wait_ge(added, it * G + k)
                        for c in range(C):
                            for a in range(2):
                                h = 2 * c + a
                                last = nc.tensor.matmul(bank_o[64 * a:64 * a + 64, c * NQ:(c + 1) * NQ],
                                                        v[k][:, h * DH:(h + 1) * DH], probT[s][:, a, c, :],
                                                        start=True, stop=True)
                        last.then_inc(pv_ready[s], 1)

                    def project_out(unit):
                        s, k = unit[1] % NS, unit[1]
                        pe.wait_ge(oT_saved[s], use(unit))
                        for c in range(C):
                            last = nc.tensor.matmul(bank_p[0][:, 0:D], oT[s][:, c, :], wo[:, k, c, :], start=(c == 0),
                                                    stop=(c == C - 1))
                        last.then_inc(o_ready[s], 1)

                    def scores(unit, before):
                        s, k = unit[1] % NS, unit[1]
                        pe.wait_ge(q_saved[s], use(unit))
                        pe.wait_ge(k_saved[s], use(unit))
                        if before is not None:
                            pe.wait_ge(shifted[before[1] % NS], use(before))
                        for c in range(C):
                            for a in range(2):
                                r = slice(64 * a, 64 * a + 64)
                                last = nc.tensor.matmul(bank_s[a][:, c * (NK + 1):(c + 1) * (NK + 1)], qT[s][r, c, :], kT[k][r, c, :],
                                                        start=True, stop=True)
                        last.then_inc(s_ready[s], 1)

                    def scatter(unit):
                        (it, k), s = unit, unit[1] % NS
                        pe.wait_ge(o_saved[s], use(unit))
                        if k == 0:
                            pe.wait_ge(hotT_ready, it + 1)
                        for u in range(TPB):
                            last = nc.tensor.matmul(bank_o[:, u * D:(u + 1) * D], hotT[:, k, u * P:(u + 1) * P], o[s][:, :],
                                                    start=True, stop=True)
                        last.then_inc(back_ready[s], 1)

                    def step(front, soft, back):
                        if front is not None:
                            gather(front)
                        if back is not None:
                            turn_probs(back)
                        if front is not None:
                            project_qk(front)
                        if back is not None:
                            values(back)
                        if front is not None:
                            project_v(front, soft)
                        if back is not None:
                            project_out(back)
                        if front is not None:
                            scores(front, soft)
                        if back is not None:
                            scatter(back)

                    pe.wait_ge(null_loaded, 16 * G)
                    pe.wait_ge(null_k_ready, G)
                    run(pe, step)

L1A_H, L1A_DK, L1A_DV, L1A_TAPS = 16, 64, 128, 4
L1A_HG = 4
L1A_GROUPS = L1A_H // L1A_HG
GROUP_BITS = L1A_GROUPS.bit_length() - 1
L1A_W = 2 * L1A_HG * L1A_DK + L1A_HG * L1A_DV
L1A_PARTS = [("wab", 2 * L1A_H), ("wgate", L1A_H * L1A_DV), ("wo", L1A_H * D), ("dt_bias", L1A_H), ("a_log", L1A_H),
             ("norm", 1)]
LEVELS = 6
HALF = P // 2


def l1_attn(nc, g, name):
    H, HG, DK, DV, NG = L1A_H, L1A_HG, L1A_DK, L1A_DV, L1A_GROUPS
    cols, width = columns(L1A_PARTS)
    N = SEQ
    PAD = L1A_TAPS - 1
    W2 = 2 * HG * DK
    with Stage(nc, name) as st:
        w = st.sb("w", [P, width])
        XT = st.sb("XT", [P, TOKENS])
        folded = st.sb("folded", [P, NG, L1A_TAPS, L1A_W])
        beta = st.sb("beta", [P, TILES, H])
        decay = st.sb("decay", [P, TILES, H])
        grown = st.sb("grown", [P, TILES, H])

        with Stage(nc, name + "_p") as sp_:
            raw = sp_.sb("raw", [P, NG, L1A_W])
            ab = sp_.sb("ab", [P, TILES, 2 * H])
            z = sp_.sb("z", [P, TILES, H])
            away = sp_.sb("away", [P, TILES, H])
            rate = sp_.sb("rate", [P, H])
            row_statistics(nc, g, name, [(w[:, :], g.dram["w_l1a"]), (raw[:, :, :], g.dram["w_l1a_qkv"]),
                                         (folded[:, :, :, :].rearrange("p a b c -> p (a b c)"),
                                          g.dram["l1a_taps"].partition_broadcast(P))])
            turn_stream(nc, g, name, XT, w[:, cols["wab"]], ab[:, :, :])
            sums = sp_.ps("sums", [P, 512])
            step = sp_.sem("step")
            z_ready = sp_.sem("z_ready")
            away_ready = sp_.sem("away_ready")
            act_step = sp_.sem("act_step")
            decay_ready = sp_.sem("decay_ready")
            summed = sp_.sem("summed")

            def each(a):
                return a.unsqueeze(1).broadcast_to([P, TILES, H])

            with nc.Block() as block:
                @block.vector
                def _(dve):
                    nc.vector.tensor_tensor(z[:, :, :], ab[:, :, 0:H], each(w[:, cols["dt_bias"]]), ALU.add).then_inc(z_ready, 1)
                    dve.wait_ge(z_ready, 1)
                    nc.vector.scalar_tensor_tensor(away[:, :, :], z[:, :, :], -1.0, z[:, :, :], ALU.mult, ALU.max).then_inc(away_ready, 1)
                    for gi in range(NG):
                        for j in range(L1A_TAPS):
                            last = nc.vector.scalar_tensor_tensor(folded[:, gi, j, :], raw[:, gi, :], 0.5, folded[:, gi, j, :],
                                                                  ALU.mult, ALU.mult)
                    nc.vector.tensor_scalar(w[:, cols["wo"]], w[:, cols["wo"]], w[:, cols["norm"]], 0.5, ALU.mult,
                                            ALU.mult).then_inc(step, 1)
                    dve.wait_ge(act_step, 4)
                    nc.vector.scalar_tensor_tensor(z[:, :, :], z[:, :, :], 0.0, away[:, :, :], ALU.max, ALU.add).then_inc(step, 1)
                    dve.wait_ge(step, 2)
                    nc.vector.scalar_tensor_tensor(decay[:, :, :], z[:, :, :], -1.0, each(rate[:, :]), ALU.mult,
                                                   ALU.mult).then_inc(decay_ready, 1)
                    nc.vector.tensor_scalar(beta[:, :, :], beta[:, :, :], 2.0, None, ALU.mult).then_inc(step, 1)

                @block.scalar
                def _(act):
                    act.wait_ge(away_ready, 1)
                    nc.scalar.activation(beta[:, :, :], ab[:, :, H:2 * H], ACT.Sigmoid).then_inc(act_step, 1)
                    nc.scalar.activation(rate[:, :], w[:, cols["a_log"]], ACT.Exp).then_inc(act_step, 1)
                    nc.scalar.activation(away[:, :, :], away[:, :, :], ACT.Exp, scale=-1.0).then_inc(act_step, 1)
                    act.wait_ge(act_step, 3)
                    nc.scalar.activation(away[:, :, :], away[:, :, :], ACT.Ln, bias=g.c("ones")[:, 0:1]).then_inc(act_step, 1)
                    act.wait_ge(summed, 1)
                    nc.scalar.activation(grown[:, :, :].rearrange("p t h -> p (t h)"), sums[:, :], ACT.Exp).then_inc(act_step, 1)

                @block.tensor
                def _(pe):
                    pe.wait_ge(decay_ready, 1)
                    nc.tensor.matmul(sums[:, :], g.c("upto"), decay[:, :, :].rearrange("p t h -> p (t h)"), start=True,
                                     stop=True).then_inc(summed, 1)

        with Stage(nc, name + "_m") as sm:
            U = range(TPB)
            UNITS = BATCH * NG
            wgate = w[:, cols["wgate"]].rearrange("p (a n) -> p a n", a=NG)
            wo = w[:, cols["wo"]].rearrange("p (h d) -> p h d", h=H)
            xpad = [sm.sb(f"xpad{u}", [P, PAD + P]) for u in U]
            t0 = [sm.sb(f"t0{u}", [P, HG, P]) for u in U]
            t1 = [sm.sb(f"t1{u}", [P, HG, P]) for u in U]
            t2 = [sm.sb(f"t2{u}", [P, HG, P]) for u in U]
            qk = [sm.sb(f"qk{u}", [P, 2 * HG, DK]) for u in U]
            rhs = [sm.sb(f"rhs{u}", [P, HG, DV]) for u in U]
            gate = [sm.sb(f"gate{u}", [P, HG, DV]) for u in U]
            length = [sm.sb(f"length{u}", [P, 2 * HG]) for u in U]
            qkT = [sm.sb(f"qkT{u}", [P, 4, P]) for u in U]
            terms = [sm.sb(f"terms{u}", [P, HG, P]) for u in U]
            fade = [sm.sb(f"fade{u}", [P, HG, P]) for u in U]
            NT = [sm.sb(f"NT{u}", [P, HG, P]) for u in U]
            mixT = [sm.sb(f"mixT{u}", [P, HG, P]) for u in U]
            W = [sm.sb(f"W{u}", [P, HG, HALF]) for u in U]
            X = [sm.sb(f"X{u}", [P, HG, P]) for u in U]
            Y = [sm.sb(f"Y{u}", [P, HG, P]) for u in U]
            kfade = sm.sb("kfade", [P, HG, DK])
            state = sm.sb("state", [P, 2, DV])
            read_k = sm.sb("read_k", [P, HG, DV])
            read_q = sm.sb("read_q", [P, HG, DV])
            ms = [sm.sb(f"ms{u}", [P, HG]) for u in U]
            bank = [[sm.ps(f"bank{u}_{i}", [P, 512]) for i in range(4)] for u in U]
            pad_clear = sm.sem("pad_clear")
            xpad_ready = sm.sems("xpad_ready", TPB)
            qk_projected = sm.sems("qk_projected", TPB)
            v_projected = sm.sems("v_projected", TPB)
            gate_projected = sm.sems("gate_projected", TPB)
            qk_tanh = sm.sems("qk_tanh", TPB)
            v_tanh = sm.sems("v_tanh", TPB)
            gate_tanh = sm.sems("gate_tanh", TPB)
            qk_silu = sm.sems("qk_silu", TPB)
            v_silu = sm.sems("v_silu", TPB)
            gate_silu = sm.sems("gate_silu", TPB)
            squared = sm.sems("squared", TPB)
            length_step = sm.sems("length_step", TPB)
            length_ready = sm.sems("length_ready", TPB)
            unit = sm.sems("unit", TPB)
            qk_turned = sm.sems("qk_turned", TPB)
            qkT_saved = sm.sems("qkT_saved", TPB)
            terms_ready = sm.sems("terms_ready", TPB)
            diff_ready = sm.sems("diff_ready", TPB)
            fade_done = sm.sems("fade_done", TPB)
            faded_beta = sm.sems("faded_beta", TPB)
            dots_ready = sm.sems("dots_ready", TPB)
            NT_ready = sm.sems("NT_ready", TPB)
            mixT_begun = sm.sems("mixT_begun", TPB)
            mixT_ready = sm.sems("mixT_ready", TPB)
            Y_begun = sm.sems("Y_begun", TPB)
            Y_ready = sm.sems("Y_ready", TPB)
            Y_turned = sm.sems("Y_turned", TPB)
            X_ready = sm.sems("X_ready", TPB)
            X_turned = sm.sems("X_turned", TPB)
            Y_saved = sm.sems("Y_saved", TPB)
            W_ready = sm.sems("W_ready", TPB)
            W_masked = sm.sems("W_masked", TPB)
            XW_ready = sm.sems("XW_ready", TPB)
            merged = sm.sems("merged", TPB)
            kfade_ready = sm.sem("kfade_ready")
            solved = sm.sems("solved", TPB)
            delta_ready = sm.sems("delta_ready", TPB)
            out_ready = sm.sems("out_ready", TPB)
            state_ready = sm.sem("state_ready")
            state_saved = sm.sem("state_saved")
            read_ready = sm.sem("read_ready")
            read_saved = sm.sem("read_saved")
            rhs_ready = sm.sem("rhs_ready")
            o_saved = sm.sems("o_saved", TPB)
            o_squared = sm.sems("o_squared", TPB)
            ms_step = sm.sems("ms_step", TPB)
            ms_ready = sm.sems("ms_ready", TPB)
            o_normed = sm.sems("o_normed", TPB)
            y_ready = sm.sems("y_ready", TPB)
            y_turned = sm.sems("y_turned", TPB)
            yT_saved = sm.sems("yT_saved", TPB)
            projected = sm.sems("projected", TPB)

            def left(a, k):
                return a.rearrange("p (i two s) -> p i two s", two=2, s=2 << k)[:, :, 0, :]

            def live(k):
                return slice(HALF, P) if k == LEVELS - 1 else slice(0, P)

            def flat(a):
                return a[:, :, :].rearrange("p a b -> p (a b)")

            def by_head(a):
                return a[:, :].rearrange("p (h t) -> p h t", h=HG)

            def heads(a, n):
                return a.unsqueeze(2).broadcast_to([P, a.shape[1], n])

            def over_heads(a):
                return a.unsqueeze(1).broadcast_to([P, HG, P])

            def group(n):
                return n & (NG - 1)

            def tile_of(u, n):
                b = n >> GROUP_BITS
                return (b if isinstance(b, int) else b.with_bounds(min_val=0, max_val=BATCH - 1)) * TPB + u

            def at_gate(a, u, n, first=0, count=HG):
                return flat(a)[:, bass.ds(tile_of(u, n) * H + group(n) * HG + first, count)]

            def parity(a, half):
                return a[:, half:HG:2, :]

            def half_rows(hh):
                return slice(64 * (hh % 2), 64 * (hh % 2) + 64)

            def run(engine, first, phase):
                first()
                phase(0, 0, 1, None, 0)
                with engine.Fori(0, UNITS - 1) as n:
                    phase(1, n, 0, n, n + 1)
                    phase(0, n + 1, 1, n, n + 1)
                phase(1, UNITS - 1, 0, UNITS - 1, None)
                phase(None, None, 1, UNITS - 1, None)

            with nc.Block() as block:
                @block.tensor
                def _(pe):
                    def project_qk(u, n, taps):
                        for j in taps:
                            if j == 0:
                                pe.wait_ge(xpad_ready[u], n + 1)
                            last = nc.tensor.matmul(bank[u][0][:, :], xpad[u][:, j:j + P], folded[:, bass.ds(group(n), 1), j, 0:W2],
                                                    start=(j == 0), stop=(j == L1A_TAPS - 1))
                            if j == L1A_TAPS - 1:
                                last.then_inc(qk_projected[u], 1)

                    def project_v(u, n, taps):
                        for j in taps:
                            if j == 0:
                                pe.wait_ge(fade_done[u], n + 1)
                            last = nc.tensor.matmul(bank[u][1][:, :], xpad[u][:, j:j + P],
                                                    folded[:, bass.ds(group(n), 1), j, W2:2 * W2],
                                                    start=(j == 0), stop=(j == L1A_TAPS - 1))
                            if j == L1A_TAPS - 1:
                                last.then_inc(v_projected[u], 1)

                    def project_gate(u, n):
                        nc.tensor.matmul(bank[u][2][:, :], xpad[u][:, PAD:PAD + P], wgate[:, bass.ds(group(n), 1), :],
                                         start=True, stop=True).then_inc(gate_projected[u], 1)

                    def decays(u, n):
                        pe.wait_ge(terms_ready[u], n + 1)
                        nc.tensor.matmul(bank[u][1][:, :], g.c("after"), flat(terms[u]), start=True,
                                         stop=True).then_inc(diff_ready[u], 1)

                    def turn_qk(u, n):
                        pe.wait_ge(unit[u], n + 1)
                        for pair in range(2):
                            for i, at in ((0, HG + 2 * pair), (1, 2 * pair)):
                                last = nc.tensor.transpose(bank[u][0][:, (2 * pair + i) * P:(2 * pair + i + 1) * P],
                                                           qk[u][:, at:at + 2, :].rearrange("p h d -> p (h d)"), g.c("ident"))
                        last.then_inc(qk_turned[u], 1)

                    def dots(u, n, which):
                        if which[0] == 0:
                            pe.wait_ge(qkT_saved[u], n + 1)
                            pe.wait_ge(v_silu[u], n + 1)
                        for hh in which:
                            r, pair = half_rows(hh), hh // 2
                            last = nc.tensor.matmul(bank[u][hh % 2][:, pair * 256:pair * 256 + 256], qkT[u][r, 2 * pair, :],
                                                    qkT[u][r, 2 * pair:2 * pair + 2, :].rearrange("p a t -> p (a t)"),
                                                    start=True, stop=True)
                        if which[-1] == HG - 1:
                            last.then_inc(dots_ready[u], 1)

                    def turn_Y(u, n):
                        pe.wait_ge(gate_silu[u], n + 1)
                        pe.wait_ge(Y_ready[u], n + 1)
                        for hh in range(HG):
                            last = nc.tensor.transpose(bank[u][2][:, hh * P:(hh + 1) * P], Y[u][:, hh, :], g.c("ident"))
                        last.then_inc(Y_turned[u], 1)

                    def turn_X(u, n, k):
                        pe.wait_ge(merged[u], n * LEVELS + k)
                        for hh in range(HG):
                            last = nc.tensor.transpose(bank[u][2][:, hh * P:(hh + 1) * P], X[u][:, hh, :], g.c("ident"))
                        last.then_inc(X_turned[u], 1)

                    def products_NX(u, n, k):
                        if k == 0:
                            pe.wait_ge(mixT_begun[u], n + 1)
                            pe.wait_ge(X_ready[u], n + 1)
                        for hh in range(HG):
                            last = nc.tensor.matmul(bank[u][0][live(k), hh * HALF:(hh + 1) * HALF], NT[u][:, hh, live(k)],
                                                    left(X[u][:, hh, :], k), start=True, stop=True)
                        last.then_inc(W_ready[u], 1)

                    def products_XW(u, n, k):
                        if k > 0:
                            pe.wait_ge(Y_saved[u], n * LEVELS + k)
                        pe.wait_ge(W_masked[u], n * LEVELS + k + 1)
                        for hh in range(HG):
                            last = nc.tensor.matmul(bank[u][1][live(k), hh * HALF:(hh + 1) * HALF], Y[u][:, hh, live(k)],
                                                    W[u][:, hh, :], start=True, stop=True)
                        last.then_inc(XW_ready[u], 1)

                    def solve(u, n):
                        pe.wait_ge(Y_saved[u], (n + 1) * LEVELS)
                        if u == 1:
                            pe.wait_ge(rhs_ready, n + 1)
                        for hh in range(HG):
                            last = nc.tensor.matmul(bank[u][2][:, hh * P:(hh + 1) * P], Y[u][:, hh, :], rhs[u][:, hh, :],
                                                    start=True, stop=True)
                        last.then_inc(solved[u], 1)

                    def mix(u, n):
                        pe.wait_ge(mixT_ready[u], n + 1)
                        pe.wait_ge(delta_ready[u], n + 1)
                        for hh in range(HG):
                            last = nc.tensor.matmul(bank[u][3][:, hh * P:(hh + 1) * P], mixT[u][:, hh, :], t1[u][:, hh, :],
                                                    start=True, stop=True)
                        last.then_inc(out_ready[u], 1)

                    def new_state(n):
                        pe.wait_ge(kfade_ready, n + 1)
                        for hh in range(HG):
                            last = nc.tensor.matmul(bank[0][2][half_rows(hh), (hh // 2) * DV:(hh // 2 + 1) * DV], kfade[:, hh, :],
                                                    t1[0][:, hh, :], start=True, stop=True)
                        last.then_inc(state_ready, 1)

                    def read_state(n, half):
                        if half == 0:
                            pe.wait_ge(state_saved, n + 1)
                        else:
                            pe.wait_ge(read_saved, n * 2 + 1)
                        for pair in range(HG // 2):
                            for i in range(2):
                                last = nc.tensor.matmul(bank[1][3][:, (2 * i + pair) * DV:(2 * i + pair + 1) * DV],
                                                        qkT[1][half_rows(half), 2 * pair + i, :], state[half_rows(half), pair, :],
                                                        start=True, stop=True)
                        last.then_inc(read_ready, 1)

                    def turn_y(u, n):
                        pe.wait_ge(y_ready[u], n + 1)
                        for hh in range(HG):
                            last = nc.tensor.transpose(bank[u][3][:, hh * P:(hh + 1) * P], X[u][:, hh, :], g.c("ident"))
                        last.then_inc(y_turned[u], 1)

                    def project_out(u, n):
                        pe.wait_ge(yT_saved[u], n + 1)
                        for hh in range(HG):
                            last = nc.tensor.matmul(bank[u][3][:, 0:D], Y[u][:, hh, :],
                                                    wo[:, bass.ds(group(n) * HG + hh, 1), :], start=(hh == 0), stop=(hh == HG - 1))
                        last.then_inc(projected[u], 1)

                    def prepare(u, n):
                        project_qk(u, n, range(L1A_TAPS))
                        decays(u, n)
                        project_v(u, n, range(L1A_TAPS))
                        project_gate(u, n)
                        turn_qk(u, n)
                        dots(u, n, range(HG))

                    def phase(at, n, other, done, ahead):
                        if at is None:
                            solve(other, done)
                            mix(other, done)
                            turn_y(other, done)
                            project_out(other, done)
                            return
                        if ahead is not None:
                            project_qk(other, ahead, [0, 1])
                        if done is not None:
                            solve(other, done)
                        turn_Y(at, n)
                        if ahead is not None:
                            project_qk(other, ahead, [2])
                        products_NX(at, n, 0)
                        if ahead is not None:
                            project_qk(other, ahead, [3])
                        products_XW(at, n, 0)
                        if ahead is not None:
                            decays(other, ahead)
                        if done is not None:
                            mix(other, done)
                        turn_X(at, n, 1)
                        products_NX(at, n, 1)
                        if done is not None and other == 0:
                            new_state(done)
                        if ahead is not None:
                            project_v(other, ahead, [0])
                        products_XW(at, n, 1)
                        if ahead is not None:
                            project_v(other, ahead, [1])
                        turn_X(at, n, 2)
                        products_NX(at, n, 2)
                        if at == 1:
                            read_state(n, 0)
                        if ahead is not None:
                            project_gate(other, ahead)
                        products_XW(at, n, 2)
                        if ahead is not None:
                            project_v(other, ahead, [2])
                        turn_X(at, n, 3)
                        products_NX(at, n, 3)
                        if at == 1:
                            read_state(n, 1)
                        if ahead is not None:
                            project_v(other, ahead, [3])
                        products_XW(at, n, 3)
                        if done is not None:
                            turn_y(other, done)
                        turn_X(at, n, 4)
                        products_NX(at, n, 4)
                        if ahead is not None:
                            turn_qk(other, ahead)
                        products_XW(at, n, 4)
                        if done is not None:
                            project_out(other, done)
                        turn_X(at, n, 5)
                        products_NX(at, n, 5)
                        if ahead is not None:
                            dots(other, ahead, range(0, HG // 2))
                        products_XW(at, n, 5)
                        if ahead is not None:
                            dots(other, ahead, range(HG // 2, HG))
                        turn_X(at, n, 6)

                    run(pe, lambda: prepare(0, 0), phase)

                @block.scalar
                def _(act):
                    def tanh_qk(u, n):
                        act.wait_ge(qk_projected[u], n + 1)
                        nc.scalar.activation(flat(t0[u]), bank[u][0][:, :], ACT.Tanh).then_inc(qk_tanh[u], 1)

                    def tanh_v(u, n):
                        act.wait_ge(v_projected[u], n + 1)
                        nc.scalar.activation(flat(t1[u]), bank[u][1][:, :], ACT.Tanh).then_inc(v_tanh[u], 1)

                    def tanh_gate(u, n):
                        act.wait_ge(gate_projected[u], n + 1)
                        nc.scalar.activation(flat(t2[u]), bank[u][2][:, :], ACT.Tanh, scale=0.5).then_inc(gate_tanh[u], 1)

                    def square(u, n):
                        act.wait_ge(qk_silu[u], n + 1)
                        nc.scalar.activation(flat(t0[u]), flat(qk[u]), ACT.Square).then_inc(squared[u], 1)

                    def exp_decays(u, n):
                        act.wait_ge(diff_ready[u], n + 1)
                        nc.scalar.activation(flat(fade[u]), bank[u][1][:, :], ACT.Exp).then_inc(fade_done[u], 1)

                    def save_qkT(u, n):
                        act.wait_ge(qk_turned[u], n + 1)
                        nc.scalar.copy(flat(qkT[u]), bank[u][0][:, :]).then_inc(qkT_saved[u], 1)

                    def save_X(u, n):
                        act.wait_ge(Y_turned[u], n + 1)
                        nc.scalar.copy(flat(X[u]), bank[u][2][:, :]).then_inc(X_ready[u], 1)

                    def save_Y(u, n, k):
                        act.wait_ge(X_turned[u], n * LEVELS + k)
                        nc.scalar.copy(flat(Y[u]), bank[u][2][:, :]).then_inc(Y_saved[u], 1)

                    def save_state(n):
                        act.wait_ge(state_ready, n + 1)
                        nc.scalar.copy(flat(state), bank[0][2][:, 0:2 * DV]).then_inc(state_saved, 1)

                    def save_out(n):
                        act.wait_ge(out_ready[0], n + 1)
                        nc.scalar.copy(flat(X[0]), bank[0][3][:, :]).then_inc(o_saved[0], 1)

                    def square_out(u, n):
                        act.wait_ge(o_saved[u], n + 1)
                        nc.scalar.activation(flat(Y[u]), flat(X[u]), ACT.Square).then_inc(o_squared[u], 1)

                    def save_yT(u, n):
                        act.wait_ge(y_turned[u], n + 1)
                        nc.scalar.copy(flat(Y[u]), bank[u][3][:, :]).then_inc(yT_saved[u], 1)

                    def prepare(u, n):
                        tanh_qk(u, n)
                        exp_decays(u, n)
                        square(u, n)
                        tanh_v(u, n)
                        tanh_gate(u, n)
                        save_qkT(u, n)

                    def phase(at, n, other, done, ahead):
                        if at is None:
                            square_out(other, done)
                            save_yT(other, done)
                            return
                        save_X(at, n)
                        if ahead is not None:
                            tanh_qk(other, ahead)
                            exp_decays(other, ahead)
                        if done is not None and other == 0:
                            save_out(done)
                        save_Y(at, n, 1)
                        if done is not None:
                            square_out(other, done)
                            if other == 0:
                                save_state(done)
                        save_Y(at, n, 2)
                        if ahead is not None:
                            square(other, ahead)
                            tanh_gate(other, ahead)
                        save_Y(at, n, 3)
                        if ahead is not None:
                            tanh_v(other, ahead)
                        if done is not None:
                            save_yT(other, done)
                        save_Y(at, n, 4)
                        if ahead is not None:
                            save_qkT(other, ahead)
                        save_Y(at, n, 5)
                        save_Y(at, n, 6)

                    run(act, lambda: prepare(0, 0), phase)

                @block.gpsimd
                def _(pool):
                    def load_x(u, n):
                        if u == 0:
                            pool.wait_ge(pad_clear, 1)
                            nc.gpsimd.tensor_copy(xpad[0][:, PAD:PAD + P], XT[:, bass.ds(tile_of(u, n) * P, P)]).then_inc(xpad_ready[u], 1)
                        else:
                            nc.gpsimd.tensor_copy(xpad[1][:, :], XT[:, bass.ds(tile_of(u, n) * P - PAD, P + PAD)]).then_inc(xpad_ready[u], 1)

                    def decay_terms(u, n):
                        nc.gpsimd.tensor_tensor(terms[u][:, :, :], over_heads(g.c("upto")), heads(at_gate(decay, u, n), P),
                                                ALU.mult).then_inc(terms_ready[u], 1)

                    def invert_length(u, n):
                        pool.wait_ge(length_step[u], n * 2 + 2)
                        nc.gpsimd.tensor_tensor(length[u][:, :], length[u][:, :], g.c("minus_half")[:, 0:2 * HG],
                                                ALU.pow).then_inc(length_ready[u], 1)

                    def fade_beta(u, n):
                        pool.wait_ge(fade_done[u], n + 1)
                        nc.gpsimd.tensor_tensor(terms[u][:, :, :], fade[u][:, :, :], heads(at_gate(beta, u, n), P),
                                                ALU.mult).then_inc(faded_beta[u], 1)

                    def fade_k(n):
                        pool.wait_ge(unit[0], n + 1)
                        nc.gpsimd.tensor_tensor(kfade[:, :, :], qk[0][:, HG:2 * HG, :],
                                                fade[0][:, :, P - 1:P].broadcast_to([P, HG, DK]), ALU.mult).then_inc(kfade_ready, 1)

                    def mask_mixT(u, n):
                        pool.wait_ge(mixT_begun[u], n + 1)
                        nc.gpsimd.tensor_tensor(mixT[u][:, :, :], mixT[u][:, :, :], over_heads(g.c("upto")),
                                                ALU.mult).then_inc(mixT_ready[u], 1)

                    def invert_ms(u, n):
                        pool.wait_ge(ms_step[u], n * 2 + 2)
                        nc.gpsimd.tensor_tensor(ms[u][:, :], ms[u][:, :], g.c("minus_half")[:, 0:HG], ALU.pow).then_inc(ms_ready[u], 1)

                    def gate_out(u, n):
                        pool.wait_ge(o_normed[u], n + 1)
                        nc.gpsimd.tensor_tensor(X[u][:, :, :], X[u][:, :, :], gate[u][:, :, :], ALU.mult).then_inc(y_ready[u], 1)

                    def prepare(u, n):
                        load_x(u, n)
                        decay_terms(u, n)
                        invert_length(u, n)
                        fade_beta(u, n)
                        if u == 0:
                            fade_k(n)

                    def phase(at, n, other, done, ahead):
                        if ahead is not None:
                            load_x(other, ahead)
                            decay_terms(other, ahead)
                        if at is not None:
                            mask_mixT(at, n)
                        if done is not None:
                            invert_ms(other, done)
                            gate_out(other, done)
                        if ahead is not None:
                            invert_length(other, ahead)
                            fade_beta(other, ahead)
                            if other == 0:
                                fade_k(ahead)

                    def first():
                        nc.gpsimd.memset(xpad[0][:, 0:PAD], 0.0).then_inc(pad_clear, 1)
                        prepare(0, 0)

                    run(pool, first, phase)

                @block.vector
                def _(dve):
                    def silu(dst, tanh, src, u, done):
                        nc.vector.scalar_tensor_tensor(flat(dst[u]), flat(tanh[u]), 1.0, src[:, :], ALU.add, ALU.mult).then_inc(done[u], 1)

                    def silu_qk(u, n):
                        dve.wait_ge(qk_tanh[u], n + 1)
                        silu(qk, t0, bank[u][0], u, qk_silu)

                    def silu_v(u, n):
                        dve.wait_ge(v_tanh[u], n + 1)
                        silu(rhs, t1, bank[u][1], u, v_silu)

                    def silu_gate(u, n, done):
                        if done is not None:
                            dve.wait_ge(y_ready[u], done + 1)
                        dve.wait_ge(gate_tanh[u], n + 1)
                        silu(gate, t2, bank[u][2], u, gate_silu)

                    def lengths(u, n):
                        dve.wait_ge(squared[u], n + 1)
                        nc.vector.tensor_reduce(length[u][:, :], flat(t0[u]).rearrange("p (h d) -> p h d", d=DK), AX.X,
                                                ALU.add).then_inc(length_step[u], 1)
                        dve.wait_ge(length_step[u], n * 2 + 1)
                        nc.vector.scalar_tensor_tensor(length[u][:, :], length[u][:, :], 1e-6, g.c("dk_scale"), ALU.add,
                                                       ALU.mult).then_inc(length_step[u], 1)

                    def to_unit(u, n):
                        dve.wait_ge(length_ready[u], n + 1)
                        nc.vector.tensor_tensor(qk[u][:, :, :], qk[u][:, :, :], heads(length[u][:, :], DK), ALU.mult).then_inc(unit[u], 1)

                    def fade_dots(u, n):
                        dve.wait_ge(faded_beta[u], n + 1)
                        dve.wait_ge(dots_ready[u], n + 1)
                        for half in range(2):
                            kk = bank[u][half][:, :].rearrange("p (a k t) -> p a k t", a=2, k=2)[:, :, 0, :]
                            last = nc.vector.tensor_tensor(parity(NT[u], half), kk, parity(terms[u], half), ALU.mult)
                        last.then_inc(NT_ready[u], 1)

                    def begin_mixT(u, n):
                        for half in range(2):
                            kq = bank[u][half][:, :].rearrange("p (a k t) -> p a k t", a=2, k=2)[:, :, 1, :]
                            last = nc.vector.tensor_tensor(parity(mixT[u], half), kq, parity(fade[u], half), ALU.mult)
                        last.then_inc(mixT_begun[u], 1)

                    def begin_Y(u, n, done):
                        if done is not None:
                            dve.wait_ge(projected[u], done + 1)
                        dve.wait_ge(NT_ready[u], n + 1)
                        nc.vector.tensor_tensor(Y[u][:, :, :], NT[u][:, :, :], over_heads(g.c("level1nT")),
                                                ALU.mult).then_inc(Y_begun[u], 1)

                    def add_one(u, n):
                        dve.wait_ge(Y_begun[u], n + 1)
                        nc.vector.tensor_tensor(Y[u][:, :, :], Y[u][:, :, :], over_heads(g.c("ident")), ALU.add).then_inc(Y_ready[u], 1)

                    def mask_W(u, n, k):
                        dve.wait_ge(W_ready[u], n * LEVELS + k + 1)
                        nc.vector.tensor_tensor(W[u][:, :, :], bank[u][0][:, 0:HG * HALF].rearrange("p (h t) -> p h t", h=HG),
                                                g.c("level")[:, k * HALF:(k + 1) * HALF].unsqueeze(1).broadcast_to([P, HG, HALF]),
                                                ALU.mult).then_inc(W_masked[u], 1)

                    def merge(u, n, k):
                        x = left(flat(X[u]), k)[live(k), :, :]
                        dve.wait_ge(XW_ready[u], n * LEVELS + k + 1)
                        nc.vector.tensor_tensor(x, x, bank[u][1][live(k), 0:HG * HALF].rearrange("p (i s) -> p i s", s=2 << k),
                                                ALU.subtract).then_inc(merged[u], 1)

                    def delta(u, n):
                        dve.wait_ge(solved[u], n + 1)
                        nc.vector.tensor_tensor(t1[u][:, :, :], by_head(bank[u][2]), heads(at_gate(beta, u, n), P),
                                                ALU.mult).then_inc(delta_ready[u], 1)

                    def take_read(n, half):
                        dve.wait_ge(read_ready, n * 2 + half + 1)
                        for i, dst in ((0, read_k), (1, read_q)):
                            src = bank[1][3][:, i * 256:i * 256 + 256].rearrange("p (a d) -> p a d", a=2)
                            last = nc.vector.tensor_tensor(parity(dst, half), src, heads(at_gate(grown, 1, n)[:, half:HG:2], DV), ALU.mult)
                        last.then_inc(read_saved, 1)

                    def subtract_read(n):
                        dve.wait_ge(read_saved, n * 2 + 2)
                        nc.vector.tensor_tensor(flat(rhs[1]), flat(rhs[1]), flat(read_k), ALU.subtract).then_inc(rhs_ready, 1)

                    def add_read(n):
                        dve.wait_ge(out_ready[1], n + 1)
                        nc.vector.tensor_tensor(flat(X[1]), bank[1][3][:, :], flat(read_q), ALU.add).then_inc(o_saved[1], 1)

                    def mean_square(u, n):
                        dve.wait_ge(o_squared[u], n + 1)
                        nc.vector.tensor_reduce(ms[u][:, :], Y[u][:, :, :], AX.X, ALU.add).then_inc(ms_step[u], 1)
                        dve.wait_ge(ms_step[u], n * 2 + 1)
                        nc.vector.tensor_scalar(ms[u][:, :], ms[u][:, :], 1.0 / DV, 1e-5, ALU.mult, ALU.add).then_inc(ms_step[u], 1)

                    def norm(u, n):
                        dve.wait_ge(ms_ready[u], n + 1)
                        nc.vector.tensor_tensor(X[u][:, :, :], X[u][:, :, :], heads(ms[u][:, :], DV), ALU.mult).then_inc(o_normed[u], 1)

                    def add(u, n):
                        x = g.tile(tile_of(u, n)).rearrange("p t d -> p (t d)")
                        dve.wait_ge(projected[u], n + 1)
                        nc.vector.tensor_tensor(x, x, bank[u][3][:, 0:D], ALU.add)

                    def prepare(u, n):
                        silu_qk(u, n)
                        lengths(u, n)
                        to_unit(u, n)
                        silu_v(u, n)
                        silu_gate(u, n, None)
                        fade_dots(u, n)
                        begin_mixT(u, n)
                        begin_Y(u, n, None)
                        add_one(u, n)

                    def phase(at, n, other, done, ahead):
                        if at is None:
                            delta(other, done)
                            add_read(done)
                            mean_square(other, done)
                            norm(other, done)
                            add(other, done)
                            return
                        mask_W(at, n, 0)
                        if done is not None:
                            delta(other, done)
                        merge(at, n, 0)
                        if done is not None and other == 1:
                            add_read(done)
                        mask_W(at, n, 1)
                        if done is not None:
                            mean_square(other, done)
                        merge(at, n, 1)
                        if done is not None:
                            norm(other, done)
                        if ahead is not None:
                            silu_qk(other, ahead)
                        mask_W(at, n, 2)
                        if at == 1:
                            take_read(n, 0)
                        if ahead is not None:
                            lengths(other, ahead)
                        merge(at, n, 2)
                        mask_W(at, n, 3)
                        if ahead is not None:
                            to_unit(other, ahead)
                        if at == 1:
                            take_read(n, 1)
                        merge(at, n, 3)
                        if ahead is not None:
                            silu_gate(other, ahead, done)
                            silu_v(other, ahead)
                        mask_W(at, n, 4)
                        if at == 1:
                            subtract_read(n)
                        merge(at, n, 4)
                        mask_W(at, n, 5)
                        merge(at, n, 5)
                        if ahead is not None:
                            fade_dots(other, ahead)
                            begin_Y(other, ahead, done)
                            add_one(other, ahead)
                            begin_mixT(other, ahead)
                        if done is not None:
                            add(other, done)

                    run(dve, lambda: prepare(0, 0), phase)


def turn_stream(nc, g, name, XT, wide=None, wide_out=None):
    NS = 4
    n = wide.shape[1] if wide is not None else 0
    with Stage(nc, name + "_turn") as st:
        xn = [st.sb(f"xn{s}", [P, D]) for s in range(NS)]
        xt = [st.sb(f"xt{s}", [P, P]) for s in range(NS)]
        turn = [st.ps(f"turn{s}", [P, 512]) for s in range(NS)]
        prod = st.ps("prod", [P, max(512, TILES * n)])
        slot_free = st.sems("slot_free", NS)
        xn_ready = st.sems("xn_ready", NS)
        turned = st.sems("turned", NS)
        xt_ready = st.sems("xt_ready", NS)
        xt_used = st.sems("xt_used", NS)
        prod_saved = st.sem("prod_saved")
        with nc.Block() as block:
            @block.vector
            def _(dve):
                for s in range(NS):
                    dve.sem_inc(slot_free[s], 1)
                with dve.Fori(0, TILES // NS) as it:
                    for s in range(NS):
                        t = it * NS + s
                        dve.wait_ge(slot_free[s], it + 1)
                        nc.vector.tensor_scalar(xn[s][:, :], g.tile(t), g.mean[:, bass.ds(t, 1)],
                                                g.rstd[:, bass.ds(t, 1)], ALU.subtract, ALU.mult).then_inc(xn_ready[s], 1)
                if n:
                    for s in range(NS):
                        dve.wait_ge(xt_used[s], TILES // NS + 1)
                    nc.vector.tensor_copy(wide_out.rearrange("p t n -> p (t n)"), prod[:, 0:TILES * n]).then_inc(prod_saved, 1)

            @block.tensor
            def _(pe):
                with pe.Fori(0, TILES // NS) as it:
                    for s in range(NS):
                        pe.wait_ge(xn_ready[s], it + 1)
                        nc.tensor.transpose(turn[s][:, 0:P], xn[s][:, :], g.c("ident")).then_inc(turned[s], 1)
                    if n:
                        for s in range(NS):
                            pe.wait_ge(xt_ready[s], it + 1)
                            nc.tensor.matmul(prod[:, bass.ds((it * NS + s) * n, n)], xt[s][:, :], wide, start=True,
                                             stop=True).then_inc(xt_used[s], 1)

            @block.scalar
            def _(act):
                for s in range(NS):
                    act.sem_inc(xt_used[s], 1)
                with act.Fori(0, TILES // NS) as it:
                    for s in range(NS):
                        act.wait_ge(turned[s], it + 1)
                        if n:
                            act.wait_ge(xt_used[s], it + 1)
                        nc.scalar.copy(xt[s][:, :], turn[s][:, 0:P]).then_inc(xt_ready[s], 1)

            @block.gpsimd
            def _(pool):
                with pool.Fori(0, TILES // NS) as it:
                    for s in range(NS):
                        pool.wait_ge(xt_ready[s], it + 1)
                        nc.gpsimd.tensor_copy(XT[:, bass.ds((it * NS + s) * P, P)], xt[s][:, :]).then_inc(slot_free[s], 1)


L2_EXPERTS, L2_SHARED, L2_TOP = 8, 2, 2
L2F_ALL = L2_EXPERTS + L2_SHARED
L2F_PARTS = [("gate", L2_EXPERTS), ("bias", L2_EXPERTS), ("w1", L2F_ALL * 128), ("w3", L2F_ALL * 128),
             ("w2", L2F_ALL * 128)]


def l2_ffn(nc, g, name):
    E, EA = L2_EXPERTS, L2F_ALL
    cols, width = columns(L2F_PARTS)
    N = 512
    JT = N // P
    NS = 2
    USES = EA // NS
    with Stage(nc, name) as st:
        w = st.sb("w", [P, width])
        XT = st.sb("XT", [P, TOKENS])
        logits = st.sb("logits", [P, TILES, E])
        gate = st.sb("gate", [P, TILES, E])
        row_statistics(nc, g, name, [(w[:, :], g.dram["w_l2f"])])
        turn_stream(nc, g, name, XT, w[:, cols["gate"]], logits[:, :, :])

        with Stage(nc, name + "_gate") as sg:
            top = sg.sb("top", [P, TILES])
            score = sg.sb("score", [P, TILES, E])
            picked = sg.sb("picked", [P, TILES, E])
            above = sg.sb("above", [P, TILES, E, E])
            equal = sg.sb("equal", [P, TILES, E, E])
            rank = sg.sb("rank", [P, TILES, E])
            step = sg.sem("step")
            shifted = sg.sem("shifted")
            exped = sg.sem("exped")

            def each(a):
                return a.unsqueeze(2).broadcast_to([P, TILES, E])

            mine = picked[:, :, :].unsqueeze(3).broadcast_to([P, TILES, E, E])
            other = picked[:, :, :].unsqueeze(2).broadcast_to([P, TILES, E, E])
            before = g.c("before8").rearrange("p (e j) -> p e j", e=E).unsqueeze(1).broadcast_to([P, TILES, E, E])
            with nc.Block() as block:
                @block.vector
                def _(dve):
                    nc.vector.tensor_reduce(top[:, :], logits[:, :, :], AX.X, ALU.max).then_inc(step, 1)
                    dve.wait_ge(step, 1)
                    nc.vector.tensor_tensor(score[:, :, :], logits[:, :, :], each(top[:, :]),
                                            ALU.subtract).then_inc(shifted, 1)
                    dve.wait_ge(exped, 1)
                    nc.vector.tensor_reduce(top[:, :], score[:, :, :], AX.X, ALU.add).then_inc(step, 1)
                    dve.wait_ge(step, 2)
                    nc.vector.reciprocal(top[:, :], top[:, :]).then_inc(step, 1)
                    dve.wait_ge(step, 3)
                    nc.vector.tensor_tensor(score[:, :, :], score[:, :, :], each(top[:, :]), ALU.mult).then_inc(step, 1)
                    dve.wait_ge(step, 4)
                    nc.vector.tensor_tensor(picked[:, :, :], score[:, :, :],
                                            w[:, cols["bias"]].unsqueeze(1).broadcast_to([P, TILES, E]),
                                            ALU.add).then_inc(step, 1)
                    dve.wait_ge(step, 5)
                    nc.vector.tensor_tensor(above[:, :, :, :], other, mine, ALU.is_gt).then_inc(step, 1)
                    nc.vector.tensor_tensor(equal[:, :, :, :], other, mine, ALU.is_equal).then_inc(step, 1)
                    dve.wait_ge(step, 7)
                    nc.vector.tensor_tensor(equal[:, :, :, :], equal[:, :, :, :], before, ALU.mult).then_inc(step, 1)
                    dve.wait_ge(step, 8)
                    nc.vector.tensor_tensor(above[:, :, :, :], above[:, :, :, :], equal[:, :, :, :],
                                            ALU.add).then_inc(step, 1)
                    dve.wait_ge(step, 9)
                    nc.vector.tensor_reduce(rank[:, :, :], above[:, :, :, :], AX.X, ALU.add).then_inc(step, 1)
                    dve.wait_ge(step, 10)
                    nc.vector.tensor_scalar(rank[:, :, :], rank[:, :, :], float(L2_TOP), 0.5, ALU.is_lt,
                                            ALU.mult).then_inc(step, 1)
                    dve.wait_ge(step, 11)
                    nc.vector.tensor_tensor(gate[:, :, :], rank[:, :, :], score[:, :, :], ALU.mult).then_inc(step, 1)

                @block.scalar
                def _(act):
                    act.wait_ge(shifted, 1)
                    nc.scalar.activation(score[:, :, :], score[:, :, :], ACT.Exp).then_inc(exped, 1)

        with Stage(nc, name + "_mix") as sm:
            silu = [sm.sb(f"silu{s}", [P, N]) for s in range(NS)]
            hid = [sm.sb(f"hid{s}", [P, N]) for s in range(NS)]
            up1 = [sm.ps(f"up1{s}", [P, N]) for s in range(NS)]
            up3 = [sm.ps(f"up3{s}", [P, N]) for s in range(NS)]
            down = [sm.ps(f"down{s}", [P, N]) for s in range(NS)]
            up1_ready = sm.sems("up1_ready", NS)
            up3_ready = sm.sems("up3_ready", NS)
            silu_done = sm.sems("silu_done", NS)
            hid_ready = sm.sems("hid_ready", NS)
            down_ready = sm.sems("down_ready", NS)
            mixed = sm.sems("mixed", NS)
            with nc.Block() as block:
                @block.tensor
                def _(pe):
                    def up_1(it, e):
                        s = e % NS
                        nc.tensor.matmul(up1[s][:, :], w[:, cols["w1"]][:, e * P:(e + 1) * P], XT[:, bass.ds(it * N, N)], start=True,
                                         stop=True).then_inc(up1_ready[s], 1)

                    def up_3(it, e):
                        s = e % NS
                        nc.tensor.matmul(up3[s][:, :], w[:, cols["w3"]][:, e * P:(e + 1) * P], XT[:, bass.ds(it * N, N)], start=True,
                                         stop=True).then_inc(up3_ready[s], 1)

                    def turn_down(it, e):
                        s, use = e % NS, it * USES + e // NS + 1
                        pe.wait_ge(hid_ready[s], use)
                        pe.wait_ge(mixed[s], use)
                        for j in range(JT):
                            last = nc.tensor.matmul(down[s][:, j * D:(j + 1) * D], hid[s][:, j * P:(j + 1) * P],
                                                    w[:, cols["w2"]][:, e * D:(e + 1) * D], start=True, stop=True)
                        last.then_inc(down_ready[s], 1)

                    for s in range(NS):
                        pe.sem_inc(mixed[s], 1)
                    with pe.Fori(0, TOKENS // N) as it:
                        up_1(it, 0)
                        up_3(it, 0)
                        for e in range(1, EA):
                            up_1(it, e)
                            turn_down(it, e - 1)
                            up_3(it, e)
                        turn_down(it, EA - 1)

                @block.scalar
                def _(act):
                    with act.Fori(0, TOKENS // N) as it:
                        for e in range(EA):
                            s, use = e % NS, it * USES + e // NS + 1
                            act.wait_ge(up1_ready[s], use)
                            nc.scalar.activation(silu[s][:, :], up1[s][:, :], ACT.Silu).then_inc(silu_done[s], 1)

                @block.vector
                def _(dve):
                    def gated(it, e):
                        s, use = e % NS, it * USES + e // NS + 1
                        dve.wait_ge(silu_done[s], use)
                        dve.wait_ge(up3_ready[s], use)
                        nc.vector.tensor_tensor(hid[s][:, :], silu[s][:, :], up3[s][:, :], ALU.mult).then_inc(hid_ready[s], 1)

                    def mix(it, e):
                        s, use = e % NS, it * USES + e // NS + 1
                        dve.wait_ge(down_ready[s], use)
                        dve.wait_ge(mixed[1 - s], use + s)
                        if e < E:
                            for j in range(JT):
                                t = it * JT + j
                                last = nc.vector.scalar_tensor_tensor(
                                    g.tile(t), down[s][:, j * D:(j + 1) * D], gate[:, bass.ds(t, 1), e:e + 1], g.tile(t),
                                    ALU.mult, ALU.add)
                        else:
                            x = g.X[:, bass.ds(it * JT, JT), :].rearrange("p t d -> p (t d)")
                            last = nc.vector.scalar_tensor_tensor(x, down[s][:, :], 0.5, x, ALU.mult, ALU.add)
                        last.then_inc(mixed[s], 1)

                    with dve.Fori(0, TOKENS // N) as it:
                        gated(it, 0)
                        for e in range(1, EA):
                            gated(it, e)
                            mix(it, e - 1)
                        mix(it, EA - 1)


BF16 = mybir.dt.bfloat16
RMS_EPS = 1e-6


def rms_scales(nc, g, name, scale_out):
    NS = 4
    with Stage(nc, name + "_rms") as st:
        x1 = [st.sb(f"x1{s}", [P, D]) for s in range(NS)]
        square = [st.sb(f"square{s}", [P, D]) for s in range(NS)]
        ss = st.sb("ss", [P, TILES])
        slot_free = st.sems("slot_free", NS)
        x1_ready = st.sems("x1_ready", NS)
        rooted = st.sem("rooted")
        step = st.sem("step")
        with nc.Block() as block:
            @block.vector
            def _(dve):
                for s in range(NS):
                    dve.sem_inc(slot_free[s], 1)
                with dve.Fori(0, TILES // NS) as it:
                    for s in range(NS):
                        t = it * NS + s
                        dve.wait_ge(slot_free[s], it + 1)
                        nc.vector.tensor_scalar(x1[s][:, :], g.tile(t), g.mean[:, bass.ds(t, 1)],
                                                g.rstd[:, bass.ds(t, 1)], ALU.subtract, ALU.mult).then_inc(x1_ready[s], 1)
                dve.wait_ge(rooted, 1)
                nc.vector.reciprocal(ss[:, :], ss[:, :]).then_inc(step, 1)
                dve.wait_ge(step, 1)
                nc.vector.tensor_tensor(scale_out, ss[:, :], g.rstd[:, :], ALU.mult).then_inc(step, 1)

            @block.scalar
            def _(act):
                with act.Fori(0, TILES // NS) as it:
                    for s in range(NS):
                        act.wait_ge(x1_ready[s], it + 1)
                        nc.scalar.activation(square[s][:, :], x1[s][:, :], ACT.Square,
                                             accum_out=ss[:, bass.ds(it * NS + s, 1)]).then_inc(slot_free[s], 1)
                for s in range(NS):
                    act.wait_ge(slot_free[s], TILES // NS + 1)
                nc.scalar.activation(ss[:, :], ss[:, :], ACT.Sqrt, scale=1.0 / D, bias=g.c("eps_l2")).then_inc(rooted, 1)


L2A_HEADS, L2A_HD = 16, 8
L2A_PARTS = [("wq", D), ("wk", D), ("wv", D), ("wo", D), ("norm", D), ("bv", D), ("bo", D), ("bq", 1), ("bk", 1)]


def l2_attn(nc, g, name):
    H, HD = L2A_HEADS, L2A_HD
    cols, width = columns(L2A_PARTS)
    SCALE = float(HD) ** -0.5
    N = SEQ
    PAIRS = H // 2
    SHIFT = P + HD
    with Stage(nc, name) as st:
        w = st.sb("w", [P, width])
        scale = st.sb("scale", [P, TILES])
        row_statistics(nc, g, name, [(w[:, :], g.dram["w_l2a"])])
        rms_scales(nc, g, name, scale[:, :])
        Y = range(2)
        ident_b = st.ctx.enter_context(nc.sbuf_tensor(name + "_ident_b", [P, P], BF16))
        causal_b = st.ctx.enter_context(nc.sbuf_tensor(name + "_causal_b", [P, P], BF16))
        kT = [st.sb(f"kT{y}", [P, N]) for y in Y]
        q16 = [st.sb(f"q16{y}", [P, H, N]) for y in Y]
        vm = [st.sb(f"vm{y}", [P, TPB, H * SHIFT]) for y in Y]
        x0 = st.sb("x0", [P, TPB, D])
        xn = st.sb("xn", [P, TPB, D])
        xT = st.sb("xT", [P, N])
        qT = st.sb("qT", [P, N])
        oT = st.sb("oT", [P, N])
        low = [st.sb(f"low{s}", [P, TPB, 2]) for s in range(2)]
        bias = [st.sb(f"bias{s}", [P, TPB, 2]) for s in range(2)]
        den = [st.sb(f"den{s}", [P, TPB, 2]) for s in range(4)]
        prob = [st.sb(f"prob{s}", [P, 2, 3 * P]) for s in range(4)]
        probT = [st.sb(f"probT{s}", [P, 6, P]) for s in range(2)]
        misc = st.ps("misc", [P, 512])
        O = st.ps("O", [P, 512])
        wideS = [st.ps(f"wideS{s}", [P, 512]) for s in range(2)]
        slimS = [st.ps(f"slimS{s}", [P, 512]) for s in range(2)]
        wideT = st.ps("wideT", [P, 512])
        slimT = st.ps("slimT", [P, 512])
        cast = st.sem("cast")
        x0_ready = st.sem("x0_ready")
        xn_ready = st.sem("xn_ready")
        xn_added = st.sem("xn_added")
        turned = st.sem("turned")
        xT_ready = st.sem("xT_ready")
        qk_ready = st.sem("qk_ready")
        qk_saved = st.sem("qk_saved")
        q16_ready = st.sem("q16_ready")
        v_ready = st.sem("v_ready")
        v_saved = st.sem("v_saved")
        s_ready = st.sem("s_ready")
        low_ready = st.sem("low_ready")
        bias_ready = st.sem("bias_ready")
        exp_done = st.sem("exp_done")
        inverted = st.sem("inverted")
        normed = st.sem("normed")
        pT_ready = st.sem("pT_ready")
        wide_saved = st.sem("wide_saved")
        slim_saved = st.sem("slim_saved")
        pv_done = st.sem("pv_done")
        oT_saved = st.sem("oT_saved")
        out_ready = st.sem("out_ready")
        out_added = st.sem("out_added")

        def count(pair):
            return pair[0] * PAIRS + pair[1] + 1

        def run(engine, start, step, between):
            def pairs(b, y, first=False, last=False):
                for i in range(PAIRS):
                    at = [(b, i - d, y) if i >= d else None if first else (b - 1, PAIRS + i - d, 1 - y) for d in range(3)]
                    step(*at)
                    between(b, i, y, first, last)

            start()
            pairs(0, 0, first=True)
            with engine.Fori(0, BATCH // 2 - 1) as it:
                pairs(it * 2 + 1, 1)
                pairs(it * 2 + 2, 0)
            pairs(BATCH - 1, 1, last=True)
            step(None, (BATCH - 1, PAIRS - 1, 1), (BATCH - 1, PAIRS - 2, 1))
            step(None, None, (BATCH - 1, PAIRS - 1, 1))

        with nc.Block() as block:
            @block.vector
            def _(dve):
                def batch_of(b):
                    return g.X[:, bass.ds(b * TPB, TPB), :].rearrange("p u d -> p (u d)")

                def norm_tokens(b):
                    for u in range(TPB):
                        t = b * TPB + u
                        last = nc.vector.tensor_scalar(x0[:, u, :], g.tile(t), g.mean[:, bass.ds(t, 1)],
                                                       scale[:, bass.ds(t, 1)], ALU.subtract, ALU.mult)
                    last.then_inc(x0_ready, 1)
                    dve.wait_ge(x0_ready, b + 1)
                    nc.vector.tensor_tensor(xn[:, :, :], x0[:, :, :], w[:, cols["norm"]].unsqueeze(1).broadcast_to([P, TPB, D]),
                                            ALU.mult).then_inc(xn_ready, 1)
                    dve.wait_ge(xn_ready, b + 1)
                    nc.vector.tensor_tensor(batch_of(b), batch_of(b), xn[:, :, :].rearrange("p u d -> p (u d)"),
                                            ALU.add).then_inc(xn_added, 1)

                def add_out(b):
                    dve.wait_ge(out_ready, b + 1)
                    dve.wait_ge(xn_added, b + 1)
                    nc.vector.tensor_tensor(batch_of(b), batch_of(b), misc[:, 256:512], ALU.add).then_inc(out_added, 1)

                def shift(pair):
                    s, n = pair[1] % 2, count(pair)
                    dve.wait_ge(s_ready, n)
                    nc.vector.tensor_reduce(low[s][:, 0, :], slimS[s][:, 0:2 * P].rearrange("p (h k) -> p h k", h=2), AX.X,
                                            ALU.max, negate=True)
                    nc.vector.tensor_reduce(low[s][:, 1, :], wideS[s][:, :].rearrange("p (h k) -> p h k", h=2), AX.X,
                                            ALU.max, negate=True).then_inc(low_ready, 1)
                    dve.wait_ge(low_ready, n)
                    nc.vector.tensor_scalar(bias[s][:, :, :], low[s][:, :, :], SCALE, None, ALU.mult).then_inc(bias_ready, 1)

                def divide(pair):
                    s, n = pair[1] % 4, count(pair)
                    dve.wait_ge(exp_done, n)
                    nc.vector.reciprocal(den[s][:, :, :], den[s][:, :, :]).then_inc(inverted, 1)
                    dve.wait_ge(inverted, n)
                    for hh in range(2):
                        for u, part in ((0, prob[s][:, hh, 0:P]), (1, prob[s][:, hh, P:3 * P])):
                            last = nc.vector.tensor_scalar(part, part, den[s][:, u, hh:hh + 1], None, ALU.mult)
                    last.then_inc(normed, 1)

                def save(pair):
                    dve.wait_ge(pT_ready, count(pair))
                    nc.vector.tensor_copy(probT[pair[1] % 2][:, 4:6, :], slimT[:, 0:2 * P].rearrange("p (b q) -> p b q", b=2)
                                          ).then_inc(slim_saved, 1)

                def start():
                    nc.vector.tensor_copy(ident_b[:, :], g.c("ident")).then_inc(cast, 1)
                    nc.vector.tensor_copy(causal_b[:, :], g.c("causal")).then_inc(cast, 1)
                    norm_tokens(0)

                def step(now, before, earlier):
                    if earlier is not None:
                        save(earlier)
                    if before is not None:
                        divide(before)
                    if now is not None:
                        shift(now)

                def between(b, i, y, first, last):
                    if i == 1 and not last:
                        norm_tokens(b + 1)
                    if i == 3 and not first:
                        add_out(b - 1)

                run(dve, start, step, between)
                add_out(BATCH - 1)

            @block.tensor
            def _(pe):
                def turn_tokens(b):
                    pe.wait_ge(xn_ready, b + 1)
                    for u in range(TPB):
                        last = nc.tensor.transpose(misc[:, u * P:(u + 1) * P], xn[:, u, :], g.c("ident"))
                    last.then_inc(turned, 1)

                def project_qk(b):
                    pe.wait_ge(xT_ready, b + 1)
                    nc.tensor.matmul(misc[:, 0:N], w[:, cols["wq"]], xT[:, :], start=True, stop=True)
                    nc.tensor.matmul(misc[:, N:2 * N], w[:, cols["wk"]], xT[:, :], start=True, stop=True).then_inc(qk_ready, 1)

                def project_v(b):
                    pe.wait_ge(qk_saved, b + 1)
                    for u in range(TPB):
                        o = misc[:, u * D:(u + 1) * D]
                        nc.tensor.matmul(o, xT[:, u * P:(u + 1) * P], w[:, cols["wv"]], start=True, stop=False)
                        last = nc.tensor.matmul(o, g.c("ones")[0:1, :], w[0:1, cols["bv"]], start=False, stop=True)
                    last.then_inc(v_ready, 1)

                def project_out(b):
                    pe.wait_ge(oT_saved, b + 1)
                    for u in range(TPB):
                        o = misc[:, 256 + u * D:256 + (u + 1) * D]
                        nc.tensor.matmul(o, oT[:, u * P:(u + 1) * P], w[:, cols["wo"]], start=True, stop=False)
                        last = nc.tensor.matmul(o, g.c("ones")[0:1, :], w[0:1, cols["bo"]], start=False, stop=True)
                    last.then_inc(out_ready, 1)

                def scores(pair, earlier):
                    b, i, y = pair
                    s = i % 2
                    if i % (PAIRS // 2) == 0:
                        pe.wait_ge(q16_ready, b * 2 + i // (PAIRS // 2) + 1)
                    if earlier is not None:
                        pe.wait_ge(exp_done, count(earlier))
                    for hh in range(2):
                        q = q16[y][:, 2 * i + hh, :]
                        o = wideS[s][:, hh * 256:hh * 256 + 256]
                        nc.tensor.matmul(o[:, 0:P], q[:, P:2 * P], kT[y][:, 0:P], start=True, stop=True)
                        nc.tensor.matmul(o[:, P:2 * P], q[:, P:2 * P], kT[y][:, P:2 * P], start=True, stop=False)
                        nc.tensor.matmul(o[:, P:2 * P], ident_b[:, :], causal_b[:, :], start=False, stop=True)
                        o = slimS[s][:, hh * P:hh * P + P]
                        nc.tensor.matmul(o, q[:, 0:P], kT[y][:, 0:P], start=True, stop=False)
                        last = nc.tensor.matmul(o, ident_b[:, :], causal_b[:, :], start=False, stop=True)
                    last.then_inc(s_ready, 1)

                def turn(pair):
                    pe.wait_ge(normed, count(pair))
                    for n in range(6):
                        o = wideT[:, n * P:n * P + P] if n < 4 else slimT[:, (n - 4) * P:(n - 3) * P]
                        last = nc.tensor.transpose(o, prob[pair[1] % 4][:, n // 3, (n % 3) * P:(n % 3) * P + P], g.c("ident"))
                    last.then_inc(pT_ready, 1)

                def weigh(pair, first):
                    b, i, y = pair
                    t = probT[i % 2]
                    pe.wait_ge(wide_saved, count(pair))
                    pe.wait_ge(slim_saved, count(pair))
                    if i == 0:
                        pe.wait_ge(v_saved, b + 1)
                        if not first:
                            pe.wait_ge(oT_saved, b)
                    for hh in range(2):
                        h = 2 * i + hh
                        nc.tensor.matmul(O[:, 0:N], vm[y][:, 0, h * P:(h + 1) * P],
                                         t[:, 3 * hh:3 * hh + 2, :].rearrange("p b q -> p (b q)"), start=(h == 0), stop=False)
                        last = nc.tensor.matmul(O[:, P:N], vm[y][:, 1, h * P:(h + 1) * P], t[:, 3 * hh + 2, :],
                                                start=False, stop=(h == H - 1))
                    last.then_inc(pv_done, 1)

                def start():
                    pe.wait_ge(cast, 4)
                    turn_tokens(0)
                    project_qk(0)
                    project_v(0)

                def step(now, before, earlier):
                    if earlier is not None:
                        turn(earlier)
                    if now is not None:
                        scores(now, earlier)
                    if earlier is not None:
                        weigh(earlier, isinstance(earlier[0], int) and earlier[0] == 0)

                def between(b, i, y, first, last):
                    if i == 2 and not first:
                        project_out(b - 1)
                    if i == 3 and not last:
                        if not first:
                            pe.wait_ge(out_added, b)
                        turn_tokens(b + 1)
                    if i == 4 and not last:
                        project_qk(b + 1)
                    if i == 5 and not last:
                        project_v(b + 1)

                run(pe, start, step, between)
                project_out(BATCH - 1)

            @block.scalar
            def _(act):
                def save_tokens(b):
                    act.wait_ge(turned, b + 1)
                    nc.scalar.copy(xT[:, :], misc[:, 0:N]).then_inc(xT_ready, 1)

                def save_qk(b, y):
                    act.wait_ge(qk_ready, b + 1)
                    nc.scalar.activation(kT[y][:, :], misc[:, N:2 * N], ACT.Identity, bias=w[:, cols["bk"]])
                    nc.scalar.activation(qT[:, :], misc[:, 0:N], ACT.Identity, bias=w[:, cols["bq"]]).then_inc(qk_saved, 1)

                def save_v(b, y):
                    act.wait_ge(v_ready, b + 1)
                    nc.scalar.copy(vm[y][:, :, :].rearrange("p u (h x) -> p u h x", x=SHIFT)[:, :, :, 0:HD],
                                   misc[:, 0:TPB * D].rearrange("p (u h e) -> p u h e", u=TPB, e=HD)).then_inc(v_saved, 1)

                def save_out(b):
                    act.wait_ge(pv_done, b * PAIRS + PAIRS)
                    nc.scalar.copy(oT[:, :], O[:, 0:N]).then_inc(oT_saved, 1)

                def exps(pair):
                    i = pair[1]
                    s, p = i % 2, prob[i % 4]
                    act.wait_ge(bias_ready, count(pair))
                    for hh in range(2):
                        nc.scalar.activation(p[:, hh, 0:P], slimS[s][:, hh * P:hh * P + P], ACT.Exp, scale=SCALE,
                                             bias=bias[s][:, 0, hh:hh + 1], accum_out=den[i % 4][:, 0, hh:hh + 1])
                        last = nc.scalar.activation(p[:, hh, P:3 * P], wideS[s][:, hh * 256:hh * 256 + 256], ACT.Exp,
                                                    scale=SCALE, bias=bias[s][:, 1, hh:hh + 1], accum_out=den[i % 4][:, 1, hh:hh + 1])
                    last.then_inc(exp_done, 1)

                def save(pair):
                    act.wait_ge(pT_ready, count(pair))
                    nc.scalar.copy(probT[pair[1] % 2][:, 0:4, :], wideT[:, :].rearrange("p (b q) -> p b q", b=4)).then_inc(wide_saved, 1)

                def start():
                    save_tokens(0)
                    save_qk(0, 0)
                    act.wait_ge(cast, 4)
                    save_v(0, 0)

                def step(now, before, earlier):
                    if before is not None:
                        exps(before)
                    if earlier is not None:
                        save(earlier)

                def between(b, i, y, first, last):
                    if i == 2 and not first:
                        save_out(b - 1)
                    if i == 4 and not last:
                        save_tokens(b + 1)
                    if i == 5 and not last:
                        save_qk(b + 1, 1 - y)
                    if i == 6 and not last:
                        save_v(b + 1, 1 - y)

                run(act, start, step, between)
                save_out(BATCH - 1)

            @block.gpsimd
            def _(pool):
                def queries(b, y):
                    pool.wait_ge(qk_saved, b + 1)
                    for half in range(2):
                        h = slice(half * H // 2, (half + 1) * H // 2)
                        nc.gpsimd.tensor_tensor(q16[y][:, h, :], qT[:, :].unsqueeze(1).broadcast_to([P, H // 2, N]),
                                                g.c("heads8")[:, h].unsqueeze(2).broadcast_to([P, H // 2, N]),
                                                ALU.mult).then_inc(q16_ready, 1)

                for y in Y:
                    nc.gpsimd.memset(vm[y][:, :, :], 0.0).then_inc(cast, 1)
                queries(0, 0)
                with pool.Fori(0, BATCH // 2 - 1) as it:
                    queries(it * 2 + 1, 1)
                    queries(it * 2 + 2, 0)
                queries(BATCH - 1, 1)


L3_HID = 512
L3_C = L3_HID // P
L3F_PARTS = [("w1", L3_HID), ("w2", L3_HID), ("h1", L3_C * L3_HID), ("h2", L3_C * L3_HID), ("w3", L3_C * D),
             ("s1", L3_C), ("s2", L3_C), ("sh1", L3_C), ("sh2", L3_C), ("s3", D)]


def l3_ffn(nc, g, name):
    cols, width = columns(L3F_PARTS)
    C = L3_C
    N = 512
    JT = N // P
    NS = 2
    with Stage(nc, name) as st:
        w = st.sb("w", [P, width])
        XT = st.sb("XT", [P, TOKENS])
        row_statistics(nc, g, name, [(w[:, :], g.dram["w_l3f"])])
        turn_stream(nc, g, name, XT)
        h1 = w[:, cols["h1"]].rearrange("p (k o) -> p k o", k=C)
        h2 = w[:, cols["h2"]].rearrange("p (k o) -> p k o", k=C)
        w3 = w[:, cols["w3"]].rearrange("p (k o) -> p k o", k=C)
        silu = [st.sb(f"silu{s}", [P, C, N]) for s in range(NS)]
        hid = [st.sb(f"hid{s}", [P, C, N]) for s in range(NS)]
        gelu1 = [st.sb(f"gelu1{s}", [P, C, N]) for s in range(NS)]
        gelu2 = [st.sb(f"gelu2{s}", [P, C, N]) for s in range(NS)]
        scaled = [st.sb(f"scaled{s}", [P, N]) for s in range(NS)]
        bank = [[st.ps(f"bank{s}_{c}", [P, N]) for c in range(C)] for s in range(NS)]
        slot_free = st.sems("slot_free", NS)
        a_ready = st.sems("a_ready", NS)
        b_ready = st.sems("b_ready", NS)
        silu_done = st.sems("silu_done", NS)
        hid_ready = st.sems("hid_ready", NS)
        sq1_ready = st.sems("sq1_ready", NS)
        gelu1_done = st.sems("gelu1_done", NS)
        sq2_ready = st.sems("sq2_ready", NS)
        gelu2_done = st.sems("gelu2_done", NS)
        out_ready = st.sems("out_ready", NS)
        scale_done = st.sems("scale_done", NS)
        with nc.Block() as block:
            @block.tensor
            def _(pe):
                for s in range(NS):
                    pe.sem_inc(slot_free[s], 1)
                with pe.Fori(0, TOKENS // N // NS) as it:
                    for c in range(C):
                        for s in range(NS):
                            x = XT[:, bass.ds((it * NS + s) * N, N)]
                            if c == 0:
                                pe.wait_ge(slot_free[s], it + 1)
                            if c >= 2:
                                pe.wait_ge(hid_ready[s], it * C + c - 1)
                            nc.tensor.matmul(bank[s][c % 2][:, :], w[:, cols["w1"]][:, c * P:(c + 1) * P], x, start=True,
                                             stop=True).then_inc(a_ready[s], 1)
                            nc.tensor.matmul(bank[s][2 + c % 2][:, :], w[:, cols["w2"]][:, c * P:(c + 1) * P], x, start=True,
                                             stop=True).then_inc(b_ready[s], 1)
                    for layer, src, needs, ready in ((h1, hid, hid_ready, sq1_ready), (h2, gelu1, gelu1_done, sq2_ready)):
                        for s in range(NS):
                            pe.wait_ge(needs[s], it * C + C)
                            for c in range(C):
                                for k in range(C):
                                    last = nc.tensor.matmul(bank[s][c][:, :], layer[:, k, c * P:(c + 1) * P], src[s][:, k, :],
                                                            start=(k == 0), stop=(k == C - 1))
                                last.then_inc(ready[s], 1)
                    for s in range(NS):
                        pe.wait_ge(gelu2_done[s], it * C + C)
                        for j in range(JT):
                            for k in range(C):
                                last = nc.tensor.matmul(bank[s][0][:, j * D:(j + 1) * D], gelu2[s][:, k, j * P:(j + 1) * P],
                                                        w3[:, k, :], start=(k == 0), stop=(k == C - 1))
                        last.then_inc(out_ready[s], 1)

            @block.scalar
            def _(act):
                with act.Fori(0, TOKENS // N // NS) as it:
                    for c in range(C):
                        for s in range(NS):
                            act.wait_ge(a_ready[s], it * C + c + 1)
                            nc.scalar.activation(silu[s][:, c, :], bank[s][c % 2][:, :], ACT.Silu,
                                                 scale=w[:, cols["s1"]][:, c:c + 1]).then_inc(silu_done[s], 1)
                    for dst, scale, ready, done in ((gelu1, "sh1", sq1_ready, gelu1_done), (gelu2, "sh2", sq2_ready, gelu2_done)):
                        for s in range(NS):
                            for c in range(C):
                                act.wait_ge(ready[s], it * C + c + 1)
                                nc.scalar.activation(dst[s][:, c, :], bank[s][c][:, :], ACT.Gelu,
                                                     scale=w[:, cols[scale]][:, c:c + 1]).then_inc(done[s], 1)

            @block.vector
            def _(dve):
                with dve.Fori(0, TOKENS // N // NS) as it:
                    for c in range(C):
                        for s in range(NS):
                            dve.wait_ge(silu_done[s], it * C + c + 1)
                            dve.wait_ge(b_ready[s], it * C + c + 1)
                            nc.vector.scalar_tensor_tensor(hid[s][:, c, :], bank[s][2 + c % 2][:, :],
                                                           w[:, cols["s2"]][:, c:c + 1], silu[s][:, c, :],
                                                           ALU.mult, ALU.mult).then_inc(hid_ready[s], 1)
                    for s in range(NS):
                        dve.wait_ge(out_ready[s], it + 1)
                        nc.vector.tensor_tensor(scaled[s][:, :].rearrange("p (j d) -> p j d", j=JT),
                                                bank[s][0][:, :].rearrange("p (j d) -> p j d", j=JT),
                                                w[:, cols["s3"]].unsqueeze(1).broadcast_to([P, JT, D]),
                                                ALU.mult).then_inc(scale_done[s], 1)
                    for s in range(NS):
                        x = g.X[:, bass.ds((it * NS + s) * JT, JT), :].rearrange("p t d -> p (t d)")
                        dve.wait_ge(scale_done[s], it + 1)
                        nc.vector.scalar_tensor_tensor(x, scaled[s][:, :], 0.5, x, ALU.mult, ALU.add).then_inc(slot_free[s], 1)


L3A_HEADS, L3A_HD, L3A_TAPS, L3A_INNER = 16, 8, 4, 345
L3A_ALPHA_BIAS = 4.0
L3A_PARTS = [("wq", D), ("wk", D), ("wv", D), ("wba", 2 * L3A_HEADS), ("wo", D), ("wg", L3A_INNER), ("wu", L3A_INNER),
             ("wd", 3 * D), ("norm1", D), ("norm2", D), ("taps", L3A_TAPS), ("conv_b", 1)]


def l3_attn(nc, g, name):
    H, HD = L3A_HEADS, L3A_HD
    cols, width = columns(L3A_PARTS)
    N = SEQ
    NS = 2
    NF = 4
    G = BATCH * H // P
    STEP = 32
    ROUNDS = SEQ // STEP
    PAD = L3A_TAPS - 1
    inner = [(c * P, min(P, L3A_INNER - c * P)) for c in range(3)]
    with Stage(nc, name) as st:
        w = st.sb("w", [P, width])
        scale = st.sb("scale", [P, TILES])
        row_statistics(nc, g, name, [(w[:, :], g.dram["w_l3a"])])
        rms_scales(nc, g, name, scale[:, :])
        qkv_d = nc.dram_tensor(name + "_qkv", (3, BATCH, P, N), F32, kind="Internal").ap()
        gates_d = nc.dram_tensor(name + "_gates", (2, BATCH, H, N), F32, kind="Internal").ap()
        o_d = nc.dram_tensor(name + "_o", (BATCH, P, N), F32, kind="Internal").ap()

        with Stage(nc, name + "_a") as sa:
            x0 = [sa.sb(f"x0{s}", [P, TPB, D]) for s in range(NF)]
            xn = [sa.sb(f"xn{s}", [P, TPB, D]) for s in range(NF)]
            xT = [sa.sb(f"xT{s}", [P, PAD + N]) for s in range(NF)]
            conv = [sa.sb(f"conv{s}", [P, L3A_TAPS, N]) for s in range(NF)]
            xc = [sa.sb(f"xc{s}", [P, N]) for s in range(NF)]
            qkv = [sa.sb(f"qkv{s}", [P, 3, N]) for s in range(NF)]
            gates = [sa.sb(f"gates{s}", [2 * H, N]) for s in range(NF)]
            qk = [sa.ps(f"qk{s}", [P, 512]) for s in range(NF)]
            vg = [sa.ps(f"vg{s}", [P, 512]) for s in range(NF)]
            x0_ready = sa.sems("x0_ready", NF)
            xn_ready = sa.sems("xn_ready", NF)
            turned = sa.sems("turned", NF)
            xT_ready = sa.sems("xT_ready", NF)
            conv_step = sa.sems("conv_step", NF)
            xc_ready = sa.sems("xc_ready", NF)
            proj_ready = sa.sems("proj_ready", NF)
            saved = sa.sems("saved", NF)
            stored = sa.sems("stored", NF)
            with nc.Block() as block:
                @block.vector
                def _(dve):
                    for s in range(NF):
                        nc.vector.memset(xT[s][:, 0:PAD], 0.0).then_inc(conv_step[s], 1)
                    with dve.Fori(0, BATCH // NF) as it:
                        for s in range(NF):
                            for u in range(TPB):
                                t = (it * NF + s) * TPB + u
                                last = nc.vector.tensor_scalar(x0[s][:, u, :], g.tile(t), g.mean[:, bass.ds(t, 1)],
                                                               scale[:, bass.ds(t, 1)], ALU.subtract, ALU.mult)
                            last.then_inc(x0_ready[s], 1)
                        for s in range(NF):
                            dve.wait_ge(x0_ready[s], it + 1)
                            nc.vector.tensor_tensor(xn[s][:, :, :], x0[s][:, :, :],
                                                    w[:, cols["norm1"]].unsqueeze(1).broadcast_to([P, TPB, D]),
                                                    ALU.mult).then_inc(xn_ready[s], 1)
                        for j in range(L3A_TAPS):
                            for s in range(NF):
                                tap = w[:, cols["taps"]][:, j:j + 1]
                                if j == 0:
                                    dve.wait_ge(xT_ready[s], it + 1)
                                    nc.vector.tensor_scalar(conv[s][:, 0, :], xT[s][:, 0:N], tap, w[:, cols["conv_b"]],
                                                            ALU.mult, ALU.add).then_inc(conv_step[s], 1)
                                else:
                                    dve.wait_ge(conv_step[s], it * L3A_TAPS + j + 1)
                                    nc.vector.scalar_tensor_tensor(conv[s][:, j, :], xT[s][:, j:j + N], tap,
                                                                   conv[s][:, j - 1, :], ALU.mult, ALU.add
                                                                   ).then_inc(conv_step[s], 1)

                @block.tensor
                def _(pe):
                    for s in range(NF):
                        pe.sem_inc(saved[s], 1)
                        pe.sem_inc(stored[s], 1)
                    with pe.Fori(0, BATCH // NF) as it:
                        for s in range(NF):
                            pe.wait_ge(xn_ready[s], it + 1)
                            pe.wait_ge(saved[s], it + 1)
                            for u in range(TPB):
                                last = nc.tensor.transpose(qk[s][:, u * P:(u + 1) * P], xn[s][:, u, :], g.c("ident"))
                            last.then_inc(turned[s], 1)
                        for s in range(NF):
                            pe.wait_ge(xc_ready[s], it + 1)
                            nc.tensor.matmul(qk[s][:, 0:N], w[:, cols["wq"]], xc[s][:, :], start=True, stop=True)
                            nc.tensor.matmul(qk[s][:, N:2 * N], w[:, cols["wk"]], xc[s][:, :], start=True, stop=True)
                            nc.tensor.matmul(vg[s][:, 0:N], w[:, cols["wv"]], xc[s][:, :], start=True, stop=True)
                            nc.tensor.matmul(vg[s][0:2 * H, N:2 * N], w[:, cols["wba"]], xc[s][:, :], start=True,
                                             stop=True).then_inc(proj_ready[s], 1)

                @block.scalar
                def _(act):
                    with act.Fori(0, BATCH // NF) as it:
                        for s in range(NF):
                            if s == 0:
                                for z in range(NF):
                                    act.wait_ge(conv_step[z], 1)
                            act.wait_ge(turned[s], it + 1)
                            nc.scalar.copy(xT[s][:, PAD:PAD + N], qk[s][:, 0:N]).then_inc(xT_ready[s], 1)
                        for s in range(NF):
                            act.wait_ge(conv_step[s], it * L3A_TAPS + L3A_TAPS + 1)
                            nc.scalar.activation(xc[s][:, :], conv[s][:, L3A_TAPS - 1, :], ACT.Silu).then_inc(xc_ready[s], 1)
                        for s in range(NF):
                            act.wait_ge(proj_ready[s], it + 1)
                            act.wait_ge(stored[s], it * 48 + 1)
                            nc.scalar.copy(qkv[s][:, 0:2, :], qk[s][:, :].rearrange("p (k t) -> p k t", k=2))
                            nc.scalar.copy(qkv[s][:, 2, :], vg[s][:, 0:N])
                            nc.scalar.copy(gates[s][:, :], vg[s][0:2 * H, N:2 * N]).then_inc(saved[s], 1)

                @block.sync
                def _(sp):
                    with sp.Fori(0, BATCH // NF) as it:
                        for s in range(NF):
                            b = it * NF + s
                            sp.wait_ge(saved[s], it + 2)
                            sp.dma_start(qkv_d[:, bass.ds(b, 1), :, :].rearrange("k b p t -> p (k b) t"), qkv[s][:, :, :]
                                         ).then_inc(stored[s], 16)
                            for k in range(2):
                                sp.dma_start(gates_d[k, bass.ds(b, 1), :, :].rearrange("b h t -> (b h) t"),
                                             gates[s][k * H:(k + 1) * H, :]).then_inc(stored[s], 16)
                    for s in range(NF):
                        sp.wait_ge(stored[s], BATCH // NF * 48 + 1)

        with Stage(nc, name + "_s") as ss:
            qkv = ss.sb("qkv", [P, 3, G, HD, N])
            kg = ss.sb("kg", [P, G, HD, N])
            gates = ss.sb("gates", [P, 2, G, N])
            both = ss.sb("both", [P, G, N])
            length = ss.sb("length", [P, 2, G, N])
            hist = [ss.sb(f"hist{z}", [P, STEP + 1, G, HD, HD]) for z in range(2)]
            prod = ss.sb("prod", [P, G, HD, HD])
            kg_now, k_now, v_now = ([ss.sb(f"{n}_now{z}", [P, STEP, G, HD]) for z in range(2)] for n in ("kg", "k", "v"))
            alpha_now = [ss.sb(f"alpha_now{z}", [P, STEP, G]) for z in range(2)]
            pred = ss.sb("pred", [P, G, HD])
            delta = ss.sb("delta", [P, G, HD])
            outer = ss.sb("outer", [P, G, HD, HD])
            read = ss.sb("read", [P, STEP, HD, HD])
            o = ss.sb("o", [P, G, HD, N])
            loaded = ss.sem("loaded")
            gates_done = ss.sem("gates_done")
            step = ss.sem("step")
            squared = ss.sem("squared")
            rooted = ss.sem("rooted")
            done = ss.sems("done", G)
            round_loaded = ss.sem("round_loaded")
            round_done = ss.sem("round_done")
            read_done = ss.sem("read_done")
            summed = ss.sem("summed")
            stored = ss.sem("stored")
            q, k, v = (qkv[:, i, :, :, :] for i in range(3))
            CELLS = 5

            def over_d(a):
                return a.unsqueeze(2).broadcast_to([P, G, HD, N])

            with nc.Block() as block:
                @block.sync
                def _(sp):
                    for i in range(3):
                        sp.dma_start(qkv[:, i, :, :, :].rearrange("p g d t -> p g (d t)"),
                                     qkv_d[i].rearrange("(g b) (h d) t -> (b h) g (d t)", g=G, h=H)).then_inc(loaded, 16)
                    for i in range(2):
                        sp.dma_start(gates[:, i, :, :], gates_d[i].rearrange("(g b) h t -> (b h) g t", g=G)).then_inc(loaded, 16)
                    sp.wait_ge(summed, ROUNDS * G)
                    sp.dma_start(o_d.rearrange("(g b) (h d) t -> (b h) g (d t)", g=G, h=H),
                                 o[:, :, :, :].rearrange("p g d t -> p g (d t)")).then_inc(stored, 16)
                    sp.wait_ge(stored, 16)

                @block.scalar
                def _(act):
                    act.wait_ge(loaded, 80)
                    nc.scalar.activation(gates[:, 0, :, :], gates[:, 0, :, :], ACT.Sigmoid)
                    nc.scalar.activation(gates[:, 1, :, :], gates[:, 1, :, :], ACT.Sigmoid,
                                         bias=g.c("alpha_bias")).then_inc(gates_done, 1)
                    act.wait_ge(squared, 1)
                    nc.scalar.activation(length[:, :, :, :], length[:, :, :, :], ACT.Sqrt, bias=g.c("eps_l2")).then_inc(rooted, 1)

                    def load_round(R, z):
                        at = bass.ds(R * STEP, STEP)
                        for now, a in ((kg_now, kg), (k_now, k), (v_now, v)):
                            nc.scalar.copy(now[z][:, :, :, :], a[:, :, :, at].rearrange("p g d t -> p t g d"))
                        nc.scalar.copy(alpha_now[z][:, :, :], gates[:, 1, :, at].rearrange("p g t -> p t g")).then_inc(round_loaded, 1)

                    act.wait_ge(step, 9)
                    load_round(0, 0)
                    load_round(1, 1)
                    with act.Fori(0, ROUNDS // 2 - 1) as r:
                        for z in range(2):
                            act.wait_ge(round_done, r * 2 + z + 1)
                            load_round(r * 2 + 2 + z, z)

                @block.vector
                def _(dve):
                    square = hist[0][:, 0:STEP, :, :, :].rearrange("p s g a b -> p (s g a b)").rearrange(
                        "p (g d t) -> p g d t", g=G, d=HD)
                    dve.wait_ge(loaded, 80)
                    for i, a in enumerate((q, k)):
                        if i:
                            dve.wait_ge(step, 2)
                        nc.vector.tensor_tensor(square, a, a, ALU.mult).then_inc(step, 1)
                        dve.wait_ge(step, 2 * i + 1)
                        last = nc.vector.tensor_reduce(length[:, i, :, :], square.rearrange("p g d t -> p g t d"), AX.X, ALU.add)
                        last.then_inc(squared if i else step, 1)
                    dve.wait_ge(rooted, 1)
                    nc.vector.reciprocal(length[:, :, :, :], length[:, :, :, :]).then_inc(step, 1)
                    dve.wait_ge(step, 4)
                    nc.vector.tensor_tensor(q, q, over_d(length[:, 0, :, :]), ALU.mult)
                    nc.vector.tensor_tensor(k, k, over_d(length[:, 1, :, :]), ALU.mult).then_inc(step, 1)
                    dve.wait_ge(gates_done, 1)
                    nc.vector.tensor_tensor(v, v, over_d(gates[:, 0, :, :]), ALU.mult).then_inc(step, 1)
                    nc.vector.tensor_tensor(both[:, :, :], gates[:, 0, :, :], gates[:, 1, :, :], ALU.mult).then_inc(step, 1)
                    dve.wait_ge(step, 7)
                    nc.vector.tensor_tensor(kg[:, :, :, :], k, over_d(both[:, :, :]), ALU.mult).then_inc(step, 1)
                    nc.vector.memset(hist[1][:, STEP, :, :, :], 0.0).then_inc(step, 1)
                    dve.wait_ge(step, 9)

                    def along_k(a, z, i, gi):
                        return a[z][:, i, gi, :].unsqueeze(1).broadcast_to([P, HD, HD])

                    def cell(z, i):
                        old = hist[z][:, i, :, :, :] if i else hist[1 - z][:, STEP, :, :, :]
                        new = hist[z][:, i + 1, :, :, :]
                        for gi in range(G):
                            if i:
                                dve.wait_ge(done[gi], i * CELLS)
                            nc.vector.tensor_tensor(prod[:, gi, :, :], old[:, gi, :, :], along_k(kg_now, z, i, gi),
                                                    ALU.mult).then_inc(done[gi], 1)
                        for gi in range(G):
                            dve.wait_ge(done[gi], i * CELLS + 1)
                            nc.vector.tensor_reduce(pred[:, gi, :], prod[:, gi, :, :], AX.X, ALU.add, negate=True).then_inc(done[gi], 1)
                        for gi in range(G):
                            dve.wait_ge(done[gi], i * CELLS + 2)
                            nc.vector.tensor_tensor(delta[:, gi, :], pred[:, gi, :], v_now[z][:, i, gi, :], ALU.add).then_inc(done[gi], 1)
                        for gi in range(G):
                            dve.wait_ge(done[gi], i * CELLS + 3)
                            nc.vector.tensor_tensor(outer[:, gi, :, :], delta[:, gi, :].unsqueeze(2).broadcast_to([P, HD, HD]),
                                                    along_k(k_now, z, i, gi), ALU.mult).then_inc(done[gi], 1)
                        for gi in range(G):
                            dve.wait_ge(done[gi], i * CELLS + 4)
                            nc.vector.scalar_tensor_tensor(new[:, gi, :, :], old[:, gi, :, :], alpha_now[z][:, i, gi:gi + 1],
                                                           outer[:, gi, :, :], ALU.mult, ALU.add).then_inc(done[gi], 1)

                    def readout(R, gi):
                        dve.wait_ge(read_done, R * G + gi + 1)
                        nc.vector.tensor_reduce(o[:, gi, :, bass.ds(R * STEP, STEP)].rearrange("p d t -> p t d"),
                                                read[:, :, :, :], AX.X, ALU.add).then_inc(summed, 1)

                    def round_(R, z, earlier):
                        dve.wait_ge(round_loaded, R + 1)
                        for i in range(STEP):
                            cell(z, i)
                            if earlier is not None and i % (STEP // G) == STEP // G - 1:
                                readout(earlier, i // (STEP // G))
                        for gi in range(G):
                            dve.wait_ge(done[gi], STEP * CELLS)
                            dve.sem_clear(done[gi])
                        dve.sem_inc(round_done, 1)

                    round_(0, 0, None)
                    with dve.Fori(0, ROUNDS // 2 - 1) as r:
                        round_(r * 2 + 1, 1, r * 2)
                        round_(r * 2 + 2, 0, r * 2 + 1)
                    round_(ROUNDS - 1, 1, ROUNDS - 2)
                    for gi in range(G):
                        readout(ROUNDS - 1, gi)

                @block.gpsimd
                def _(pool):
                    def products(R, z):
                        pool.wait_ge(round_done, R + 1)
                        for gi in range(G):
                            if not (isinstance(R, int) and R == 0 and gi == 0):
                                pool.wait_ge(summed, R * G + gi)
                            qt = q[:, gi, :, bass.ds(R * STEP, STEP)].rearrange("p d t -> p t d").unsqueeze(
                                2).broadcast_to([P, STEP, HD, HD])
                            nc.gpsimd.tensor_tensor(read[:, :, :, :], hist[z][:, 1:STEP + 1, gi, :, :], qt,
                                                    ALU.mult).then_inc(read_done, 1)

                    products(0, 0)
                    with pool.Fori(0, ROUNDS // 2 - 1) as r:
                        products(r * 2 + 1, 1)
                        products(r * 2 + 2, 0)
                    products(ROUNDS - 1, 1)

        hid = st.sb("hid", [P, TILES, D])
        hscale = st.sb("hscale", [P, TILES])
        with Stage(nc, name + "_h") as sh:
            x1 = [sh.sb(f"x1{s}", [P, TPB, D]) for s in range(NS)]
            PARTS = 4
            per_part = BATCH // PARTS
            oT = sh.sb("oT", [P, BATCH, N])
            hs = [sh.sb(f"hs{s}", [P, TPB, D]) for s in range(NS)]
            square = [sh.sb(f"square{s}", [P, TPB, D]) for s in range(NS)]
            mix = [sh.ps(f"mix{s}", [P, 512]) for s in range(NS)]
            o_loaded = sh.sems("o_loaded", PARTS)
            squared = sh.sems("squared", NS)
            mix_ready = sh.sems("mix_ready", NS)
            x1_ready = sh.sems("x1_ready", NS)
            h_ready = sh.sems("h_ready", NS)
            rooted = sh.sem("rooted")
            with nc.Block() as block:
                @block.sync
                def _(sp):
                    for c in range(PARTS):
                        part = slice(c * per_part, (c + 1) * per_part)
                        sp.dma_start(oT[:, part, :], o_d[part, :, :].rearrange("b p t -> p b t")).then_inc(o_loaded[c], 16)

                @block.tensor
                def _(pe):
                    def project_heads(it, s):
                        if it > 0:
                            pe.wait_ge(h_ready[s], it)
                        b = it * NS + s
                        for u in range(TPB):
                            last = nc.tensor.matmul(mix[s][:, u * D:(u + 1) * D], oT[:, b, u * P:(u + 1) * P], w[:, cols["wo"]], start=True, stop=True)
                        last.then_inc(mix_ready[s], 1)

                    for c in range(PARTS):
                        pe.wait_ge(o_loaded[c], 16)
                        for it in range(c * per_part // NS, (c + 1) * per_part // NS):
                            for s in range(NS):
                                project_heads(it, s)

                @block.vector
                def _(dve):
                    with dve.Fori(0, BATCH // NS) as it:
                        for s in range(NS):
                            dve.wait_ge(mix_ready[s], it + 1)
                            for u in range(TPB):
                                t = (it * NS + s) * TPB + u
                                last = nc.vector.tensor_scalar(x1[s][:, u, :], g.tile(t), g.mean[:, bass.ds(t, 1)],
                                                               g.rstd[:, bass.ds(t, 1)], ALU.subtract, ALU.mult)
                            last.then_inc(x1_ready[s], 1)
                        for s in range(NS):
                            t = (it * NS + s) * TPB
                            dve.wait_ge(x1_ready[s], it + 1)
                            nc.vector.tensor_tensor(hid[:, bass.ds(t, TPB), :].rearrange("p u d -> p (u d)"),
                                                    x1[s][:, :, :].rearrange("p u d -> p (u d)"),
                                                    mix[s][:, 0:TPB * D], ALU.add).then_inc(h_ready[s], 1)
                    dve.wait_ge(rooted, 1)
                    nc.vector.reciprocal(hscale[:, :], hscale[:, :]).then_inc(rooted, 1)

                @block.scalar
                def _(act):
                    for s in range(NS):
                        act.sem_inc(squared[s], 1)
                    with act.Fori(0, BATCH // NS) as it:
                        for s in range(NS):
                            act.wait_ge(h_ready[s], it + 1)
                            act.wait_ge(squared[s], it + 1)
                            for u in range(TPB):
                                t = (it * NS + s) * TPB + u
                                last = nc.scalar.activation(square[s][:, u, :], hid[:, bass.ds(t, 1), :], ACT.Square,
                                                            accum_out=hscale[:, bass.ds(t, 1)])
                            last.then_inc(squared[s], 1)
                    for s in range(NS):
                        act.wait_ge(squared[s], BATCH // NS + 1)
                    nc.scalar.activation(hscale[:, :], hscale[:, :], ACT.Sqrt, scale=1.0 / D, bias=g.c("eps_l2")).then_inc(rooted, 1)

        with Stage(nc, name + "_f") as sf:
            h0 = [sf.sb(f"h0{s}", [P, D]) for s in range(NF)]
            hn = [sf.sb(f"hn{s}", [P, D]) for s in range(NF)]
            hT = [sf.sb(f"hT{s}", [P, P]) for s in range(NF)]
            silu = [sf.sb(f"silu{s}", [P, 3, P]) for s in range(NF)]
            act_ = [sf.sb(f"act{s}", [P, 3, P]) for s in range(NF)]
            total = [sf.sb(f"total{s}", [P, D]) for s in range(NF)]
            gate = [sf.ps(f"gate{s}", [P, 512]) for s in range(NF)]
            up = [sf.ps(f"up{s}", [P, 512]) for s in range(NF)]
            slot_free = sf.sems("slot_free", NF)
            h0_ready = sf.sems("h0_ready", NF)
            hn_ready = sf.sems("hn_ready", NF)
            turned = sf.sems("turned", NF)
            hT_ready = sf.sems("hT_ready", NF)
            gate_ready = sf.sems("gate_ready", NF)
            up_ready = sf.sems("up_ready", NF)
            silu_done = sf.sems("silu_done", NF)
            act_ready = sf.sems("act_ready", NF)
            down_ready = sf.sems("down_ready", NF)
            total_ready = sf.sems("total_ready", NF)
            with nc.Block() as block:
                @block.vector
                def _(dve):
                    for s in range(NF):
                        dve.sem_inc(slot_free[s], 1)
                    with dve.Fori(0, TILES // NF) as it:
                        for s in range(NF):
                            t = it * NF + s
                            dve.wait_ge(slot_free[s], it + 1)
                            nc.vector.tensor_scalar(h0[s][:, :], hid[:, bass.ds(t, 1), :], hscale[:, bass.ds(t, 1)], None,
                                                    ALU.mult).then_inc(h0_ready[s], 1)
                        for s in range(NF):
                            dve.wait_ge(h0_ready[s], it + 1)
                            nc.vector.tensor_tensor(hn[s][:, :], h0[s][:, :], w[:, cols["norm2"]], ALU.mult).then_inc(hn_ready[s], 1)
                        for s in range(NF):
                            dve.wait_ge(silu_done[s], it + 1)
                            dve.wait_ge(up_ready[s], it + 1)
                            for c, (at, m) in enumerate(inner):
                                last = nc.vector.tensor_tensor(act_[s][0:m, c, :], silu[s][0:m, c, :],
                                                               up[s][0:m, c * P:(c + 1) * P], ALU.mult)
                            last.then_inc(act_ready[s], 1)
                        for s in range(NF):
                            t = it * NF + s
                            dve.wait_ge(down_ready[s], it + 1)
                            nc.vector.tensor_tensor(total[s][:, :], up[s][:, 3 * P:4 * P],
                                                    hid[:, bass.ds(t, 1), :].rearrange("p t d -> p (t d)"), ALU.add
                                                    ).then_inc(total_ready[s], 1)
                        for s in range(NF):
                            t = it * NF + s
                            x = g.tile(t).rearrange("p t d -> p (t d)")
                            dve.wait_ge(total_ready[s], it + 1)
                            nc.vector.tensor_tensor(x, x, total[s][:, :], ALU.add).then_inc(slot_free[s], 1)

                @block.tensor
                def _(pe):
                    with pe.Fori(0, TILES // NF) as it:
                        for s in range(NF):
                            pe.wait_ge(hn_ready[s], it + 1)
                            nc.tensor.transpose(gate[s][:, 3 * P:4 * P], hn[s][:, :], g.c("ident")).then_inc(turned[s], 1)
                        for s in range(NF):
                            pe.wait_ge(hT_ready[s], it + 1)
                            for bank, part, done in ((gate[s], "wg", gate_ready[s]), (up[s], "wu", up_ready[s])):
                                for c, (at, m) in enumerate(inner):
                                    last = nc.tensor.matmul(bank[0:m, c * P:(c + 1) * P], w[:, cols[part]][:, at:at + m],
                                                            hT[s][:, :], start=True, stop=True)
                                last.then_inc(done, 1)
                        for s in range(NF):
                            pe.wait_ge(act_ready[s], it + 1)
                            for c, (at, m) in enumerate(inner):
                                last = nc.tensor.matmul(up[s][:, 3 * P:4 * P], act_[s][0:m, c, :],
                                                        w[0:m, cols["wd"]][:, c * D:(c + 1) * D], start=(c == 0), stop=(c == 2))
                            last.then_inc(down_ready[s], 1)

                @block.scalar
                def _(act):
                    with act.Fori(0, TILES // NF) as it:
                        for s in range(NF):
                            act.wait_ge(turned[s], it + 1)
                            nc.scalar.copy(hT[s][:, :], gate[s][:, 3 * P:4 * P]).then_inc(hT_ready[s], 1)
                        for s in range(NF):
                            act.wait_ge(gate_ready[s], it + 1)
                            for c, (at, m) in enumerate(inner):
                                last = nc.scalar.activation(silu[s][0:m, c, :], gate[s][0:m, c * P:(c + 1) * P], ACT.Silu)
                            last.then_inc(silu_done[s], 1)


PIPELINE = {0: (l0_ffn, "l0f"), 1: (l0_attn, "l0a"), 2: (l0_ffn, "l0f"),
            3: (l1_ffn, "l1f"), 4: (l1_attn, "l1a"), 5: (l1_ffn, "l1f"), 6: (l2_ffn, "l2f"), 7: (l2_attn, "l2a"), 8: (l2_ffn, "l2f"), 9: (l3_ffn, "l3f"), 10: (l3_attn, "l3a"),
            11: (l3_ffn, "l3f")}


def build(nc, dram, out):
    Stage.pool = [nc.alloc_semaphore(f"s{i}") for i in range(SEMAPHORES)]
    Stage.taken = 0
    with ExitStack() as ctx:
        g = Globals(nc, ctx, dram, out)
        load_stream(nc, g)
        for n in STEPS:
            step, name = PIPELINE[n]
            step(nc, g, f"{name}_{n}")
        store_stream(nc, g)


def constants():
    import numpy as np
    p = np.arange(P)[:, None]
    j = np.arange(P)[None, :]
    levels = []
    for k in range(1, 7):
        s = 1 << k
        c = np.arange(P // 2)[None, :]
        levels.append(p // s == 2 * (c // s) + 1)
    level1T = (j == p + 1) & (p % 2 == 0)
    rows = np.arange(P)[:, None]
    tables = {
        "ident": p == j, "ones": np.ones((P, P)), "iota": j + 0 * p, "rev_iota": P - j + 0 * p,
        "upto": p <= j, "after": p > j, "blocks8": p // 8 == j // 8, "heads8": p // 8 == np.arange(16)[None, :],
        "level1nT": -1.0 * level1T, "level": np.concatenate(levels, axis=1),
        "row_index": rows, "is_query": (rows % 8) < 4, "quarter": (rows % 32) // 8 == np.arange(4)[None, :],
        "minus_half": np.full((P, 8), -0.5),
        "dk_scale": np.where(np.arange(8) < L1A_HG, L1A_DK, 1.0) + 0.0 * p, "eps_ln": np.full((P, 1), LN_EPS), "eps_l2": np.full((P, 1), 1e-6),
        "causal": np.where(j <= p, 0.0, -1e30),
        "alpha_bias": np.full((P, 1), L3A_ALPHA_BIAS),
        "before8": np.broadcast_to((np.arange(8)[None, :] < np.arange(8)[:, None]).reshape(1, 64), (P, 64)),
    }
    return np.ascontiguousarray(np.concatenate([tables[n] for n, _ in CONST_PARTS], axis=1).astype(np.float32))


def lay_out(inputs):
    import numpy as np

    def rows(a):
        return np.broadcast_to(np.reshape(a, (1, -1)), (P, a.size))

    def side(*parts):
        return np.ascontiguousarray(np.concatenate(parts, axis=1))

    i = inputs
    arrays = {"x": np.ascontiguousarray(np.reshape(i["L0_attn_x"], (TOKENS, D))), "consts": constants()}
    we = np.reshape(np.transpose(i["L0_ffn_We"], (1, 0, 2)), (D, -1))
    arrays["w_l0f"] = side(i["L0_ffn_Wg"], we, rows(i["L0_ffn_bg"]))
    arrays["l0f_be"] = np.ascontiguousarray(i["L0_ffn_be"])
    w_phi = i["L0_attn_weights"]
    phi = np.zeros((L0A_HEADS, L0A_HD, L0A_HEADS, L0A_HD), np.float32)
    for h in range(L0A_HEADS):
        phi[h, :, h, :] = w_phi[h].T
    arrays["w_l0a"] = side(i["L0_attn_Wq"].T, i["L0_attn_Wk"].T, i["L0_attn_Wv"].T, phi.reshape(D, D),
                           rows(i["L0_attn_bv"]), i["L0_attn_bq"][:, None], i["L0_attn_bk"][:, None])

    def chunks(a):
        return np.reshape(np.transpose(np.reshape(a, (-1, P, a.shape[1])), (1, 0, 2)), (P, -1))

    w1 = np.reshape(np.transpose(i["L2_ffn_w1"], (2, 0, 1)), (D, -1))
    w3 = np.reshape(np.transpose(i["L2_ffn_w3"], (2, 0, 1)), (D, -1))
    w2 = np.reshape(np.transpose(i["L2_ffn_w2"], (2, 0, 1)), (P, -1))
    arrays["w_l2f"] = side(i["L2_ffn_gate_w"].T, rows(i["L2_ffn_gate_bias"]), w1, i["L2_ffn_sw1"].T,
                           w3, i["L2_ffn_sw3"].T, w2, chunks(i["L2_ffn_sw2"].T))
    arrays["w_l3f"] = side(i["L3_ffn_w1_w"].T, i["L3_ffn_w2_w"].T, chunks(i["L3_ffn_h1_w"].T), chunks(i["L3_ffn_h2_w"].T),
                           chunks(i["L3_ffn_w3_w"].T), *[i["L3_ffn_" + s][:, None].reshape(L3_C, P).T
                                                         for s in ("w1_s", "w2_s", "h1_s", "h2_s")],
                           rows(i["L3_ffn_w3_s"]))
    arrays["w_l2a"] = side(*[i["L2_attn_" + n].T for n in ("Wq", "Wk", "Wv", "Wo")], rows(i["L2_attn_norm_w"]),
                           rows(i["L2_attn_bv"]), rows(i["L2_attn_bo"]), i["L2_attn_bq"][:, None], i["L2_attn_bk"][:, None])
    down = np.zeros((3 * P, D), np.float32)
    down[:L3A_INNER] = i["L3_attn_wd"]
    arrays["w_l3a"] = side(i["L3_attn_wq"], i["L3_attn_wk"], i["L3_attn_wv"], i["L3_attn_wb"], i["L3_attn_wa"],
                           i["L3_attn_wo"], i["L3_attn_wg"], i["L3_attn_wu"], chunks(down), rows(i["L3_attn_norm1_w"]),
                           rows(i["L3_attn_norm2_w"]), i["L3_attn_conv_w"], i["L3_attn_conv_b"][:, None])
    null_k = i["L1_ffn_null_kv"][0, :, :, 0, :]
    null_k = np.reshape(np.transpose(np.reshape(null_k, (L1_G, L1_C, 2, L1_DH)), (2, 3, 0, 1)), (P, -1))
    w_kv = i["L1_ffn_w_kv"]

    def by_group(a):
        return np.reshape(np.transpose(a, (2, 0, 1)), (D, -1))

    wo = np.reshape(i["L1_ffn_w_out"], (L1_G, D, L1_C, P))
    arrays["w_l1f"] = side(i["L1_ffn_w_qr"].T, i["L1_ffn_w_kvr"].T, by_group(i["L1_ffn_w_q"]),
                           by_group(w_kv[:, :L1_DI]), by_group(w_kv[:, L1_DI:]),
                           np.reshape(np.transpose(wo, (3, 0, 2, 1)), (P, -1)), null_k, rows(i["L1_ffn_null_token"]))
    arrays["null_v"] = np.ascontiguousarray(np.reshape(i["L1_ffn_null_kv"][1], (L1_G, L1_DI)))

    def by_heads(q, k, v):
        return np.concatenate([np.reshape(a, (a.shape[0], L1A_GROUPS, -1)) for a in (q, k, v)], axis=2)

    arrays["w_l1a_qkv"] = np.ascontiguousarray(by_heads(i["L1_attn_w_q"], i["L1_attn_w_k"], i["L1_attn_w_v"]))
    taps = by_heads(i["L1_attn_conv_q"].T, i["L1_attn_conv_k"].T, i["L1_attn_conv_v"].T)
    arrays["l1a_taps"] = np.ascontiguousarray(np.transpose(taps, (1, 0, 2))).reshape(-1)
    arrays["w_l1a"] = side(i["L1_attn_w_a"], i["L1_attn_w_b"], i["L1_attn_w_g"], chunks(i["L1_attn_w_out"]),
                           rows(i["L1_attn_dt_bias"]), rows(i["L1_attn_A_log"]), i["L1_attn_norm_w"][:, None])
    return arrays


def kernel(**inputs):
    import numpy as np
    import concourse.bacc as bacc
    from concourse.bass_utils import run_bass_kernel_spmd

    nc = bacc.Bacc("TRN2", target_bir_lowering=False, num_devices=1)
    arrays = lay_out({k: np.asarray(v) for k, v in inputs.items()})
    dram = {k: nc.dram_tensor(f"in_{k}", a.shape, mybir.dt.from_np(a.dtype), kind="ExternalInput").ap()
            for k, a in arrays.items()}
    out = nc.dram_tensor("out_x", (TOKENS, D), F32, kind="ExternalOutput").ap()
    build(nc, dram, out)
    r = run_bass_kernel_spmd(nc, [{f"in_{k}": a for k, a in arrays.items()}], core_ids=[0])
    return np.reshape(r.results[0]["out_x"], (BATCH, SEQ, D))
```
